# Optimizing a Trainium2 kernel written in Bass

```python
import numpy as np
import jax
import jax.numpy as jnp

def _softmax(x, axis=-1):
    return jax.nn.softmax(x, axis=axis)

def _gelu(x):
    return jax.nn.gelu(x, approximate=True)

def _silu(x):
    return jax.nn.silu(x)

def _sigmoid(x):
    return jax.nn.sigmoid(x)

def _layernorm(x, axis=-1, eps=1e-05):
    m = jnp.mean(x, axis=axis, keepdims=True)
    v = jnp.var(x, axis=axis, keepdims=True)
    return (x - m) / jnp.sqrt(v + eps)

def _scatter_add(tgt, idx, src, axis=0):
    return tgt.at[idx].add(src)

def _segment_sum(src, seg, n):
    return jax.ops.segment_sum(src, seg, n)
kernel_name = 'mk_gps_d4_gnn_r16_6aedaf'

def setup_inputs(seed: int=0):
    np.random.seed(seed)
    _w = jnp.asarray

    def _rec_inputs():
        import jax
        import jax.numpy as jnp
        _gk = jax.random.key(seed)
        x = -0.0003713 + 1 * jax.random.normal(jax.random.fold_in(_gk, 1), (3125, 256), jnp.float32)
        src = jax.random.randint(jax.random.fold_in(_gk, 2), (50000,), 0, 3125, jnp.int32)
        dst = jnp.minimum((3125 * jax.random.uniform(jax.random.fold_in(_gk, 3), (50000,)) ** 2.0).astype(jnp.int32), 49999)
        _o = jnp.argsort(dst, stable=True)
        src = src[_o]
        dst = dst[_o]
        edge_type_8 = jax.random.randint(jax.random.fold_in(_gk, 14), (50000,), 0, 8, jnp.int32)
        edge_weight = jax.random.uniform(jax.random.fold_in(_gk, 15), (50000,), jnp.float32, 0.0, 0.999999)
        return (x, src, dst, edge_type_8, edge_weight)
    x, src, dst, edge_type_8, edge_weight = _rec_inputs()

    def _L0_gnn_setup():
        import jax, jax.numpy as jnp
        import numpy as np
        N_NODES = 3125
        N_EDGES = 50000
        DIM = 256
        HEADS = 8
        DIM_OUT = 32
        key = jax.random.key(seed)
        ks = jax.random.split(key, 9)
        s = 1.0 / np.sqrt(DIM)
        inner = HEADS * DIM_OUT
        return {'x': jax.random.normal(ks[0], (N_NODES, DIM), dtype=jnp.float32), 'Wq': jax.random.uniform(ks[1], (DIM, inner), jnp.float32, -s, s), 'bq': jax.random.uniform(ks[2], (inner,), jnp.float32, -s, s), 'Wk': jax.random.uniform(ks[3], (DIM, inner), jnp.float32, -s, s), 'bk': jax.random.uniform(ks[4], (inner,), jnp.float32, -s, s), 'Wv': jax.random.uniform(ks[5], (DIM, inner), jnp.float32, -s, s), 'bv': jax.random.uniform(ks[6], (inner,), jnp.float32, -s, s), 'src': jax.random.randint(ks[7], (N_EDGES,), 0, N_NODES), 'dst': jax.random.randint(ks[8], (N_EDGES,), 0, N_NODES)}
    _L0_gnn_all = _L0_gnn_setup()
    _L0_gnn_in = {k: v for k, v in _L0_gnn_all.items() if k in ('Wq', 'bq', 'Wk', 'bk', 'Wv', 'bv')}
    del _L0_gnn_all

    def _L0_mix_setup():
        import jax, jax.numpy as jnp
        import numpy as np
        HEADS = 4
        DIM_HEAD = 32
        key = jax.random.key(seed)
        k1, k2, k3 = jax.random.split(key, 3)
        B, L, D = (16, 512, 256)
        hidden = HEADS * DIM_HEAD
        x = jax.random.normal(k1, (B, L, D), dtype=jnp.float32)
        W_qkv = jax.random.normal(k2, (D, 3 * hidden), dtype=jnp.float32) * D ** (-0.5)
        W_out = jax.random.normal(k3, (hidden, D), dtype=jnp.float32) * hidden ** (-0.5)
        b_out = jnp.zeros((D,), dtype=jnp.float32)
        return {'x': x, 'W_qkv': W_qkv, 'W_out': W_out, 'b_out': b_out}
    _L0_mix_all = _L0_mix_setup()
    _L0_mix_in = {k: v for k, v in _L0_mix_all.items() if k in ('W_qkv', 'W_out', 'b_out')}
    del _L0_mix_all

    def _L0_ffn_setup():
        import jax, jax.numpy as jnp
        import numpy as np
        B, S, H, F, E, K = (8, 256, 256, 512, 16, 2)
        EPS = 1e-05
        key = jax.random.key(seed)
        ks = jax.random.split(key, 9)
        sc = 0.02
        return {'x': jax.random.normal(ks[0], (B, S, H), dtype=jnp.float32), 'gate_w': jax.random.normal(ks[1], (H, E), dtype=jnp.float32) * sc, 'gate_b': jnp.zeros((E,), dtype=jnp.float32), 'w1': jax.random.normal(ks[2], (E, H, F), dtype=jnp.float32) * sc, 'b1': jnp.zeros((E, F), dtype=jnp.float32), 'w2': jax.random.normal(ks[3], (E, F, H), dtype=jnp.float32) * sc, 'b2': jnp.zeros((E, H), dtype=jnp.float32), 'gamma': jnp.ones((H,), dtype=jnp.float32), 'beta': jnp.zeros((H,), dtype=jnp.float32)}
    _L0_ffn_all = _L0_ffn_setup()
    _L0_ffn_in = {k: v for k, v in _L0_ffn_all.items() if k in ('gate_w', 'gate_b', 'w1', 'b1', 'w2', 'b2', 'gamma', 'beta')}
    del _L0_ffn_all

    def _L1_gnn_setup():
        import jax, jax.numpy as jnp
        import numpy as np
        N_NODES = 3125
        N_EDGES = 37500
        C_IN = 256
        C_OUT = 256
        N_REL = 8
        key = jax.random.key(seed)
        ks = jax.random.split(key, 7)
        x = jax.random.normal(ks[0], (N_NODES, C_IN), dtype=jnp.float32)
        edge_index = jax.random.randint(ks[1], (2, N_EDGES), 0, N_NODES, dtype=jnp.int64)
        edge_type = jax.random.randint(ks[2], (N_EDGES,), 0, N_REL, dtype=jnp.int64)
        edge_weight = jax.random.uniform(ks[3], (N_EDGES,), dtype=jnp.float32)
        weight = jax.random.normal(ks[4], (N_REL, C_IN, C_OUT), dtype=jnp.float32) * (1.0 / np.sqrt(C_IN))
        root = jax.random.normal(ks[5], (C_IN, C_OUT), dtype=jnp.float32) * (1.0 / np.sqrt(C_IN))
        bias = jnp.zeros((C_OUT,), dtype=jnp.float32)
        return {'x': x, 'edge_index': edge_index, 'edge_type': edge_type, 'edge_weight': edge_weight, 'weight': weight, 'root': root, 'bias': bias}
    _L1_gnn_all = _L1_gnn_setup()
    _L1_gnn_in = {k: v for k, v in _L1_gnn_all.items() if k in ('weight', 'root', 'bias')}
    del _L1_gnn_all

    def _L1_mix_setup():
        import jax, jax.numpy as jnp
        import numpy as np
        DIM = 256
        HEADS = 4
        DIM_HEAD = 32
        NUM_MEM = 4
        HIDDEN = HEADS * DIM_HEAD
        SCALE = DIM_HEAD ** (-0.5)

        def rmsnorm(x, g):
            n = jnp.linalg.norm(x, axis=-1, keepdims=True)
            return x / jnp.maximum(n, 1e-12) * g * x.shape[-1] ** 0.5
        key = jax.random.key(seed)
        ks = jax.random.split(key, 8)
        B, N = (4, 1024)
        return {'x': jax.random.normal(ks[0], (B, N, DIM), jnp.float32), 't': jax.random.normal(ks[1], (B,), jnp.float32), 'w_qkv': jax.random.normal(ks[2], (DIM, 3 * HIDDEN), jnp.float32) * 0.02, 'mem_kv': jax.random.normal(ks[3], (2, HEADS, DIM_HEAD, NUM_MEM), jnp.float32), 'w_out': jax.random.normal(ks[4], (HIDDEN, DIM), jnp.float32) * 0.02, 'b_out': jnp.zeros((DIM,), jnp.float32), 'g_out': jnp.ones((DIM,), jnp.float32), 'g_pre': jnp.ones((DIM,), jnp.float32)}
    _L1_mix_all = _L1_mix_setup()
    _L1_mix_in = {k: v for k, v in _L1_mix_all.items() if k in ('t', 'w_qkv', 'mem_kv', 'w_out', 'b_out', 'g_out', 'g_pre')}
    del _L1_mix_all

    def _L1_ffn_setup():
        import math
        import jax, jax.numpy as jnp
        import numpy as np
        CAPACITY_FACTOR = 1.25
        key = jax.random.key(seed)
        ks = jax.random.split(key, 5)
        B, L, D, F, E = (8, 512, 256, 1024, 8)
        h = jax.random.normal(ks[0], (B, L, D), dtype=jnp.float32)
        gate_w = jax.random.normal(ks[1], (D, E), dtype=jnp.float32) * 0.02
        gate_b = jnp.zeros((E,), dtype=jnp.float32)
        w1 = jax.random.normal(ks[2], (E, D, F), dtype=jnp.float32) * (1.0 / math.sqrt(D))
        b1 = jnp.zeros((E, F), dtype=jnp.float32)
        w2 = jax.random.normal(ks[3], (E, F, D), dtype=jnp.float32) * (1.0 / math.sqrt(F))
        b2 = jnp.zeros((E, D), dtype=jnp.float32)
        return {'h': h, 'gate_w': gate_w, 'gate_b': gate_b, 'w1': w1, 'b1': b1, 'w2': w2, 'b2': b2}
    _L1_ffn_all = _L1_ffn_setup()
    _L1_ffn_in = {k: v for k, v in _L1_ffn_all.items() if k in ('gate_w', 'gate_b', 'w1', 'b1', 'w2', 'b2')}
    del _L1_ffn_all

    def _L2_gnn_setup():
        import jax, jax.numpy as jnp
        import numpy as np
        BN_EPS = 1e-05

        def _batchnorm(h, gamma, beta):
            mean = jnp.mean(h, axis=0, keepdims=True)
            var = jnp.var(h, axis=0, keepdims=True)
            return (h - mean) * jax.lax.rsqrt(var + BN_EPS) * gamma + beta
        key = jax.random.key(seed)
        ks = jax.random.split(key, 10)
        N, E, D = (6250, 200000, 256)
        x = jax.random.normal(ks[0], (N, D), dtype=jnp.float32)
        edge_src = jax.random.randint(ks[1], (E,), 0, N, dtype=jnp.int32)
        edge_dst = jax.random.randint(ks[2], (E,), 0, N, dtype=jnp.int32)
        edge_vals = jnp.ones((E,), dtype=jnp.float32)
        n_norm = jax.random.uniform(ks[3], (N, 1), dtype=jnp.float32)
        s = 1.0 / np.sqrt(D)
        w1 = jax.random.uniform(ks[4], (D, D), jnp.float32, -s, s)
        gamma1 = jnp.ones((D,), jnp.float32)
        beta1 = jnp.zeros((D,), jnp.float32)
        w2 = jax.random.uniform(ks[5], (D, D), jnp.float32, -s, s)
        eps_weight = jnp.zeros((1,), jnp.float32)
        gamma_h = jnp.ones((D,), jnp.float32)
        beta_h = jnp.zeros((D,), jnp.float32)
        return {'x': x, 'edge_src': edge_src, 'edge_dst': edge_dst, 'edge_vals': edge_vals, 'n_norm': n_norm, 'w1': w1, 'gamma1': gamma1, 'beta1': beta1, 'w2': w2, 'eps_weight': eps_weight, 'gamma_h': gamma_h, 'beta_h': beta_h}
    _L2_gnn_all = _L2_gnn_setup()
    _L2_gnn_in = {k: v for k, v in _L2_gnn_all.items() if k in ('w1', 'gamma1', 'beta1', 'w2', 'eps_weight', 'gamma_h', 'beta_h')}
    del _L2_gnn_all

    def _L2_mix_setup():
        import jax, jax.numpy as jnp
        import numpy as np
        HEADS = 8
        EPS = 1e-05

        def _ln(t, w, b, headc):
            m = jnp.mean(t, axis=-1, keepdims=True)
            d = t - m
            std = jnp.sqrt(jnp.sum(d * d, axis=-1, keepdims=True) / (headc - 1))
            return w * (d / (std + EPS)) + b
        key = jax.random.key(seed)
        B, N, C = (32, 256, 256)
        headc = C // HEADS
        x = jax.random.normal(key, (B, N, C), dtype=jnp.float32)
        return {'x': x, 'kln_weight': jnp.ones((HEADS, 1, headc), dtype=jnp.float32), 'kln_bias': jnp.zeros((HEADS, 1, headc), dtype=jnp.float32), 'vln_weight': jnp.ones((HEADS, 1, headc), dtype=jnp.float32), 'vln_bias': jnp.zeros((HEADS, 1, headc), dtype=jnp.float32)}
    _L2_mix_all = _L2_mix_setup()
    _L2_mix_in = {k: v for k, v in _L2_mix_all.items() if k in ('kln_weight', 'kln_bias', 'vln_weight', 'vln_bias')}
    del _L2_mix_all

    def _L2_ffn_setup():
        import jax, jax.numpy as jnp
        import numpy as np
        TOP_K = 2
        LN_EPS = 1e-05
        key = jax.random.key(seed)
        ks = jax.random.split(key, 8)
        B, S, D, E, H = (16, 1024, 256, 8, 1024)
        x = jax.random.normal(ks[0], (B, S, D), dtype=jnp.float32)
        Wr = jax.random.normal(ks[1], (D, E), dtype=jnp.float32) * 0.1
        br = jnp.zeros((E,), dtype=jnp.float32)
        ln_g = jnp.ones((E, D), dtype=jnp.float32)
        ln_b = jnp.zeros((E, D), dtype=jnp.float32)
        W1 = jax.random.normal(ks[2], (E, D, H), dtype=jnp.float32) * (1.0 / np.sqrt(D))
        b1 = jnp.zeros((E, H), dtype=jnp.float32)
        W2 = jax.random.normal(ks[3], (E, H, D), dtype=jnp.float32) * (1.0 / np.sqrt(H))
        b2 = jnp.zeros((E, D), dtype=jnp.float32)
        return {'x': x, 'Wr': Wr, 'br': br, 'ln_g': ln_g, 'ln_b': ln_b, 'W1': W1, 'b1': b1, 'W2': W2, 'b2': b2}
    _L2_ffn_all = _L2_ffn_setup()
    _L2_ffn_in = {k: v for k, v in _L2_ffn_all.items() if k in ('Wr', 'br', 'ln_g', 'ln_b', 'W1', 'b1', 'W2', 'b2')}
    del _L2_ffn_all

    def _L3_gnn_setup():
        import jax, jax.numpy as jnp
        import numpy as np
        N = 3125
        E_RAND = 50000
        F_IN = 256
        F_OUT = 256
        ALPHA = 0.2
        key = jax.random.key(seed)
        k1, k2, k3, k4 = jax.random.split(key, 4)
        x = jax.random.normal(k1, (N, F_IN), dtype=jnp.float32)
        edge_rand = jax.random.randint(k2, (2, E_RAND), 0, N)
        loops = jnp.arange(N)
        edge = jnp.concatenate([edge_rand, jnp.stack([loops, loops])], axis=1)
        W = jax.random.normal(k3, (F_IN, F_OUT), dtype=jnp.float32) * 0.05
        a = jax.random.normal(k4, (2 * F_OUT,), dtype=jnp.float32) * 0.05
        return {'x': x, 'edge': edge, 'W': W, 'a': a}
    _L3_gnn_all = _L3_gnn_setup()
    _L3_gnn_in = {k: v for k, v in _L3_gnn_all.items() if k in ('W', 'a')}
    del _L3_gnn_all

    def _L3_mix_setup():
        import math
        import jax, jax.numpy as jnp
        import numpy as np
        EPS_DIV = 1e-07
        EPS_NORM = 1e-12

        def _l2_normalize(x, axis):
            n = jnp.sqrt(jnp.sum(x * x, axis=axis, keepdims=True))
            return x / jnp.maximum(n, EPS_NORM)
        key = jax.random.key(seed)
        ks = jax.random.split(key, 5)
        b, N, C = (8, 256, 256)
        x = jax.random.normal(ks[0], (b, N, C), dtype=jnp.float32)
        W_qkv = jax.random.normal(ks[1], (C, 3 * C), dtype=jnp.float32) * (1.0 / math.sqrt(C))
        b_qkv = jax.random.normal(ks[2], (3 * C,), dtype=jnp.float32) * 0.02
        W_out = jax.random.normal(ks[3], (C, C), dtype=jnp.float32) * (1.0 / math.sqrt(C))
        b_out = jax.random.normal(ks[4], (C,), dtype=jnp.float32) * 0.02
        return {'x': x, 'W_qkv': W_qkv, 'b_qkv': b_qkv, 'W_out': W_out, 'b_out': b_out}
    _L3_mix_all = _L3_mix_setup()
    _L3_mix_in = {k: v for k, v in _L3_mix_all.items() if k in ('W_qkv', 'b_qkv', 'W_out', 'b_out')}
    del _L3_mix_all

    def _L3_ffn_setup():
        import jax, jax.numpy as jnp
        import numpy as np
        B, S, D = (8, 256, 256)
        H = 4 * D
        CAPACITY = 0.5
        key = jax.random.key(seed)
        ks = jax.random.split(key, 6)
        x = jax.random.normal(ks[0], (B, S, D), dtype=jnp.float32)
        attention_mask = jnp.zeros((B, 1, 1, S), dtype=jnp.float32)
        wr = jax.random.normal(ks[1], (D, 1), dtype=jnp.float32) * 0.02
        br = jnp.zeros((1,), dtype=jnp.float32)
        w1 = jax.random.normal(ks[2], (D, H), dtype=jnp.float32) * 0.02
        b1 = jnp.zeros((H,), dtype=jnp.float32)
        w2 = jax.random.normal(ks[3], (H, D), dtype=jnp.float32) * 0.02
        b2 = jnp.zeros((D,), dtype=jnp.float32)
        return {'x': x, 'attention_mask': attention_mask, 'wr': wr, 'br': br, 'w1': w1, 'b1': b1, 'w2': w2, 'b2': b2}
    _L3_ffn_all = _L3_ffn_setup()
    _L3_ffn_in = {k: v for k, v in _L3_ffn_all.items() if k in ('attention_mask', 'wr', 'br', 'w1', 'b1', 'w2', 'b2')}
    del _L3_ffn_all
    return {'x': x, 'src': src, 'dst': dst, 'edge_type_8': edge_type_8, 'edge_weight': edge_weight, 'L0_gnn_Wq': _L0_gnn_in['Wq'], 'L0_gnn_bq': _L0_gnn_in['bq'], 'L0_gnn_Wk': _L0_gnn_in['Wk'], 'L0_gnn_bk': _L0_gnn_in['bk'], 'L0_gnn_Wv': _L0_gnn_in['Wv'], 'L0_gnn_bv': _L0_gnn_in['bv'], 'L0_mix_W_qkv': _L0_mix_in['W_qkv'], 'L0_mix_W_out': _L0_mix_in['W_out'], 'L0_mix_b_out': _L0_mix_in['b_out'], 'L0_ffn_gate_w': _L0_ffn_in['gate_w'], 'L0_ffn_gate_b': _L0_ffn_in['gate_b'], 'L0_ffn_w1': _L0_ffn_in['w1'], 'L0_ffn_b1': _L0_ffn_in['b1'], 'L0_ffn_w2': _L0_ffn_in['w2'], 'L0_ffn_b2': _L0_ffn_in['b2'], 'L0_ffn_gamma': _L0_ffn_in['gamma'], 'L0_ffn_beta': _L0_ffn_in['beta'], 'L1_gnn_weight': _L1_gnn_in['weight'], 'L1_gnn_root': _L1_gnn_in['root'], 'L1_gnn_bias': _L1_gnn_in['bias'], 'L1_mix_t': _L1_mix_in['t'], 'L1_mix_w_qkv': _L1_mix_in['w_qkv'], 'L1_mix_mem_kv': _L1_mix_in['mem_kv'], 'L1_mix_w_out': _L1_mix_in['w_out'], 'L1_mix_b_out': _L1_mix_in['b_out'], 'L1_mix_g_out': _L1_mix_in['g_out'], 'L1_mix_g_pre': _L1_mix_in['g_pre'], 'L1_ffn_gate_w': _L1_ffn_in['gate_w'], 'L1_ffn_gate_b': _L1_ffn_in['gate_b'], 'L1_ffn_w1': _L1_ffn_in['w1'], 'L1_ffn_b1': _L1_ffn_in['b1'], 'L1_ffn_w2': _L1_ffn_in['w2'], 'L1_ffn_b2': _L1_ffn_in['b2'], 'L2_gnn_w1': _L2_gnn_in['w1'], 'L2_gnn_gamma1': _L2_gnn_in['gamma1'], 'L2_gnn_beta1': _L2_gnn_in['beta1'], 'L2_gnn_w2': _L2_gnn_in['w2'], 'L2_gnn_eps_weight': _L2_gnn_in['eps_weight'], 'L2_gnn_gamma_h': _L2_gnn_in['gamma_h'], 'L2_gnn_beta_h': _L2_gnn_in['beta_h'], 'L2_mix_kln_weight': _L2_mix_in['kln_weight'], 'L2_mix_kln_bias': _L2_mix_in['kln_bias'], 'L2_mix_vln_weight': _L2_mix_in['vln_weight'], 'L2_mix_vln_bias': _L2_mix_in['vln_bias'], 'L2_ffn_Wr': _L2_ffn_in['Wr'], 'L2_ffn_br': _L2_ffn_in['br'], 'L2_ffn_ln_g': _L2_ffn_in['ln_g'], 'L2_ffn_ln_b': _L2_ffn_in['ln_b'], 'L2_ffn_W1': _L2_ffn_in['W1'], 'L2_ffn_b1': _L2_ffn_in['b1'], 'L2_ffn_W2': _L2_ffn_in['W2'], 'L2_ffn_b2': _L2_ffn_in['b2'], 'L3_gnn_W': _L3_gnn_in['W'], 'L3_gnn_a': _L3_gnn_in['a'], 'L3_mix_W_qkv': _L3_mix_in['W_qkv'], 'L3_mix_b_qkv': _L3_mix_in['b_qkv'], 'L3_mix_W_out': _L3_mix_in['W_out'], 'L3_mix_b_out': _L3_mix_in['b_out'], 'L3_ffn_attention_mask': _L3_ffn_in['attention_mask'], 'L3_ffn_wr': _L3_ffn_in['wr'], 'L3_ffn_br': _L3_ffn_in['br'], 'L3_ffn_w1': _L3_ffn_in['w1'], 'L3_ffn_b1': _L3_ffn_in['b1'], 'L3_ffn_w2': _L3_ffn_in['w2'], 'L3_ffn_b2': _L3_ffn_in['b2']}

def reference(x, src, dst, edge_type_8, edge_weight, L0_gnn_Wq, L0_gnn_bq, L0_gnn_Wk, L0_gnn_bk, L0_gnn_Wv, L0_gnn_bv, L0_mix_W_qkv, L0_mix_W_out, L0_mix_b_out, L0_ffn_gate_w, L0_ffn_gate_b, L0_ffn_w1, L0_ffn_b1, L0_ffn_w2, L0_ffn_b2, L0_ffn_gamma, L0_ffn_beta, L1_gnn_weight, L1_gnn_root, L1_gnn_bias, L1_mix_t, L1_mix_w_qkv, L1_mix_mem_kv, L1_mix_w_out, L1_mix_b_out, L1_mix_g_out, L1_mix_g_pre, L1_ffn_gate_w, L1_ffn_gate_b, L1_ffn_w1, L1_ffn_b1, L1_ffn_w2, L1_ffn_b2, L2_gnn_w1, L2_gnn_gamma1, L2_gnn_beta1, L2_gnn_w2, L2_gnn_eps_weight, L2_gnn_gamma_h, L2_gnn_beta_h, L2_mix_kln_weight, L2_mix_kln_bias, L2_mix_vln_weight, L2_mix_vln_bias, L2_ffn_Wr, L2_ffn_br, L2_ffn_ln_g, L2_ffn_ln_b, L2_ffn_W1, L2_ffn_b1, L2_ffn_W2, L2_ffn_b2, L3_gnn_W, L3_gnn_a, L3_mix_W_qkv, L3_mix_b_qkv, L3_mix_W_out, L3_mix_b_out, L3_ffn_attention_mask, L3_ffn_wr, L3_ffn_br, L3_ffn_w1, L3_ffn_b1, L3_ffn_w2, L3_ffn_b2):
    import jax
    import jax.numpy as jnp

    def _L0_gnn_ref(x, Wq, bq, Wk, bk, Wv, bv, src, dst):
        import jax, jax.numpy as jnp
        import numpy as np
        N_NODES = 3125
        N_EDGES = 50000
        DIM = 256
        HEADS = 8
        DIM_OUT = 32
        n = x.shape[0]
        q = (x @ Wq + bq).reshape(n, HEADS, DIM_OUT)
        k = (x @ Wk + bk).reshape(n, HEADS, DIM_OUT)
        v = (x @ Wv + bv).reshape(n, HEADS, DIM_OUT)
        scores = jnp.einsum('ehd,ehd->eh', q[src], k[dst]) / jnp.sqrt(jnp.asarray(DIM_OUT, dtype=x.dtype))
        m = jax.ops.segment_max(scores, dst, num_segments=n)
        m = jnp.where(jnp.isfinite(m), m, 0.0)
        e = jnp.exp(scores - m[dst])
        z = jax.ops.segment_sum(e, dst, num_segments=n)
        p = e / jnp.maximum(z[dst], 1e-16)
        out = jax.ops.segment_sum(v[src] * p[:, :, None], dst, num_segments=n)
        return out.reshape(n, HEADS * DIM_OUT)

    def _L0_mix_ref(x, W_qkv, W_out, b_out):
        import jax, jax.numpy as jnp
        import numpy as np
        HEADS = 4
        DIM_HEAD = 32
        B, L, D = x.shape
        scale = DIM_HEAD ** (-0.5)
        qkv = jnp.einsum('bld,df->blf', x, W_qkv)
        qkv = qkv.reshape(B, L, 3, HEADS, DIM_HEAD)
        q = jnp.transpose(qkv[:, :, 0], (0, 2, 1, 3)) * scale
        k = jax.nn.softmax(jnp.transpose(qkv[:, :, 1], (0, 2, 1, 3)), axis=2)
        v = jnp.transpose(qkv[:, :, 2], (0, 2, 1, 3))
        context = jnp.einsum('bhld,bhle->bhde', k, v)
        out = jnp.einsum('bhde,bhld->bhle', context, q)
        out = jnp.transpose(out, (0, 2, 1, 3)).reshape(B, L, HEADS * DIM_HEAD)
        return jnp.einsum('blf,fd->bld', out, W_out) + b_out

    def _L0_ffn_ref(x, gate_w, gate_b, w1, b1, w2, b2, gamma, beta):
        import jax, jax.numpy as jnp
        import numpy as np
        B, S, H, F, E, K = (8, 256, 256, 512, 16, 2)
        EPS = 1e-05
        gate_logits = x @ gate_w + gate_b
        topk_vals, topk_idx = jax.lax.top_k(gate_logits, K)
        topk_w = jax.nn.softmax(topk_vals, axis=-1)
        h = jax.nn.relu(jnp.einsum('bsh,ehf->bsef', x, w1) + b1)
        expert_out = jnp.einsum('bsef,efh->bseh', h, w2) + b2
        sel = jnp.take_along_axis(expert_out, topk_idx[:, :, :, None], axis=2)
        moe = jnp.sum(topk_w[..., None] * sel, axis=2)
        y = x + moe
        mu = jnp.mean(y, axis=-1, keepdims=True)
        var = jnp.var(y, axis=-1, keepdims=True)
        return (y - mu) / jnp.sqrt(var + EPS) * gamma + beta

    def _L1_gnn_ref(x, edge_index, edge_type, edge_weight, weight, root, bias):
        import jax, jax.numpy as jnp
        import numpy as np
        N_NODES = 3125
        N_EDGES = 37500
        C_IN = 256
        C_OUT = 256
        N_REL = 8
        "RGCNConv (no bases/blocks), aggr='mean', root_weight=True, bias=True.\n\n            Equivalent to the PyG per-relation loop:\n                for r: out += scatter_mean(x[src_r] * w_r, dst_r) @ weight[r]\n                out += x @ root + bias\n            but fused: one segmented mean over (relation, dst) pairs followed by a\n            grouped GEMM over relations.\n            "
        N, C = x.shape
        R = weight.shape[0]
        src, dst = (edge_index[0], edge_index[1])
        msg = x[src] * edge_weight[:, None]
        seg = edge_type * N + dst
        sums = jax.ops.segment_sum(msg, seg, num_segments=R * N)
        cnt = jax.ops.segment_sum(jnp.ones_like(edge_weight), seg, num_segments=R * N)
        h = sums / jnp.maximum(cnt, 1.0)[:, None]
        h = h.reshape(R, N, C)
        out = jnp.einsum('rnc,rco->no', h, weight)
        out = out + x @ root + bias
        return out

    def _L1_mix_ref(x, t, w_qkv, mem_kv, w_out, b_out, g_out, g_pre):
        import jax, jax.numpy as jnp
        import numpy as np
        DIM = 256
        HEADS = 4
        DIM_HEAD = 32
        NUM_MEM = 4
        HIDDEN = HEADS * DIM_HEAD
        SCALE = DIM_HEAD ** (-0.5)

        def rmsnorm(x, g):
            n = jnp.linalg.norm(x, axis=-1, keepdims=True)
            return x / jnp.maximum(n, 1e-12) * g * x.shape[-1] ** 0.5
        b, n, c = x.shape
        xn = rmsnorm(x, g_pre)
        qkv = xn @ w_qkv
        q, k, v = jnp.split(qkv, 3, axis=-1)

        def to_heads(z):
            return z.reshape(b, n, HEADS, DIM_HEAD).transpose(0, 2, 3, 1)
        q, k, v = map(to_heads, (q, k, v))
        mk = jnp.broadcast_to(mem_kv[0], (b, HEADS, DIM_HEAD, NUM_MEM))
        mv = jnp.broadcast_to(mem_kv[1], (b, HEADS, DIM_HEAD, NUM_MEM))
        k = jnp.concatenate([mk, k], axis=-1)
        v = jnp.concatenate([mv, v], axis=-1)
        q = jax.nn.softmax(q, axis=-2) * SCALE
        k = jax.nn.softmax(k, axis=-1)
        context = jnp.einsum('bhdn,bhen->bhde', k, v)
        out = jnp.einsum('bhde,bhdn->bhen', context, q)
        out = out.transpose(0, 3, 1, 2).reshape(b, n, HIDDEN)
        out = rmsnorm(out @ w_out + b_out, g_out)
        return out + x

    def _L1_ffn_ref(h, gate_w, gate_b, w1, b1, w2, b2):
        import math
        import jax, jax.numpy as jnp
        import numpy as np
        CAPACITY_FACTOR = 1.25
        B, L, D = h.shape
        E = gate_w.shape[1]
        T = B * L
        C = max(1, math.ceil(CAPACITY_FACTOR * T / E))
        x = h.reshape(T, D)
        logits = x @ gate_w + gate_b
        probs = jax.nn.softmax(logits, axis=-1)
        idx = jnp.argmax(probs, axis=-1)
        prb = jnp.take_along_axis(probs, idx[:, None], axis=1)[:, 0]
        one_hot = jax.nn.one_hot(idx, E, dtype=jnp.float32)
        pos = (jnp.cumsum(one_hot, axis=0) * one_hot).sum(-1).astype(jnp.int32) - 1
        kept = pos < C
        pos_safe = jnp.where(kept, pos, C)
        buf = jnp.zeros((E, C, D), dtype=h.dtype).at[idx, pos_safe].set(x, mode='drop')
        hmid = jax.nn.relu(jnp.einsum('ecd,edf->ecf', buf, w1) + b1[:, None, :])
        ybuf = jnp.einsum('ecf,efd->ecd', hmid, w2) + b2[:, None, :]
        pos_g = jnp.minimum(pos, C - 1)
        y_tok = ybuf[idx, pos_g] * (prb * kept)[:, None]
        y = y_tok.reshape(B, L, D)
        y = jnp.nan_to_num(y, nan=0.0, posinf=10000.0, neginf=-10000.0)
        return y

    def _L2_gnn_ref(x, edge_src, edge_dst, edge_vals, n_norm, w1, gamma1, beta1, w2, eps_weight, gamma_h, beta_h):
        import jax, jax.numpy as jnp
        import numpy as np
        BN_EPS = 1e-05

        def _batchnorm(h, gamma, beta):
            mean = jnp.mean(h, axis=0, keepdims=True)
            var = jnp.var(h, axis=0, keepdims=True)
            return (h - mean) * jax.lax.rsqrt(var + BN_EPS) * gamma + beta
        N = x.shape[0]
        msgs = edge_vals[:, None] * x[edge_src]
        agg = jax.ops.segment_sum(msgs, edge_dst, num_segments=N)
        y = agg + eps_weight * x
        h = jax.nn.relu(_batchnorm(y @ w1.T, gamma1, beta1))
        y = h @ w2.T
        y = y * n_norm
        y = _batchnorm(y, gamma_h, beta_h)
        y = jax.nn.relu(y)
        y = y + x
        return y

    def _L2_mix_ref(x, kln_weight, kln_bias, vln_weight, vln_bias):
        import jax, jax.numpy as jnp
        import numpy as np
        HEADS = 8
        EPS = 1e-05

        def _ln(t, w, b, headc):
            m = jnp.mean(t, axis=-1, keepdims=True)
            d = t - m
            std = jnp.sqrt(jnp.sum(d * d, axis=-1, keepdims=True) / (headc - 1))
            return w * (d / (std + EPS)) + b
        B, N, C = x.shape
        headc = C // HEADS
        qkv = x.reshape(B, N, HEADS, headc).transpose(0, 2, 1, 3)
        k = _ln(qkv, kln_weight, kln_bias, headc)
        v = _ln(qkv, vln_weight, vln_bias, headc)
        kv = jnp.einsum('bhnd,bhne->bhde', k, v) / N
        out = jnp.einsum('bhnd,bhde->bhne', qkv, kv)
        out = out.transpose(0, 2, 1, 3).reshape(B, N, C)
        return out + x

    def _L2_ffn_ref(x, Wr, br, ln_g, ln_b, W1, b1, W2, b2):
        import jax, jax.numpy as jnp
        import numpy as np
        TOP_K = 2
        LN_EPS = 1e-05
        B, S, D = x.shape
        N = B * S
        xt = x.reshape(N, D)
        logits = xt @ Wr + br
        probs = jax.nn.softmax(logits, axis=-1)
        top_p, top_idx = jax.lax.top_k(probs, TOP_K)
        weights = top_p / top_p.sum(axis=-1, keepdims=True)
        mu = xt.mean(axis=-1, keepdims=True)
        var = ((xt - mu) ** 2).mean(axis=-1, keepdims=True)
        xn = (xt - mu) * jax.lax.rsqrt(var + LN_EPS)
        xe = xn[None, :, :] * ln_g[:, None, :] + ln_b[:, None, :]
        h = jax.nn.gelu(jnp.einsum('end,edh->enh', xe, W1) + b1[:, None, :], approximate=False)
        y = jnp.einsum('enh,ehd->end', h, W2) + b2[:, None, :]
        y_tok = jnp.transpose(y, (1, 0, 2))
        sel = jnp.take_along_axis(y_tok, top_idx[:, :, None], axis=1)
        out = (weights[:, :, None] * sel).sum(axis=1)
        return out.reshape(B, S, D)

    def _L3_gnn_ref(x, edge, W, a):
        import jax, jax.numpy as jnp
        import numpy as np
        N = 3125
        E_RAND = 50000
        F_IN = 256
        F_OUT = 256
        ALPHA = 0.2
        n = x.shape[0]
        f_out = W.shape[1]
        h = x @ W
        src, dst = (edge[0], edge[1])
        s = h @ a[:f_out]
        t = h @ a[f_out:]
        logit = s[src] + t[dst]
        e = jnp.exp(-jax.nn.leaky_relu(logit, ALPHA))
        rowsum = jax.ops.segment_sum(e, src, num_segments=n)
        msg = e[:, None] * h[dst]
        h_prime = jax.ops.segment_sum(msg, src, num_segments=n)
        h_prime = h_prime / rowsum[:, None]
        return jax.nn.relu(h_prime)

    def _L3_mix_ref(x, W_qkv, b_qkv, W_out, b_out):
        import math
        import jax, jax.numpy as jnp
        import numpy as np
        EPS_DIV = 1e-07
        EPS_NORM = 1e-12

        def _l2_normalize(x, axis):
            n = jnp.sqrt(jnp.sum(x * x, axis=axis, keepdims=True))
            return x / jnp.maximum(n, EPS_NORM)
        b, N, C = x.shape
        qkv = x @ W_qkv + b_qkv
        q, k, v = jnp.split(qkv, 3, axis=2)
        q = q - jnp.mean(q, axis=2, keepdims=True)
        k = k - jnp.mean(k, axis=2, keepdims=True)
        q2 = q * q
        k2 = k * k
        q2s = jnp.sum(q2, axis=2, keepdims=True)
        k2s = jnp.sum(k2, axis=2, keepdims=True)
        k2 = _l2_normalize(k2 / (k2s + EPS_DIV), axis=-2)
        q2 = _l2_normalize(q2 / (q2s + EPS_DIV), axis=-1)
        kv = jnp.einsum('bnc,bnd->bcd', k2, v)
        t2 = jnp.einsum('bnc,bcd->bnd', q2, kv) / math.sqrt(N)
        attn = v + t2
        return attn @ W_out + b_out

    def _L3_ffn_ref(x, attention_mask, wr, br, w1, b1, w2, b2):
        import jax, jax.numpy as jnp
        import numpy as np
        B, S, D = (8, 256, 256)
        H = 4 * D
        CAPACITY = 0.5
        b, s, d = x.shape
        weights = (jnp.einsum('bsd,do->bso', x, wr) + br)[..., 0]
        k = max(1, int(CAPACITY * s))
        kk = k - 1 if k > 1 else 1
        _, idx = jax.lax.top_k(weights, k)
        sel_idx = idx[:, :kk]
        sel = jnp.take_along_axis(x, sel_idx[:, :, None], axis=1)
        h = jax.nn.gelu(jnp.einsum('bkd,dh->bkh', sel, w1) + b1)
        y = jnp.einsum('bkh,hd->bkd', h, w2) + b2
        w_sel = jnp.take_along_axis(weights, sel_idx, axis=1)
        y = y * w_sel[..., None]
        batch_idx = jnp.arange(b)[:, None]
        processed = jnp.zeros_like(x).at[batch_idx, sel_idx].set(y)
        return processed + x
    edge_index = jnp.stack([src, dst])
    deg = jnp.maximum(jax.ops.segment_sum(jnp.ones(dst.shape, jnp.float32), dst, num_segments=3125), 1.0)
    deg_isqrt = deg ** (-0.5)
    xn = _layernorm(x, axis=-1)
    x = x + _L0_gnn_ref(xn, L0_gnn_Wq, L0_gnn_bq, L0_gnn_Wk, L0_gnn_bk, L0_gnn_Wv, L0_gnn_bv, src, dst) + _L0_mix_ref(xn[None], L0_mix_W_qkv, L0_mix_W_out, L0_mix_b_out)[0]
    x = x + _L0_ffn_ref(_layernorm(x, axis=-1)[None], L0_ffn_gate_w, L0_ffn_gate_b, L0_ffn_w1, L0_ffn_b1, L0_ffn_w2, L0_ffn_b2, L0_ffn_gamma, L0_ffn_beta)[0]
    xn = _layernorm(x, axis=-1)
    x = x + _L1_gnn_ref(xn, edge_index, edge_type_8, edge_weight, L1_gnn_weight, L1_gnn_root, L1_gnn_bias) + _L1_mix_ref(xn[None], L1_mix_t, L1_mix_w_qkv, L1_mix_mem_kv, L1_mix_w_out, L1_mix_b_out, L1_mix_g_out, L1_mix_g_pre)[0]
    x = x + _L1_ffn_ref(_layernorm(x, axis=-1)[None], L1_ffn_gate_w, L1_ffn_gate_b, L1_ffn_w1, L1_ffn_b1, L1_ffn_w2, L1_ffn_b2)[0]
    xn = _layernorm(x, axis=-1)
    x = x + _L2_gnn_ref(xn, src, dst, edge_weight, deg_isqrt[:, None], L2_gnn_w1, L2_gnn_gamma1, L2_gnn_beta1, L2_gnn_w2, L2_gnn_eps_weight, L2_gnn_gamma_h, L2_gnn_beta_h) + _L2_mix_ref(xn[None], L2_mix_kln_weight, L2_mix_kln_bias, L2_mix_vln_weight, L2_mix_vln_bias)[0]
    x = x + _L2_ffn_ref(_layernorm(x, axis=-1)[None], L2_ffn_Wr, L2_ffn_br, L2_ffn_ln_g, L2_ffn_ln_b, L2_ffn_W1, L2_ffn_b1, L2_ffn_W2, L2_ffn_b2)[0]
    xn = _layernorm(x, axis=-1)
    x = x + _L3_gnn_ref(xn, edge_index, L3_gnn_W, L3_gnn_a) + _L3_mix_ref(xn[None], L3_mix_W_qkv, L3_mix_b_qkv, L3_mix_W_out, L3_mix_b_out)[0]
    x = x + _L3_ffn_ref(_layernorm(x, axis=-1)[None], L3_ffn_attention_mask, L3_ffn_wr, L3_ffn_br, L3_ffn_w1, L3_ffn_b1, L3_ffn_w2, L3_ffn_b2)[0]
    return x

_drawn_inputs = setup_inputs


def setup_inputs(seed=0):
    import zlib

    import numpy as np

    out = dict(_drawn_inputs(seed))
    spreads = {'L0_mix_b_out': (0.0, 0.1),
     'L0_ffn_gate_b': (0.0, 0.1),
     'L0_ffn_b1': (0.0, 0.637),
     'L0_ffn_b2': (0.0, 0.1),
     'L0_ffn_gamma': (1.0, 0.2),
     'L0_ffn_beta': (0.0, 0.1),
     'L1_gnn_bias': (0.0, 0.1),
     'L1_mix_b_out': (0.0, 0.1),
     'L1_mix_g_out': (1.0, 0.2),
     'L1_mix_g_pre': (1.0, 0.6),
     'L1_ffn_gate_b': (0.0, 0.489),
     'L1_ffn_b1': (0.0, 0.8),
     'L1_ffn_b2': (0.0, 0.8),
     'L2_gnn_gamma1': (1.0, 0.6),
     'L2_gnn_beta1': (0.0, 0.588),
     'L2_gnn_gamma_h': (1.0, 0.6),
     'L2_gnn_beta_h': (0.0, 0.701),
     'L2_mix_kln_weight': (1.0, 0.2),
     'L2_mix_kln_bias': (0.0, 0.292),
     'L2_mix_vln_weight': (1.0, 0.2),
     'L2_mix_vln_bias': (0.0, 0.1),
     'L2_ffn_br': (0.0, 0.747),
     'L2_ffn_ln_g': (1.0, 0.6),
     'L2_ffn_ln_b': (0.0, 0.8),
     'L2_ffn_b1': (0.0, 0.8),
     'L2_ffn_b2': (0.0, 0.704),
     'L3_ffn_b1': (0.0, 0.8),
     'L3_ffn_b2': (0.0, 0.8)}
    factors = {'L0_gnn_bq': 8.0,
     'L0_gnn_bk': 8.0,
     'L1_mix_w_qkv': 6.311,
     'L1_mix_mem_kv': 8.0,
     'L1_mix_w_out': 5.702,
     'L3_gnn_a': 8.0,
     'L3_mix_b_qkv': 2.958,
     'L3_mix_b_out': 8.0,
     'L3_ffn_wr': 8.0,
     'L3_ffn_w1': 8.0,
     'L3_ffn_w2': 8.0}
    for name, (base, spread) in spreads.items():
        noise = np.random.default_rng([zlib.crc32(name.encode()), seed]).standard_normal(out[name].shape)
        drawn = base * np.exp(spread * noise) if base else spread * noise
        out[name] = jnp.asarray(drawn.astype(out[name].dtype))
    for name, factor in factors.items():
        out[name] = (out[name] * factor).astype(out[name].dtype)
    return out
```

```python
from contextlib import ExitStack

import concourse.bass as bass
from concourse import mybir
import numpy as np

F32 = mybir.dt.float32
BF16 = mybir.dt.bfloat16
I32 = mybir.dt.int32
U32 = mybir.dt.uint32
ALU = mybir.AluOpType
ACT = mybir.ActivationFunctionType
AX = mybir.AxisListType
ds = bass.ds

N, D, E = 3125, 256, 50000
P = 125
NT = N // P
KC = D // 128
EC = E // P
GE = 512
GT = GE // 128
NG = E // GE + NT
NG += NG % 2
REC = 5
R_IDX, R_ROW, R_LOC, R_REL, R_W = range(REC)
NOWHERE = 999.0
H0, DH = 8, 32
LN_EPS = 1e-5
NEG = -1.0e30
MEM = 4
CHUNK = 4 * P
NCH = N // CHUNK


class Resident:

    def __init__(self, nc, ctx):
        def sb(name, shape, dt=F32):
            return ctx.enter_context(nc.sbuf_tensor(name, shape, dt))

        self.nc = nc
        self.X = sb("X", [P, NT * D])
        self.XN = sb("XN", [P, NT * D])
        self.XNT = sb("XNT", [128, KC, N])
        self.identf = sb("identf", [128, 128])
        self.identb = sb("identb", [128, 4, 128], BF16)
        self.iota = sb("iota", [128, 128])
        self.onesf = sb("onesf", [128, 128])
        self.before = sb("before", [128, 128])
        self.upto = sb("upto", [128, 128])
        self.tile_dst = sb("tile_dst", [128, NG], I32)
        self.tile_src = sb("tile_src", [128, NG], I32)
        self.inv_count = sb("inv_count", [P, NT * 8])
        self.rec_dst = nc.dram_tensor("rec_dst", (NG * GE, REC), I32).ap()
        self.rec_src = nc.dram_tensor("rec_src", (NG * GE, REC), I32).ap()
        self.norm_row = nc.dram_tensor("norm_row", (NT, P), F32).ap()


def node_tile(buf, t, width=D):
    return buf[:, ds(t * width, width)]


def is_first(n):
    return isinstance(n, int) and n < 2


def pairs(eng, count, body, peel=False):
    if peel:
        body(0, 0)
        body(1, 1)
    if count > (3 if peel else 1):
        with eng.Fori(int(peel), count // 2) as i:
            body(i * 2, 0)
            body(i * 2 + 1, 1)
    if count % 2:
        body(count - 1, 0)


def setup_stage(nc, R, x):
    with ExitStack() as ctx:
        x_loaded = nc.alloc_semaphore("x_loaded")
        zeroed = nc.alloc_semaphore("zeroed")
        masks = nc.alloc_semaphore("masks")
        block = ctx.enter_context(nc.Block())

        @block.sync
        def _(sp):
            sp.dma_start(R.X[:, :].rearrange("p (t d) -> p t d", d=D),
                         x.rearrange("(t p) d -> p t d", p=P)).then_inc(x_loaded, 16)
            sp.wait_ge(x_loaded, 16)

        @block.gpsimd
        def _(pool):
            pool.memset(R.identf[:, :], 0.0).then_inc(zeroed, 1)
            pool.memset(R.onesf[:, :], 1.0).then_inc(zeroed, 1)
            pool.iota(R.iota[:, :], pattern=[[1, 128]], base=0, channel_multiplier=0,
                      allow_small_or_imprecise_dtypes=True)
            pool.wait_ge(zeroed, 2)
            pool.affine_select(out=R.identf[:, :], in_=R.identf[:, :], compare_op=ALU.not_equal, fill=1.0,
                               base=0, pattern=[[-1, 128]], channel_multiplier=1).then_inc(masks, 1)
            pool.affine_select(out=R.before[:, :], in_=R.onesf[:, :], compare_op=ALU.is_gt, fill=0.0,
                               base=0, pattern=[[1, 128]], channel_multiplier=-1)
            pool.affine_select(out=R.upto[:, :], in_=R.onesf[:, :], compare_op=ALU.is_ge, fill=0.0,
                               base=0, pattern=[[1, 128]], channel_multiplier=-1)

        @block.vector
        def _(dve):
            dve.wait_ge(masks, 1)
            for h in range(4):
                dve.tensor_copy(R.identb[:, h, :], R.identf[:, :])


def sort_stage(nc, R, name, key, gather, rec, tile_of, relation=None, weight=None):
    with ExitStack() as ctx:
        def sb(n, shape, dt=F32):
            return ctx.enter_context(nc.sbuf_tensor(f"{name}_{n}", shape, dt))

        def sem(n):
            return nc.alloc_semaphore(f"{name}_{n}")

        ki = sb("ki", [P, EC], I32)
        kf = sb("kf", [P, EC])
        rc = sb("rc", [P, EC, REC], I32)
        rcf = rc[:, :, :].bitcast(F32)
        gi = sb("gi", [P, EC], I32)
        ri = sb("ri", [P, EC], I32)
        wf = sb("wf", [P, EC])
        gef = sb("gef", [P, 2, EC])
        inb = sb("inb", [P, NT, EC], BF16)
        run = sb("run", [P, 2, EC])
        slot = sb("slot", [P, EC])
        sloti = sb("sloti", [P, EC], I32)
        cnt = sb("cnt", [P, NT])
        tot = sb("tot", [128, NT])
        grp = sb("grp", [128, NT])
        grpi = sb("grpi", [128, NT], I32)
        endg = sb("endg", [128, NT])
        zer = sb("zer", [128, NT])
        one = sb("one", [128, NT])
        first = sb("first", [P, NT])
        gid = sb("gid", [128, NG])
        tf = sb("tf", [128, NG])
        W8 = 8
        stage_i = sb("stage_i", [P, 2, W8], I32)
        stage_r = sb("stage_r", [P, 2, W8, REC], I32)
        FILL = NG * GE // 128
        empty = sb("empty", [128, FILL, REC], I32)
        ps = ctx.enter_context(nc.psum_tensor(f"{name}_ps", [128, 2 * NT], F32))
        loaded, emptied, counted, summed, slotted = sem("loaded"), sem("emptied"), sem("counted"), sem("summed"), sem("slotted")
        made_empty, staged, iotad = sem("made_empty"), sem("staged"), sem("iotad")
        scattered = [sem("scattered0"), sem("scattered1")]
        issued = sem("issued")
        block = ctx.enter_context(nc.Block())

        def edges(a):
            return a.rearrange("(p c) -> p c", c=EC)

        @block.sync
        def _(sp):
            sp.dma_start(ki[:, :], edges(key)).then_inc(loaded, 16)
            sp.dma_start(gi[:, :], edges(gather)).then_inc(loaded, 16)
            if relation is not None:
                sp.dma_start(ri[:, :], edges(relation)).then_inc(loaded, 16)
                sp.dma_start(wf[:, :], edges(weight)).then_inc(loaded, 16)
            sp.wait_ge(made_empty, 1)
            sp.dma_start(rec.rearrange("(p c) r -> p (c r)", p=128),
                         empty[:, :, :].rearrange("p c r -> p (c r)")).then_inc(emptied, 16)

        @block.gpsimd
        def _(pool):
            pool.iota(gid[:, :], pattern=[[1, NG]], base=0, channel_multiplier=0,
                      allow_small_or_imprecise_dtypes=True).then_inc(iotad, 1)
            pool.wait_ge(emptied, 16)

            def scatter(n, k):
                pool.wait_ge(staged, n + 1)
                pool.sem_inc(issued, 1)
                for c in range(W8):
                    pool.indirect_dma_start(rec, bass.IndirectOffsetOnAxis(stage_i[:, k, c:c + 1], 0),
                                            stage_r[:, k, c, :], None).then_inc(scattered[k], 16)

            pairs(pool, EC // W8, scatter)
            for k in range(2):
                pool.wait_ge(scattered[k], 16 * W8 * (EC // W8 // 2))

        @block.vector
        def _(dve):
            dve.memset(empty[:, :, :], 0)
            dve.memset(zer[:, :], 0.0)
            dve.memset(one[:, :], 1.0)
            dve.memset(slot[:, :], 0.0)
            dve.drain()
            dve.memset(empty[:, :, :].bitcast(F32)[:, :, R_LOC], NOWHERE).then_inc(made_empty, 1)
            dve.wait_ge(loaded, 64 if relation is not None else 32)
            dve.tensor_copy(kf[:, :], ki[:, :])
            dve.tensor_copy(rc[:, :, R_IDX], gi[:, :])
            if relation is not None:
                dve.tensor_scalar(run[:, 0, :], ri[:, :], float(N), None, ALU.mult)
                dve.drain()
                dve.tensor_tensor(rc[:, :, R_ROW], run[:, 0, :], gi[:, :], ALU.add)
                dve.tensor_copy(rcf[:, :, R_REL], ri[:, :])
                dve.tensor_copy(rcf[:, :, R_W], wf[:, :])
            else:
                dve.memset(rc[:, :, R_ROW], 0)
                dve.memset(rcf[:, :, R_REL], 0.0)
                dve.memset(rcf[:, :, R_W], 0.0)
            dve.drain()
            dve.tensor_copy(rcf[:, :, R_LOC], kf[:, :])
            dve.memset(gef[:, 0, :], 1.0)
            for b in range(NT):
                dve.tensor_scalar(gef[:, (b + 1) % 2, :], kf[:, :], float(P * (b + 1)), None, ALU.is_ge)
                dve.drain()
                dve.tensor_tensor(inb[:, b, :], gef[:, b % 2, :], gef[:, (b + 1) % 2, :], ALU.subtract)
                dve.scalar_tensor_tensor(out=rcf[:, :, R_LOC], in0=gef[:, (b + 1) % 2, :], scalar=-float(P),
                                         in1=rcf[:, :, R_LOC], op0=ALU.mult, op1=ALU.add)
                dve.drain()
                dve.tensor_reduce(cnt[:, b:b + 1], inb[:, b, :], AX.X, ALU.add)
            dve.drain().then_inc(counted, 1)
            dve.wait_ge(summed, 1)
            dve.tensor_copy(tot[:, :], ps[:, 0:NT])
            dve.drain()
            dve.tensor_scalar(grpi[:, :], tot[:, :], float(GE - 1), None, ALU.add)
            dve.drain()
            dve.tensor_scalar(grpi[:, :], grpi[:, :], 9, None, ALU.arith_shift_right)
            dve.drain()
            dve.tensor_scalar(grp[:, :], grpi[:, :], 1.0, None, ALU.max)
            dve.drain()
            dve.tensor_tensor_scan(endg[:, :], one[:, :], grp[:, :], 0.0, ALU.mult, ALU.add)
            dve.drain()
            dve.tensor_tensor(grp[:, :], endg[:, :], grp[:, :], ALU.subtract)
            dve.drain()
            dve.tensor_scalar(grp[:, :], grp[:, :], float(GE), -1.0, ALU.mult, ALU.add)
            dve.drain()
            dve.tensor_tensor(first[:, :], grp[0:P, :], ps[0:P, NT:2 * NT], ALU.add)
            dve.wait_ge(iotad, 1)
            dve.memset(tf[:, :], 0.0)
            for b in range(NT - 1):
                dve.drain()
                dve.scalar_tensor_tensor(out=tf[:, :], in0=gid[:, :], scalar=endg[:, b:b + 1], in1=tf[:, :],
                                         op0=ALU.is_ge, op1=ALU.add)
            dve.drain()
            dve.tensor_copy(tile_of[:, :], tf[:, :])
            dve.memset(gef[:, 0, :], 1.0)
            dve.drain()
            for b in range(NT):
                k = b % 2
                dve.tensor_tensor_scan(run[:, k, :], gef[:, 0, :], inb[:, b, :], first[:, b:b + 1], ALU.mult, ALU.add)
                dve.drain()
                dve.tensor_tensor(run[:, k, :], run[:, k, :], inb[:, b, :], ALU.mult)
                dve.drain()
                dve.tensor_tensor(slot[:, :], slot[:, :], run[:, k, :], ALU.add)
            dve.drain()
            dve.tensor_copy(sloti[:, :], slot[:, :])
            dve.drain()

            def stage(n, k):
                if not is_first(n):
                    dve.wait_ge(scattered[k], (n - k) * (8 * W8))
                dve.tensor_copy(stage_i[:, k, :], sloti[:, ds(n * W8, W8)])
                dve.tensor_copy(stage_r[:, k, :, :], rc[:, ds(n * W8, W8), :])
                dve.drain().then_inc(staged, 1)

            pairs(dve, EC // W8, stage, peel=True)

        @block.tensor
        def _(pe):
            pe.wait_ge(counted, 1)
            pe.matmul(ps[:, 0:NT], R.onesf[0:P, :], cnt[:, :], start=True, stop=True)
            pe.matmul(ps[:, NT:2 * NT], R.before[0:P, :], cnt[:, :], start=True, stop=True).then_inc(summed, 1)


def chunks_of(w, width):
    return w.rearrange("(c k) n -> k c n", k=128)


def row_of(v, parts):
    return v.rearrange("(a n) -> a n", a=1).partition_broadcast(parts)


def normalize_stage(nc, R, name, src, dst):
    with ExitStack() as ctx:
        def sem(n):
            return nc.alloc_semaphore(f"{name}_{n}")

        def sb(n, shape, dt=F32):
            return ctx.enter_context(nc.sbuf_tensor(f"{name}_{n}", shape, dt))

        stats = sb("stats", [P, 2, nc.vector.BN_STATS_DIM])
        mv = sb("mv", [P, 2, nc.vector.BN_AGGR_DIM])
        mean = sb("mean", [P, NT])
        var = sb("var", [P, NT])
        std = sb("std", [P, NT])
        rstd = sb("rstd", [P, NT])
        rows = sb("rows", [P, 2, D])
        pt = [ctx.enter_context(nc.psum_tensor(f"{name}_pt{k}", [128, KC * P], F32)) for k in range(2)]
        have_var, have_std, normed, turned, evacuated = sem("have_var"), sem("have_std"), sem("normed"), sem("turned"), sem("evacuated")
        copied = sem("copied")
        block = ctx.enter_context(nc.Block())

        @block.vector
        def _(dve):
            def moments(t, k):
                dve.bn_stats(stats[:, k, :], node_tile(src, t))
                dve.drain()
                dve.bn_aggr(mv[:, k, :], stats[:, k, :])
                dve.drain()
                dve.tensor_copy(mean[:, ds(t, 1)], mv[:, k, 0:1])
                dve.tensor_scalar(var[:, ds(t, 1)], mv[:, k, 1:2], LN_EPS, None, ALU.add)

            pairs(dve, NT, moments)
            dve.drain().then_inc(have_var, 1)
            dve.wait_ge(have_std, 1)
            dve.reciprocal(rstd[:, :], std[:, :])
            dve.drain()
            dve.sem_inc(copied, 2)

            def scale(t, k):
                dve.wait_ge(copied, t + 1)
                dve.tensor_scalar(rows[:, k, :], node_tile(src, t), mean[:, ds(t, 1)], rstd[:, ds(t, 1)],
                                  ALU.subtract, ALU.mult).then_inc(normed, 1)

            pairs(dve, NT, scale)

        @block.scalar
        def _(act):
            act.wait_ge(have_var, 1)
            act.activation(std[:, :], var[:, :], ACT.Sqrt).then_inc(have_std, 1)

            def evacuate(t, k):
                act.wait_ge(turned, t + 1)
                act.activation(R.XNT[:, :, ds(t * P, P)], pt[k][:, :].rearrange("k (c p) -> k c p", p=P),
                               ACT.Copy).then_inc(evacuated, 1)

            act.sem_inc(evacuated, 2)
            pairs(act, NT, evacuate)

        @block.gpsimd
        def _(pool):
            def keep(t, k):
                pool.wait_ge(turned, t + 1)
                pool.tensor_copy(node_tile(dst, t), rows[:, k, :]).then_inc(copied, 1)

            pairs(pool, NT, keep)

        @block.tensor
        def _(pe):
            def turn(t, k):
                pe.wait_ge(normed, t + 1)
                pe.wait_ge(evacuated, t + 1)
                for c in range(KC):
                    last = pe.transpose(pt[k][:, c * P:(c + 1) * P], rows[:, k, c * 128:(c + 1) * 128],
                                        R.identf[0:P, 0:P])
                last.then_inc(turned, 1)

            pairs(pe, NT, turn)


def rows_stage(nc, R, name, weights, width, finish, rows=None, stride=D, offset=0,
               loads=(), store=None, before=None, cols=None):
    chunks = weights.shape[1]
    with ExitStack() as ctx:
        def sem(n):
            return nc.alloc_semaphore(f"{name}_{n}")

        def sb(n, shape, dt=F32):
            return ctx.enter_context(nc.sbuf_tensor(f"{name}_{n}", shape, dt))

        xt = sb("xt", [128, 2, chunks, P])
        staged = sb("staged", [P, 2, chunks * 128]) if rows is not None else None
        out = sb("out", [P, 2, width])
        pt = [ctx.enter_context(nc.psum_tensor(f"{name}_pt{k}", [128, chunks * P], F32)) for k in range(2)]
        ps = [ctx.enter_context(nc.psum_tensor(f"{name}_ps{k}", [P, width], F32)) for k in range(2)]
        loaded, copied, turned, ready, multiplied, finished = (sem(n) for n in (
            "loaded", "copied", "turned", "ready", "multiplied", "finished"))
        stored = [sem("stored0"), sem("stored1")]
        block = ctx.enter_context(nc.Block())

        @block.sync
        def _(sp):
            for to, of in loads:
                sp.dma_start(to, of).then_inc(loaded, 16)
            sp.wait_ge(loaded, 16 * len(loads)) if loads else None
            if store is not None:
                def put(t, k):
                    sp.wait_ge(finished, t + 3)
                    sp.dma_start(store(t), out[:, k, :]).then_inc(stored[k], 16)

                pairs(sp, NT, put)
                sp.wait_ge(stored[0], 16 * (NT - NT // 2))
                sp.wait_ge(stored[1], 16 * (NT // 2))

        @block.gpsimd
        def _(pool):
            if rows is not None:
                pool.wait_ge(loaded, 16 * len(loads)) if loads else None

                def stage(t, k):
                    pool.wait_ge(turned, t + 1)
                    pool.tensor_copy(staged[:, k, :], rows[:, ds(t * stride + offset, chunks * 128)]).then_inc(copied, 1)

                pairs(pool, NT, stage)
            else:
                def stage(t, k):
                    pool.wait_ge(multiplied, t + 1)
                    pool.tensor_copy(xt[:, k, :, :], (R.XNT if cols is None else cols)[:, :, ds(t * P, P)]).then_inc(ready, 1)

                pairs(pool, NT, stage)

        @block.scalar
        def _(act):
            if rows is not None:
                def evacuate(t, k):
                    act.wait_ge(turned, t + 3)
                    act.wait_ge(multiplied, t + 1)
                    act.activation(xt[:, k, :, :], pt[k][:, :].rearrange("k (c p) -> k c p", p=P),
                                   ACT.Copy).then_inc(ready, 1)

                pairs(act, NT, evacuate)

        @block.tensor
        def _(pe):
            pe.sem_inc(turned, 2)
            pe.sem_inc(multiplied, 2)
            pe.wait_ge(loaded, 16 * len(loads)) if loads else None

            def turn(t, k):
                pe.wait_ge(copied, t + 1)
                pe.wait_ge(ready, t - 1) if not isinstance(t, int) or t >= 2 else None
                for c in range(chunks):
                    last = pe.transpose(pt[k][:, c * P:(c + 1) * P], staged[:, k, c * 128:(c + 1) * 128],
                                        R.identf[0:P, 0:P])
                last.then_inc(turned, 1)

            def multiply(t, k):
                pe.wait_ge(ready, t + 1)
                pe.wait_ge(finished, t + 1)
                for a in range(0, width, 512):
                    b = min(a + 512, width)
                    for c in range(chunks):
                        last = pe.matmul(ps[k][:, a:b], xt[:, k, c, :], weights[:, c, a:b], start=(c == 0),
                                         stop=(c == chunks - 1))
                last.then_inc(multiplied, 1)

            if rows is None:
                pairs(pe, NT, multiply)
            else:
                turn(0, 0)
                turn(1, 1)
                with pe.Fori(0, NT // 2 - 1) as i:
                    multiply(i * 2, 0)
                    turn(i * 2 + 2, 0)
                    multiply(i * 2 + 1, 1)
                    turn(i * 2 + 3, 1)
                multiply(NT - 3, 0)
                turn(NT - 1, 0)
                multiply(NT - 2, 1)
                multiply(NT - 1, 0)

        @block.vector
        def _(dve):
            dve.sem_inc(finished, 2)
            dve.wait_ge(loaded, 16 * len(loads)) if loads else None
            if before is not None:
                before(dve)
                dve.drain()

            def take(t, k):
                dve.wait_ge(multiplied, t + 3)
                if store is not None and not is_first(t):
                    dve.wait_ge(stored[k], (t - k) * 8)
                finish(dve, t, ps[k], out[:, k, :])
                dve.drain().then_inc(finished, 1)

            pairs(dve, NT, take, peel=store is not None)


def edge_stage(nc, R, name, mode, rec, tile_of, acc, width, table=None, idx=R_IDX, spread=None):
    sw = 8 if mode == "relation" else 1
    with ExitStack() as ctx:
        def sem(n):
            return nc.alloc_semaphore(f"{name}_{n}")

        def sb(n, shape, dt=F32):
            return ctx.enter_context(nc.sbuf_tensor(f"{name}_{n}", shape, dt))

        rc = sb("rc", [128, 2, GT, REC], I32)
        rcf = rc[:, :, :, :].bitcast(F32)
        wide = table.shape[1] if table is not None else 8
        got = sb("got", [128, 2, GT, wide])
        place = sb("place", [128, 2, GT, P])
        placew = sb("placew", [128, 2, GT, P])
        placet = sb("placet", [P, 2, GT, 128])
        small = sb("small", [128, 2, GT, 8])
        rel = sb("rel", [128, 2, GT, 8])
        coef = sb("coef", [128, 2, GT])
        coef2 = sb("coef2", [128, 2, GT])
        pt = ctx.enter_context(nc.psum_tensor(f"{name}_pt", [P, 2, 512], F32))
        pq = ctx.enter_context(nc.psum_tensor(f"{name}_pq", [128, 2, 512], F32))
        pa = [ctx.enter_context(nc.psum_tensor(f"{name}_pa{k}", [P, 512], F32)) for k in range(2)]
        rec_in = [sem("rec_in0"), sem("rec_in1")]
        got_in = [sem("got_in0"), sem("got_in1")]
        names = ("placed", "weighed", "turned", "evacuated", "spreaded", "logit", "expd", "summed", "added", "ordered")
        placed, weighed, turned, evacuated, spreaded, logit, expd, summed, added, ordered = (sem(n) for n in names)
        needs_spread = mode in ("relation", "gat")
        block = ctx.enter_context(nc.Block())

        @block.sync
        def _(sp):
            def fetch(g, k):
                sp.wait_ge(added, g + 1)
                sp.dma_start(rc[:, k, :, :].rearrange("p j r -> p (j r)"),
                             rec[ds(g * GE, GE), :].rearrange("(p j) r -> p (j r)", j=GT)).then_inc(rec_in[k], 16)

            pairs(sp, NG, fetch)

        @block.gpsimd
        def _(pool):
            if table is not None:
                def gather(g, k):
                    pool.wait_ge(rec_in[k], (g - k) * 8 + 16)
                    pool.sem_inc(ordered, 1)
                    for j in range(GT):
                        pool.indirect_dma_start(got[:, k, j, :], None, table,
                                                bass.IndirectOffsetOnAxis(rc[:, k, j, idx:idx + 1], 0)).then_inc(got_in[k], 16)

                pairs(pool, NG, gather)

        @block.scalar
        def _(act):
            if needs_spread:
                def step(g, k):
                    act.wait_ge(turned, g + 1)
                    act.activation(placet[:, k, :, :], pt[:, k, :].rearrange("p (j e) -> p j e", e=128),
                                   ACT.Copy).then_inc(evacuated, 1)
                    if mode == "gat":
                        act.wait_ge(logit, g + 1)
                        act.activation(coef2[:, k, :], coef[:, k, :], ACT.Exp, scale=-1.0).then_inc(expd, 1)

                pairs(act, NG, step)

        @block.tensor
        def _(pe):
            tile_reg = pe.alloc_register(f"{name}_pe_tile")

            def step(g, k):
                if needs_spread:
                    pe.wait_ge(placed, g + 1)
                    for j in range(GT):
                        last = pe.transpose(pt[:, k, j * 128:(j + 1) * 128], place[:, k, j, :], R.identf[:, :])
                    last.then_inc(turned, 1)
                    pe.reg_load(tile_reg, tile_of[0:1, ds(g, 1)])
                    b = pe.snap(tile_reg)
                    pe.wait_ge(evacuated, g + 1)
                    for j in range(GT):
                        last = pe.matmul(pq[:, k, j * 8:j * 8 + sw], placet[:, k, j, :], spread[:, ds(b * sw, sw)],
                                         start=True, stop=True)
                    last.then_inc(spreaded, 1)
                pe.wait_ge(weighed, g + 1)
                if table is not None:
                    pe.wait_ge(got_in[k], (g - k) * (8 * GT) + 16 * GT)
                for j in range(GT):
                    rhs = rel[:, k, j, :] if mode == "count" else got[:, k, j, 0:width]
                    lhs = place if mode == "count" else placew
                    last = pe.matmul(pa[k][:, 0:width], lhs[:, k, j, :], rhs, start=(j == 0), stop=(j == GT - 1))
                last.then_inc(summed, 1)

            pairs(pe, NG, step)

        @block.vector
        def _(dve):
            tile_reg = dve.alloc_register(f"{name}_dve_tile")
            dve.memset(acc, 0.0)
            dve.drain()
            dve.sem_inc(added, 2)

            def step(g, k):
                dve.wait_ge(rec_in[k], (g - k) * 8 + 16)
                for j in range(GT):
                    loc, w = rcf[:, k, j, R_LOC:R_LOC + 1], rcf[:, k, j, R_W:R_W + 1]
                    if mode == "weight":
                        dve.tensor_scalar(placew[:, k, j, :], R.iota[:, 0:P], loc, w, ALU.is_equal, ALU.mult)
                    else:
                        dve.tensor_scalar(place[:, k, j, :], R.iota[:, 0:P], loc, None, ALU.is_equal)
                    if mode in ("count", "relation"):
                        dve.tensor_scalar(rel[:, k, j, :], R.iota[:, 0:8], rcf[:, k, j, R_REL:R_REL + 1], None,
                                          ALU.is_equal)
                dve.drain().then_inc(placed, 1)
                if mode == "relation":
                    dve.wait_ge(spreaded, g + 1)
                    dve.tensor_tensor(small[:, k, :, :], pq[:, k, 0:GT * 8].rearrange("p (j r) -> p j r", r=8),
                                      rel[:, k, :, :], ALU.mult)
                    dve.drain()
                    dve.tensor_reduce(coef[:, k, :], small[:, k, :, :], AX.X, ALU.add)
                    dve.drain()
                    dve.tensor_tensor(coef2[:, k, :], coef[:, k, :], rcf[:, k, :, R_W], ALU.mult)
                    dve.drain()
                if mode == "gat":
                    dve.wait_ge(spreaded, g + 1)
                    dve.wait_ge(got_in[k], (g - k) * (8 * GT) + 16 * GT)
                    dve.tensor_copy(coef2[:, k, :], got[:, k, :, wide - 1])
                    dve.drain()
                    dve.tensor_tensor(coef[:, k, :], pq[:, k, 0:GT * 8].rearrange("p (j r) -> p j r", r=8)[:, :, 0],
                                      coef2[:, k, :], ALU.add)
                    dve.drain()
                    dve.scalar_tensor_tensor(out=coef[:, k, :], in0=coef[:, k, :], scalar=0.2, in1=coef[:, k, :],
                                             op0=ALU.mult, op1=ALU.max)
                    dve.drain().then_inc(logit, 1)
                    dve.wait_ge(expd, g + 1)
                if needs_spread:
                    for j in range(GT):
                        dve.tensor_scalar(placew[:, k, j, :], place[:, k, j, :], coef2[:, k, j:j + 1], None, ALU.mult)
                    dve.drain()
                dve.sem_inc(weighed, 1)
                dve.reg_load(tile_reg, tile_of[0:1, ds(g, 1)])
                b = dve.snap(tile_reg)
                dve.wait_ge(summed, g + 1)
                into = acc[:, ds(b * width, width)]
                dve.tensor_tensor(into, into, pa[k][:, 0:width], ALU.add)
                dve.drain().then_inc(added, 1)

            pairs(dve, NG, step)


def attention_edge_stage(nc, R, name, table, keys, acc):
    W = D + H0
    with ExitStack() as ctx:
        def sem(n):
            return nc.alloc_semaphore(f"{name}_{n}")

        def sb(n, shape, dt=F32):
            return ctx.enter_context(nc.sbuf_tensor(f"{name}_{n}", shape, dt))

        rc = sb("rc", [128, 2, GT, REC], I32)
        rcf = rc[:, :, :, :].bitcast(F32)
        got = sb("got", [128, 2, GT, 2 * D])
        place = sb("place", [128, 2, GT, P])
        placeb = sb("placeb", [128, 2, GT, P], BF16)
        outside = sb("outside", [128, 2, GT, P], BF16)
        placet = sb("placet", [P, 2, GT, 128])
        prod = sb("prod", [128, GT, D])
        score = sb("score", [128, 2, GT, H0])
        diag = sb("diag", [128, 2, H0, 128], BF16)
        msg = sb("msg", [128, 2, GT, W])
        tmax = sb("tmax", [P, GT, H0])
        gmax = sb("gmax", [P, H0])
        high = sb("high", [P, NT * H0])
        new = sb("new", [P, 2, H0])
        drop = sb("drop", [P, 2, H0])
        alpha = sb("alpha", [P, 2, H0])
        shifted = sb("shifted", [128, 2, GT, H0])
        keyed = ctx.enter_context(nc.psum_tensor(f"{name}_keyed", [128, GT * D], F32))
        spread = ctx.enter_context(nc.psum_tensor(f"{name}_spread", [P, H0 * 128], F32))
        pt = ctx.enter_context(nc.psum_tensor(f"{name}_pt", [P, 512], F32))
        pm = ctx.enter_context(nc.psum_tensor(f"{name}_pm", [128, 512], F32))
        pa = [ctx.enter_context(nc.psum_tensor(f"{name}_pa{k}", [P, 512], F32)) for k in range(2)]
        rec_in = [sem("rec_in0"), sem("rec_in1")]
        got_in = [sem("got_in0"), sem("got_in1")]
        names = ("ordered", "placed", "turned", "evacuated", "keys_spread", "scored", "diagonal", "spread_out",
                 "reduced", "maxed", "max_spread", "shifted", "exped", "messaged", "summed", "added")
        (ordered, placed, turned, evacuated, keys_spread, scored, diagonal, spread_out, reduced, maxed, max_spread,
         have_shifted, exped, messaged, summed, added) = (sem(n) for n in names)
        block = ctx.enter_context(nc.Block())

        @block.sync
        def _(sp):
            def fetch(g, k):
                sp.wait_ge(added, g + 1)
                sp.dma_start(rc[:, k, :, :].rearrange("p j r -> p (j r)"),
                             rec[ds(g * GE, GE), :].rearrange("(p j) r -> p (j r)", j=GT)).then_inc(rec_in[k], 16)

            rec = R.rec_dst
            pairs(sp, NG, fetch)

        @block.gpsimd
        def _(pool):
            def gather(g, k):
                pool.wait_ge(rec_in[k], (g - k) * 8 + 16)
                pool.sem_inc(ordered, 1)
                for j in range(GT):
                    pool.indirect_dma_start(got[:, k, j, :], None, table,
                                            bass.IndirectOffsetOnAxis(rc[:, k, j, R_IDX:R_IDX + 1], 0)).then_inc(got_in[k], 16)

            pairs(pool, NG, gather)

        @block.scalar
        def _(act):
            def step(g, k):
                act.wait_ge(turned, g + 1)
                act.activation(placet[:, k, :, :], pt[:, :].rearrange("p (j e) -> p j e", e=128),
                               ACT.Copy).then_inc(evacuated, 1)
                act.wait_ge(maxed, g + 1)
                act.activation(alpha[:, k, :], drop[:, k, :], ACT.Exp)
                act.wait_ge(have_shifted, g + 1)
                act.activation(msg[:, k, :, D:W], shifted[:, k, :, :], ACT.Exp)
                act.drain().then_inc(exped, 1)

            pairs(act, NG, step)

        @block.tensor
        def _(pe):
            tile_reg = pe.alloc_register(f"{name}_pe_tile")

            def step(g, k):
                pe.reg_load(tile_reg, R.tile_dst[0:1, ds(g, 1)])
                b = pe.snap(tile_reg)
                pe.wait_ge(placed, g + 1)
                for j in range(GT):
                    last = pe.transpose(pt[:, j * 128:(j + 1) * 128], place[:, k, j, :], R.identf[:, :])
                last.then_inc(turned, 1)
                pe.wait_ge(evacuated, g + 1)
                for j in range(GT):
                    last = pe.matmul(keyed[:, j * D:(j + 1) * D], placet[:, k, j, :], keys[:, ds(b * D, D)],
                                     start=True, stop=True)
                last.then_inc(keys_spread, 1)
                for j in range(GT):
                    pe.wait_ge(diagonal, g * GT + j + 1)
                    pe.wait_ge(reduced, g * GT + (j + 1))
                    for h in range(0, H0, 4):
                        pe.matmul(spread[:, h * 128:(h + 4) * 128], placeb[:, k, j, :], diag[:, j % 2, h:h + 4, :],
                                  start=True, stop=False)
                        last = pe.matmul(spread[:, h * 128:(h + 4) * 128], outside[:, k, j, :], R.identb[:, :, :],
                                         start=False, stop=True)
                    last.then_inc(spread_out, 1)
                pe.wait_ge(maxed, g + 1)
                for j in range(GT):
                    last = pe.matmul(pm[:, j * H0:(j + 1) * H0], placet[:, k, j, :], new[:, k, :], start=True, stop=True)
                last.then_inc(max_spread, 1)
                pe.wait_ge(messaged, g + 1)
                for j in range(GT):
                    last = pe.matmul(pa[k][:, 0:W], place[:, k, j, :], msg[:, k, j, :], start=(j == 0), stop=(j == GT - 1))
                last.then_inc(summed, 1)

            pairs(pe, NG, step)

        @block.vector
        def _(dve):
            tile_reg = dve.alloc_register(f"{name}_dve_tile")
            dve.memset(acc, 0.0)
            dve.memset(high[:, :], NEG)
            dve.drain()
            dve.sem_inc(added, 2)
            dve.sem_inc(reduced, 1)

            def step(g, k):
                dve.reg_load(tile_reg, R.tile_dst[0:1, ds(g, 1)])
                b = dve.snap(tile_reg)
                dve.wait_ge(rec_in[k], (g - k) * 8 + 16)
                for j in range(GT):
                    loc = rcf[:, k, j, R_LOC:R_LOC + 1]
                    dve.tensor_scalar(place[:, k, j, :], R.iota[:, 0:P], loc, None, ALU.is_equal)
                    dve.tensor_scalar(placeb[:, k, j, :], R.iota[:, 0:P], loc, None, ALU.is_equal)
                    dve.tensor_scalar(outside[:, k, j, :], R.iota[:, 0:P], loc, NEG, ALU.not_equal, ALU.mult)
                dve.drain().then_inc(placed, 1)
                dve.wait_ge(keys_spread, g + 1)
                dve.wait_ge(got_in[k], (g - k) * (8 * GT) + 16 * GT)
                dve.tensor_tensor(prod[:, :, :], keyed[:, :].rearrange("p (j d) -> p j d", d=D), got[:, k, :, 0:D], ALU.mult)
                dve.drain()
                dve.tensor_reduce(score[:, k, :, :], prod[:, :, :].rearrange("p j (h e) -> p j h e", e=DH), AX.X, ALU.add)
                dve.drain()
                dve.tensor_scalar(score[:, k, :, :], score[:, k, :, :], float(DH) ** -0.5, None, ALU.mult)
                dve.drain()

                def diagonals(j):
                    dve.tensor_tensor(diag[:, j % 2, :, :],
                                      R.identb[:, 0:1, :].broadcast_to([128, H0, 128]),
                                      score[:, k, j, :].rearrange("p (h a) -> p h a", a=1).broadcast_to([128, H0, 128]),
                                      ALU.mult).then_inc(diagonal, 1)

                diagonals(0)
                for j in range(GT):
                    if j + 1 < GT:
                        diagonals(j + 1)
                    dve.wait_ge(spread_out, g * GT + j + 1)
                    dve.tensor_reduce(tmax[:, j, :], spread[:, :].rearrange("p (h e) -> p h e", e=128), AX.X,
                                      ALU.max).then_inc(reduced, 1)
                dve.drain()
                dve.tensor_reduce(gmax[:, :], tmax[:, :, :].rearrange("p j h -> p h j"), AX.X, ALU.max)
                dve.drain()
                old = high[:, ds(b * H0, H0)]
                dve.tensor_tensor(new[:, k, :], old, gmax[:, :], ALU.max)
                dve.drain()
                dve.tensor_tensor(drop[:, k, :], old, new[:, k, :], ALU.subtract)
                dve.drain()
                dve.tensor_copy(old, new[:, k, :])
                dve.drain().then_inc(maxed, 1)
                dve.wait_ge(max_spread, g + 1)
                dve.tensor_tensor(shifted[:, k, :, :], score[:, k, :, :],
                                  pm[:, 0:GT * H0].rearrange("p (j h) -> p j h", h=H0), ALU.subtract)
                dve.drain().then_inc(have_shifted, 1)
                dve.wait_ge(exped, g + 1)
                into = acc[:, ds(b * W, W)]
                intov = acc[:, ds(b * W, D)].rearrange("p (h e) -> p h e", e=DH)
                dve.tensor_tensor(msg[:, k, :, 0:D].rearrange("p j (h e) -> p j h e", e=DH),
                                  got[:, k, :, D:2 * D].rearrange("p j (h e) -> p j h e", e=DH),
                                  msg[:, k, :, D:W].rearrange("p j (h a) -> p j h a", a=1).broadcast_to([128, GT, H0, DH]),
                                  ALU.mult)
                dve.tensor_tensor(intov, intov,
                                  alpha[:, k, :].rearrange("p (h a) -> p h a", a=1).broadcast_to([P, H0, DH]), ALU.mult)
                dve.tensor_tensor(acc[:, ds(b * W + D, H0)], acc[:, ds(b * W + D, H0)], alpha[:, k, :], ALU.mult)
                dve.drain().then_inc(messaged, 1)
                dve.wait_ge(summed, g + 1)
                dve.tensor_tensor(into, into, pa[k][:, 0:W], ALU.add)
                dve.drain().then_inc(added, 1)

            pairs(dve, NG, step)


def first_graph_layer(nc, R, a):
    W = D + H0
    with ExitStack() as ctx:
        def sb(n, shape, dt=F32):
            return ctx.enter_context(nc.sbuf_tensor(f"g0_{n}", shape, dt))

        keys = sb("keys", [P, NT * D])
        acc = sb("acc", [P, NT * W])
        table = nc.dram_tensor("g0_table", (N, 2 * D), F32).ap()
        with ExitStack() as inner:
            wsb = inner.enter_context(nc.sbuf_tensor("g0_w", [128, KC, 3 * D], F32))
            bsb = inner.enter_context(nc.sbuf_tensor("g0_b", [P, 3 * D], F32))

            def finish(dve, t, ps, out):
                dve.tensor_tensor(out, ps[:, 0:2 * D], bsb[:, 0:2 * D], ALU.add)

            rows_stage(nc, R, "g0qv", wsb[:, :, 0:2 * D], 2 * D, finish,
                       loads=[(wsb[:, :, 0:D], chunks_of(a["L0_gnn_Wq"], D)), (wsb[:, :, D:2 * D], chunks_of(a["L0_gnn_Wv"], D)),
                              (bsb[:, 0:D], row_of(a["L0_gnn_bq"], P)), (bsb[:, D:2 * D], row_of(a["L0_gnn_bv"], P))],
                       store=lambda t: table[ds(t * P, P), :])

            def finish_k(dve, t, ps, out):
                dve.tensor_tensor(node_tile(keys, t), ps[:, 0:D], bsb[:, 2 * D:3 * D], ALU.add)

            rows_stage(nc, R, "g0k", wsb[:, :, 2 * D:3 * D], D, finish_k,
                       loads=[(wsb[:, :, 2 * D:3 * D], chunks_of(a["L0_gnn_Wk"], D)),
                              (bsb[:, 2 * D:3 * D], row_of(a["L0_gnn_bk"], P))])
        attention_edge_stage(nc, R, "g0e", table, keys, acc[:, :])
        z = sb("z", [P, NT, H0])
        block = ctx.enter_context(nc.Block())

        @block.vector
        def _(dve):
            accv = acc[:, :].rearrange("p (t w) -> p t w", w=W)
            dve.tensor_scalar(z[:, :, :], accv[:, :, D:W], 1e-16, None, ALU.max)
            dve.drain()
            dve.reciprocal(z[:, :, :], z[:, :, :])
            dve.drain()

            def normalize(t, k):
                v = acc[:, ds(t * W, D)].rearrange("p (h e) -> p h e", e=DH)
                zt = z[:, ds(t, 1), :].rearrange("p a h -> p h a").broadcast_to([P, H0, DH])
                dve.tensor_tensor(v, v, zt, ALU.mult)
                dve.drain()
                dve.tensor_tensor(node_tile(R.X, t), node_tile(R.X, t), acc[:, ds(t * W, D)], ALU.add)

            pairs(dve, NT, normalize)


def softmax_mixer(nc, R, name, w_qkv, w_out, b_out, g_pre=None, mem_kv=None, g_out=None):
    HID, HEADS, HD = 128, 4, 32
    S = 3 * HID + 1
    second = g_pre is not None
    with ExitStack() as ctx:
        def sb(n, shape, dt=F32):
            return ctx.enter_context(nc.sbuf_tensor(f"{name}_{n}", shape, dt))

        def sem(n):
            return nc.alloc_semaphore(f"{name}_{n}")

        qkv = sb("qkv", [P, NT * S])
        view = qkv[:, :].rearrange("p (t s) -> p t s", s=S)
        wout = sb("wout", [128, D])
        bout = sb("bout", [P, D])
        M = sb("M", [128, 1, D])
        tmp = sb("tmp", [P, NT * D])
        rn = sb("rn", [P, NT])
        ss = sb("ss", [P, NT])
        if second:
            rms_stage(nc, f"{name}_pre", R.XN, tmp, ss, rn)
            gp = sb("gp", [128, KC])
            gout = sb("gout", [P, D])
            memk = sb("memk", [MEM, HID])
            memkt = sb("memkt", [HID, MEM])
            memv = sb("memv", [MEM, HID + 1])
            O = sb("O", [P, NT * D])
        with ExitStack() as inner:
            w = inner.enter_context(nc.sbuf_tensor(f"{name}_w", [128, KC, 3 * HID], F32))
            loads = [(w[:, :, :], chunks_of(w_qkv, 3 * HID)), (wout[:, :], w_out), (bout[:, :], row_of(b_out, P))]
            if second:
                loads += [(gp[:, :], g_pre)]
                loads += [(gout[:, :], row_of(g_out, P)),
                          (memk[:, :].rearrange("m (h d) -> m h d", d=HD), mem_kv[0].rearrange("h d m -> m h d")),
                          (memv[:, 0:HID].rearrange("m (h d) -> m h d", d=HD), mem_kv[1].rearrange("h d m -> m h d")),
                          (memkt[:, :], mem_kv[0].rearrange("h d m -> (h d) m"))]

            def before(dve):
                dve.memset(view[:, :, 3 * HID:S], 1.0)

            def finish(dve, t, ps, out):
                if second:
                    dve.tensor_scalar(qkv[:, ds(t * S, 3 * HID)], ps[:, 0:3 * HID], rn[:, ds(t, 1)], None, ALU.mult)
                else:
                    dve.tensor_copy(qkv[:, ds(t * S, 3 * HID)], ps[:, 0:3 * HID])

            if second:
                scale_weights_stage(nc, f"{name}_sw", loads, w, gp, float(D) ** 0.5)
                loads = []
            rows_stage(nc, R, f"{name}_qkv", w[:, :, :], 3 * HID, finish, loads=loads, before=before)

        cmax = sb("cmax", [P, HID])
        kmax = sb("kmax", [HID, 1])
        mmax = sb("mmax", [HID, 1])
        dmax = sb("dmax", [HID, HID])
        rowmax = sb("rowmax", [P, HID])
        ctx_sb = sb("ctx_sb", [HID, HID])
        ctx_t = sb("ctx_t", [HID, HID])
        zr = sb("zr", [HID, 1])
        heads = sb("heads", [HID, HEADS])
        qred = sb("qred", [P, NT * HEADS])
        (have_cmax, cmax_turned, have_diag, row_spread, ready, exped, summed, have_ctx, ctx_turned, have_t, have_m,
         q_ready, q_exped) = (sem(n) for n in (
             "have_cmax", "cmax_turned", "have_diag", "row_spread", "shifted", "exped", "summed", "have_ctx",
             "ctx_turned", "have_t", "have_m", "q_ready", "q_exped"))
        with nc.psum_tensor(f"{name}_p", [128, 5, 512], F32) as banks, nc.Block() as block:
            p1, p2, p3, p4, p5 = (banks[:, n, :] for n in range(5))
            keysv = view[:, :, HID:2 * HID]
            queries = view[:, :, 0:HID].rearrange("p t (h e) -> p t h e", e=HD)
            qr = qred[:, :].rearrange("p (t h a) -> p t h a", h=HEADS, a=1).broadcast_to([P, NT, HEADS, HD])

            @block.vector
            def _(dve):
                if second:
                    dve.memset(memv[:, HID:HID + 1], 1.0)
                    dve.tensor_reduce(qred[:, :], queries, AX.X, ALU.max)
                    dve.drain()
                    dve.tensor_tensor(queries, queries, qr, ALU.subtract)
                    dve.drain().then_inc(q_ready, 1)
                dve.tensor_reduce(cmax[:, :], view[:, :, HID:2 * HID].rearrange("p t c -> p c t"), AX.X, ALU.max)
                dve.drain().then_inc(have_cmax, 1)
                dve.wait_ge(cmax_turned, 1)
                dve.tensor_reduce(kmax[:, :], p1[:, 0:P], AX.X, ALU.max)
                dve.drain()
                if second:
                    dve.tensor_reduce(mmax[:, :], memkt[:, :], AX.X, ALU.max)
                    dve.drain()
                    dve.tensor_tensor(kmax[:, :], kmax[:, :], mmax[:, :], ALU.max)
                    dve.drain()
                dve.tensor_scalar(dmax[:, :], R.identf[:, :], kmax[:, :], None, ALU.mult)
                dve.drain().then_inc(have_diag, 1)
                dve.wait_ge(row_spread, 1)
                dve.tensor_copy(rowmax[:, :], p2[0:P, 0:HID])
                dve.drain()
                dve.tensor_tensor(keysv, keysv, rowmax[:, :].rearrange("p (a c) -> p a c", a=1).broadcast_to([P, NT, HID]),
                                  ALU.subtract)
                if second:
                    dve.tensor_tensor(memk[:, :], memk[:, :], rowmax[0:MEM, :], ALU.subtract)
                dve.drain().then_inc(ready, 1)
                if second:
                    dve.wait_ge(q_exped, 1)
                    dve.tensor_reduce(qred[:, :], queries, AX.X, ALU.add)
                    dve.drain()
                    dve.reciprocal(qred[:, :], qred[:, :])
                    dve.drain()
                    dve.tensor_tensor(queries, queries, qr, ALU.mult)
                dve.memset(heads[:, :], 0.0)
                dve.drain()
                for h in range(HEADS):
                    dve.memset(heads[h * HD:(h + 1) * HD, h:h + 1], float(HD) ** -0.5)
                dve.wait_ge(summed, 1)
                dve.reciprocal(zr[:, :], p3[:, HID:HID + 1])
                dve.drain()
                for h in range(HEADS):
                    dve.tensor_scalar(ctx_sb[:, h * HD:(h + 1) * HD], p3[:, h * HD:(h + 1) * HD], zr[:, :],
                                      heads[:, h:h + 1], ALU.mult, ALU.mult)
                dve.drain().then_inc(have_ctx, 1)
                dve.wait_ge(ctx_turned, 1)
                dve.tensor_copy(ctx_t[:, :], p4[:, 0:HID])
                dve.drain().then_inc(have_t, 1)
                dve.wait_ge(have_m, 1)
                dve.tensor_copy(M[:, 0, :], p5[:, 0:D])

            @block.scalar
            def _(act):
                if second:
                    act.wait_ge(q_ready, 1)
                    act.activation(queries, queries, ACT.Exp)
                    act.drain().then_inc(q_exped, 1)
                act.wait_ge(ready, 1)
                act.activation(keysv, keysv, ACT.Exp)
                if second:
                    act.activation(memk[:, :], memk[:, :], ACT.Exp)
                act.drain().then_inc(exped, 1)

            @block.tensor
            def _(pe):
                pe.wait_ge(have_cmax, 1)
                pe.transpose(p1[:, 0:P], cmax[:, :], R.identf[0:P, 0:P]).then_inc(cmax_turned, 1)
                pe.wait_ge(have_diag, 1)
                pe.matmul(p2[:, 0:HID], R.onesf[:, :], dmax[:, :], start=True, stop=True).then_inc(row_spread, 1)
                pe.wait_ge(exped, 1)
                for t in range(NT):
                    last = pe.matmul(p3[:, 0:HID + 1], view[:, t, HID:2 * HID], view[:, t, 2 * HID:S], start=(t == 0),
                                     stop=(t == NT - 1 and not second))
                if second:
                    last = pe.matmul(p3[:, 0:HID + 1], memk[:, :], memv[:, :], start=False, stop=True)
                last.then_inc(summed, 1)
                pe.wait_ge(have_ctx, 1)
                pe.transpose(p4[:, 0:HID], ctx_sb[:, :], R.identf[:, :]).then_inc(ctx_turned, 1)
                pe.wait_ge(have_t, 1)
                pe.matmul(p5[:, 0:D], ctx_t[:, :], wout[:, :], start=True, stop=True).then_inc(have_m, 1)

        if not second:
            def finish_out(dve, t, ps, out):
                x = node_tile(R.X, t)
                dve.tensor_tensor(x, x, ps[:, 0:D], ALU.add)
                dve.drain()
                dve.tensor_tensor(x, x, bout[:, :], ALU.add)

            rows_stage(nc, R, f"{name}_out", M[:, :, :], D, finish_out, rows=qkv, stride=S)
            return

        def finish_out(dve, t, ps, out):
            dve.tensor_tensor(node_tile(O, t), ps[:, 0:D], bout[:, :], ALU.add)

        rows_stage(nc, R, f"{name}_out", M[:, :, :], D, finish_out, rows=qkv, stride=S)
        rms_stage(nc, f"{name}_post", O, tmp, ss, rn)
        with nc.Block() as block:
            @block.vector
            def _(dve):
                dve.tensor_scalar(gout[:, :], gout[:, :], float(D) ** 0.5, None, ALU.mult)
                dve.drain()

                def add(t, k):
                    o, x = node_tile(O, t), node_tile(R.X, t)
                    dve.scalar_tensor_tensor(out=o, in0=o, scalar=rn[:, ds(t, 1)], in1=gout[:, :], op0=ALU.mult, op1=ALU.mult)
                    dve.tensor_tensor(x, x, node_tile(R.XN, t), ALU.add)
                    dve.drain()
                    dve.tensor_tensor(x, x, o, ALU.add)

                pairs(dve, NT, add)


def rms_stage(nc, name, src, tmp, ss, rn):
    with ExitStack() as ctx:
        squared = nc.alloc_semaphore(f"{name}_squared")
        added = nc.alloc_semaphore(f"{name}_added")
        rooted = nc.alloc_semaphore(f"{name}_rooted")
        block = ctx.enter_context(nc.Block())

        @block.scalar
        def _(act):
            act.activation(tmp[:, :], src[:, :], ACT.Square)
            act.drain().then_inc(squared, 1)
            act.wait_ge(added, 1)
            act.activation(rn[:, :], ss[:, :], ACT.Sqrt).then_inc(rooted, 1)

        @block.vector
        def _(dve):
            dve.wait_ge(squared, 1)
            dve.tensor_reduce(ss[:, :], tmp[:, :].rearrange("p (t d) -> p t d", d=D), AX.X, ALU.add)
            dve.drain().then_inc(added, 1)
            dve.wait_ge(rooted, 1)
            dve.tensor_scalar(rn[:, :], rn[:, :], 1e-12, None, ALU.max)
            dve.drain()
            dve.reciprocal(rn[:, :], rn[:, :])


def scale_weights_stage(nc, name, loads, w, g, factor):
    with ExitStack() as ctx:
        loaded = nc.alloc_semaphore(f"{name}_loaded")
        block = ctx.enter_context(nc.Block())

        @block.sync
        def _(sp):
            with nc.allow_non_contiguous_dma(reason="a few hundred words"):
                for to, of in loads:
                    sp.dma_start(to, of).then_inc(loaded, 16)
            sp.wait_ge(loaded, 16 * len(loads))

        @block.vector
        def _(dve):
            dve.wait_ge(loaded, 16 * len(loads))
            for c in range(KC):
                dve.tensor_scalar(w[:, c, :], w[:, c, :], g[:, c:c + 1], factor, ALU.mult, ALU.mult)


def router_stage(nc, R, name, experts, gate_w, gate_b, G, top, capacity=None):
    with ExitStack() as ctx:
        def sb(n, shape, dt=F32):
            return ctx.enter_context(nc.sbuf_tensor(f"{name}_{n}", shape, dt))

        def sem(n):
            return nc.alloc_semaphore(f"{name}_{n}")

        gw = sb("gw", [128, KC, experts])
        gb = sb("gb", [P, experts])
        lg = sb("lg", [P, NT * experts])
        lgv = lg[:, :].rearrange("p (t e) -> p t e", e=experts)
        best = sb("best", [P, NT, 8])
        besti = sb("besti", [P, NT, 8])

        def finish(dve, t, ps, out):
            dve.tensor_tensor(lg[:, ds(t * experts, experts)], ps[:, 0:experts], gb[:, :], ALU.add)

        rows_stage(nc, R, f"{name}_lg", gw[:, :, :], experts, finish,
                   loads=[(gw[:, :, :], chunks_of(gate_w, experts)), (gb[:, :], row_of(gate_b, P))])
        row = sb("row", [P, 2, experts])
        top8 = sb("top8", [P, 2, 8])
        idx8 = sb("idx8", [P, 2, 8], U32)
        w1 = sb("w1", [P, NT])
        w2 = sb("w2", [P, NT])
        diff = sb("diff", [P, NT])
        pick = sb("pick", [P, NT, experts])
        cum = sb("cum", [P, NT, experts])
        ones = sb("ones", [P, NT])
        base = sb("base", [P, NT, experts])
        totals = sb("totals", [P, NT, experts])
        ex = sb("ex", [P, NT, experts])
        ps = ctx.enter_context(nc.psum_tensor(f"{name}_ps", [P, 512], F32))
        ps2 = ctx.enter_context(nc.psum_tensor(f"{name}_ps2", [P, 512], F32))
        shifted, exped, picked, counted = sem("shifted"), sem("exped"), sem("picked"), sem("counted")
        block = ctx.enter_context(nc.Block())
        Gv = G[:, :].rearrange("p (t e) -> p t e", e=experts)
        shape = [P, NT, experts]

        def wide(a):
            return a.rearrange("p (t a) -> p t a", a=1).broadcast_to(shape)

        @block.scalar
        def _(act):
            act.wait_ge(shifted, 1)
            if top == 2:
                act.activation(w2[:, :], diff[:, :], ACT.Exp)
            else:
                act.activation(ex[:, :, :], ex[:, :, :], ACT.Exp)
            act.drain().then_inc(exped, 1)

        @block.tensor
        def _(pe):
            if top == 1:
                pe.wait_ge(picked, 1)
                flat = pick[:, :, :].rearrange("p t e -> p (t e)")
                pe.matmul(ps[:, 0:NT * experts], R.upto[0:P, 0:P], flat, start=True, stop=True)
                pe.matmul(ps2[:, 0:NT * experts], R.onesf[0:P, 0:P], flat, start=True, stop=True).then_inc(counted, 1)

        @block.vector
        def _(dve):
            def largest(t, k):
                dve.tensor_copy(row[:, k, :], lg[:, ds(t * experts, experts)])
                dve.drain()
                dve.max(top8[:, k, :], row[:, k, :])
                dve.drain()
                dve.max_index(idx8[:, k, :], top8[:, k, :], row[:, k, :])
                dve.drain()
                dve.tensor_copy(best[:, ds(t, 1), :], top8[:, k, :].rearrange("p (a e) -> p a e", a=1))
                dve.tensor_copy(besti[:, ds(t, 1), :], idx8[:, k, :].rearrange("p (a e) -> p a e", a=1))

            pairs(dve, NT, largest)
            dve.drain()
            iota = R.iota[0:P, 0:experts].rearrange("p (a e) -> p a e", a=1).broadcast_to(shape)
            dve.tensor_tensor(pick[:, :, :], iota, besti[:, :, 0:1].broadcast_to(shape), ALU.is_equal)
            if top == 2:
                dve.tensor_tensor(diff[:, :], best[:, :, 1], best[:, :, 0], ALU.subtract)
                dve.drain().then_inc(shifted, 1)
                dve.wait_ge(exped, 1)
                dve.tensor_scalar(w1[:, :], w2[:, :], 1.0, None, ALU.add)
                dve.drain()
                dve.reciprocal(w1[:, :], w1[:, :])
                dve.drain()
                dve.tensor_tensor(w2[:, :], w2[:, :], w1[:, :], ALU.mult)
                dve.tensor_tensor(Gv, pick[:, :, :], wide(w1[:, :]), ALU.mult)
                dve.drain()
                dve.tensor_tensor(pick[:, :, :], iota, besti[:, :, 1:2].broadcast_to(shape), ALU.is_equal)
                dve.drain()
                dve.tensor_tensor(pick[:, :, :], pick[:, :, :], wide(w2[:, :]), ALU.mult)
                dve.drain()
                dve.tensor_tensor(Gv, Gv, pick[:, :, :], ALU.add)
                return
            dve.tensor_tensor(ex[:, :, :], lgv, best[:, :, 0:1].broadcast_to(shape), ALU.subtract)
            dve.memset(ones[:, :], 1.0)
            dve.drain().then_inc(shifted, 1)
            dve.sem_inc(picked, 1)
            dve.wait_ge(exped, 1)
            dve.tensor_reduce(w1[:, :], ex[:, :, :], AX.X, ALU.add)
            dve.drain()
            dve.reciprocal(w1[:, :], w1[:, :])
            dve.wait_ge(counted, 1)
            dve.tensor_copy(totals[:, :, :], ps2[:, 0:NT * experts].rearrange("p (t e) -> p t e", e=experts))
            dve.tensor_copy(cum[:, :, :], ps[:, 0:NT * experts].rearrange("p (t e) -> p t e", e=experts))
            dve.drain()
            for e in range(experts):
                dve.tensor_tensor_scan(base[:, :, e], ones[:, :], totals[:, :, e], 0.0, ALU.mult, ALU.add)
            dve.drain()
            dve.tensor_tensor(base[:, :, :], base[:, :, :], totals[:, :, :], ALU.subtract)
            dve.drain()
            dve.tensor_tensor(cum[:, :, :], cum[:, :, :], base[:, :, :], ALU.add)
            dve.drain()
            dve.tensor_scalar(cum[:, :, :], cum[:, :, :], float(capacity), None, ALU.is_le)
            dve.tensor_tensor(pick[:, :, :], pick[:, :, :], wide(w1[:, :]), ALU.mult)
            dve.drain()
            dve.tensor_tensor(Gv, pick[:, :, :], cum[:, :, :], ALU.mult)


def experts_stage(nc, R, name, experts, F, w1, b1, w2, b2, G, acc, func, ln=None):
    NF = F // 128
    NQ = NCH + 1
    with ExitStack() as ctx:
        def sb(n, shape, dt=F32):
            return ctx.enter_context(nc.sbuf_tensor(f"{name}_{n}", shape, dt))

        def sem(n):
            return nc.alloc_semaphore(f"{name}_{n}")

        w1s = sb("w1s", [128, 2, KC, F])
        w2s = sb("w2s", [128, 2, NF, D])
        b1s = sb("b1s", [128, 2, NF])
        b2s = sb("b2s", [P, 2, D])
        fold = ln is not None
        if fold:
            lgs = sb("lgs", [128, 2, 2 * KC])
            w1g = sb("w1g", [128, KC, F])
            b1g = sb("b1g", [128, 2, NF])
        hid = sb("hid", [128, NF, CHUNK])
        y = sb("y", [P, 2, D])
        p1 = [ctx.enter_context(nc.psum_tensor(f"{name}_p1{k}", [128, 512], F32)) for k in range(4)]
        p2 = [ctx.enter_context(nc.psum_tensor(f"{name}_p2{k}", [P, 512], F32)) for k in range(4)]
        w_in = [sem("w_in0"), sem("w_in1")]
        first, acted, second, taken, expert_done, folded, bias_ready, begun = (sem(n) for n in (
            "first", "acted", "second", "taken", "expert_done", "folded", "bias_ready", "begun"))
        LOADS = 5 if fold else 4
        block = ctx.enter_context(nc.Block())

        @block.sync
        def _(sp):
            def load(e, k):
                sp.wait_ge(expert_done, e + 1)
                one = ds(e, 1)
                sp.dma_start(w1s[:, k, :, :], w1[one].rearrange("a (c k) f -> k (a c) f", k=128)).then_inc(w_in[k], 16)
                sp.dma_start(w2s[:, k, :, :], w2[one].rearrange("a (c k) d -> k (a c) d", k=128)).then_inc(w_in[k], 16)
                sp.dma_start(b1s[:, k, :], b1[one].rearrange("a k c -> (a k) c")).then_inc(w_in[k], 16)
                sp.dma_start(b2s[:, k, :], b2[one].broadcast_to([P, D])).then_inc(w_in[k], 16)
                if fold:
                    sp.dma_start(lgs[:, k, :], ln[one].rearrange("a k c -> (a k) c")).then_inc(w_in[k], 16)

            pairs(sp, experts, load)

        def chunk_loop(eng, e, k, body):
            eng.sem_inc(begun, 1)
            with eng.Fori(0, NCH) as c:
                body(e * NQ + c, c * CHUNK, 4, c * 4)
            body(e * NQ + NCH, NCH * CHUNK, NT - 4 * NCH, 4 * NCH)

        @block.tensor
        def _(pe):
            def expert(e, k):
                pe.wait_ge(w_in[k], (e - k) * (8 * LOADS) + 16 * LOADS)
                wk = w1g if fold else w1s[:, k, :, :]
                if fold:
                    pe.wait_ge(taken, e * NT + 4)
                    for f in range(NF):
                        for c in range(KC):
                            last = pe.matmul(p1[0][:, f:f + 1],
                                             w1s[:, k, c, f * 128:(f + 1) * 128], lgs[:, k, KC + c:KC + c + 1],
                                             start=(c == 0), stop=(c == KC - 1))
                    last.then_inc(bias_ready, 1)
                    pe.wait_ge(folded, e + 1)

                def chunk(q, at, tiles, tile):
                    n = tiles * P
                    for f in range(NF):
                        pe.wait_ge(acted, q * NF + (f + 1))
                        for c in range(KC):
                            last = pe.matmul(p1[f % 4][:, 0:n], wk[:, c, f * 128:(f + 1) * 128], R.XNT[:, c, ds(at, n)],
                                             start=(c == 0), stop=(c == KC - 1))
                        last.then_inc(first, 1)
                    pe.wait_ge(acted, q * NF + (NF + 4))
                    for j in range(tiles):
                        pe.wait_ge(taken, e * NT + tile + (j + 1 if j > 0 else 4))
                        for f in range(NF):
                            last = pe.matmul(p2[j][:, 0:D], hid[:, f, j * P:(j + 1) * P], w2s[:, k, f, :], start=(f == 0),
                                             stop=(f == NF - 1))
                        last.then_inc(second, 1)

                chunk_loop(pe, e, k, chunk)

            pairs(pe, experts, expert)

        @block.scalar
        def _(act):
            act.sem_inc(acted, 4)

            def expert(e, k):
                act.wait_ge(w_in[k], (e - k) * (8 * LOADS) + 16 * LOADS)
                bias = b1s
                if fold:
                    act.wait_ge(folded, e + 1)
                    bias = b1g

                def chunk(q, at, tiles, tile):
                    n = tiles * P
                    for f in range(NF):
                        act.wait_ge(first, q * NF + (f + 1))
                        act.activation(hid[:, f, 0:n], p1[f % 4][:, 0:n], func, bias=bias[:, k, f:f + 1]).then_inc(acted, 1)

                chunk_loop(act, e, k, chunk)

            pairs(act, experts, expert)

        @block.vector
        def _(dve):
            dve.sem_inc(taken, 4)
            dve.sem_inc(expert_done, 2)

            def expert(e, k):
                dve.wait_ge(w_in[k], (e - k) * (8 * LOADS) + 16 * LOADS)
                if fold:
                    dve.wait_ge(bias_ready, e + 1)
                    dve.tensor_tensor(b1g[:, k, :], p1[0][:, 0:NF], b1s[:, k, :], ALU.add)
                    for c in range(KC):
                        dve.tensor_scalar(w1g[:, c, :], w1s[:, k, c, :], lgs[:, k, c:c + 1], None, ALU.mult)
                    dve.drain().then_inc(folded, 1)

                def chunk(q, at, tiles, tile):
                    for j in range(tiles):
                        dve.wait_ge(second, e * NT + tile + (j + 1))
                        dve.tensor_tensor(y[:, j % 2, :], p2[j][:, 0:D], b2s[:, k, :], ALU.add)
                        dve.drain().then_inc(taken, 1)
                        to = acc[:, ds((tile + j) * D, D)]
                        dve.scalar_tensor_tensor(out=to, in0=y[:, j % 2, :], scalar=G[:, ds((tile + j) * experts + e, 1)],
                                                 in1=to, op0=ALU.mult, op1=ALU.add)
                        dve.drain()

                chunk_loop(dve, e, k, chunk)
                dve.sem_inc(expert_done, 1)

            pairs(dve, experts, expert)


def add_stage(nc, pieces):
    with nc.Block() as block:
        @block.vector
        def _(dve):
            for to, of in pieces:
                def add(t, k):
                    dve.tensor_tensor(node_tile(to, t), node_tile(to, t), node_tile(of, t), ALU.add)

                pairs(dve, NT, add)
                dve.drain()


def first_feed_forward(nc, R, a):
    E0, F0 = a["L0_ffn_w1"].shape[0], a["L0_ffn_w1"].shape[2]
    with ExitStack() as ctx:
        G = ctx.enter_context(nc.sbuf_tensor("f0_G", [P, NT * E0], F32))
        gamma = ctx.enter_context(nc.sbuf_tensor("f0_gamma", [P, D], F32))
        beta = ctx.enter_context(nc.sbuf_tensor("f0_beta", [P, D], F32))
        loaded = nc.alloc_semaphore("f0_loaded")
        normalize_stage(nc, R, "f0ln", R.X, R.XN)
        router_stage(nc, R, "f0r", E0, a["L0_ffn_gate_w"], a["L0_ffn_gate_b"], G, 2)
        experts_stage(nc, R, "f0", E0, F0, a["L0_ffn_w1"], a["L0_ffn_b1"], a["L0_ffn_w2"], a["L0_ffn_b2"], G, R.XN[:, :],
                      ACT.Relu)
        normalize_stage(nc, R, "f0ln2", R.XN, R.XN)
        with nc.Block() as block:
            @block.sync
            def _(sp):
                sp.dma_start(gamma[:, :], row_of(a["L0_ffn_gamma"], P)).then_inc(loaded, 16)
                sp.dma_start(beta[:, :], row_of(a["L0_ffn_beta"], P)).then_inc(loaded, 16)

            @block.vector
            def _(dve):
                dve.wait_ge(loaded, 32)

                def add(t, k):
                    n, x = node_tile(R.XN, t), node_tile(R.X, t)
                    dve.tensor_tensor(n, n, gamma[:, :], ALU.mult)
                    dve.tensor_tensor(x, x, beta[:, :], ALU.add)
                    dve.drain()
                    dve.tensor_tensor(x, x, n, ALU.add)

                pairs(dve, NT, add)


def count_stage(nc, R):
    edge_stage(nc, R, "cnt", "count", R.rec_dst, R.tile_dst, R.inv_count[:, :], 8)
    with ExitStack() as ctx:
        deg = ctx.enter_context(nc.sbuf_tensor("deg", [P, NT], F32))
        turned = ctx.enter_context(nc.sbuf_tensor("deg_turned", [NT, P], F32))
        pt = ctx.enter_context(nc.psum_tensor("deg_pt", [NT, P], F32))
        have_deg, rooted, inverted, have_t, copied, stored = (nc.alloc_semaphore(f"deg_{n}") for n in (
            "have", "rooted", "inverted", "have_t", "copied", "stored"))
        block = ctx.enter_context(nc.Block())

        @block.vector
        def _(dve):
            counts = R.inv_count[:, :].rearrange("p (t r) -> p t r", r=8)
            dve.tensor_reduce(deg[:, :], counts, AX.X, ALU.add)
            dve.drain()
            dve.tensor_scalar(deg[:, :], deg[:, :], 1.0, None, ALU.max)
            dve.tensor_scalar(R.inv_count[:, :], R.inv_count[:, :], 1.0, None, ALU.max)
            dve.drain().then_inc(have_deg, 1)
            dve.reciprocal(R.inv_count[:, :], R.inv_count[:, :])
            dve.wait_ge(rooted, 1)
            dve.reciprocal(deg[:, :], deg[:, :])
            dve.drain().then_inc(inverted, 1)
            dve.wait_ge(have_t, 1)
            dve.tensor_copy(turned[:, :], pt[:, :]).then_inc(copied, 1)

        @block.scalar
        def _(act):
            act.wait_ge(have_deg, 1)
            act.activation(deg[:, :], deg[:, :], ACT.Sqrt).then_inc(rooted, 1)

        @block.tensor
        def _(pe):
            pe.wait_ge(inverted, 1)
            pe.transpose(pt[:, :], deg[:, :], R.identf[0:P, 0:P]).then_inc(have_t, 1)

        @block.sync
        def _(sp):
            sp.wait_ge(copied, 1)
            sp.dma_start(R.norm_row, turned[:, :]).then_inc(stored, 16)
            sp.wait_ge(stored, 16)


def relation_graph_layer(nc, R, a):
    W = a["L1_gnn_weight"]
    RN = W.shape[0]
    table = nc.dram_tensor("g1_table", (RN * N, D), F32).ap()
    to = table.rearrange("(r n) d -> n r d", r=RN)
    with ExitStack() as ctx:
        w = ctx.enter_context(nc.sbuf_tensor("g1_w", [128, KC, 2 * D], F32))
        for r in range(0, RN, 2):
            def finish(dve, t, ps, out):
                dve.tensor_copy(out, ps[:, 0:2 * D])

            rows_stage(nc, R, f"g1t{r}", w[:, :, :], 2 * D, finish,
                       loads=[(w[:, :, 0:D], chunks_of(W[r], D)), (w[:, :, D:2 * D], chunks_of(W[r + 1], D))],
                       store=lambda t, r=r: to[ds(t * P, P), r:r + 2, :])
    with ExitStack() as ctx:
        w = ctx.enter_context(nc.sbuf_tensor("g1_root", [128, KC, D], F32))
        b = ctx.enter_context(nc.sbuf_tensor("g1_bias", [P, D], F32))

        def finish_root(dve, t, ps, out):
            x = node_tile(R.X, t)
            dve.tensor_tensor(x, x, ps[:, 0:D], ALU.add)
            dve.drain()
            dve.tensor_tensor(x, x, b[:, :], ALU.add)

        rows_stage(nc, R, "g1root", w[:, :, :], D, finish_root,
                   loads=[(w[:, :, :], chunks_of(a["L1_gnn_root"], D)), (b[:, :], row_of(a["L1_gnn_bias"], P))])
    with ExitStack() as ctx:
        acc = ctx.enter_context(nc.sbuf_tensor("g1_acc", [P, NT * D], F32))
        edge_stage(nc, R, "g1e", "relation", R.rec_dst, R.tile_dst, acc[:, :], D, table=table, idx=R_ROW,
                   spread=R.inv_count[:, :])
        add_stage(nc, [(R.X, acc)])


def second_feed_forward(nc, R, a):
    E1, F1 = a["L1_ffn_w1"].shape[0], a["L1_ffn_w1"].shape[2]
    capacity = -(-5 * N // (4 * E1))
    with ExitStack() as ctx:
        G = ctx.enter_context(nc.sbuf_tensor("f1_G", [P, NT * E1], F32))
        normalize_stage(nc, R, "f1ln", R.X, R.XN)
        router_stage(nc, R, "f1r", E1, a["L1_ffn_gate_w"], a["L1_ffn_gate_b"], G, 1, capacity)
        with ExitStack() as inner:
            with nc.Block() as block:
                @block.vector
                def _(dve):
                    dve.memset(R.XN[:, :], 0.0)
            experts_stage(nc, R, "f1", E1, F1, a["L1_ffn_w1"], a["L1_ffn_b1"], a["L1_ffn_w2"], a["L1_ffn_b2"], G,
                          R.XN[:, :], ACT.Relu)
            mask = inner.enter_context(nc.sbuf_tensor("f1_mask", [P, NT * D], U32))
            clean = inner.enter_context(nc.sbuf_tensor("f1_clean", [P, NT * D], F32))
            fill = inner.enter_context(nc.sbuf_tensor("f1_fill", [P, 1], F32))
            with nc.Block() as block:
                @block.vector
                def _(dve):
                    dve.tensor_tensor(mask[:, :], R.XN[:, :], R.XN[:, :], ALU.is_equal)
                    dve.memset(clean[:, :], 0.0)
                    dve.memset(fill[:, :], 1e4)
                    dve.drain()
                    dve.copy_predicated(clean[:, :], mask[:, :], R.XN[:, :])
                    dve.drain()
                    dve.tensor_scalar(mask[:, :], clean[:, :], 3.4028235e38, None, ALU.is_gt)
                    dve.drain()
                    dve.copy_predicated(clean[:, :], mask[:, :], fill[:, 0:1].broadcast_to([P, NT * D]))
                    dve.drain()
                    dve.tensor_scalar(mask[:, :], clean[:, :], -3.4028235e38, None, ALU.is_lt)
                    dve.memset(fill[:, :], -1e4)
                    dve.drain()
                    dve.copy_predicated(clean[:, :], mask[:, :], fill[:, 0:1].broadcast_to([P, NT * D]))
            add_stage(nc, [(R.X, clean)])


def turn_stage(nc, R, name, src, dst):
    with ExitStack() as ctx:
        staged = ctx.enter_context(nc.sbuf_tensor(f"{name}_staged", [P, 2, D], F32))
        pt = [ctx.enter_context(nc.psum_tensor(f"{name}_pt{k}", [128, KC * P], F32)) for k in range(2)]
        copied, turned, evacuated = (nc.alloc_semaphore(f"{name}_{n}") for n in ("copied", "turned", "evacuated"))
        block = ctx.enter_context(nc.Block())

        @block.gpsimd
        def _(pool):
            def stage(t, k):
                pool.wait_ge(turned, t + 1)
                pool.tensor_copy(staged[:, k, :], node_tile(src, t)).then_inc(copied, 1)

            pairs(pool, NT, stage)

        @block.tensor
        def _(pe):
            pe.sem_inc(turned, 2)

            def turn(t, k):
                pe.wait_ge(copied, t + 1)
                pe.wait_ge(evacuated, t + 1)
                for c in range(KC):
                    last = pe.transpose(pt[k][:, c * P:(c + 1) * P], staged[:, k, c * 128:(c + 1) * 128],
                                        R.identf[0:P, 0:P])
                last.then_inc(turned, 1)

            pairs(pe, NT, turn)

        @block.scalar
        def _(act):
            act.sem_inc(evacuated, 2)

            def evacuate(t, k):
                act.wait_ge(turned, t + 3)
                act.activation(dst[:, :, ds(t * P, P)], pt[k][:, :].rearrange("k (c p) -> k c p", p=P),
                               ACT.Copy).then_inc(evacuated, 1)

            pairs(act, NT, evacuate)


def batchnorm_product_stage(nc, R, name, w, src, dst, cols, scale_row=None):
    NQ = NCH + 1
    with ExitStack() as ctx:
        def sb(n, shape, dt=F32):
            return ctx.enter_context(nc.sbuf_tensor(f"{name}_{n}", shape, dt))

        def sem(n):
            return nc.alloc_semaphore(f"{name}_{n}")

        ws = sb("ws", [128, KC, D])
        gb = sb("gb", [128, 2, KC])
        stats = sb("stats", [128, NT * nc.vector.BN_STATS_DIM])
        mv = sb("mv", [128, KC, nc.vector.BN_AGGR_DIM])
        std = sb("std", [128, KC])
        scale = sb("scale", [128, KC])
        shift = sb("shift", [128, KC])
        row = sb("row", [128, N]) if scale_row is not None else None
        ps = [ctx.enter_context(nc.psum_tensor(f"{name}_ps{k}", [128, KC, 512], F32)) for k in range(2)]
        loaded, multiplied, taken, have_var, rooted, scaled = (sem(n) for n in (
            "loaded", "multiplied", "taken", "have_var", "rooted", "scaled"))
        LOADS = 3 + (scale_row is not None)
        block = ctx.enter_context(nc.Block())

        def chunk_pairs(eng, body):
            with eng.Fori(0, NCH // 2) as i:
                for k in range(2):
                    body(i * 2 + k, k, i * (2 * CHUNK) + k * CHUNK, CHUNK)
            body(NCH, 0, NCH * CHUNK, N - NCH * CHUNK)

        @block.sync
        def _(sp):
            sp.dma_start(ws[:, :, :], chunks_of(w, D)).then_inc(loaded, 16)
            sp.dma_start(gb[:, 0, :], cols[0]).then_inc(loaded, 16)
            sp.dma_start(gb[:, 1, :], cols[1]).then_inc(loaded, 16)
            if row is not None:
                sp.dma_start(row[:, :], scale_row.rearrange("t p -> (t p)").rearrange("(a n) -> a n", a=1)
                             .partition_broadcast(128)).then_inc(loaded, 16)

        @block.tensor
        def _(pe):
            pe.wait_ge(loaded, 16 * LOADS)

            def chunk(q, k, at, n):
                pe.wait_ge(taken, q + 1)
                for m in range(KC):
                    for c in range(KC):
                        last = pe.matmul(ps[k][:, m, 0:n], ws[:, c, m * 128:(m + 1) * 128], src[:, c, ds(at, n)],
                                         start=(c == 0), stop=(c == KC - 1))
                last.then_inc(multiplied, 1)

            chunk_pairs(pe, chunk)

        @block.vector
        def _(dve):
            dve.wait_ge(loaded, 16 * LOADS)
            dve.sem_inc(taken, 2)

            def chunk(q, k, at, n):
                dve.wait_ge(multiplied, q + 1)
                for m in range(KC):
                    if row is not None:
                        dve.tensor_tensor(dst[:, m, ds(at, n)], ps[k][:, m, 0:n], row[:, ds(at, n)], ALU.mult)
                    else:
                        dve.tensor_copy(dst[:, m, ds(at, n)], ps[k][:, m, 0:n])
                dve.drain().then_inc(taken, 1)

            chunk_pairs(dve, chunk)
            for m in range(KC):
                def moments(t, k):
                    dve.bn_stats(stats[:, ds(t * nc.vector.BN_STATS_DIM, nc.vector.BN_STATS_DIM)], dst[:, m, ds(t * P, P)])

                dve.drain()
                pairs(dve, NT, moments)
                dve.drain()
                dve.bn_aggr(mv[:, m, :], stats[:, :])
            dve.drain()
            dve.tensor_scalar(std[:, :], mv[:, :, 1], LN_EPS, None, ALU.add)
            dve.drain().then_inc(have_var, 1)
            dve.wait_ge(rooted, 1)
            dve.reciprocal(std[:, :], std[:, :])
            dve.drain()
            dve.tensor_tensor(scale[:, :], gb[:, 0, :], std[:, :], ALU.mult)
            dve.drain()
            dve.tensor_tensor(shift[:, :], mv[:, :, 0], scale[:, :], ALU.mult)
            dve.drain()
            dve.tensor_tensor(shift[:, :], gb[:, 1, :], shift[:, :], ALU.subtract)
            dve.drain().then_inc(scaled, 1)

        @block.scalar
        def _(act):
            act.wait_ge(have_var, 1)
            act.activation(std[:, :], std[:, :], ACT.Sqrt).then_inc(rooted, 1)
            act.wait_ge(scaled, 1)
            for m in range(KC):
                act.activation(dst[:, m, :], dst[:, m, :], ACT.Relu, bias=shift[:, m:m + 1], scale=scale[:, m:m + 1])


def store_rows_stage(nc, name, src, table):
    stored = nc.alloc_semaphore(f"{name}_stored")
    with nc.Block() as block:
        @block.sync
        def _(sp):
            sp.dma_start(table.rearrange("(t p) d -> p t d", p=P),
                         src[:, :].rearrange("p (t d) -> p t d", d=D)).then_inc(stored, 16)
            sp.wait_ge(stored, 16)


def isomorphism_graph_layer(nc, R, a):
    table = nc.dram_tensor("g2_table", (N, D), F32).ap()
    store_rows_stage(nc, "g2t", R.XN, table)
    with ExitStack() as ctx:
        acc = ctx.enter_context(nc.sbuf_tensor("g2_acc", [P, NT * D], F32))
        eps = ctx.enter_context(nc.sbuf_tensor("g2_eps", [P, 1], F32))
        loaded = nc.alloc_semaphore("g2_loaded")
        edge_stage(nc, R, "g2e", "weight", R.rec_dst, R.tile_dst, acc[:, :], D, table=table)
        with nc.Block() as block:
            @block.sync
            def _(sp):
                sp.dma_start(eps[:, :], row_of(a["L2_gnn_eps_weight"], P)).then_inc(loaded, 16)

            @block.vector
            def _(dve):
                dve.wait_ge(loaded, 16)

                def add(t, k):
                    dve.scalar_tensor_tensor(out=node_tile(acc, t), in0=node_tile(R.XN, t), scalar=eps[:, 0:1],
                                             in1=node_tile(acc, t), op0=ALU.mult, op1=ALU.add)

                pairs(dve, NT, add)
        yt = ctx.enter_context(nc.sbuf_tensor("g2_yt", [128, KC, N], F32))
        zt = ctx.enter_context(nc.sbuf_tensor("g2_zt", [128, KC, N], F32))
        turn_stage(nc, R, "g2turn", acc, yt)
        batchnorm_product_stage(nc, R, "g2a", a["L2_gnn_w1"], yt, zt,
                                (a["L2_gnn_gamma1"], a["L2_gnn_beta1"]))
        batchnorm_product_stage(nc, R, "g2b", a["L2_gnn_w2"], zt, yt,
                                (a["L2_gnn_gamma_h"], a["L2_gnn_beta_h"]), scale_row=R.norm_row)
        eye = ctx.enter_context(nc.sbuf_tensor("g2_eye", [128, KC, D], F32))

        def before(dve):
            dve.memset(eye[:, :, :], 0.0)
            dve.drain()
            for c in range(KC):
                dve.tensor_copy(eye[:, c, c * 128:(c + 1) * 128], R.identf[:, :])
            dve.drain()

        with nc.Block() as block:
            @block.vector
            def _(dve):
                before(dve)

        def finish(dve, t, ps, out):
            x = node_tile(R.X, t)
            dve.tensor_tensor(x, x, ps[:, 0:D], ALU.add)
            dve.drain()
            dve.tensor_tensor(x, x, node_tile(R.XN, t), ALU.add)

        rows_stage(nc, R, "g2back", eye[:, :, :], D, finish, cols=yt)


def head_norm_mixer(nc, R, a):
    HEADS = D // DH
    with ExitStack() as ctx:
        def sb(n, shape, dt=F32):
            return ctx.enter_context(nc.sbuf_tensor(f"m2_{n}", shape, dt))

        def sem(n):
            return nc.alloc_semaphore(f"m2_{n}")

        K = sb("K", [P, NT * D])
        V = sb("V", [P, NT * D])
        dev = sb("dev", [P, NT * D])
        red = sb("red", [P, NT * HEADS])
        par = sb("par", [P, 4, D])
        M = sb("M", [128, KC, D])
        loaded, deviated, squared, summed, rooted, ready, multiplied = (sem(n) for n in (
            "loaded", "deviated", "squared", "summed", "rooted", "ready", "multiplied"))

        def by_head(b):
            return b[:, :].rearrange("p (t e) -> p t e", e=DH)

        redw = red[:, :].rearrange("p (t a) -> p t a", a=1).broadcast_to([P, NT * HEADS, DH])
        with nc.psum_tensor("m2_ps", [128, KC, 512], F32) as ps, nc.Block() as block:
            @block.sync
            def _(sp):
                for n, v in enumerate(("kln_weight", "kln_bias", "vln_weight", "vln_bias")):
                    sp.dma_start(par[:, n, :], row_of(a[f"L2_mix_{v}"].rearrange("h a e -> (h a e)"), P)).then_inc(loaded, 16)

            @block.vector
            def _(dve):
                dve.tensor_reduce(red[:, :], by_head(R.XN), AX.X, ALU.add)
                dve.drain()
                dve.tensor_scalar(red[:, :], red[:, :], 1.0 / DH, None, ALU.mult)
                dve.drain()
                dve.tensor_tensor(by_head(dev), by_head(R.XN), redw, ALU.subtract)
                dve.drain().then_inc(deviated, 1)
                dve.wait_ge(squared, 1)
                dve.tensor_reduce(red[:, :], by_head(K), AX.X, ALU.add)
                dve.drain().then_inc(summed, 1)
                dve.wait_ge(rooted, 1)
                dve.tensor_scalar(red[:, :], red[:, :], LN_EPS, None, ALU.add)
                dve.drain()
                dve.reciprocal(red[:, :], red[:, :])
                dve.drain()
                dve.tensor_tensor(by_head(dev), by_head(dev), redw, ALU.mult)
                dve.drain()
                dve.wait_ge(loaded, 64)
                for n, to in ((0, K), (2, V)):
                    def affine(t, k):
                        dve.tensor_tensor(node_tile(to, t), node_tile(dev, t), par[:, n, :], ALU.mult)
                        dve.drain()
                        dve.tensor_tensor(node_tile(to, t), node_tile(to, t), par[:, n + 1, :], ALU.add)

                    pairs(dve, NT, affine)
                dve.drain().then_inc(ready, 1)
                dve.memset(M[:, :, :], 0.0)
                dve.wait_ge(multiplied, 1)
                dve.drain()
                for c in range(KC):
                    for h in range(128 // DH):
                        b, at = slice(h * DH, (h + 1) * DH), c * 128 + h * DH
                        dve.tensor_scalar(M[b, c, at:at + DH], ps[b, c, h * DH:(h + 1) * DH], 1.0 / N, None, ALU.mult)

            @block.scalar
            def _(act):
                act.wait_ge(deviated, 1)
                act.activation(K[:, :], dev[:, :], ACT.Square)
                act.drain().then_inc(squared, 1)
                act.wait_ge(summed, 1)
                act.activation(red[:, :], red[:, :], ACT.Sqrt, scale=1.0 / (DH - 1))
                act.drain().then_inc(rooted, 1)

            @block.tensor
            def _(pe):
                pe.wait_ge(ready, 1)
                for c in range(KC):
                    for t in range(NT):
                        b = slice(t * D + c * 128, t * D + (c + 1) * 128)
                        last = pe.matmul(ps[:, c, 0:128], K[:, b], V[:, b], start=(t == 0), stop=(t == NT - 1))
                last.then_inc(multiplied, 1)

        def finish(dve, t, ps, out):
            x = node_tile(R.X, t)
            dve.tensor_tensor(x, x, ps[:, 0:D], ALU.add)
            dve.drain()
            dve.tensor_tensor(x, x, node_tile(R.XN, t), ALU.add)

        rows_stage(nc, R, "m2out", M[:, :, :], D, finish)


def third_feed_forward(nc, R, a):
    E2, F2 = a["L2_ffn_W1"].shape[0], a["L2_ffn_W1"].shape[2]
    with ExitStack() as ctx:
        G = ctx.enter_context(nc.sbuf_tensor("f2_G", [P, NT * E2], F32))
        normalize_stage(nc, R, "f2ln", R.X, R.XN)
        router_stage(nc, R, "f2r", E2, a["L2_ffn_Wr"], a["L2_ffn_br"], G, 2)
        normalize_stage(nc, R, "f2ln2", R.XN, R.XN)
        experts_stage(nc, R, "f2", E2, F2, a["L2_ffn_W1"], a["L2_ffn_b1"], a["L2_ffn_W2"], a["L2_ffn_b2"], G, R.X[:, :],
                      ACT.Gelu, ln=a["L2_ffn_ln"])


def attention_graph_layer(nc, R, a):
    W = D + 1
    table = nc.dram_tensor("g3_table", (N, D + 2), F32).ap()
    with ExitStack() as ctx:
        def sb(n, shape, dt=F32):
            return ctx.enter_context(nc.sbuf_tensor(f"g3_{n}", shape, dt))

        S = sb("S", [P, NT])
        acc = sb("acc", [P, NT * W])
        with ExitStack() as inner:
            w = inner.enter_context(nc.sbuf_tensor("g3_w", [128, KC, D + 2], F32))
            av = inner.enter_context(nc.sbuf_tensor("g3_a", [P, 2, D], F32))
            tmp = inner.enter_context(nc.sbuf_tensor("g3_tmp", [P, 2, D], F32))

            def finish(dve, t, ps, out):
                dve.tensor_copy(out[:, 0:D], ps[:, 0:D])
                dve.memset(out[:, D:D + 1], 1.0)
                dve.tensor_tensor(tmp[:, 0, :], ps[:, 0:D], av[:, 0, :], ALU.mult)
                dve.tensor_tensor(tmp[:, 1, :], ps[:, 0:D], av[:, 1, :], ALU.mult)
                dve.drain()
                dve.tensor_reduce(S[:, ds(t, 1)], tmp[:, 0, :], AX.X, ALU.add)
                dve.tensor_reduce(out[:, D + 1:D + 2], tmp[:, 1, :], AX.X, ALU.add)

            def before(dve):
                dve.memset(w[:, :, D:D + 2], 0.0)

            with nc.Block() as block:
                @block.vector
                def _(dve):
                    before(dve)

            rows_stage(nc, R, "g3h", w[:, :, :], D + 2, finish,
                       loads=[(w[:, :, 0:D], chunks_of(a["L3_gnn_W"], D)),
                              (av[:, 0, :], row_of(a["L3_gnn_a"][0:D], P)), (av[:, 1, :], row_of(a["L3_gnn_a"][D:2 * D], P))],
                       store=lambda t: table[ds(t * P, P), :])
        edge_stage(nc, R, "g3e", "gat", R.rec_src, R.tile_src, acc[:, :], W, table=table, spread=S[:, :])
        accv = acc[:, :].rearrange("p (t w) -> p t w", w=W)
        with nc.Block() as block:
            @block.vector
            def _(dve):
                dve.reciprocal(S[:, :], accv[:, :, D])
                dve.drain()

                def add(t, k):
                    h = acc[:, ds(t * W, D)]
                    dve.tensor_scalar(h, h, 0.0, None, ALU.max)
                    dve.drain()
                    dve.scalar_tensor_tensor(out=node_tile(R.X, t), in0=h, scalar=S[:, ds(t, 1)], in1=node_tile(R.X, t),
                                             op0=ALU.mult, op1=ALU.add)

                pairs(dve, NT, add)


def squared_mixer(nc, R, a):
    S = 3 * D
    with ExitStack() as ctx:
        def sb(n, shape, dt=F32):
            return ctx.enter_context(nc.sbuf_tensor(f"m3_{n}", shape, dt))

        def sem(n):
            return nc.alloc_semaphore(f"m3_{n}")

        q, kk, v = sb("q", [P, NT * D]), sb("k", [P, NT * D]), sb("v", [P, NT * D])
        wout = sb("wout", [128, KC, D])
        bout = sb("bout", [P, D])
        M = sb("M", [128, KC, D])
        with ExitStack() as inner:
            w = inner.enter_context(nc.sbuf_tensor("m3_w", [128, KC, D], F32))
            b = inner.enter_context(nc.sbuf_tensor("m3_b", [P, D], F32))
            for n, to in enumerate((q, kk, v)):
                part = slice(n * D, (n + 1) * D)

                def finish(dve, t, ps, out):
                    dve.tensor_tensor(node_tile(to, t), ps[:, 0:D], b[:, :], ALU.add)

                rows_stage(nc, R, f"m3p{n}", w[:, :, :], D, finish,
                           loads=[(w[:, :, :], chunks_of(a["L3_mix_W_qkv"][:, part], D)),
                                  (b[:, :], row_of(a["L3_mix_b_qkv"][part], P))])
        tmp = sb("tmp", [P, NT * D])
        red = sb("red", [P, 2, NT])
        ss = sb("ss", [P, 2, NT])
        ksum = sb("ksum", [128, KC])
        (centered, squared, normed, squared2, summed, rooted, have_norm, norm_rooted, have_kv, loaded) = (sem(n) for n in (
            "centered", "squared", "normed", "squared2", "summed", "rooted", "have_norm", "norm_rooted", "have_kv", "loaded"))
        with nc.psum_tensor("m3_ps", [128, KC, 512], F32) as ps, nc.psum_tensor("m3_pn", [128, KC, 512], F32) as pn, \
                nc.Block() as block:
            def tiles(x):
                return x[:, :].rearrange("p (t d) -> p t d", d=D)

            def wide(r):
                return r.rearrange("p (t a) -> p t a", a=1).broadcast_to([P, NT, D])

            @block.sync
            def _(sp):
                sp.dma_start(wout[:, :, :], chunks_of(a["L3_mix_W_out"], D)).then_inc(loaded, 16)
                sp.dma_start(bout[:, :], row_of(a["L3_mix_b_out"], P)).then_inc(loaded, 16)
                sp.wait_ge(loaded, 32)

            @block.vector
            def _(dve):
                both = ((0, q), (1, kk))
                for n, x in both:
                    dve.tensor_reduce(red[:, n, :], tiles(x), AX.X, ALU.add)
                dve.drain()
                dve.tensor_scalar(red[:, :, :], red[:, :, :], 1.0 / D, None, ALU.mult)
                dve.drain()
                for n, x in both:
                    dve.tensor_tensor(tiles(x), tiles(x), wide(red[:, n, :]), ALU.subtract)
                dve.drain().then_inc(centered, 1)
                dve.wait_ge(squared, 1)
                for n, x in both:
                    dve.tensor_reduce(red[:, n, :], tiles(x), AX.X, ALU.add)
                dve.drain()
                dve.tensor_scalar(red[:, :, :], red[:, :, :], 1e-7, None, ALU.add)
                dve.drain()
                dve.reciprocal(red[:, :, :], red[:, :, :])
                dve.drain()
                for n, x in both:
                    dve.tensor_tensor(tiles(x), tiles(x), wide(red[:, n, :]), ALU.mult)
                dve.drain().then_inc(normed, 1)
                dve.wait_ge(squared2, 1)
                dve.tensor_reduce(ss[:, 0, :], tiles(tmp), AX.X, ALU.add)
                dve.drain().then_inc(summed, 1)
                dve.wait_ge(rooted, 1)
                dve.tensor_scalar(ss[:, 0, :], ss[:, 0, :], 1e-12, None, ALU.max)
                dve.drain()
                dve.reciprocal(ss[:, 0, :], ss[:, 0, :])
                dve.drain()
                dve.tensor_tensor(tiles(q), tiles(q), wide(ss[:, 0, :]), ALU.mult)
                dve.wait_ge(have_kv, 1)
                dve.tensor_copy(ksum[:, :], pn[:, :, 0])
                dve.drain().then_inc(have_norm, 1)
                dve.wait_ge(norm_rooted, 1)
                dve.tensor_scalar(ksum[:, :], ksum[:, :], 1e-12, None, ALU.max)
                dve.drain()
                dve.reciprocal(ksum[:, :], ksum[:, :])
                dve.drain()
                for c in range(KC):
                    dve.tensor_scalar(M[:, c, :], ps[:, c, 0:D], ksum[:, c:c + 1], float(N) ** -0.5, ALU.mult, ALU.mult)

            @block.scalar
            def _(act):
                act.wait_ge(centered, 1)
                act.activation(q[:, :], q[:, :], ACT.Square)
                act.activation(kk[:, :], kk[:, :], ACT.Square)
                act.drain().then_inc(squared, 1)
                act.wait_ge(normed, 1)
                act.activation(tmp[:, :], q[:, :], ACT.Square)
                act.drain().then_inc(squared2, 1)
                act.wait_ge(summed, 1)
                act.activation(ss[:, 0, :], ss[:, 0, :], ACT.Sqrt)
                act.activation(tmp[:, :], kk[:, :], ACT.Square)
                act.drain().then_inc(rooted, 1)
                act.wait_ge(have_norm, 1)
                act.activation(ksum[:, :], ksum[:, :], ACT.Sqrt)
                act.drain().then_inc(norm_rooted, 1)

            @block.tensor
            def _(pe):
                pe.wait_ge(rooted, 1)
                for c in range(KC):
                    for t in range(NT):
                        at = t * D + c * 128
                        pe.matmul(ps[:, c, 0:D], kk[:, at:at + 128], v[:, t * D:(t + 1) * D], start=(t == 0), stop=(t == NT - 1))
                        last = pe.matmul(pn[:, c, 0:1], tmp[:, at:at + 128], R.onesf[0:P, 0:1], start=(t == 0), stop=(t == NT - 1))
                last.then_inc(have_kv, 1)

        def add_v(dve, t, ps, out):
            dve.tensor_tensor(node_tile(v, t), node_tile(v, t), ps[:, 0:D], ALU.add)

        rows_stage(nc, R, "m3a", M[:, :, :], D, add_v, rows=q)

        def finish_out(dve, t, ps, out):
            x = node_tile(R.X, t)
            dve.tensor_tensor(x, x, ps[:, 0:D], ALU.add)
            dve.drain()
            dve.tensor_tensor(x, x, bout[:, :], ALU.add)

        rows_stage(nc, R, "m3b", wout[:, :, :], D, finish_out, rows=v)


def fourth_feed_forward(nc, R, a):
    CAP = max(1, int(0.5 * N))
    CHOSEN = CAP - 1 if CAP > 1 else 1
    F3 = a["L3_ffn_w1"].shape[1]
    with ExitStack() as ctx:
        def sb(n, shape, dt=F32):
            return ctx.enter_context(nc.sbuf_tensor(f"f3_{n}", shape, dt))

        normalize_stage(nc, R, "f3ln", R.X, R.XN)
        add_stage(nc, [(R.X, R.XN)])
        G = sb("G", [P, NT])
        with ExitStack() as inner:
            def sbi(n, shape, dt=F32):
                return inner.enter_context(nc.sbuf_tensor(f"f3_{n}", shape, dt))

            wr = sbi("wr", [128, KC, 1])
            br = sbi("br", [P, 1])

            def finish(dve, t, ps, out):
                dve.tensor_tensor(G[:, ds(t, 1)], ps[:, 0:1], br[:, :], ALU.add)

            rows_stage(nc, R, "f3r", wr[:, :, :], 1, finish,
                       loads=[(wr[:, :, :].rearrange("k c a -> k (c a)"), a["L3_ffn_wr"]), (br[:, :], row_of(a["L3_ffn_br"], P))])
            row_dram = nc.dram_tensor("f3_row_dram", (NT, P), F32).ap()
            turned = sbi("turned", [NT, P])
            row = sbi("row", [P, N])
            ge = sbi("ge", [P, 2, N])
            own = sbi("own", [P, 2, P])
            rank = sbi("rank", [P, 3, NT])
            pt = inner.enter_context(nc.psum_tensor("f3_pt", [NT, P], F32))
            have_t, copied, stored, spread = (nc.alloc_semaphore(f"f3_{n}") for n in (
                "have_t", "copied", "stored", "spread"))
            with nc.Block() as block:
                @block.tensor
                def _(pe):
                    pe.transpose(pt[:, :], G[:, :], R.identf[0:P, 0:P]).then_inc(have_t, 1)

                @block.sync
                def _(sp):
                    sp.wait_ge(copied, 1)
                    sp.dma_start(row_dram, turned[:, :]).then_inc(stored, 16)
                    sp.wait_ge(stored, 16)
                    sp.dma_start(row[:, :], row_dram.rearrange("t p -> (t p)").rearrange("(a n) -> a n", a=1)
                                 .partition_broadcast(P)).then_inc(spread, 16)

                @block.vector
                def _(dve):
                    dve.wait_ge(have_t, 1)
                    dve.tensor_copy(turned[:, :], pt[:, :]).then_inc(copied, 1)
                    dve.wait_ge(spread, 16)

                    for t in range(NT):
                        k = t % 2
                        mine = G[:, t:t + 1]
                        at = t * P
                        if t > 0:
                            dve.tensor_scalar(ge[:, k, 0:at], row[:, 0:at], mine, None, ALU.is_ge)
                        dve.tensor_scalar(ge[:, k, at:N], row[:, at:N], mine, None, ALU.is_gt)
                        dve.tensor_scalar(own[:, k, :], row[:, at:at + P], mine, None, ALU.is_equal)
                        dve.drain()
                        dve.scalar_tensor_tensor(out=own[:, k, :], in0=R.upto[0:P, 0:P], scalar=0.0, in1=own[:, k, :],
                                                 op0=ALU.is_equal, op1=ALU.mult)
                        dve.tensor_reduce(rank[:, 0, t:t + 1], ge[:, k, :], AX.X, ALU.add)
                        dve.drain()
                        dve.tensor_reduce(rank[:, 1, t:t + 1], own[:, k, :], AX.X, ALU.add)
                    dve.drain()
                    dve.tensor_tensor(rank[:, 2, :], rank[:, 0, :], rank[:, 1, :], ALU.add)
                    dve.drain()
                    dve.tensor_scalar(rank[:, 2, :], rank[:, 2, :], float(CHOSEN), None, ALU.is_lt)
                    dve.drain()
                    dve.tensor_tensor(G[:, :], G[:, :], rank[:, 2, :], ALU.mult)
        experts_stage(nc, R, "f3", 1, F3, a["L3_ffn_w1"].rearrange("(a d) f -> a d f", a=1), a["L3_ffn_b1"],
                      a["L3_ffn_w2"].rearrange("(a f) d -> a f d", a=1), a["L3_ffn_b2"].rearrange("(a d) -> a d", a=1), G,
                      R.X[:, :], ACT.Gelu_apprx_tanh)


def program(nc, a, out):
    with ExitStack() as ctx:
        R = Resident(nc, ctx)
        with nc.cleanup_on_exit():
            setup_stage(nc, R, a["x"])
            sort_stage(nc, R, "bydst", a["dst"], a["src"], R.rec_dst, R.tile_dst, a["edge_type_8"], a["edge_weight"])
            sort_stage(nc, R, "bysrc", a["src"], a["dst"], R.rec_src, R.tile_src)
            count_stage(nc, R)
        with nc.cleanup_on_exit():
            normalize_stage(nc, R, "ln0", R.X, R.XN)
            first_graph_layer(nc, R, a)
            softmax_mixer(nc, R, "m0", a["L0_mix_W_qkv"], a["L0_mix_W_out"], a["L0_mix_b_out"])
        with nc.cleanup_on_exit():
            first_feed_forward(nc, R, a)
        with nc.cleanup_on_exit():
            normalize_stage(nc, R, "ln1", R.X, R.XN)
            relation_graph_layer(nc, R, a)
        with nc.cleanup_on_exit():
            softmax_mixer(nc, R, "m1", a["L1_mix_w_qkv"], a["L1_mix_w_out"], a["L1_mix_b_out"], a["L1_mix_g_pre"],
                          a["L1_mix_mem_kv"], a["L1_mix_g_out"])
        with nc.cleanup_on_exit():
            second_feed_forward(nc, R, a)
        with nc.cleanup_on_exit():
            normalize_stage(nc, R, "ln2", R.X, R.XN)
            isomorphism_graph_layer(nc, R, a)
            head_norm_mixer(nc, R, a)
        with nc.cleanup_on_exit():
            third_feed_forward(nc, R, a)
        with nc.cleanup_on_exit():
            normalize_stage(nc, R, "ln3", R.X, R.XN)
            attention_graph_layer(nc, R, a)
        with nc.cleanup_on_exit():
            squared_mixer(nc, R, a)
        with nc.cleanup_on_exit():
            fourth_feed_forward(nc, R, a)
            store_rows_stage(nc, "out", R.X, out)


_OUT = "out_0_dram"


def _columns(a):
    return np.ascontiguousarray(np.moveaxis(a.reshape(a.shape[:-1] + (-1, 128)), -1, -2))


def kernel(**inputs):
    import concourse.bacc as _bacc
    from concourse.bass_utils import run_bass_kernel_spmd as _run

    columns = ("L0_ffn_b1", "L1_ffn_b1", "L2_ffn_b1", "L3_ffn_b1", "L2_gnn_gamma1", "L2_gnn_beta1", "L2_gnn_gamma_h",
               "L2_gnn_beta_h", "L1_mix_g_pre")
    arrays = {}
    for name, value in inputs.items():
        value = np.asarray(value)
        if name in ("L1_mix_t", "L3_ffn_attention_mask"):
            continue
        if name in ("L2_gnn_w1", "L2_gnn_w2"):
            value = value.T
        if name == "L3_ffn_wr":
            value = _columns(value[:, 0])
        if name in columns:
            value = _columns(value.reshape(1, -1) if name == "L3_ffn_b1" else value)
        arrays[name] = np.ascontiguousarray(value)
    arrays["L2_ffn_ln"] = np.ascontiguousarray(
        np.concatenate([_columns(arrays.pop("L2_ffn_ln_g")), _columns(arrays.pop("L2_ffn_ln_b"))], axis=-1))

    nc = _bacc.Bacc("TRN2", target_bir_lowering=False, num_devices=1)
    ap = {name: nc.dram_tensor(f"in_{name}", v.shape, mybir.dt.from_np(v.dtype), kind="ExternalInput").ap()
          for name, v in arrays.items()}
    out = nc.dram_tensor(_OUT, (N, D), F32, kind="ExternalOutput").ap()
    program(nc, ap, out)
    result = _run(nc, [{f"in_{name}": v for name, v in arrays.items()}], core_ids=[0])
    return result.results[0][_OUT]
```

```python
from contextlib import ExitStack

import concourse.bass as bass
from concourse import mybir
import numpy as np

F32 = mybir.dt.float32
BF16 = mybir.dt.bfloat16
I32 = mybir.dt.int32
U32 = mybir.dt.uint32
ALU = mybir.AluOpType
ACT = mybir.ActivationFunctionType
AX = mybir.AxisListType
ds = bass.ds

N, D, E = 3125, 256, 50000
P = 125
NT = N // P
KC = D // 128
EC = E // P
GE = 512
GT = GE // 128
NG = E // GE + NT
NG += -NG % 4
REC = 5
R_IDX, R_ROW, R_LOC, R_REL, R_W = range(REC)
NOWHERE = 999.0
H0, DH = 8, 32
LN_EPS = 1e-5
NEG = -1.0e30
MEM = 4
CHUNK = 4 * P
NCH = N // CHUNK


class Resident:

    def __init__(self, nc, ctx):
        def sb(name, shape, dt=F32):
            return ctx.enter_context(nc.sbuf_tensor(name, shape, dt))

        self.nc = nc
        self.X = sb("X", [P, NT * D])
        self.XN = sb("XN", [P, NT * D])
        self.XNT = sb("XNT", [128, KC, N])
        self.identf = sb("identf", [128, 128])
        self.identb = sb("identb", [128, 4, 128], BF16)
        self.iota = sb("iota", [128, 128])
        self.onesf = sb("onesf", [128, 128])
        self.before = sb("before", [128, 128])
        self.upto = sb("upto", [128, 128])
        self.tile_dst = sb("tile_dst", [128, NG], I32)
        self.tile_src = sb("tile_src", [128, NG], I32)
        self.inv_count = sb("inv_count", [P, NT * 8])
        self.rec_dst = nc.dram_tensor("rec_dst", (NG * GE, REC), I32).ap()
        self.rec_src = nc.dram_tensor("rec_src", (NG * GE, REC), I32).ap()
        self.norm_row = nc.dram_tensor("norm_row", (NT, P), F32).ap()


def node_tile(buf, t, width=D):
    return buf[:, ds(t * width, width)]


def is_first(n):
    return isinstance(n, int) and n < 2


def pairs(eng, count, body, peel=False):
    if peel:
        body(0, 0)
        body(1, 1)
    if count > (3 if peel else 1):
        with eng.Fori(int(peel), count // 2) as i:
            body(i * 2, 0)
            body(i * 2 + 1, 1)
    if count % 2:
        body(count - 1, 0)


def rounds(eng, count, depth, body):
    with eng.Fori(0, count // depth) as i:
        for k in range(depth):
            body(i * depth + k, k)
    for n in range(count - count % depth, count):
        body(n, n % depth)


DEPTH = 4
LEAD = 3


def skewed(eng, count, turn):
    for n in range(-LEAD, 0):
        turn(n, n % DEPTH)
    with eng.Fori(0, count // DEPTH - 1) as i:
        for k in range(DEPTH):
            turn(i * DEPTH + k, k)
    for n in range(count - DEPTH, count):
        turn(n, n % DEPTH)


def there(n, count=NG):
    return not isinstance(n, int) or 0 <= n < count


def landed(g, slot, transfers=1):
    return (g - slot) * (16 * transfers // DEPTH) + 16 * transfers


def setup_stage(nc, R, x):
    with ExitStack() as ctx:
        x_loaded = nc.alloc_semaphore("x_loaded")
        zeroed = nc.alloc_semaphore("zeroed")
        masks = nc.alloc_semaphore("masks")
        block = ctx.enter_context(nc.Block())

        @block.sync
        def _(sp):
            sp.dma_start(R.X[:, :].rearrange("p (t d) -> p t d", d=D),
                         x.rearrange("(t p) d -> p t d", p=P)).then_inc(x_loaded, 16)
            sp.wait_ge(x_loaded, 16)

        @block.gpsimd
        def _(pool):
            pool.memset(R.identf[:, :], 0.0).then_inc(zeroed, 1)
            pool.memset(R.onesf[:, :], 1.0).then_inc(zeroed, 1)
            pool.iota(R.iota[:, :], pattern=[[1, 128]], base=0, channel_multiplier=0,
                      allow_small_or_imprecise_dtypes=True)
            pool.wait_ge(zeroed, 2)
            pool.affine_select(out=R.identf[:, :], in_=R.identf[:, :], compare_op=ALU.not_equal, fill=1.0,
                               base=0, pattern=[[-1, 128]], channel_multiplier=1).then_inc(masks, 1)
            pool.affine_select(out=R.before[:, :], in_=R.onesf[:, :], compare_op=ALU.is_gt, fill=0.0,
                               base=0, pattern=[[1, 128]], channel_multiplier=-1)
            pool.affine_select(out=R.upto[:, :], in_=R.onesf[:, :], compare_op=ALU.is_ge, fill=0.0,
                               base=0, pattern=[[1, 128]], channel_multiplier=-1)

        @block.vector
        def _(dve):
            dve.wait_ge(masks, 1)
            for h in range(4):
                dve.tensor_copy(R.identb[:, h, :], R.identf[:, :])


def sort_stage(nc, R, name, key, gather, rec, tile_of, relation=None, weight=None):
    with ExitStack() as ctx:
        def sb(n, shape, dt=F32):
            return ctx.enter_context(nc.sbuf_tensor(f"{name}_{n}", shape, dt))

        def sem(n):
            return nc.alloc_semaphore(f"{name}_{n}")

        ki = sb("ki", [P, EC], I32)
        kf = sb("kf", [P, EC])
        rc = sb("rc", [P, EC, REC], I32)
        rcf = rc[:, :, :].bitcast(F32)
        gi = sb("gi", [P, EC], I32)
        ri = sb("ri", [P, EC], I32)
        wf = sb("wf", [P, EC])
        gef = sb("gef", [P, 2, EC])
        inb = sb("inb", [P, NT, EC], BF16)
        run = sb("run", [P, 2, EC])
        slot = sb("slot", [P, EC])
        sloti = sb("sloti", [P, EC], I32)
        cnt = sb("cnt", [P, NT])
        tot = sb("tot", [128, NT])
        grp = sb("grp", [128, NT])
        grpi = sb("grpi", [128, NT], I32)
        endg = sb("endg", [128, NT])
        zer = sb("zer", [128, NT])
        one = sb("one", [128, NT])
        first = sb("first", [P, NT])
        gid = sb("gid", [128, NG])
        tf = sb("tf", [128, NG])
        W8 = 8
        stage_i = sb("stage_i", [P, 2, W8], I32)
        stage_r = sb("stage_r", [P, 2, W8, REC], I32)
        FILL = NG * GE // 128
        empty = sb("empty", [128, FILL, REC], I32)
        ps = ctx.enter_context(nc.psum_tensor(f"{name}_ps", [128, 2 * NT], F32))
        loaded, emptied, counted, summed, slotted = sem("loaded"), sem("emptied"), sem("counted"), sem("summed"), sem("slotted")
        made_empty, staged, iotad = sem("made_empty"), sem("staged"), sem("iotad")
        scattered = [sem("scattered0"), sem("scattered1")]
        issued = sem("issued")
        block = ctx.enter_context(nc.Block())

        def edges(a):
            return a.rearrange("(p c) -> p c", c=EC)

        @block.sync
        def _(sp):
            sp.dma_start(ki[:, :], edges(key)).then_inc(loaded, 16)
            sp.dma_start(gi[:, :], edges(gather)).then_inc(loaded, 16)
            if relation is not None:
                sp.dma_start(ri[:, :], edges(relation)).then_inc(loaded, 16)
                sp.dma_start(wf[:, :], edges(weight)).then_inc(loaded, 16)
            sp.wait_ge(made_empty, 1)
            sp.dma_start(rec.rearrange("(p c) r -> p (c r)", p=128),
                         empty[:, :, :].rearrange("p c r -> p (c r)")).then_inc(emptied, 16)

        @block.gpsimd
        def _(pool):
            pool.iota(gid[:, :], pattern=[[1, NG]], base=0, channel_multiplier=0,
                      allow_small_or_imprecise_dtypes=True).then_inc(iotad, 1)
            pool.wait_ge(emptied, 16)

            def scatter(n, k):
                pool.wait_ge(staged, n + 1)
                pool.sem_inc(issued, 1)
                for c in range(W8):
                    pool.indirect_dma_start(rec, bass.IndirectOffsetOnAxis(stage_i[:, k, c:c + 1], 0),
                                            stage_r[:, k, c, :], None).then_inc(scattered[k], 16)

            pairs(pool, EC // W8, scatter)
            for k in range(2):
                pool.wait_ge(scattered[k], 16 * W8 * (EC // W8 // 2))

        @block.vector
        def _(dve):
            dve.memset(empty[:, :, :], 0)
            dve.memset(zer[:, :], 0.0)
            dve.memset(one[:, :], 1.0)
            dve.memset(slot[:, :], 0.0)
            dve.drain()
            dve.memset(empty[:, :, :].bitcast(F32)[:, :, R_LOC], NOWHERE).then_inc(made_empty, 1)
            dve.wait_ge(loaded, 64 if relation is not None else 32)
            dve.tensor_copy(kf[:, :], ki[:, :])
            dve.tensor_copy(rc[:, :, R_IDX], gi[:, :])
            if relation is not None:
                dve.tensor_scalar(run[:, 0, :], ri[:, :], float(N), None, ALU.mult)
                dve.drain()
                dve.tensor_tensor(rc[:, :, R_ROW], run[:, 0, :], gi[:, :], ALU.add)
                dve.tensor_copy(rcf[:, :, R_REL], ri[:, :])
                dve.tensor_copy(rcf[:, :, R_W], wf[:, :])
            else:
                dve.memset(rc[:, :, R_ROW], 0)
                dve.memset(rcf[:, :, R_REL], 0.0)
                dve.memset(rcf[:, :, R_W], 0.0)
            dve.drain()
            dve.tensor_copy(rcf[:, :, R_LOC], kf[:, :])
            dve.memset(gef[:, 0, :], 1.0)
            for b in range(NT):
                dve.tensor_scalar(gef[:, (b + 1) % 2, :], kf[:, :], float(P * (b + 1)), None, ALU.is_ge)
                dve.drain()
                dve.tensor_tensor(inb[:, b, :], gef[:, b % 2, :], gef[:, (b + 1) % 2, :], ALU.subtract)
                dve.scalar_tensor_tensor(out=rcf[:, :, R_LOC], in0=gef[:, (b + 1) % 2, :], scalar=-float(P),
                                         in1=rcf[:, :, R_LOC], op0=ALU.mult, op1=ALU.add)
                dve.drain()
                dve.tensor_reduce(cnt[:, b:b + 1], inb[:, b, :], AX.X, ALU.add)
            dve.drain().then_inc(counted, 1)
            dve.wait_ge(summed, 1)
            dve.tensor_copy(tot[:, :], ps[:, 0:NT])
            dve.drain()
            dve.tensor_scalar(grpi[:, :], tot[:, :], float(GE - 1), None, ALU.add)
            dve.drain()
            dve.tensor_scalar(grpi[:, :], grpi[:, :], 9, None, ALU.arith_shift_right)
            dve.drain()
            dve.tensor_scalar(grp[:, :], grpi[:, :], 1.0, None, ALU.max)
            dve.drain()
            dve.tensor_tensor_scan(endg[:, :], one[:, :], grp[:, :], 0.0, ALU.mult, ALU.add)
            dve.drain()
            dve.tensor_tensor(grp[:, :], endg[:, :], grp[:, :], ALU.subtract)
            dve.drain()
            dve.tensor_scalar(grp[:, :], grp[:, :], float(GE), -1.0, ALU.mult, ALU.add)
            dve.drain()
            dve.tensor_tensor(first[:, :], grp[0:P, :], ps[0:P, NT:2 * NT], ALU.add)
            dve.wait_ge(iotad, 1)
            dve.memset(tf[:, :], 0.0)
            for b in range(NT - 1):
                dve.drain()
                dve.scalar_tensor_tensor(out=tf[:, :], in0=gid[:, :], scalar=endg[:, b:b + 1], in1=tf[:, :],
                                         op0=ALU.is_ge, op1=ALU.add)
            dve.drain()
            dve.tensor_copy(tile_of[:, :], tf[:, :])
            dve.memset(gef[:, 0, :], 1.0)
            dve.drain()
            for b in range(NT):
                k = b % 2
                dve.tensor_tensor_scan(run[:, k, :], gef[:, 0, :], inb[:, b, :], first[:, b:b + 1], ALU.mult, ALU.add)
                dve.drain()
                dve.tensor_tensor(run[:, k, :], run[:, k, :], inb[:, b, :], ALU.mult)
                dve.drain()
                dve.tensor_tensor(slot[:, :], slot[:, :], run[:, k, :], ALU.add)
            dve.drain()
            dve.tensor_copy(sloti[:, :], slot[:, :])
            dve.drain()

            def stage(n, k):
                if not is_first(n):
                    dve.wait_ge(scattered[k], (n - k) * (8 * W8))
                dve.tensor_copy(stage_i[:, k, :], sloti[:, ds(n * W8, W8)])
                dve.tensor_copy(stage_r[:, k, :, :], rc[:, ds(n * W8, W8), :])
                dve.drain().then_inc(staged, 1)

            pairs(dve, EC // W8, stage, peel=True)

        @block.tensor
        def _(pe):
            pe.wait_ge(counted, 1)
            pe.matmul(ps[:, 0:NT], R.onesf[0:P, :], cnt[:, :], start=True, stop=True)
            pe.matmul(ps[:, NT:2 * NT], R.before[0:P, :], cnt[:, :], start=True, stop=True).then_inc(summed, 1)


def chunks_of(w, width):
    return w.rearrange("(c k) n -> k c n", k=128)


def row_of(v, parts):
    return v.rearrange("(a n) -> a n", a=1).partition_broadcast(parts)


def normalize_stage(nc, R, name, src, dst):
    with ExitStack() as ctx:
        def sem(n):
            return nc.alloc_semaphore(f"{name}_{n}")

        def sb(n, shape, dt=F32):
            return ctx.enter_context(nc.sbuf_tensor(f"{name}_{n}", shape, dt))

        stats = sb("stats", [P, 2, nc.vector.BN_STATS_DIM])
        mv = sb("mv", [P, 2, nc.vector.BN_AGGR_DIM])
        mean = sb("mean", [P, NT])
        var = sb("var", [P, NT])
        std = sb("std", [P, NT])
        rstd = sb("rstd", [P, NT])
        rows = sb("rows", [P, 2, D])
        pt = [ctx.enter_context(nc.psum_tensor(f"{name}_pt{k}", [128, KC * P], F32)) for k in range(2)]
        have_var, have_std, normed, turned, evacuated = sem("have_var"), sem("have_std"), sem("normed"), sem("turned"), sem("evacuated")
        copied = sem("copied")
        block = ctx.enter_context(nc.Block())

        @block.vector
        def _(dve):
            def moments(t, k):
                dve.bn_stats(stats[:, k, :], node_tile(src, t))
                dve.drain()
                dve.bn_aggr(mv[:, k, :], stats[:, k, :])
                dve.drain()
                dve.tensor_copy(mean[:, ds(t, 1)], mv[:, k, 0:1])
                dve.tensor_scalar(var[:, ds(t, 1)], mv[:, k, 1:2], LN_EPS, None, ALU.add)

            pairs(dve, NT, moments)
            dve.drain().then_inc(have_var, 1)
            dve.wait_ge(have_std, 1)
            dve.reciprocal(rstd[:, :], std[:, :])
            dve.drain()
            dve.sem_inc(copied, 2)

            def scale(t, k):
                dve.wait_ge(copied, t + 1)
                dve.tensor_scalar(rows[:, k, :], node_tile(src, t), mean[:, ds(t, 1)], rstd[:, ds(t, 1)],
                                  ALU.subtract, ALU.mult).then_inc(normed, 1)

            pairs(dve, NT, scale)

        @block.scalar
        def _(act):
            act.wait_ge(have_var, 1)
            act.activation(std[:, :], var[:, :], ACT.Sqrt).then_inc(have_std, 1)

            def evacuate(t, k):
                act.wait_ge(turned, t + 1)
                act.activation(R.XNT[:, :, ds(t * P, P)], pt[k][:, :].rearrange("k (c p) -> k c p", p=P),
                               ACT.Copy).then_inc(evacuated, 1)

            act.sem_inc(evacuated, 2)
            pairs(act, NT, evacuate)

        @block.gpsimd
        def _(pool):
            def keep(t, k):
                pool.wait_ge(turned, t + 1)
                pool.tensor_copy(node_tile(dst, t), rows[:, k, :]).then_inc(copied, 1)

            pairs(pool, NT, keep)

        @block.tensor
        def _(pe):
            def turn(t, k):
                pe.wait_ge(normed, t + 1)
                pe.wait_ge(evacuated, t + 1)
                for c in range(KC):
                    last = pe.transpose(pt[k][:, c * P:(c + 1) * P], rows[:, k, c * 128:(c + 1) * 128],
                                        R.identf[0:P, 0:P])
                last.then_inc(turned, 1)

            pairs(pe, NT, turn)


def rows_stage(nc, R, name, weights, width, finish, rows=None, stride=D, offset=0,
               loads=(), store=None, before=None, cols=None):
    chunks = weights.shape[1]
    with ExitStack() as ctx:
        def sem(n):
            return nc.alloc_semaphore(f"{name}_{n}")

        def sb(n, shape, dt=F32):
            return ctx.enter_context(nc.sbuf_tensor(f"{name}_{n}", shape, dt))

        xt = sb("xt", [128, 2, chunks, P])
        staged = sb("staged", [P, 2, chunks * 128]) if rows is not None else None
        out = sb("out", [P, 2, width])
        pt = [ctx.enter_context(nc.psum_tensor(f"{name}_pt{k}", [128, chunks * P], F32)) for k in range(2)]
        ps = [ctx.enter_context(nc.psum_tensor(f"{name}_ps{k}", [P, width], F32)) for k in range(2)]
        loaded, copied, turned, ready, multiplied, finished = (sem(n) for n in (
            "loaded", "copied", "turned", "ready", "multiplied", "finished"))
        stored = [sem("stored0"), sem("stored1")]
        block = ctx.enter_context(nc.Block())

        @block.sync
        def _(sp):
            for to, of in loads:
                sp.dma_start(to, of).then_inc(loaded, 16)
            sp.wait_ge(loaded, 16 * len(loads)) if loads else None
            if store is not None:
                def put(t, k):
                    sp.wait_ge(finished, t + 3)
                    sp.dma_start(store(t), out[:, k, :]).then_inc(stored[k], 16)

                pairs(sp, NT, put)
                sp.wait_ge(stored[0], 16 * (NT - NT // 2))
                sp.wait_ge(stored[1], 16 * (NT // 2))

        @block.gpsimd
        def _(pool):
            if rows is not None:
                pool.wait_ge(loaded, 16 * len(loads)) if loads else None

                def stage(t, k):
                    pool.wait_ge(turned, t + 1)
                    pool.tensor_copy(staged[:, k, :], rows[:, ds(t * stride + offset, chunks * 128)]).then_inc(copied, 1)

                pairs(pool, NT, stage)
            else:
                def stage(t, k):
                    pool.wait_ge(multiplied, t + 1)
                    pool.tensor_copy(xt[:, k, :, :], (R.XNT if cols is None else cols)[:, :, ds(t * P, P)]).then_inc(ready, 1)

                pairs(pool, NT, stage)

        @block.scalar
        def _(act):
            if rows is not None:
                def evacuate(t, k):
                    act.wait_ge(turned, t + 3)
                    act.wait_ge(multiplied, t + 1)
                    act.activation(xt[:, k, :, :], pt[k][:, :].rearrange("k (c p) -> k c p", p=P),
                                   ACT.Copy).then_inc(ready, 1)

                pairs(act, NT, evacuate)

        @block.tensor
        def _(pe):
            pe.sem_inc(turned, 2)
            pe.sem_inc(multiplied, 2)
            pe.wait_ge(loaded, 16 * len(loads)) if loads else None

            def turn(t, k):
                pe.wait_ge(copied, t + 1)
                pe.wait_ge(ready, t - 1) if not isinstance(t, int) or t >= 2 else None
                for c in range(chunks):
                    last = pe.transpose(pt[k][:, c * P:(c + 1) * P], staged[:, k, c * 128:(c + 1) * 128],
                                        R.identf[0:P, 0:P])
                last.then_inc(turned, 1)

            def multiply(t, k):
                pe.wait_ge(ready, t + 1)
                pe.wait_ge(finished, t + 1)
                for a in range(0, width, 512):
                    b = min(a + 512, width)
                    for c in range(chunks):
                        last = pe.matmul(ps[k][:, a:b], xt[:, k, c, :], weights[:, c, a:b], start=(c == 0),
                                         stop=(c == chunks - 1))
                last.then_inc(multiplied, 1)

            if rows is None:
                pairs(pe, NT, multiply)
            else:
                turn(0, 0)
                turn(1, 1)
                with pe.Fori(0, NT // 2 - 1) as i:
                    multiply(i * 2, 0)
                    turn(i * 2 + 2, 0)
                    multiply(i * 2 + 1, 1)
                    turn(i * 2 + 3, 1)
                multiply(NT - 3, 0)
                turn(NT - 1, 0)
                multiply(NT - 2, 1)
                multiply(NT - 1, 0)

        @block.vector
        def _(dve):
            dve.sem_inc(finished, 2)
            dve.wait_ge(loaded, 16 * len(loads)) if loads else None
            if before is not None:
                before(dve)
                dve.drain()

            def take(t, k):
                dve.wait_ge(multiplied, t + 3)
                if store is not None and not is_first(t):
                    dve.wait_ge(stored[k], (t - k) * 8)
                finish(dve, t, ps[k], out[:, k, :])
                dve.drain().then_inc(finished, 1)

            pairs(dve, NT, take, peel=store is not None)


def edge_stage(nc, R, name, mode, rec, tile_of, acc, width, table=None, idx=R_IDX, spread=None):
    sw = 8 if mode == "relation" else 1
    needs_spread = mode in ("relation", "gat")
    with ExitStack() as ctx:
        def sem(n):
            return nc.alloc_semaphore(f"{name}_{n}")

        def sb(n, shape, dt=F32):
            return ctx.enter_context(nc.sbuf_tensor(f"{name}_{n}", shape, dt))

        rc = sb("rc", [128, DEPTH, GT, REC], I32)
        rcf = rc[:, :, :, :].bitcast(F32)
        wide = table.shape[1] if table is not None else 8
        got = sb("got", [128, DEPTH, GT, wide])
        place = sb("place", [128, DEPTH, GT, P])
        placew = sb("placew", [128, DEPTH, GT, P])
        placet = sb("placet", [P, DEPTH, GT, 128])
        small = sb("small", [128, DEPTH, GT, 8])
        rel = sb("rel", [128, DEPTH, GT, 8])
        coef = sb("coef", [128, DEPTH, GT])
        coef2 = sb("coef2", [128, DEPTH, GT])
        pt = ctx.enter_context(nc.psum_tensor(f"{name}_pt", [P, 2, 512], F32))
        pq = ctx.enter_context(nc.psum_tensor(f"{name}_pq", [128, 2, 512], F32))
        pa = ctx.enter_context(nc.psum_tensor(f"{name}_pa", [P, 2, 512], F32))
        rec_in = [sem(f"rec_in{k}") for k in range(DEPTH)]
        got_in = [sem(f"got_in{k}") for k in range(DEPTH)]
        names = ("ordered", "placed", "weighed", "turned", "evacuated", "spreaded", "logit", "expd", "summed", "added")
        ordered, placed, weighed, turned, evacuated, spreaded, logit, expd, summed, added = (sem(n) for n in names)
        block = ctx.enter_context(nc.Block())

        @block.sync
        def _(sp):
            def turn(n, k):
                g, s = n + 3, (k + 3) % DEPTH
                if not there(g):
                    return
                sp.wait_ge(added, g + 1)
                sp.dma_start(rc[:, s, :, :].rearrange("p j r -> p (j r)"),
                             rec[ds(g * GE, GE), :].rearrange("(p j) r -> p (j r)", j=GT)).then_inc(rec_in[s], 16)

            skewed(sp, NG, turn)

        @block.gpsimd
        def _(pool):
            def turn(n, k):
                g, s = n + 3, (k + 3) % DEPTH
                if not there(g):
                    return
                pool.wait_ge(rec_in[s], landed(g, s))
                pool.sem_inc(ordered, 1)
                for j in range(GT):
                    pool.indirect_dma_start(got[:, s, j, :], None, table,
                                            bass.IndirectOffsetOnAxis(rc[:, s, j, idx:idx + 1], 0)).then_inc(got_in[s], 16)

            if table is not None:
                skewed(pool, NG, turn)

        @block.scalar
        def _(act):
            act.sem_inc(evacuated, 2)

            def turn(n, k):
                g, s = n + 1, (k + 1) % DEPTH
                if mode == "gat" and there(g):
                    act.wait_ge(logit, g + 1)
                    act.activation(coef2[:, s, :], coef[:, s, :], ACT.Exp, scale=-1.0).then_inc(expd, 1)
                g, s = n + 2, (k + 2) % DEPTH
                if there(g):
                    act.wait_ge(turned, g + 1)
                    act.activation(placet[:, s, :, :], pt[:, s % 2, :].rearrange("p (j e) -> p j e", e=128),
                                   ACT.Copy).then_inc(evacuated, 1)

            if needs_spread:
                skewed(act, NG, turn)

        @block.tensor
        def _(pe):
            tile_reg = pe.alloc_register(f"{name}_pe_tile")

            def turn(n, k):
                g, s = n + 1, (k + 1) % DEPTH
                if there(g):
                    pe.wait_ge(weighed, g + 1)
                    if table is not None:
                        pe.wait_ge(got_in[s], landed(g, s, GT))
                    for j in range(GT):
                        rhs = rel[:, s, j, :] if mode == "count" else got[:, s, j, 0:width]
                        lhs = place if mode == "count" else placew
                        last = pe.matmul(pa[:, s % 2, 0:width], lhs[:, s, j, :], rhs, start=(j == 0), stop=(j == GT - 1))
                    last.then_inc(summed, 1)
                g, s = n + 2, (k + 2) % DEPTH
                if needs_spread and there(g):
                    pe.wait_ge(placed, g + 1)
                    pe.wait_ge(evacuated, g + 1)
                    for j in range(GT):
                        last = pe.transpose(pt[:, s % 2, j * 128:(j + 1) * 128], place[:, s, j, :], R.identf[:, :])
                    last.then_inc(turned, 1)
                    pe.reg_load(tile_reg, tile_of[0:1, ds(g, 1)])
                    b = pe.snap(tile_reg)
                    pe.wait_ge(evacuated, g + 3)
                    for j in range(GT):
                        last = pe.matmul(pq[:, s % 2, j * 8:j * 8 + sw], placet[:, s, j, :], spread[:, ds(b * sw, sw)],
                                         start=True, stop=True)
                    last.then_inc(spreaded, 1)

            skewed(pe, NG, turn)

        @block.vector
        def _(dve):
            tile_reg = dve.alloc_register(f"{name}_dve_tile")
            dve.memset(acc, 0.0)
            dve.drain()
            dve.sem_inc(added, DEPTH)

            def turn(n, k):
                g, s = n + 1, (k + 1) % DEPTH
                if there(g) and mode == "relation":
                    dve.wait_ge(spreaded, g + 1)
                    dve.tensor_tensor(small[:, s, :, :], pq[:, s % 2, 0:GT * 8].rearrange("p (j r) -> p j r", r=8),
                                      rel[:, s, :, :], ALU.mult)
                    dve.drain()
                    dve.tensor_reduce(coef[:, s, :], small[:, s, :, :], AX.X, ALU.add)
                    dve.drain()
                    dve.tensor_tensor(coef2[:, s, :], coef[:, s, :], rcf[:, s, :, R_W], ALU.mult)
                    dve.drain()
                if there(g) and mode == "gat":
                    dve.wait_ge(spreaded, g + 1)
                    dve.wait_ge(got_in[s], landed(g, s, GT))
                    dve.tensor_tensor(coef[:, s, :], pq[:, s % 2, 0:GT * 8].rearrange("p (j r) -> p j r", r=8)[:, :, 0],
                                      got[:, s, :, wide - 1], ALU.add)
                    dve.drain()
                    dve.scalar_tensor_tensor(out=coef[:, s, :], in0=coef[:, s, :], scalar=0.2, in1=coef[:, s, :],
                                             op0=ALU.mult, op1=ALU.max)
                    dve.drain().then_inc(logit, 1)
                if there(n):
                    dve.reg_load(tile_reg, tile_of[0:1, ds(n, 1)])
                    b = dve.snap(tile_reg)
                    dve.wait_ge(summed, n + 1)
                    into = acc[:, ds(b * width, width)]
                    dve.tensor_tensor(into, into, pa[:, k % 2, 0:width], ALU.add)
                    dve.drain().then_inc(added, 1)
                if there(g):
                    if mode == "gat":
                        dve.wait_ge(expd, g + 1)
                    if needs_spread:
                        for j in range(GT):
                            dve.tensor_scalar(placew[:, s, j, :], place[:, s, j, :], coef2[:, s, j:j + 1], None, ALU.mult)
                    dve.drain().then_inc(weighed, 1)
                g, s = n + 2, (k + 2) % DEPTH
                if there(g):
                    dve.wait_ge(rec_in[s], landed(g, s))
                    for j in range(GT):
                        loc, w = rcf[:, s, j, R_LOC:R_LOC + 1], rcf[:, s, j, R_W:R_W + 1]
                        if mode == "weight":
                            dve.tensor_scalar(placew[:, s, j, :], R.iota[:, 0:P], loc, w, ALU.is_equal, ALU.mult)
                        else:
                            dve.tensor_scalar(place[:, s, j, :], R.iota[:, 0:P], loc, None, ALU.is_equal)
                        if mode in ("count", "relation"):
                            dve.tensor_scalar(rel[:, s, j, :], R.iota[:, 0:8], rcf[:, s, j, R_REL:R_REL + 1], None,
                                              ALU.is_equal)
                    if needs_spread:
                        dve.drain().then_inc(placed, 1)

            skewed(dve, NG, turn)


def attention_edge_stage(nc, R, name, table, keys, acc):
    W = D + H0
    JH = GT * H0
    with ExitStack() as ctx:
        def sem(n):
            return nc.alloc_semaphore(f"{name}_{n}")

        def sb(n, shape, dt=F32):
            return ctx.enter_context(nc.sbuf_tensor(f"{name}_{n}", shape, dt))

        rc = sb("rc", [128, DEPTH, GT, REC], I32)
        rcf = rc[:, :, :, :].bitcast(F32)
        got = sb("got", [128, DEPTH, GT, 2 * D])
        place = sb("place", [128, DEPTH, GT, P])
        outside = sb("outside", [128, DEPTH, GT, P], BF16)
        placet = sb("placet", [P, DEPTH, GT, 128])
        prod = sb("prod", [128, GT, D])
        score = sb("score", [128, DEPTH, GT, H0])
        by_head = sb("by_head", [JH, H0])
        by_tile = sb("by_tile", [JH, GT, P], BF16)
        tiles32 = sb("tiles32", [JH, GT])
        heads32 = sb("heads32", [JH, H0])
        expanded = sb("expanded", [JH, 2, H0, 128], BF16)
        msg = sb("msg", [128, 2, GT, W])
        tmax = sb("tmax", [P, GT, H0])
        gmax = sb("gmax", [P, H0])
        high = sb("high", [P, NT * H0])
        new = sb("new", [P, 2, H0])
        drop = sb("drop", [P, 2, H0])
        alpha = sb("alpha", [P, 2, H0])
        shifted = sb("shifted", [128, 2, GT, H0])
        keyed = ctx.enter_context(nc.psum_tensor(f"{name}_keyed", [128, GT * D], F32))
        spread = ctx.enter_context(nc.psum_tensor(f"{name}_spread", [P, 2, 512], F32))
        pt = ctx.enter_context(nc.psum_tensor(f"{name}_pt", [P, 512], F32))
        ps = ctx.enter_context(nc.psum_tensor(f"{name}_ps", [JH, 512], F32))
        pm = ctx.enter_context(nc.psum_tensor(f"{name}_pm", [128, 512], F32))
        pa = ctx.enter_context(nc.psum_tensor(f"{name}_pa", [P, 512], F32))
        rec_in = [sem(f"rec_in{k}") for k in range(DEPTH)]
        got_in = [sem(f"got_in{k}") for k in range(DEPTH)]
        names = ("ordered", "placed", "turned", "evacuated", "keys_spread", "multiplied", "scored", "scores_turned",
                 "have_expanded", "spread_out", "reduced", "maxed", "max_spread", "shifted", "exped", "messaged", "summed",
                 "added", "masks")
        (ordered, placed, turned, evacuated, keys_spread, multiplied, scored, scores_turned, have_expanded, spread_out,
         reduced, maxed, max_spread, have_shifted, exped, messaged, summed, added, masks) = (sem(n) for n in names)
        block = ctx.enter_context(nc.Block())

        @block.sync
        def _(sp):
            def turn(n, k):
                g, s = n + 3, (k + 3) % DEPTH
                if not there(g):
                    return
                sp.wait_ge(added, g + 1)
                sp.dma_start(rc[:, s, :, :].rearrange("p j r -> p (j r)"),
                             R.rec_dst[ds(g * GE, GE), :].rearrange("(p j) r -> p (j r)", j=GT)).then_inc(rec_in[s], 16)

            skewed(sp, NG, turn)

        @block.gpsimd
        def _(pool):
            pool.memset(heads32[:, :], 0.0).then_inc(masks, 1)
            pool.memset(tiles32[:, :], 1.0).then_inc(masks, 1)
            for j in range(GT):
                pool.wait_ge(masks, 2 + j)
                pool.affine_select(out=heads32[:, :], in_=heads32[:, :], compare_op=ALU.not_equal, fill=1.0,
                                   base=-H0 * j, pattern=[[-1, H0]], channel_multiplier=1).then_inc(masks, 1)
            pool.wait_ge(masks, 2 + GT)
            pool.affine_select(out=tiles32[:, :], in_=tiles32[:, :], compare_op=ALU.is_ge, fill=0.0,
                               base=0, pattern=[[-H0, GT]], channel_multiplier=1).then_inc(masks, 1)
            pool.wait_ge(masks, 3 + GT)
            pool.affine_select(out=tiles32[:, :], in_=tiles32[:, :], compare_op=ALU.is_ge, fill=0.0,
                               base=H0 - 1, pattern=[[H0, GT]], channel_multiplier=-1).then_inc(masks, 1)

            def turn(n, k):
                g, s = n + 3, (k + 3) % DEPTH
                if not there(g):
                    return
                pool.wait_ge(rec_in[s], landed(g, s))
                pool.sem_inc(ordered, 1)
                for j in range(GT):
                    pool.indirect_dma_start(got[:, s, j, :], None, table,
                                            bass.IndirectOffsetOnAxis(rc[:, s, j, R_IDX:R_IDX + 1], 0)).then_inc(got_in[s], 16)

            skewed(pool, NG, turn)

        @block.scalar
        def _(act):
            act.sem_inc(evacuated, 1)

            def turn(n, k):
                g, s = n + 3, (k + 3) % DEPTH
                if there(g):
                    act.wait_ge(turned, g + 1)
                    act.activation(outside[:, s, :, :], place[:, s, :, :], ACT.Copy, bias=NEG, scale=-NEG)
                    act.activation(placet[:, s, :, :], pt[:, :].rearrange("p (j e) -> p j e", e=128), ACT.Copy)
                    act.drain().then_inc(evacuated, 1)
                g, s = n + 1, (k + 1) % DEPTH
                if there(g):
                    act.wait_ge(have_shifted, g + 1)
                    act.activation(alpha[:, s % 2, :], drop[:, s % 2, :], ACT.Exp)
                    act.activation(msg[:, s % 2, :, D:W], shifted[:, s % 2, :, :], ACT.Exp)
                    act.drain().then_inc(exped, 1)

            skewed(act, NG, turn)

        @block.tensor
        def _(pe):
            tile_reg = pe.alloc_register(f"{name}_pe_tile")

            def turn(n, k):
                g, s = n + 3, (k + 3) % DEPTH
                if there(g):
                    pe.wait_ge(placed, g + 1)
                    pe.wait_ge(evacuated, g + 1)
                    for j in range(GT):
                        last = pe.transpose(pt[:, j * 128:(j + 1) * 128], place[:, s, j, :], R.identf[:, :])
                    last.then_inc(turned, 1)
                g, s = n + 1, (k + 1) % DEPTH
                if there(g):
                    pe.wait_ge(have_expanded, g + 1)
                    for u in range(2 * GT):
                        j, h = u // 2, (u % 2) * 4
                        pe.wait_ge(reduced, g * (2 * GT) + (u + 1))
                        pe.matmul(spread[:, u % 2, :], by_tile[:, j, :], expanded[:, s % 2, h:h + 4, :], start=True, stop=False)
                        pe.matmul(spread[:, u % 2, :], outside[:, s, j, :], R.identb[:, :, :], start=False,
                                  stop=True).then_inc(spread_out, 1)
                g, s = n + 3, (k + 3) % DEPTH
                if there(g):
                    pe.reg_load(tile_reg, R.tile_dst[0:1, ds(g, 1)])
                    b = pe.snap(tile_reg)
                    pe.wait_ge(evacuated, g + 2)
                    pe.wait_ge(multiplied, g + 1)
                    for j in range(GT):
                        last = pe.matmul(keyed[:, j * D:(j + 1) * D], placet[:, s, j, :], keys[:, ds(b * D, D)],
                                         start=True, stop=True)
                    last.then_inc(keys_spread, 1)
                g, s = n + 2, (k + 2) % DEPTH
                if there(g):
                    pe.wait_ge(scored, g + 1)
                    pe.transpose(ps[:, 0:128], score[:, s, :, :].rearrange("p j h -> p (j h)"), R.identf[:, :])\
                        .then_inc(scores_turned, 1)
                g, s = n + 1, (k + 1) % DEPTH
                if there(g):
                    pe.wait_ge(maxed, g + 1)
                    for j in range(GT):
                        last = pe.matmul(pm[:, j * H0:(j + 1) * H0], placet[:, s, j, :], new[:, s % 2, :], start=True, stop=True)
                    last.then_inc(max_spread, 1)
                    pe.wait_ge(messaged, g + 1)
                    for j in range(GT):
                        last = pe.matmul(pa[:, 0:W], place[:, s, j, :], msg[:, s % 2, j, :], start=(j == 0), stop=(j == GT - 1))
                    last.then_inc(summed, 1)

            skewed(pe, NG, turn)

        @block.vector
        def _(dve):
            tile_reg = dve.alloc_register(f"{name}_dve_tile")
            dve.memset(acc, 0.0)
            dve.memset(high[:, :], NEG)
            dve.memset(by_tile[:, :, :], 0.0)
            dve.wait_ge(masks, 4 + GT)
            dve.drain()
            dve.tensor_copy(by_head[:, :], heads32[:, :])
            for j in range(GT):
                dve.tensor_scalar(by_tile[:, j, :], by_tile[:, j, :], tiles32[:, j:j + 1], None, ALU.add)
            dve.drain()
            dve.sem_inc(added, DEPTH)
            dve.sem_inc(reduced, 2)
            dve.sem_inc(multiplied, 1)

            def turn(n, k):
                g, s = n + 3, (k + 3) % DEPTH
                if there(g):
                    dve.wait_ge(rec_in[s], landed(g, s))
                    for j in range(GT):
                        last = dve.tensor_scalar(place[:, s, j, :], R.iota[:, 0:P], rcf[:, s, j, R_LOC:R_LOC + 1], None,
                                                 ALU.is_equal)
                    dve.drain().then_inc(placed, 1)
                g, s = n + 2, (k + 2) % DEPTH
                if there(g):
                    dve.wait_ge(keys_spread, g + 1)
                    dve.wait_ge(got_in[s], landed(g, s, GT))
                    dve.tensor_tensor(prod[:, :, :], keyed[:, :].rearrange("p (j d) -> p j d", d=D), got[:, s, :, 0:D],
                                      ALU.mult)
                    dve.drain().then_inc(multiplied, 1)
                    dve.tensor_reduce(score[:, s, :, :], prod[:, :, :].rearrange("p j (h e) -> p j h e", e=DH), AX.X, ALU.add)
                    dve.drain().then_inc(scored, 1)
                g, s = n + 1, (k + 1) % DEPTH
                if there(g):
                    for u in range(2 * GT):
                        j, h = u // 2, (u % 2) * 4
                        dve.wait_ge(spread_out, g * (2 * GT) + (u + 1))
                        dve.tensor_reduce(tmax[:, j, h:h + 4], spread[:, u % 2, :].rearrange("p (h e) -> p h e", e=128), AX.X,
                                          ALU.max).then_inc(reduced, 1)
                    dve.drain()
                    dve.tensor_reduce(gmax[:, :], tmax[:, :, :].rearrange("p j h -> p h j"), AX.X, ALU.max)
                    dve.reg_load(tile_reg, R.tile_dst[0:1, ds(g, 1)])
                    b1 = dve.snap(tile_reg)
                    old = high[:, ds(b1 * H0, H0)]
                    dve.drain()
                    dve.tensor_tensor(new[:, s % 2, :], old, gmax[:, :], ALU.max)
                    dve.drain()
                    dve.sem_inc(maxed, 1)
                    dve.tensor_tensor(drop[:, s % 2, :], old, new[:, s % 2, :], ALU.subtract)
                    dve.drain()
                    dve.tensor_copy(old, new[:, s % 2, :])
                g2, s2 = n + 2, (k + 2) % DEPTH
                if there(g2):
                    dve.wait_ge(scores_turned, g2 + 1)
                    dve.tensor_tensor(expanded[:, s2 % 2, :, :],
                                      ps[:, 0:128].rearrange("q (a e) -> q a e", a=1).broadcast_to([JH, H0, 128]),
                                      by_head[:, :].rearrange("q (h a) -> q h a", a=1).broadcast_to([JH, H0, 128]),
                                      ALU.mult)
                    dve.drain().then_inc(have_expanded, 1)
                if there(g):
                    dve.wait_ge(max_spread, g + 1)
                    dve.tensor_tensor(shifted[:, s % 2, :, :], score[:, s, :, :],
                                      pm[:, 0:JH].rearrange("p (j h) -> p j h", h=H0), ALU.subtract)
                    dve.drain().then_inc(have_shifted, 1)
                if there(n):
                    dve.reg_load(tile_reg, R.tile_dst[0:1, ds(n, 1)])
                    b0 = dve.snap(tile_reg)
                    dve.wait_ge(summed, n + 1)
                    into = acc[:, ds(b0 * W, W)]
                    dve.tensor_tensor(into, into, pa[:, 0:W], ALU.add)
                    dve.drain().then_inc(added, 1)
                if there(g):
                    dve.reg_load(tile_reg, R.tile_dst[0:1, ds(g, 1)])
                    b1 = dve.snap(tile_reg)
                    dve.wait_ge(exped, g + 1)
                    dve.tensor_tensor(msg[:, s % 2, :, 0:D].rearrange("p j (h e) -> p j h e", e=DH),
                                      got[:, s, :, D:2 * D].rearrange("p j (h e) -> p j h e", e=DH),
                                      msg[:, s % 2, :, D:W].rearrange("p j (h a) -> p j h a", a=1)
                                      .broadcast_to([128, GT, H0, DH]), ALU.mult)
                    dve.drain().then_inc(messaged, 1)
                    intov = acc[:, ds(b1 * W, D)].rearrange("p (h e) -> p h e", e=DH)
                    dve.tensor_tensor(intov, intov, alpha[:, s % 2, :].rearrange("p (h a) -> p h a", a=1)
                                      .broadcast_to([P, H0, DH]), ALU.mult)
                    dve.tensor_tensor(acc[:, ds(b1 * W + D, H0)], acc[:, ds(b1 * W + D, H0)], alpha[:, s % 2, :], ALU.mult)
                    dve.drain()

            skewed(dve, NG, turn)


def first_graph_layer(nc, R, a):
    W = D + H0
    with ExitStack() as ctx:
        def sb(n, shape, dt=F32):
            return ctx.enter_context(nc.sbuf_tensor(f"g0_{n}", shape, dt))

        keys = sb("keys", [P, NT * D])
        acc = sb("acc", [P, NT * W])
        table = nc.dram_tensor("g0_table", (N, 2 * D), F32).ap()
        with ExitStack() as inner:
            wsb = inner.enter_context(nc.sbuf_tensor("g0_w", [128, KC, 3 * D], F32))
            bsb = inner.enter_context(nc.sbuf_tensor("g0_b", [P, 3 * D], F32))

            def finish(dve, t, ps, out):
                dve.tensor_tensor(out, ps[:, 0:2 * D], bsb[:, 0:2 * D], ALU.add)
                dve.drain()
                dve.tensor_scalar(out[:, 0:D], out[:, 0:D], float(DH) ** -0.5, None, ALU.mult)

            rows_stage(nc, R, "g0qv", wsb[:, :, 0:2 * D], 2 * D, finish,
                       loads=[(wsb[:, :, 0:D], chunks_of(a["L0_gnn_Wq"], D)), (wsb[:, :, D:2 * D], chunks_of(a["L0_gnn_Wv"], D)),
                              (bsb[:, 0:D], row_of(a["L0_gnn_bq"], P)), (bsb[:, D:2 * D], row_of(a["L0_gnn_bv"], P))],
                       store=lambda t: table[ds(t * P, P), :])

            def finish_k(dve, t, ps, out):
                dve.tensor_tensor(node_tile(keys, t), ps[:, 0:D], bsb[:, 2 * D:3 * D], ALU.add)

            rows_stage(nc, R, "g0k", wsb[:, :, 2 * D:3 * D], D, finish_k,
                       loads=[(wsb[:, :, 2 * D:3 * D], chunks_of(a["L0_gnn_Wk"], D)),
                              (bsb[:, 2 * D:3 * D], row_of(a["L0_gnn_bk"], P))])
        attention_edge_stage(nc, R, "g0e", table, keys, acc[:, :])
        z = sb("z", [P, NT, H0])
        block = ctx.enter_context(nc.Block())

        @block.vector
        def _(dve):
            accv = acc[:, :].rearrange("p (t w) -> p t w", w=W)
            dve.tensor_scalar(z[:, :, :], accv[:, :, D:W], 1e-16, None, ALU.max)
            dve.drain()
            dve.reciprocal(z[:, :, :], z[:, :, :])
            dve.drain()

            def normalize(t, k):
                v = acc[:, ds(t * W, D)].rearrange("p (h e) -> p h e", e=DH)
                zt = z[:, ds(t, 1), :].rearrange("p a h -> p h a").broadcast_to([P, H0, DH])
                dve.tensor_tensor(v, v, zt, ALU.mult)
                dve.drain()
                dve.tensor_tensor(node_tile(R.X, t), node_tile(R.X, t), acc[:, ds(t * W, D)], ALU.add)

            pairs(dve, NT, normalize)


def softmax_mixer(nc, R, name, w_qkv, w_out, b_out, g_pre=None, mem_kv=None, g_out=None):
    HID, HEADS, HD = 128, 4, 32
    S = 3 * HID + 1
    second = g_pre is not None
    with ExitStack() as ctx:
        def sb(n, shape, dt=F32):
            return ctx.enter_context(nc.sbuf_tensor(f"{name}_{n}", shape, dt))

        def sem(n):
            return nc.alloc_semaphore(f"{name}_{n}")

        qkv = sb("qkv", [P, NT * S])
        view = qkv[:, :].rearrange("p (t s) -> p t s", s=S)
        wout = sb("wout", [128, D])
        bout = sb("bout", [P, D])
        M = sb("M", [128, 1, D])
        tmp = sb("tmp", [P, NT * D])
        rn = sb("rn", [P, NT])
        ss = sb("ss", [P, NT])
        if second:
            rms_stage(nc, f"{name}_pre", R.XN, tmp, ss, rn)
            gp = sb("gp", [128, KC])
            gout = sb("gout", [P, D])
            memk = sb("memk", [MEM, HID])
            memkt = sb("memkt", [HID, MEM])
            memv = sb("memv", [MEM, HID + 1])
            O = sb("O", [P, NT * D])
        with ExitStack() as inner:
            w = inner.enter_context(nc.sbuf_tensor(f"{name}_w", [128, KC, 3 * HID], F32))
            loads = [(w[:, :, :], chunks_of(w_qkv, 3 * HID)), (wout[:, :], w_out), (bout[:, :], row_of(b_out, P))]
            if second:
                loads += [(gp[:, :], g_pre)]
                loads += [(gout[:, :], row_of(g_out, P)),
                          (memk[:, :].rearrange("m (h d) -> m h d", d=HD), mem_kv[0].rearrange("h d m -> m h d")),
                          (memv[:, 0:HID].rearrange("m (h d) -> m h d", d=HD), mem_kv[1].rearrange("h d m -> m h d")),
                          (memkt[:, :], mem_kv[0].rearrange("h d m -> (h d) m"))]

            def before(dve):
                dve.memset(view[:, :, 3 * HID:S], 1.0)

            def finish(dve, t, ps, out):
                if second:
                    dve.tensor_scalar(qkv[:, ds(t * S, 3 * HID)], ps[:, 0:3 * HID], rn[:, ds(t, 1)], None, ALU.mult)
                else:
                    dve.tensor_copy(qkv[:, ds(t * S, 3 * HID)], ps[:, 0:3 * HID])

            if second:
                scale_weights_stage(nc, f"{name}_sw", loads, w, gp, float(D) ** 0.5)
                loads = []
            rows_stage(nc, R, f"{name}_qkv", w[:, :, :], 3 * HID, finish, loads=loads, before=before)

        cmax = sb("cmax", [P, HID])
        kmax = sb("kmax", [HID, 1])
        mmax = sb("mmax", [HID, 1])
        dmax = sb("dmax", [HID, HID])
        rowmax = sb("rowmax", [P, HID])
        ctx_sb = sb("ctx_sb", [HID, HID])
        ctx_t = sb("ctx_t", [HID, HID])
        zr = sb("zr", [HID, 1])
        heads = sb("heads", [HID, HEADS])
        qred = sb("qred", [P, NT * HEADS])
        (have_cmax, cmax_turned, have_diag, row_spread, ready, exped, summed, have_ctx, ctx_turned, have_t, have_m,
         q_ready, q_exped) = (sem(n) for n in (
             "have_cmax", "cmax_turned", "have_diag", "row_spread", "shifted", "exped", "summed", "have_ctx",
             "ctx_turned", "have_t", "have_m", "q_ready", "q_exped"))
        with nc.psum_tensor(f"{name}_p", [128, 5, 512], F32) as banks, nc.Block() as block:
            p1, p2, p3, p4, p5 = (banks[:, n, :] for n in range(5))
            keysv = view[:, :, HID:2 * HID]
            queries = view[:, :, 0:HID].rearrange("p t (h e) -> p t h e", e=HD)
            qr = qred[:, :].rearrange("p (t h a) -> p t h a", h=HEADS, a=1).broadcast_to([P, NT, HEADS, HD])

            @block.vector
            def _(dve):
                if second:
                    dve.memset(memv[:, HID:HID + 1], 1.0)
                    dve.tensor_reduce(qred[:, :], queries, AX.X, ALU.max)
                    dve.drain()
                    dve.tensor_tensor(queries, queries, qr, ALU.subtract)
                    dve.drain().then_inc(q_ready, 1)
                dve.tensor_reduce(cmax[:, :], view[:, :, HID:2 * HID].rearrange("p t c -> p c t"), AX.X, ALU.max)
                dve.drain().then_inc(have_cmax, 1)
                dve.wait_ge(cmax_turned, 1)
                dve.tensor_reduce(kmax[:, :], p1[:, 0:P], AX.X, ALU.max)
                dve.drain()
                if second:
                    dve.tensor_reduce(mmax[:, :], memkt[:, :], AX.X, ALU.max)
                    dve.drain()
                    dve.tensor_tensor(kmax[:, :], kmax[:, :], mmax[:, :], ALU.max)
                    dve.drain()
                dve.tensor_scalar(dmax[:, :], R.identf[:, :], kmax[:, :], None, ALU.mult)
                dve.drain().then_inc(have_diag, 1)
                dve.wait_ge(row_spread, 1)
                dve.tensor_copy(rowmax[:, :], p2[0:P, 0:HID])
                dve.drain()
                dve.tensor_tensor(keysv, keysv, rowmax[:, :].rearrange("p (a c) -> p a c", a=1).broadcast_to([P, NT, HID]),
                                  ALU.subtract)
                if second:
                    dve.tensor_tensor(memk[:, :], memk[:, :], rowmax[0:MEM, :], ALU.subtract)
                dve.drain().then_inc(ready, 1)
                if second:
                    dve.wait_ge(q_exped, 1)
                    dve.tensor_reduce(qred[:, :], queries, AX.X, ALU.add)
                    dve.drain()
                    dve.reciprocal(qred[:, :], qred[:, :])
                    dve.drain()
                    dve.tensor_tensor(queries, queries, qr, ALU.mult)
                dve.memset(heads[:, :], 0.0)
                dve.drain()
                for h in range(HEADS):
                    dve.memset(heads[h * HD:(h + 1) * HD, h:h + 1], float(HD) ** -0.5)
                dve.wait_ge(summed, 1)
                dve.reciprocal(zr[:, :], p3[:, HID:HID + 1])
                dve.drain()
                for h in range(HEADS):
                    dve.tensor_scalar(ctx_sb[:, h * HD:(h + 1) * HD], p3[:, h * HD:(h + 1) * HD], zr[:, :],
                                      heads[:, h:h + 1], ALU.mult, ALU.mult)
                dve.drain().then_inc(have_ctx, 1)
                dve.wait_ge(ctx_turned, 1)
                dve.tensor_copy(ctx_t[:, :], p4[:, 0:HID])
                dve.drain().then_inc(have_t, 1)
                dve.wait_ge(have_m, 1)
                dve.tensor_copy(M[:, 0, :], p5[:, 0:D])

            @block.scalar
            def _(act):
                if second:
                    act.wait_ge(q_ready, 1)
                    act.activation(queries, queries, ACT.Exp)
                    act.drain().then_inc(q_exped, 1)
                act.wait_ge(ready, 1)
                act.activation(keysv, keysv, ACT.Exp)
                if second:
                    act.activation(memk[:, :], memk[:, :], ACT.Exp)
                act.drain().then_inc(exped, 1)

            @block.tensor
            def _(pe):
                pe.wait_ge(have_cmax, 1)
                pe.transpose(p1[:, 0:P], cmax[:, :], R.identf[0:P, 0:P]).then_inc(cmax_turned, 1)
                pe.wait_ge(have_diag, 1)
                pe.matmul(p2[:, 0:HID], R.onesf[:, :], dmax[:, :], start=True, stop=True).then_inc(row_spread, 1)
                pe.wait_ge(exped, 1)
                for t in range(NT):
                    last = pe.matmul(p3[:, 0:HID + 1], view[:, t, HID:2 * HID], view[:, t, 2 * HID:S], start=(t == 0),
                                     stop=(t == NT - 1 and not second))
                if second:
                    last = pe.matmul(p3[:, 0:HID + 1], memk[:, :], memv[:, :], start=False, stop=True)
                last.then_inc(summed, 1)
                pe.wait_ge(have_ctx, 1)
                pe.transpose(p4[:, 0:HID], ctx_sb[:, :], R.identf[:, :]).then_inc(ctx_turned, 1)
                pe.wait_ge(have_t, 1)
                pe.matmul(p5[:, 0:D], ctx_t[:, :], wout[:, :], start=True, stop=True).then_inc(have_m, 1)

        if not second:
            def finish_out(dve, t, ps, out):
                x = node_tile(R.X, t)
                dve.tensor_tensor(x, x, ps[:, 0:D], ALU.add)
                dve.drain()
                dve.tensor_tensor(x, x, bout[:, :], ALU.add)

            rows_stage(nc, R, f"{name}_out", M[:, :, :], D, finish_out, rows=qkv, stride=S)
            return

        def finish_out(dve, t, ps, out):
            dve.tensor_tensor(node_tile(O, t), ps[:, 0:D], bout[:, :], ALU.add)

        rows_stage(nc, R, f"{name}_out", M[:, :, :], D, finish_out, rows=qkv, stride=S)
        rms_stage(nc, f"{name}_post", O, tmp, ss, rn)
        with nc.Block() as block:
            @block.vector
            def _(dve):
                dve.tensor_scalar(gout[:, :], gout[:, :], float(D) ** 0.5, None, ALU.mult)
                dve.drain()

                def add(t, k):
                    o, x = node_tile(O, t), node_tile(R.X, t)
                    dve.scalar_tensor_tensor(out=o, in0=o, scalar=rn[:, ds(t, 1)], in1=gout[:, :], op0=ALU.mult, op1=ALU.mult)
                    dve.tensor_tensor(x, x, node_tile(R.XN, t), ALU.add)
                    dve.drain()
                    dve.tensor_tensor(x, x, o, ALU.add)

                pairs(dve, NT, add)


def rms_stage(nc, name, src, tmp, ss, rn):
    with ExitStack() as ctx:
        squared = nc.alloc_semaphore(f"{name}_squared")
        added = nc.alloc_semaphore(f"{name}_added")
        rooted = nc.alloc_semaphore(f"{name}_rooted")
        block = ctx.enter_context(nc.Block())

        @block.scalar
        def _(act):
            act.activation(tmp[:, :], src[:, :], ACT.Square)
            act.drain().then_inc(squared, 1)
            act.wait_ge(added, 1)
            act.activation(rn[:, :], ss[:, :], ACT.Sqrt).then_inc(rooted, 1)

        @block.vector
        def _(dve):
            dve.wait_ge(squared, 1)
            dve.tensor_reduce(ss[:, :], tmp[:, :].rearrange("p (t d) -> p t d", d=D), AX.X, ALU.add)
            dve.drain().then_inc(added, 1)
            dve.wait_ge(rooted, 1)
            dve.tensor_scalar(rn[:, :], rn[:, :], 1e-12, None, ALU.max)
            dve.drain()
            dve.reciprocal(rn[:, :], rn[:, :])


def scale_weights_stage(nc, name, loads, w, g, factor):
    with ExitStack() as ctx:
        loaded = nc.alloc_semaphore(f"{name}_loaded")
        block = ctx.enter_context(nc.Block())

        @block.sync
        def _(sp):
            with nc.allow_non_contiguous_dma(reason="a few hundred words"):
                for to, of in loads:
                    sp.dma_start(to, of).then_inc(loaded, 16)
            sp.wait_ge(loaded, 16 * len(loads))

        @block.vector
        def _(dve):
            dve.wait_ge(loaded, 16 * len(loads))
            for c in range(KC):
                dve.tensor_scalar(w[:, c, :], w[:, c, :], g[:, c:c + 1], factor, ALU.mult, ALU.mult)


TS = 256


def item_tiles(experts, top):
    return (top * N + experts * (TS - 1)) // TS


class Routing:

    def __init__(self, nc, ctx, name, experts, top):
        self.experts, self.top, self.tiles = experts, top, item_tiles(experts, top)
        self.weight = ctx.enter_context(nc.sbuf_tensor(f"{name}_weight", [P, top * NT], F32))
        self.slot = ctx.enter_context(nc.sbuf_tensor(f"{name}_slot", [P, top * NT], I32))
        self.expert_of = ctx.enter_context(nc.sbuf_tensor(f"{name}_expert_of", [P, self.tiles], I32))


def router_stage(nc, R, name, gate_w, gate_b, route, capacity=None):
    experts, top = route.experts, route.top
    with ExitStack() as ctx:
        def sb(n, shape, dt=F32):
            return ctx.enter_context(nc.sbuf_tensor(f"{name}_{n}", shape, dt))

        def sem(n):
            return nc.alloc_semaphore(f"{name}_{n}")

        gw = sb("gw", [128, KC, experts])
        gb = sb("gb", [P, experts])
        lg = sb("lg", [P, NT * experts])
        lgv = lg[:, :].rearrange("p (t e) -> p t e", e=experts)
        best = sb("best", [P, NT, 8])
        besti = sb("besti", [P, NT, 8])

        def finish(dve, t, ps, out):
            dve.tensor_tensor(lg[:, ds(t * experts, experts)], ps[:, 0:experts], gb[:, :], ALU.add)

        rows_stage(nc, R, f"{name}_lg", gw[:, :, :], experts, finish,
                   loads=[(gw[:, :, :], chunks_of(gate_w, experts)), (gb[:, :], row_of(gate_b, P))])
        items = top * NT
        row = sb("row", [P, 2, experts])
        top8 = sb("top8", [P, 2, 8])
        idx8 = sb("idx8", [P, 2, 8], U32)
        diff = sb("diff", [P, NT])
        pick = sb("pick", [P, items, experts])
        count = sb("count", [P, items, experts])
        totals = sb("totals", [P, items, experts])
        ones = sb("ones", [P, items])
        ex = sb("ex", [P, NT, experts])
        number = sb("number", [P, items])
        begin = sb("begin", [P, items])
        tiles = sb("tiles", [P, experts])
        tilesi = sb("tilesi", [P, experts], I32)
        end = sb("end", [P, experts])
        start = sb("start", [P, experts])
        ended = sb("ended", [P, route.tiles, experts])
        which = sb("which", [P, route.tiles])
        ps = [ctx.enter_context(nc.psum_tensor(f"{name}_ps{k}", [P, 512], F32)) for k in range(top)]
        ps2 = [ctx.enter_context(nc.psum_tensor(f"{name}_ps2{k}", [P, 512], F32)) for k in range(top)]
        shifted, exped, picked, counted = sem("shifted"), sem("exped"), sem("picked"), sem("counted")
        block = ctx.enter_context(nc.Block())
        shape = [P, NT, experts]
        w1, w2 = route.weight[:, 0:NT], route.weight[:, (top - 1) * NT:top * NT]

        @block.scalar
        def _(act):
            act.wait_ge(shifted, 1)
            if top == 2:
                act.activation(w2, diff[:, :], ACT.Exp)
            else:
                act.activation(ex[:, :, :], ex[:, :, :], ACT.Exp)
            act.drain().then_inc(exped, 1)

        @block.tensor
        def _(pe):
            pe.wait_ge(picked, 1)
            for k in range(top):
                flat = pick[:, k * NT:(k + 1) * NT, :].rearrange("p t e -> p (t e)")
                pe.matmul(ps[k][:, 0:NT * experts], R.upto[0:P, 0:P], flat, start=True, stop=True)
                last = pe.matmul(ps2[k][:, 0:NT * experts], R.onesf[0:P, 0:P], flat, start=True, stop=True)
            last.then_inc(counted, 1)

        @block.vector
        def _(dve):
            def largest(t, k):
                dve.tensor_copy(row[:, k, :], lg[:, ds(t * experts, experts)])
                dve.drain()
                dve.max(top8[:, k, :], row[:, k, :])
                dve.drain()
                dve.max_index(idx8[:, k, :], top8[:, k, :], row[:, k, :])
                dve.drain()
                dve.tensor_copy(best[:, ds(t, 1), :], top8[:, k, :].rearrange("p (a e) -> p a e", a=1))
                dve.tensor_copy(besti[:, ds(t, 1), :], idx8[:, k, :].rearrange("p (a e) -> p a e", a=1))

            pairs(dve, NT, largest)
            dve.drain()
            iota = R.iota[0:P, 0:experts].rearrange("p (a e) -> p a e", a=1).broadcast_to(shape)
            for k in range(top):
                dve.tensor_tensor(pick[:, k * NT:(k + 1) * NT, :], iota, besti[:, :, k:k + 1].broadcast_to(shape),
                                  ALU.is_equal)
            if top == 2:
                dve.tensor_tensor(diff[:, :], best[:, :, 1], best[:, :, 0], ALU.subtract)
            else:
                dve.tensor_tensor(ex[:, :, :], lgv, best[:, :, 0:1].broadcast_to(shape), ALU.subtract)
            dve.memset(ones[:, :], 1.0)
            dve.drain().then_inc(shifted, 1)
            dve.sem_inc(picked, 1)
            dve.wait_ge(exped, 1)
            if top == 2:
                dve.tensor_scalar(w1, w2, 1.0, None, ALU.add)
            else:
                dve.tensor_reduce(w1, ex[:, :, :], AX.X, ALU.add)
            dve.drain()
            dve.reciprocal(w1, w1)
            dve.drain()
            if top == 2:
                dve.tensor_tensor(w2, w2, w1, ALU.mult)
            dve.wait_ge(counted, 1)
            for k in range(top):
                dve.tensor_copy(totals[:, k * NT:(k + 1) * NT, :],
                                ps2[k][:, 0:NT * experts].rearrange("p (t e) -> p t e", e=experts))
            dve.drain()
            for e in range(experts):
                dve.tensor_tensor_scan(count[:, :, e], ones[:, :], totals[:, :, e], 0.0, ALU.mult, ALU.add)
            dve.drain()
            dve.tensor_scalar(tilesi[:, :], count[:, items - 1, :], float(TS - 1), None, ALU.add)
            dve.tensor_tensor(totals[:, :, :], count[:, :, :], totals[:, :, :], ALU.subtract)
            dve.drain()
            dve.tensor_scalar(tilesi[:, :], tilesi[:, :], 8, None, ALU.arith_shift_right)
            for k in range(top):
                dve.tensor_tensor(count[:, k * NT:(k + 1) * NT, :], totals[:, k * NT:(k + 1) * NT, :],
                                  ps[k][:, 0:NT * experts].rearrange("p (t e) -> p t e", e=experts), ALU.add)
            dve.drain()
            dve.tensor_copy(tiles[:, :], tilesi[:, :])
            dve.tensor_tensor(count[:, :, :], count[:, :, :], pick[:, :, :], ALU.mult)
            dve.drain()
            dve.tensor_tensor_scan(end[:, :], ones[:, 0:experts], tiles[:, :], 0.0, ALU.mult, ALU.add)
            dve.tensor_reduce(number[:, :], count[:, :, :], AX.X, ALU.add)
            dve.drain()
            dve.tensor_tensor(start[:, :], end[:, :], tiles[:, :], ALU.subtract)
            over = [P, route.tiles, experts - 1]
            dve.tensor_tensor(ended[:, :, 0:experts - 1],
                              end[:, 0:experts - 1].rearrange("p (a e) -> p a e", a=1).broadcast_to(over),
                              R.iota[0:P, 0:route.tiles].rearrange("p (s a) -> p s a", a=1).broadcast_to(over), ALU.is_le)
            dve.drain()
            dve.tensor_reduce(which[:, :], ended[:, :, 0:experts - 1], AX.X, ALU.add)
            if capacity is not None:
                dve.tensor_scalar(begin[:, :], number[:, :], float(capacity), None, ALU.is_le)
                dve.drain()
                dve.tensor_tensor(w1, w1, begin[:, :], ALU.mult)
            dve.drain()
            dve.tensor_copy(route.expert_of[:, :], which[:, :])
            dve.tensor_tensor(pick[:, :, :], pick[:, :, :],
                              start[:, :].rearrange("p (a e) -> p a e", a=1).broadcast_to([P, items, experts]), ALU.mult)
            dve.drain()
            dve.tensor_reduce(begin[:, :], pick[:, :, :], AX.X, ALU.add)
            dve.drain()
            dve.tensor_scalar(begin[:, :], begin[:, :], float(TS), -1.0, ALU.mult, ALU.add)
            dve.drain()
            dve.tensor_tensor(route.slot[:, :], begin[:, :], number[:, :], ALU.add)


def dispatch_stage(nc, R, name, route, rows, of_slot):
    W = 5 * route.top
    TURNS = route.top * NT // W
    cols = route.tiles * TS // 128
    with ExitStack() as ctx:
        def sb(n, shape, dt=F32):
            return ctx.enter_context(nc.sbuf_tensor(f"{name}_{n}", shape, dt))

        def sem(n):
            return nc.alloc_semaphore(f"{name}_{n}")

        nodes = nc.dram_tensor(f"{name}_nodes", (cols * 128, 1), F32).ap()
        none = sb("none", [cols, 128])
        node = sb("node", [P, route.top, NT])
        stage_i = sb("stage_i", [P, 2, W], I32)
        stage_n = sb("stage_n", [P, 2, W])
        back = sb("back", [cols, 128])
        pt = ctx.enter_context(nc.psum_tensor(f"{name}_pt", [128, cols], F32))
        zeroed, emptied, kept, staged, issued, all_in, back_in, turned, numbered = (sem(n) for n in (
            "zeroed", "emptied", "kept", "staged", "issued", "all_in", "back_in", "turned", "numbered"))
        scattered = [sem("scattered0"), sem("scattered1")]
        block = ctx.enter_context(nc.Block())

        @block.sync
        def _(sp):
            sp.wait_ge(zeroed, 1)
            sp.dma_start(nodes.rearrange("(c p) a -> c (p a)", p=128), none[:, :]).then_inc(emptied, 16)
            sp.dma_start(rows.rearrange("(t p) d -> p t d", p=P),
                         R.XN[:, :].rearrange("p (t d) -> p t d", d=D)).then_inc(kept, 16)
            sp.wait_ge(all_in, 1)
            sp.dma_start(back[:, :], nodes.rearrange("(c p) a -> c (p a)", p=128)).then_inc(back_in, 16)
            sp.wait_ge(kept, 16)

        @block.gpsimd
        def _(pool):
            pool.iota(node[:, :, :], pattern=[[0, route.top], [P, NT]], base=0, channel_multiplier=1,
                      allow_small_or_imprecise_dtypes=True).then_inc(numbered, 1)
            pool.wait_ge(emptied, 16)

            def scatter(n, k):
                pool.wait_ge(staged, n + 1)
                pool.sem_inc(issued, 1)
                for c in range(W):
                    pool.indirect_dma_start(nodes, bass.IndirectOffsetOnAxis(stage_i[:, k, c:c + 1], 0),
                                            stage_n[:, k, c:c + 1], None).then_inc(scattered[k], 16)

            pairs(pool, TURNS, scatter)
            pool.wait_ge(scattered[0], 16 * W * (TURNS - TURNS // 2))
            pool.wait_ge(scattered[1], 16 * W * (TURNS // 2))
            pool.sem_inc(all_in, 1)

        @block.tensor
        def _(pe):
            pe.wait_ge(back_in, 16)
            pe.transpose(pt[:, :], back[:, :], R.identf[0:cols, 0:cols]).then_inc(turned, 1)

        @block.vector
        def _(dve):
            dve.memset(none[:, :], 0.0).then_inc(zeroed, 1)
            dve.wait_ge(numbered, 1)

            def stage(n, k):
                if not is_first(n):
                    dve.wait_ge(scattered[k], (n - k) * (8 * W))
                dve.tensor_copy(stage_i[:, k, :], route.slot[:, ds(n * W, W)])
                dve.tensor_copy(stage_n[:, k, :], node[:, :, :].rearrange("p k t -> p (k t)")[:, ds(n * W, W)])
                dve.drain().then_inc(staged, 1)

            pairs(dve, TURNS, stage, peel=True)
            dve.wait_ge(turned, 1)
            dve.tensor_copy(of_slot[:, :], pt[:, :])


def routed_experts_stage(nc, R, name, F, w1, b1, w2, b2, route, func, combine, ln=None):
    NF = F // 128
    NS = route.tiles
    TJ = TS // 128
    top = route.top
    rows = nc.dram_tensor(f"{name}_rows", (N, D), F32).ap()
    results = nc.dram_tensor(f"{name}_results", (NS * TS, D), F32).ap()
    with ExitStack() as ctx:
        def sb(n, shape, dt=F32):
            return ctx.enter_context(nc.sbuf_tensor(f"{name}_{n}", shape, dt))

        def sem(n):
            return nc.alloc_semaphore(f"{name}_{n}")

        of_slot = sb("of_slot", [128, NS * TJ], I32)
        dispatch_stage(nc, R, f"{name}d", route, rows, of_slot)
        w1s = sb("w1s", [128, 2, KC, F])
        w2s = sb("w2s", [128, 2, NF, D])
        b1s = sb("b1s", [128, 2, NF])
        b2s = sb("b2s", [128, 2, D])
        lns = sb("lns", [128, 2, 2 * KC])
        node = sb("node", [128, 2, TJ], I32)
        got = sb("got", [128, 2, TJ, D])
        xt = sb("xt", [128, 2, KC, TS])
        hid = sb("hid", [128, NF, TS])
        y = sb("y", [128, 2, TJ, D])
        with ExitStack() as inner:
            pt = [inner.enter_context(nc.psum_tensor(f"{name}_pt{k}", [128, KC, TS], F32)) for k in range(2)]
            p1 = [inner.enter_context(nc.psum_tensor(f"{name}_p1{k}", [128, 512], F32)) for k in range(4)]
            p2 = [inner.enter_context(nc.psum_tensor(f"{name}_p2{k}", [128, 512], F32)) for k in range(TJ)]
            w_in = [sem("w_in0"), sem("w_in1")]
            got_in = [sem("got_in0"), sem("got_in1")]
            stored = [sem("stored0"), sem("stored1")]
            turned, ready, first, acted, second, taken, tile_done, named = (sem(n) for n in (
                "turned", "ready", "first", "acted", "second", "taken", "tile_done", "named"))
            LOADS = 5 if ln is not None else 4
            block = inner.enter_context(nc.Block())

            def weights_in(s, k):
                return (s - k) * (8 * LOADS) + 16 * LOADS

            @block.sync
            def _(sp):
                expert_reg = sp.alloc_register(f"{name}_expert")

                def load(s, k):
                    sp.wait_ge(tile_done, s + 1)
                    sp.reg_load(expert_reg, route.expert_of[0:1, ds(s, 1)])
                    one = ds(sp.snap(expert_reg), 1)
                    sp.dma_start(w1s[:, k, :, :], w1[one].rearrange("a (c k) f -> k (a c) f", k=128)).then_inc(w_in[k], 16)
                    sp.dma_start(w2s[:, k, :, :], w2[one].rearrange("a (c k) d -> k (a c) d", k=128)).then_inc(w_in[k], 16)
                    sp.dma_start(b1s[:, k, :], b1[one].rearrange("a k c -> (a k) c")).then_inc(w_in[k], 16)
                    sp.dma_start(b2s[:, k, :], b2[one].broadcast_to([128, D])).then_inc(w_in[k], 16)
                    if ln is not None:
                        sp.dma_start(lns[:, k, :], ln[one].rearrange("a k c -> (a k) c")).then_inc(w_in[k], 16)

                def put(s, k):
                    sp.wait_ge(taken, (s + 2) * TJ)
                    sp.dma_start(results[ds(s * TS, TS), :].rearrange("(j p) d -> p j d", p=128),
                                 y[:, k, :, :]).then_inc(stored[k], 16)

                def turn(s, k):
                    load(s + 1, 1 - k)
                    put(s, k)

                load(0, 0)
                pairs(sp, NS - 1, turn)
                put(NS - 1, (NS - 1) % 2)
                sp.wait_ge(stored[0], 16 * (NS - NS // 2))
                sp.wait_ge(stored[1], 16 * (NS // 2))

            @block.gpsimd
            def _(pool):
                def gather(s, k):
                    pool.wait_ge(turned, s + 1)
                    pool.tensor_copy(node[:, k, :], of_slot[:, ds(s * TJ, TJ)])
                    pool.drain()
                    for j in range(TJ):
                        pool.indirect_dma_start(got[:, k, j, :], None, rows,
                                                bass.IndirectOffsetOnAxis(node[:, k, j:j + 1], 0)).then_inc(got_in[k], 16)

                pairs(pool, NS, gather)

            @block.tensor
            def _(pe):
                def turn(s, k):
                    pe.wait_ge(got_in[k], (s - k) * (8 * TJ) + 16 * TJ)
                    pe.wait_ge(ready, s + 1)
                    for c in range(KC):
                        for j in range(TJ):
                            last = pe.transpose(pt[k][:, c, j * 128:(j + 1) * 128], got[:, k, j, c * 128:(c + 1) * 128],
                                                R.identf[:, :])
                    last.then_inc(turned, 1)

                def hidden(s, k):
                    pe.wait_ge(w_in[k], weights_in(s, k))
                    pe.wait_ge(ready, s + 3)
                    for f in range(NF):
                        pe.wait_ge(acted, s * NF + (f + 1))
                        for c in range(KC):
                            last = pe.matmul(p1[f % 4][:, 0:TS], w1s[:, k, c, f * 128:(f + 1) * 128], xt[:, k, c, :],
                                             start=(c == 0), stop=(c == KC - 1))
                        last.then_inc(first, 1)

                def result(s, k):
                    pe.wait_ge(acted, s * NF + (NF + 4))
                    for j in range(TJ):
                        pe.wait_ge(taken, s * TJ + (j + 1))
                        for f in range(NF):
                            last = pe.matmul(p2[j][:, 0:D], hid[:, f, j * 128:(j + 1) * 128], w2s[:, k, f, :],
                                             start=(f == 0), stop=(f == NF - 1))
                        last.then_inc(second, 1)

                def tile(s, k):
                    hidden(s, k)
                    turn(s + 1, 1 - k)
                    result(s, k)

                pe.sem_inc(turned, 2)
                turn(0, 0)
                pairs(pe, NS - 1, tile)
                hidden(NS - 1, (NS - 1) % 2)
                result(NS - 1, (NS - 1) % 2)

            @block.scalar
            def _(act):
                act.sem_inc(acted, 4)

                def tile(s, k):
                    act.wait_ge(w_in[k], weights_in(s, k))
                    for f in range(NF):
                        act.wait_ge(first, s * NF + (f + 1))
                        act.activation(hid[:, f, :], p1[f % 4][:, 0:TS], func, bias=b1s[:, k, f:f + 1]).then_inc(acted, 1)

                pairs(act, NS, tile)

            @block.vector
            def _(dve):
                def evacuate(s, k):
                    if ln is not None:
                        dve.wait_ge(w_in[k], weights_in(s, k))
                    dve.wait_ge(turned, s + 3)
                    if ln is None:
                        dve.tensor_copy(xt[:, k, :, :], pt[k][:, :, :])
                    else:
                        for c in range(KC):
                            dve.tensor_scalar(xt[:, k, c, :], pt[k][:, c, :], lns[:, k, c:c + 1],
                                              lns[:, k, KC + c:KC + c + 1], ALU.mult, ALU.add)
                    dve.drain().then_inc(ready, 1)

                def take(s, k):
                    dve.wait_ge(w_in[k], weights_in(s, k))
                    if not is_first(s):
                        dve.wait_ge(stored[k], (s - k) * 8)
                    for j in range(TJ):
                        dve.wait_ge(second, s * TJ + (j + 1))
                        dve.tensor_tensor(y[:, k, j, :], p2[j][:, 0:D], b2s[:, k, :], ALU.add).then_inc(taken, 1)
                    dve.drain().then_inc(tile_done, 1)

                def tile(s, k):
                    evacuate(s + 1, 1 - k)
                    take(s, k)

                dve.sem_inc(ready, 2)
                dve.sem_inc(taken, TJ)
                dve.sem_inc(tile_done, 2)
                evacuate(0, 0)
                pairs(dve, NS - 1, tile, peel=True)
                take(NS - 1, (NS - 1) % 2)

        from_slot = sb("from_slot", [P, DEPTH, top], I32)
        back = sb("back", [P, DEPTH, top, D])
        back_in = [sem(f"back_in{k}") for k in range(DEPTH)]
        combined = sem("combined")
        columns = route.slot[:, :].rearrange("p (k t) -> p t k", k=top)
        with nc.Block() as block:
            @block.gpsimd
            def _(pool):
                def fetch(t, k):
                    pool.wait_ge(combined, t + 1)
                    pool.tensor_copy(from_slot[:, k, :], columns[:, ds(t, 1), :].rearrange("p a k -> p (a k)"))
                    pool.drain()
                    for j in range(top):
                        pool.indirect_dma_start(back[:, k, j, :], None, results,
                                                bass.IndirectOffsetOnAxis(from_slot[:, k, j:j + 1], 0)).then_inc(back_in[k], 16)

                rounds(pool, NT, DEPTH, fetch)

            @block.vector
            def _(dve):
                dve.sem_inc(combined, DEPTH)

                def add(t, k):
                    dve.wait_ge(back_in[k], landed(t, k, top))
                    combine(dve, t, back[:, k, :, :])
                    dve.drain().then_inc(combined, 1)

                rounds(dve, NT, DEPTH, add)


def weighted_sum(dve, route, to, t, back):
    for j in range(route.top):
        dve.scalar_tensor_tensor(out=to, in0=back[:, j, :], scalar=route.weight[:, ds(t + j * NT, 1)], in1=to,
                                 op0=ALU.mult, op1=ALU.add)
        dve.drain()


def experts_stage(nc, R, name, experts, F, w1, b1, w2, b2, G, acc, func, ln=None):
    NF = F // 128
    NQ = NCH + 1
    with ExitStack() as ctx:
        def sb(n, shape, dt=F32):
            return ctx.enter_context(nc.sbuf_tensor(f"{name}_{n}", shape, dt))

        def sem(n):
            return nc.alloc_semaphore(f"{name}_{n}")

        w1s = sb("w1s", [128, 2, KC, F])
        w2s = sb("w2s", [128, 2, NF, D])
        b1s = sb("b1s", [128, 2, NF])
        b2s = sb("b2s", [P, 2, D])
        fold = ln is not None
        if fold:
            lgs = sb("lgs", [128, 2, 2 * KC])
            w1g = sb("w1g", [128, KC, F])
            b1g = sb("b1g", [128, 2, NF])
        hid = sb("hid", [128, NF, CHUNK])
        y = sb("y", [P, 2, D])
        p1 = [ctx.enter_context(nc.psum_tensor(f"{name}_p1{k}", [128, 512], F32)) for k in range(4)]
        p2 = [ctx.enter_context(nc.psum_tensor(f"{name}_p2{k}", [P, 512], F32)) for k in range(4)]
        w_in = [sem("w_in0"), sem("w_in1")]
        first, acted, second, taken, expert_done, folded, bias_ready, begun = (sem(n) for n in (
            "first", "acted", "second", "taken", "expert_done", "folded", "bias_ready", "begun"))
        LOADS = 5 if fold else 4
        block = ctx.enter_context(nc.Block())

        @block.sync
        def _(sp):
            def load(e, k):
                sp.wait_ge(expert_done, e + 1)
                one = ds(e, 1)
                sp.dma_start(w1s[:, k, :, :], w1[one].rearrange("a (c k) f -> k (a c) f", k=128)).then_inc(w_in[k], 16)
                sp.dma_start(w2s[:, k, :, :], w2[one].rearrange("a (c k) d -> k (a c) d", k=128)).then_inc(w_in[k], 16)
                sp.dma_start(b1s[:, k, :], b1[one].rearrange("a k c -> (a k) c")).then_inc(w_in[k], 16)
                sp.dma_start(b2s[:, k, :], b2[one].broadcast_to([P, D])).then_inc(w_in[k], 16)
                if fold:
                    sp.dma_start(lgs[:, k, :], ln[one].rearrange("a k c -> (a k) c")).then_inc(w_in[k], 16)

            pairs(sp, experts, load)

        def chunk_loop(eng, e, k, body):
            eng.sem_inc(begun, 1)
            with eng.Fori(0, NCH) as c:
                body(e * NQ + c, c * CHUNK, 4, c * 4)
            body(e * NQ + NCH, NCH * CHUNK, NT - 4 * NCH, 4 * NCH)

        @block.tensor
        def _(pe):
            def expert(e, k):
                pe.wait_ge(w_in[k], (e - k) * (8 * LOADS) + 16 * LOADS)
                wk = w1g if fold else w1s[:, k, :, :]
                if fold:
                    pe.wait_ge(taken, e * NT + 4)
                    for f in range(NF):
                        for c in range(KC):
                            last = pe.matmul(p1[0][:, f:f + 1],
                                             w1s[:, k, c, f * 128:(f + 1) * 128], lgs[:, k, KC + c:KC + c + 1],
                                             start=(c == 0), stop=(c == KC - 1))
                    last.then_inc(bias_ready, 1)
                    pe.wait_ge(folded, e + 1)

                def chunk(q, at, tiles, tile):
                    n = tiles * P
                    for f in range(NF):
                        pe.wait_ge(acted, q * NF + (f + 1))
                        for c in range(KC):
                            last = pe.matmul(p1[f % 4][:, 0:n], wk[:, c, f * 128:(f + 1) * 128], R.XNT[:, c, ds(at, n)],
                                             start=(c == 0), stop=(c == KC - 1))
                        last.then_inc(first, 1)
                    pe.wait_ge(acted, q * NF + (NF + 4))
                    for j in range(tiles):
                        pe.wait_ge(taken, e * NT + tile + (j + 1 if j > 0 else 4))
                        for f in range(NF):
                            last = pe.matmul(p2[j][:, 0:D], hid[:, f, j * P:(j + 1) * P], w2s[:, k, f, :], start=(f == 0),
                                             stop=(f == NF - 1))
                        last.then_inc(second, 1)

                chunk_loop(pe, e, k, chunk)

            pairs(pe, experts, expert)

        @block.scalar
        def _(act):
            act.sem_inc(acted, 4)

            def expert(e, k):
                act.wait_ge(w_in[k], (e - k) * (8 * LOADS) + 16 * LOADS)
                bias = b1s
                if fold:
                    act.wait_ge(folded, e + 1)
                    bias = b1g

                def chunk(q, at, tiles, tile):
                    n = tiles * P
                    for f in range(NF):
                        act.wait_ge(first, q * NF + (f + 1))
                        act.activation(hid[:, f, 0:n], p1[f % 4][:, 0:n], func, bias=bias[:, k, f:f + 1]).then_inc(acted, 1)

                chunk_loop(act, e, k, chunk)

            pairs(act, experts, expert)

        @block.vector
        def _(dve):
            dve.sem_inc(taken, 4)
            dve.sem_inc(expert_done, 2)

            def expert(e, k):
                dve.wait_ge(w_in[k], (e - k) * (8 * LOADS) + 16 * LOADS)
                if fold:
                    dve.wait_ge(bias_ready, e + 1)
                    dve.tensor_tensor(b1g[:, k, :], p1[0][:, 0:NF], b1s[:, k, :], ALU.add)
                    for c in range(KC):
                        dve.tensor_scalar(w1g[:, c, :], w1s[:, k, c, :], lgs[:, k, c:c + 1], None, ALU.mult)
                    dve.drain().then_inc(folded, 1)

                def chunk(q, at, tiles, tile):
                    for j in range(tiles):
                        dve.wait_ge(second, e * NT + tile + (j + 1))
                        dve.tensor_tensor(y[:, j % 2, :], p2[j][:, 0:D], b2s[:, k, :], ALU.add)
                        dve.drain().then_inc(taken, 1)
                        to = acc[:, ds((tile + j) * D, D)]
                        dve.scalar_tensor_tensor(out=to, in0=y[:, j % 2, :], scalar=G[:, ds((tile + j) * experts + e, 1)],
                                                 in1=to, op0=ALU.mult, op1=ALU.add)
                        dve.drain()

                chunk_loop(dve, e, k, chunk)
                dve.sem_inc(expert_done, 1)

            pairs(dve, experts, expert)


def add_stage(nc, pieces):
    with nc.Block() as block:
        @block.vector
        def _(dve):
            for to, of in pieces:
                def add(t, k):
                    dve.tensor_tensor(node_tile(to, t), node_tile(to, t), node_tile(of, t), ALU.add)

                pairs(dve, NT, add)
                dve.drain()


def first_feed_forward(nc, R, a):
    E0, F0 = a["L0_ffn_w1"].shape[0], a["L0_ffn_w1"].shape[2]
    with ExitStack() as ctx:
        route = Routing(nc, ctx, "f0", E0, 2)
        gamma = ctx.enter_context(nc.sbuf_tensor("f0_gamma", [P, D], F32))
        beta = ctx.enter_context(nc.sbuf_tensor("f0_beta", [P, D], F32))
        loaded = nc.alloc_semaphore("f0_loaded")
        normalize_stage(nc, R, "f0ln", R.X, R.XN)
        router_stage(nc, R, "f0r", a["L0_ffn_gate_w"], a["L0_ffn_gate_b"], route)
        routed_experts_stage(nc, R, "f0", F0, a["L0_ffn_w1"], a["L0_ffn_b1"], a["L0_ffn_w2"], a["L0_ffn_b2"], route,
                             ACT.Relu, lambda dve, t, back: weighted_sum(dve, route, node_tile(R.XN, t), t, back))
        normalize_stage(nc, R, "f0ln2", R.XN, R.XN)
        with nc.Block() as block:
            @block.sync
            def _(sp):
                sp.dma_start(gamma[:, :], row_of(a["L0_ffn_gamma"], P)).then_inc(loaded, 16)
                sp.dma_start(beta[:, :], row_of(a["L0_ffn_beta"], P)).then_inc(loaded, 16)

            @block.vector
            def _(dve):
                dve.wait_ge(loaded, 32)

                def add(t, k):
                    n, x = node_tile(R.XN, t), node_tile(R.X, t)
                    dve.tensor_tensor(n, n, gamma[:, :], ALU.mult)
                    dve.tensor_tensor(x, x, beta[:, :], ALU.add)
                    dve.drain()
                    dve.tensor_tensor(x, x, n, ALU.add)

                pairs(dve, NT, add)


def count_stage(nc, R):
    edge_stage(nc, R, "cnt", "count", R.rec_dst, R.tile_dst, R.inv_count[:, :], 8)
    with ExitStack() as ctx:
        deg = ctx.enter_context(nc.sbuf_tensor("deg", [P, NT], F32))
        turned = ctx.enter_context(nc.sbuf_tensor("deg_turned", [NT, P], F32))
        pt = ctx.enter_context(nc.psum_tensor("deg_pt", [NT, P], F32))
        have_deg, rooted, inverted, have_t, copied, stored = (nc.alloc_semaphore(f"deg_{n}") for n in (
            "have", "rooted", "inverted", "have_t", "copied", "stored"))
        block = ctx.enter_context(nc.Block())

        @block.vector
        def _(dve):
            counts = R.inv_count[:, :].rearrange("p (t r) -> p t r", r=8)
            dve.tensor_reduce(deg[:, :], counts, AX.X, ALU.add)
            dve.drain()
            dve.tensor_scalar(deg[:, :], deg[:, :], 1.0, None, ALU.max)
            dve.tensor_scalar(R.inv_count[:, :], R.inv_count[:, :], 1.0, None, ALU.max)
            dve.drain().then_inc(have_deg, 1)
            dve.reciprocal(R.inv_count[:, :], R.inv_count[:, :])
            dve.wait_ge(rooted, 1)
            dve.reciprocal(deg[:, :], deg[:, :])
            dve.drain().then_inc(inverted, 1)
            dve.wait_ge(have_t, 1)
            dve.tensor_copy(turned[:, :], pt[:, :]).then_inc(copied, 1)

        @block.scalar
        def _(act):
            act.wait_ge(have_deg, 1)
            act.activation(deg[:, :], deg[:, :], ACT.Sqrt).then_inc(rooted, 1)

        @block.tensor
        def _(pe):
            pe.wait_ge(inverted, 1)
            pe.transpose(pt[:, :], deg[:, :], R.identf[0:P, 0:P]).then_inc(have_t, 1)

        @block.sync
        def _(sp):
            sp.wait_ge(copied, 1)
            sp.dma_start(R.norm_row, turned[:, :]).then_inc(stored, 16)
            sp.wait_ge(stored, 16)


def relation_graph_layer(nc, R, a):
    W = a["L1_gnn_weight"]
    RN = W.shape[0]
    table = nc.dram_tensor("g1_table", (RN * N, D), F32).ap()
    to = table.rearrange("(r n) d -> n r d", r=RN)
    with ExitStack() as ctx:
        w = ctx.enter_context(nc.sbuf_tensor("g1_w", [128, KC, 2 * D], F32))
        for r in range(0, RN, 2):
            def finish(dve, t, ps, out):
                dve.tensor_copy(out, ps[:, 0:2 * D])

            rows_stage(nc, R, f"g1t{r}", w[:, :, :], 2 * D, finish,
                       loads=[(w[:, :, 0:D], chunks_of(W[r], D)), (w[:, :, D:2 * D], chunks_of(W[r + 1], D))],
                       store=lambda t, r=r: to[ds(t * P, P), r:r + 2, :])
    with ExitStack() as ctx:
        w = ctx.enter_context(nc.sbuf_tensor("g1_root", [128, KC, D], F32))
        b = ctx.enter_context(nc.sbuf_tensor("g1_bias", [P, D], F32))

        def finish_root(dve, t, ps, out):
            x = node_tile(R.X, t)
            dve.tensor_tensor(x, x, ps[:, 0:D], ALU.add)
            dve.drain()
            dve.tensor_tensor(x, x, b[:, :], ALU.add)

        rows_stage(nc, R, "g1root", w[:, :, :], D, finish_root,
                   loads=[(w[:, :, :], chunks_of(a["L1_gnn_root"], D)), (b[:, :], row_of(a["L1_gnn_bias"], P))])
    with ExitStack() as ctx:
        acc = ctx.enter_context(nc.sbuf_tensor("g1_acc", [P, NT * D], F32))
        edge_stage(nc, R, "g1e", "relation", R.rec_dst, R.tile_dst, acc[:, :], D, table=table, idx=R_ROW,
                   spread=R.inv_count[:, :])
        add_stage(nc, [(R.X, acc)])


def second_feed_forward(nc, R, a):
    E1, F1 = a["L1_ffn_w1"].shape[0], a["L1_ffn_w1"].shape[2]
    capacity = -(-5 * N // (4 * E1))
    with ExitStack() as ctx:
        route = Routing(nc, ctx, "f1", E1, 1)
        normalize_stage(nc, R, "f1ln", R.X, R.XN)
        router_stage(nc, R, "f1r", a["L1_ffn_gate_w"], a["L1_ffn_gate_b"], route, capacity)
        with ExitStack() as inner:
            def weigh(dve, t, back):
                dve.tensor_scalar(node_tile(R.XN, t), back[:, 0, :], route.weight[:, ds(t, 1)], None, ALU.mult)

            routed_experts_stage(nc, R, "f1", F1, a["L1_ffn_w1"], a["L1_ffn_b1"], a["L1_ffn_w2"], a["L1_ffn_b2"], route,
                                 ACT.Relu, weigh)
            mask = inner.enter_context(nc.sbuf_tensor("f1_mask", [P, NT * D], U32))
            clean = inner.enter_context(nc.sbuf_tensor("f1_clean", [P, NT * D], F32))
            fill = inner.enter_context(nc.sbuf_tensor("f1_fill", [P, 1], F32))
            with nc.Block() as block:
                @block.vector
                def _(dve):
                    dve.tensor_tensor(mask[:, :], R.XN[:, :], R.XN[:, :], ALU.is_equal)
                    dve.memset(clean[:, :], 0.0)
                    dve.memset(fill[:, :], 1e4)
                    dve.drain()
                    dve.copy_predicated(clean[:, :], mask[:, :], R.XN[:, :])
                    dve.drain()
                    dve.tensor_scalar(mask[:, :], clean[:, :], 3.4028235e38, None, ALU.is_gt)
                    dve.drain()
                    dve.copy_predicated(clean[:, :], mask[:, :], fill[:, 0:1].broadcast_to([P, NT * D]))
                    dve.drain()
                    dve.tensor_scalar(mask[:, :], clean[:, :], -3.4028235e38, None, ALU.is_lt)
                    dve.memset(fill[:, :], -1e4)
                    dve.drain()
                    dve.copy_predicated(clean[:, :], mask[:, :], fill[:, 0:1].broadcast_to([P, NT * D]))
            add_stage(nc, [(R.X, clean)])


def turn_stage(nc, R, name, src, dst):
    with ExitStack() as ctx:
        staged = ctx.enter_context(nc.sbuf_tensor(f"{name}_staged", [P, 2, D], F32))
        pt = [ctx.enter_context(nc.psum_tensor(f"{name}_pt{k}", [128, KC * P], F32)) for k in range(2)]
        copied, turned, evacuated = (nc.alloc_semaphore(f"{name}_{n}") for n in ("copied", "turned", "evacuated"))
        block = ctx.enter_context(nc.Block())

        @block.gpsimd
        def _(pool):
            def stage(t, k):
                pool.wait_ge(turned, t + 1)
                pool.tensor_copy(staged[:, k, :], node_tile(src, t)).then_inc(copied, 1)

            pairs(pool, NT, stage)

        @block.tensor
        def _(pe):
            pe.sem_inc(turned, 2)

            def turn(t, k):
                pe.wait_ge(copied, t + 1)
                pe.wait_ge(evacuated, t + 1)
                for c in range(KC):
                    last = pe.transpose(pt[k][:, c * P:(c + 1) * P], staged[:, k, c * 128:(c + 1) * 128],
                                        R.identf[0:P, 0:P])
                last.then_inc(turned, 1)

            pairs(pe, NT, turn)

        @block.scalar
        def _(act):
            act.sem_inc(evacuated, 2)

            def evacuate(t, k):
                act.wait_ge(turned, t + 3)
                act.activation(dst[:, :, ds(t * P, P)], pt[k][:, :].rearrange("k (c p) -> k c p", p=P),
                               ACT.Copy).then_inc(evacuated, 1)

            pairs(act, NT, evacuate)


def batchnorm_product_stage(nc, R, name, w, src, dst, cols, scale_row=None):
    NQ = NCH + 1
    with ExitStack() as ctx:
        def sb(n, shape, dt=F32):
            return ctx.enter_context(nc.sbuf_tensor(f"{name}_{n}", shape, dt))

        def sem(n):
            return nc.alloc_semaphore(f"{name}_{n}")

        ws = sb("ws", [128, KC, D])
        gb = sb("gb", [128, 2, KC])
        stats = sb("stats", [128, NT * nc.vector.BN_STATS_DIM])
        mv = sb("mv", [128, KC, nc.vector.BN_AGGR_DIM])
        std = sb("std", [128, KC])
        scale = sb("scale", [128, KC])
        shift = sb("shift", [128, KC])
        row = sb("row", [128, N]) if scale_row is not None else None
        ps = [ctx.enter_context(nc.psum_tensor(f"{name}_ps{k}", [128, KC, 512], F32)) for k in range(2)]
        loaded, multiplied, taken, have_var, rooted, scaled = (sem(n) for n in (
            "loaded", "multiplied", "taken", "have_var", "rooted", "scaled"))
        LOADS = 3 + (scale_row is not None)
        block = ctx.enter_context(nc.Block())

        def chunk_pairs(eng, body):
            with eng.Fori(0, NCH // 2) as i:
                for k in range(2):
                    body(i * 2 + k, k, i * (2 * CHUNK) + k * CHUNK, CHUNK)
            body(NCH, 0, NCH * CHUNK, N - NCH * CHUNK)

        @block.sync
        def _(sp):
            sp.dma_start(ws[:, :, :], chunks_of(w, D)).then_inc(loaded, 16)
            sp.dma_start(gb[:, 0, :], cols[0]).then_inc(loaded, 16)
            sp.dma_start(gb[:, 1, :], cols[1]).then_inc(loaded, 16)
            if row is not None:
                sp.dma_start(row[:, :], scale_row.rearrange("t p -> (t p)").rearrange("(a n) -> a n", a=1)
                             .partition_broadcast(128)).then_inc(loaded, 16)

        @block.tensor
        def _(pe):
            pe.wait_ge(loaded, 16 * LOADS)

            def chunk(q, k, at, n):
                pe.wait_ge(taken, q + 1)
                for m in range(KC):
                    for c in range(KC):
                        last = pe.matmul(ps[k][:, m, 0:n], ws[:, c, m * 128:(m + 1) * 128], src[:, c, ds(at, n)],
                                         start=(c == 0), stop=(c == KC - 1))
                last.then_inc(multiplied, 1)

            chunk_pairs(pe, chunk)

        @block.vector
        def _(dve):
            dve.wait_ge(loaded, 16 * LOADS)
            dve.sem_inc(taken, 2)

            def chunk(q, k, at, n):
                dve.wait_ge(multiplied, q + 1)
                for m in range(KC):
                    if row is not None:
                        dve.tensor_tensor(dst[:, m, ds(at, n)], ps[k][:, m, 0:n], row[:, ds(at, n)], ALU.mult)
                    else:
                        dve.tensor_copy(dst[:, m, ds(at, n)], ps[k][:, m, 0:n])
                dve.drain().then_inc(taken, 1)

            chunk_pairs(dve, chunk)
            for m in range(KC):
                def moments(t, k):
                    dve.bn_stats(stats[:, ds(t * nc.vector.BN_STATS_DIM, nc.vector.BN_STATS_DIM)], dst[:, m, ds(t * P, P)])

                dve.drain()
                pairs(dve, NT, moments)
                dve.drain()
                dve.bn_aggr(mv[:, m, :], stats[:, :])
            dve.drain()
            dve.tensor_scalar(std[:, :], mv[:, :, 1], LN_EPS, None, ALU.add)
            dve.drain().then_inc(have_var, 1)
            dve.wait_ge(rooted, 1)
            dve.reciprocal(std[:, :], std[:, :])
            dve.drain()
            dve.tensor_tensor(scale[:, :], gb[:, 0, :], std[:, :], ALU.mult)
            dve.drain()
            dve.tensor_tensor(shift[:, :], mv[:, :, 0], scale[:, :], ALU.mult)
            dve.drain()
            dve.tensor_tensor(shift[:, :], gb[:, 1, :], shift[:, :], ALU.subtract)
            dve.drain().then_inc(scaled, 1)

        @block.scalar
        def _(act):
            act.wait_ge(have_var, 1)
            act.activation(std[:, :], std[:, :], ACT.Sqrt).then_inc(rooted, 1)
            act.wait_ge(scaled, 1)
            for m in range(KC):
                act.activation(dst[:, m, :], dst[:, m, :], ACT.Relu, bias=shift[:, m:m + 1], scale=scale[:, m:m + 1])


def store_rows_stage(nc, name, src, table):
    stored = nc.alloc_semaphore(f"{name}_stored")
    with nc.Block() as block:
        @block.sync
        def _(sp):
            sp.dma_start(table.rearrange("(t p) d -> p t d", p=P),
                         src[:, :].rearrange("p (t d) -> p t d", d=D)).then_inc(stored, 16)
            sp.wait_ge(stored, 16)


def isomorphism_graph_layer(nc, R, a):
    table = nc.dram_tensor("g2_table", (N, D), F32).ap()
    store_rows_stage(nc, "g2t", R.XN, table)
    with ExitStack() as ctx:
        acc = ctx.enter_context(nc.sbuf_tensor("g2_acc", [P, NT * D], F32))
        eps = ctx.enter_context(nc.sbuf_tensor("g2_eps", [P, 1], F32))
        loaded = nc.alloc_semaphore("g2_loaded")
        edge_stage(nc, R, "g2e", "weight", R.rec_dst, R.tile_dst, acc[:, :], D, table=table)
        with nc.Block() as block:
            @block.sync
            def _(sp):
                sp.dma_start(eps[:, :], row_of(a["L2_gnn_eps_weight"], P)).then_inc(loaded, 16)

            @block.vector
            def _(dve):
                dve.wait_ge(loaded, 16)

                def add(t, k):
                    dve.scalar_tensor_tensor(out=node_tile(acc, t), in0=node_tile(R.XN, t), scalar=eps[:, 0:1],
                                             in1=node_tile(acc, t), op0=ALU.mult, op1=ALU.add)

                pairs(dve, NT, add)
        yt = ctx.enter_context(nc.sbuf_tensor("g2_yt", [128, KC, N], F32))
        zt = ctx.enter_context(nc.sbuf_tensor("g2_zt", [128, KC, N], F32))
        turn_stage(nc, R, "g2turn", acc, yt)
        batchnorm_product_stage(nc, R, "g2a", a["L2_gnn_w1"], yt, zt,
                                (a["L2_gnn_gamma1"], a["L2_gnn_beta1"]))
        batchnorm_product_stage(nc, R, "g2b", a["L2_gnn_w2"], zt, yt,
                                (a["L2_gnn_gamma_h"], a["L2_gnn_beta_h"]), scale_row=R.norm_row)
        eye = ctx.enter_context(nc.sbuf_tensor("g2_eye", [128, KC, D], F32))

        def before(dve):
            dve.memset(eye[:, :, :], 0.0)
            dve.drain()
            for c in range(KC):
                dve.tensor_copy(eye[:, c, c * 128:(c + 1) * 128], R.identf[:, :])
            dve.drain()

        with nc.Block() as block:
            @block.vector
            def _(dve):
                before(dve)

        def finish(dve, t, ps, out):
            x = node_tile(R.X, t)
            dve.tensor_tensor(x, x, ps[:, 0:D], ALU.add)
            dve.drain()
            dve.tensor_tensor(x, x, node_tile(R.XN, t), ALU.add)

        rows_stage(nc, R, "g2back", eye[:, :, :], D, finish, cols=yt)


def head_norm_mixer(nc, R, a):
    HEADS = D // DH
    with ExitStack() as ctx:
        def sb(n, shape, dt=F32):
            return ctx.enter_context(nc.sbuf_tensor(f"m2_{n}", shape, dt))

        def sem(n):
            return nc.alloc_semaphore(f"m2_{n}")

        K = sb("K", [P, NT * D])
        V = sb("V", [P, NT * D])
        dev = sb("dev", [P, NT * D])
        red = sb("red", [P, NT * HEADS])
        par = sb("par", [P, 4, D])
        M = sb("M", [128, KC, D])
        loaded, deviated, squared, summed, rooted, ready, multiplied = (sem(n) for n in (
            "loaded", "deviated", "squared", "summed", "rooted", "ready", "multiplied"))

        def by_head(b):
            return b[:, :].rearrange("p (t e) -> p t e", e=DH)

        redw = red[:, :].rearrange("p (t a) -> p t a", a=1).broadcast_to([P, NT * HEADS, DH])
        with nc.psum_tensor("m2_ps", [128, KC, 512], F32) as ps, nc.Block() as block:
            @block.sync
            def _(sp):
                for n, v in enumerate(("kln_weight", "kln_bias", "vln_weight", "vln_bias")):
                    sp.dma_start(par[:, n, :], row_of(a[f"L2_mix_{v}"].rearrange("h a e -> (h a e)"), P)).then_inc(loaded, 16)

            @block.vector
            def _(dve):
                dve.tensor_reduce(red[:, :], by_head(R.XN), AX.X, ALU.add)
                dve.drain()
                dve.tensor_scalar(red[:, :], red[:, :], 1.0 / DH, None, ALU.mult)
                dve.drain()
                dve.tensor_tensor(by_head(dev), by_head(R.XN), redw, ALU.subtract)
                dve.drain().then_inc(deviated, 1)
                dve.wait_ge(squared, 1)
                dve.tensor_reduce(red[:, :], by_head(K), AX.X, ALU.add)
                dve.drain().then_inc(summed, 1)
                dve.wait_ge(rooted, 1)
                dve.tensor_scalar(red[:, :], red[:, :], LN_EPS, None, ALU.add)
                dve.drain()
                dve.reciprocal(red[:, :], red[:, :])
                dve.drain()
                dve.tensor_tensor(by_head(dev), by_head(dev), redw, ALU.mult)
                dve.drain()
                dve.wait_ge(loaded, 64)
                for n, to in ((0, K), (2, V)):
                    def affine(t, k):
                        dve.tensor_tensor(node_tile(to, t), node_tile(dev, t), par[:, n, :], ALU.mult)
                        dve.drain()
                        dve.tensor_tensor(node_tile(to, t), node_tile(to, t), par[:, n + 1, :], ALU.add)

                    pairs(dve, NT, affine)
                dve.drain().then_inc(ready, 1)
                dve.memset(M[:, :, :], 0.0)
                dve.wait_ge(multiplied, 1)
                dve.drain()
                for c in range(KC):
                    for h in range(128 // DH):
                        b, at = slice(h * DH, (h + 1) * DH), c * 128 + h * DH
                        dve.tensor_scalar(M[b, c, at:at + DH], ps[b, c, h * DH:(h + 1) * DH], 1.0 / N, None, ALU.mult)

            @block.scalar
            def _(act):
                act.wait_ge(deviated, 1)
                act.activation(K[:, :], dev[:, :], ACT.Square)
                act.drain().then_inc(squared, 1)
                act.wait_ge(summed, 1)
                act.activation(red[:, :], red[:, :], ACT.Sqrt, scale=1.0 / (DH - 1))
                act.drain().then_inc(rooted, 1)

            @block.tensor
            def _(pe):
                pe.wait_ge(ready, 1)
                for c in range(KC):
                    for t in range(NT):
                        b = slice(t * D + c * 128, t * D + (c + 1) * 128)
                        last = pe.matmul(ps[:, c, 0:128], K[:, b], V[:, b], start=(t == 0), stop=(t == NT - 1))
                last.then_inc(multiplied, 1)

        def finish(dve, t, ps, out):
            x = node_tile(R.X, t)
            dve.tensor_tensor(x, x, ps[:, 0:D], ALU.add)
            dve.drain()
            dve.tensor_tensor(x, x, node_tile(R.XN, t), ALU.add)

        rows_stage(nc, R, "m2out", M[:, :, :], D, finish)


def third_feed_forward(nc, R, a):
    E2, F2 = a["L2_ffn_W1"].shape[0], a["L2_ffn_W1"].shape[2]
    with ExitStack() as ctx:
        route = Routing(nc, ctx, "f2", E2, 2)
        normalize_stage(nc, R, "f2ln", R.X, R.XN)
        router_stage(nc, R, "f2r", a["L2_ffn_Wr"], a["L2_ffn_br"], route)
        normalize_stage(nc, R, "f2ln2", R.XN, R.XN)
        routed_experts_stage(nc, R, "f2", F2, a["L2_ffn_W1"], a["L2_ffn_b1"], a["L2_ffn_W2"], a["L2_ffn_b2"], route,
                             ACT.Gelu, lambda dve, t, back: weighted_sum(dve, route, node_tile(R.X, t), t, back),
                             ln=a["L2_ffn_ln"])


def attention_graph_layer(nc, R, a):
    W = D + 1
    table = nc.dram_tensor("g3_table", (N, D + 2), F32).ap()
    with ExitStack() as ctx:
        def sb(n, shape, dt=F32):
            return ctx.enter_context(nc.sbuf_tensor(f"g3_{n}", shape, dt))

        S = sb("S", [P, NT])
        acc = sb("acc", [P, NT * W])
        with ExitStack() as inner:
            w = inner.enter_context(nc.sbuf_tensor("g3_w", [128, KC, D + 2], F32))
            av = inner.enter_context(nc.sbuf_tensor("g3_a", [P, 2, D], F32))
            tmp = inner.enter_context(nc.sbuf_tensor("g3_tmp", [P, 2, D], F32))

            def finish(dve, t, ps, out):
                dve.tensor_copy(out[:, 0:D], ps[:, 0:D])
                dve.memset(out[:, D:D + 1], 1.0)
                dve.tensor_tensor(tmp[:, 0, :], ps[:, 0:D], av[:, 0, :], ALU.mult)
                dve.tensor_tensor(tmp[:, 1, :], ps[:, 0:D], av[:, 1, :], ALU.mult)
                dve.drain()
                dve.tensor_reduce(S[:, ds(t, 1)], tmp[:, 0, :], AX.X, ALU.add)
                dve.tensor_reduce(out[:, D + 1:D + 2], tmp[:, 1, :], AX.X, ALU.add)

            def before(dve):
                dve.memset(w[:, :, D:D + 2], 0.0)

            with nc.Block() as block:
                @block.vector
                def _(dve):
                    before(dve)

            rows_stage(nc, R, "g3h", w[:, :, :], D + 2, finish,
                       loads=[(w[:, :, 0:D], chunks_of(a["L3_gnn_W"], D)),
                              (av[:, 0, :], row_of(a["L3_gnn_a"][0:D], P)), (av[:, 1, :], row_of(a["L3_gnn_a"][D:2 * D], P))],
                       store=lambda t: table[ds(t * P, P), :])
        edge_stage(nc, R, "g3e", "gat", R.rec_src, R.tile_src, acc[:, :], W, table=table, spread=S[:, :])
        accv = acc[:, :].rearrange("p (t w) -> p t w", w=W)
        with nc.Block() as block:
            @block.vector
            def _(dve):
                dve.reciprocal(S[:, :], accv[:, :, D])
                dve.drain()

                def add(t, k):
                    h = acc[:, ds(t * W, D)]
                    dve.tensor_scalar(h, h, 0.0, None, ALU.max)
                    dve.drain()
                    dve.scalar_tensor_tensor(out=node_tile(R.X, t), in0=h, scalar=S[:, ds(t, 1)], in1=node_tile(R.X, t),
                                             op0=ALU.mult, op1=ALU.add)

                pairs(dve, NT, add)


def squared_mixer(nc, R, a):
    S = 3 * D
    with ExitStack() as ctx:
        def sb(n, shape, dt=F32):
            return ctx.enter_context(nc.sbuf_tensor(f"m3_{n}", shape, dt))

        def sem(n):
            return nc.alloc_semaphore(f"m3_{n}")

        q, kk, v = sb("q", [P, NT * D]), sb("k", [P, NT * D]), sb("v", [P, NT * D])
        wout = sb("wout", [128, KC, D])
        bout = sb("bout", [P, D])
        M = sb("M", [128, KC, D])
        with ExitStack() as inner:
            w = inner.enter_context(nc.sbuf_tensor("m3_w", [128, KC, D], F32))
            b = inner.enter_context(nc.sbuf_tensor("m3_b", [P, D], F32))
            for n, to in enumerate((q, kk, v)):
                part = slice(n * D, (n + 1) * D)

                def finish(dve, t, ps, out):
                    dve.tensor_tensor(node_tile(to, t), ps[:, 0:D], b[:, :], ALU.add)

                rows_stage(nc, R, f"m3p{n}", w[:, :, :], D, finish,
                           loads=[(w[:, :, :], chunks_of(a["L3_mix_W_qkv"][:, part], D)),
                                  (b[:, :], row_of(a["L3_mix_b_qkv"][part], P))])
        tmp = sb("tmp", [P, NT * D])
        red = sb("red", [P, 2, NT])
        ss = sb("ss", [P, 2, NT])
        ksum = sb("ksum", [128, KC])
        (centered, squared, normed, squared2, summed, rooted, have_norm, norm_rooted, have_kv, loaded) = (sem(n) for n in (
            "centered", "squared", "normed", "squared2", "summed", "rooted", "have_norm", "norm_rooted", "have_kv", "loaded"))
        with nc.psum_tensor("m3_ps", [128, KC, 512], F32) as ps, nc.psum_tensor("m3_pn", [128, KC, 512], F32) as pn, \
                nc.Block() as block:
            def tiles(x):
                return x[:, :].rearrange("p (t d) -> p t d", d=D)

            def wide(r):
                return r.rearrange("p (t a) -> p t a", a=1).broadcast_to([P, NT, D])

            @block.sync
            def _(sp):
                sp.dma_start(wout[:, :, :], chunks_of(a["L3_mix_W_out"], D)).then_inc(loaded, 16)
                sp.dma_start(bout[:, :], row_of(a["L3_mix_b_out"], P)).then_inc(loaded, 16)
                sp.wait_ge(loaded, 32)

            @block.vector
            def _(dve):
                both = ((0, q), (1, kk))
                for n, x in both:
                    dve.tensor_reduce(red[:, n, :], tiles(x), AX.X, ALU.add)
                dve.drain()
                dve.tensor_scalar(red[:, :, :], red[:, :, :], 1.0 / D, None, ALU.mult)
                dve.drain()
                for n, x in both:
                    dve.tensor_tensor(tiles(x), tiles(x), wide(red[:, n, :]), ALU.subtract)
                dve.drain().then_inc(centered, 1)
                dve.wait_ge(squared, 1)
                for n, x in both:
                    dve.tensor_reduce(red[:, n, :], tiles(x), AX.X, ALU.add)
                dve.drain()
                dve.tensor_scalar(red[:, :, :], red[:, :, :], 1e-7, None, ALU.add)
                dve.drain()
                dve.reciprocal(red[:, :, :], red[:, :, :])
                dve.drain()
                for n, x in both:
                    dve.tensor_tensor(tiles(x), tiles(x), wide(red[:, n, :]), ALU.mult)
                dve.drain().then_inc(normed, 1)
                dve.wait_ge(squared2, 1)
                dve.tensor_reduce(ss[:, 0, :], tiles(tmp), AX.X, ALU.add)
                dve.drain().then_inc(summed, 1)
                dve.wait_ge(rooted, 1)
                dve.tensor_scalar(ss[:, 0, :], ss[:, 0, :], 1e-12, None, ALU.max)
                dve.drain()
                dve.reciprocal(ss[:, 0, :], ss[:, 0, :])
                dve.drain()
                dve.tensor_tensor(tiles(q), tiles(q), wide(ss[:, 0, :]), ALU.mult)
                dve.wait_ge(have_kv, 1)
                dve.tensor_copy(ksum[:, :], pn[:, :, 0])
                dve.drain().then_inc(have_norm, 1)
                dve.wait_ge(norm_rooted, 1)
                dve.tensor_scalar(ksum[:, :], ksum[:, :], 1e-12, None, ALU.max)
                dve.drain()
                dve.reciprocal(ksum[:, :], ksum[:, :])
                dve.drain()
                for c in range(KC):
                    dve.tensor_scalar(M[:, c, :], ps[:, c, 0:D], ksum[:, c:c + 1], float(N) ** -0.5, ALU.mult, ALU.mult)

            @block.scalar
            def _(act):
                act.wait_ge(centered, 1)
                act.activation(q[:, :], q[:, :], ACT.Square)
                act.activation(kk[:, :], kk[:, :], ACT.Square)
                act.drain().then_inc(squared, 1)
                act.wait_ge(normed, 1)
                act.activation(tmp[:, :], q[:, :], ACT.Square)
                act.drain().then_inc(squared2, 1)
                act.wait_ge(summed, 1)
                act.activation(ss[:, 0, :], ss[:, 0, :], ACT.Sqrt)
                act.activation(tmp[:, :], kk[:, :], ACT.Square)
                act.drain().then_inc(rooted, 1)
                act.wait_ge(have_norm, 1)
                act.activation(ksum[:, :], ksum[:, :], ACT.Sqrt)
                act.drain().then_inc(norm_rooted, 1)

            @block.tensor
            def _(pe):
                pe.wait_ge(rooted, 1)
                for c in range(KC):
                    for t in range(NT):
                        at = t * D + c * 128
                        pe.matmul(ps[:, c, 0:D], kk[:, at:at + 128], v[:, t * D:(t + 1) * D], start=(t == 0), stop=(t == NT - 1))
                        last = pe.matmul(pn[:, c, 0:1], tmp[:, at:at + 128], R.onesf[0:P, 0:1], start=(t == 0), stop=(t == NT - 1))
                last.then_inc(have_kv, 1)

        def add_v(dve, t, ps, out):
            dve.tensor_tensor(node_tile(v, t), node_tile(v, t), ps[:, 0:D], ALU.add)

        rows_stage(nc, R, "m3a", M[:, :, :], D, add_v, rows=q)

        def finish_out(dve, t, ps, out):
            x = node_tile(R.X, t)
            dve.tensor_tensor(x, x, ps[:, 0:D], ALU.add)
            dve.drain()
            dve.tensor_tensor(x, x, bout[:, :], ALU.add)

        rows_stage(nc, R, "m3b", wout[:, :, :], D, finish_out, rows=v)


def fourth_feed_forward(nc, R, a):
    CAP = max(1, int(0.5 * N))
    CHOSEN = CAP - 1 if CAP > 1 else 1
    F3 = a["L3_ffn_w1"].shape[1]
    with ExitStack() as ctx:
        def sb(n, shape, dt=F32):
            return ctx.enter_context(nc.sbuf_tensor(f"f3_{n}", shape, dt))

        normalize_stage(nc, R, "f3ln", R.X, R.XN)
        add_stage(nc, [(R.X, R.XN)])
        G = sb("G", [P, NT])
        with ExitStack() as inner:
            def sbi(n, shape, dt=F32):
                return inner.enter_context(nc.sbuf_tensor(f"f3_{n}", shape, dt))

            wr = sbi("wr", [128, KC, 1])
            br = sbi("br", [P, 1])

            def finish(dve, t, ps, out):
                dve.tensor_tensor(G[:, ds(t, 1)], ps[:, 0:1], br[:, :], ALU.add)

            rows_stage(nc, R, "f3r", wr[:, :, :], 1, finish,
                       loads=[(wr[:, :, :].rearrange("k c a -> k (c a)"), a["L3_ffn_wr"]), (br[:, :], row_of(a["L3_ffn_br"], P))])
            row_dram = nc.dram_tensor("f3_row_dram", (NT, P), F32).ap()
            turned = sbi("turned", [NT, P])
            row = sbi("row", [P, N])
            ge = sbi("ge", [P, 2, N])
            own = sbi("own", [P, 2, P])
            rank = sbi("rank", [P, 3, NT])
            pt = inner.enter_context(nc.psum_tensor("f3_pt", [NT, P], F32))
            have_t, copied, stored, spread = (nc.alloc_semaphore(f"f3_{n}") for n in (
                "have_t", "copied", "stored", "spread"))
            with nc.Block() as block:
                @block.tensor
                def _(pe):
                    pe.transpose(pt[:, :], G[:, :], R.identf[0:P, 0:P]).then_inc(have_t, 1)

                @block.sync
                def _(sp):
                    sp.wait_ge(copied, 1)
                    sp.dma_start(row_dram, turned[:, :]).then_inc(stored, 16)
                    sp.wait_ge(stored, 16)
                    sp.dma_start(row[:, :], row_dram.rearrange("t p -> (t p)").rearrange("(a n) -> a n", a=1)
                                 .partition_broadcast(P)).then_inc(spread, 16)

                @block.vector
                def _(dve):
                    dve.wait_ge(have_t, 1)
                    dve.tensor_copy(turned[:, :], pt[:, :]).then_inc(copied, 1)
                    dve.wait_ge(spread, 16)

                    for t in range(NT):
                        k = t % 2
                        mine = G[:, t:t + 1]
                        at = t * P
                        if t > 0:
                            dve.tensor_scalar(ge[:, k, 0:at], row[:, 0:at], mine, None, ALU.is_ge)
                        dve.tensor_scalar(ge[:, k, at:N], row[:, at:N], mine, None, ALU.is_gt)
                        dve.tensor_scalar(own[:, k, :], row[:, at:at + P], mine, None, ALU.is_equal)
                        dve.drain()
                        dve.scalar_tensor_tensor(out=own[:, k, :], in0=R.upto[0:P, 0:P], scalar=0.0, in1=own[:, k, :],
                                                 op0=ALU.is_equal, op1=ALU.mult)
                        dve.tensor_reduce(rank[:, 0, t:t + 1], ge[:, k, :], AX.X, ALU.add)
                        dve.drain()
                        dve.tensor_reduce(rank[:, 1, t:t + 1], own[:, k, :], AX.X, ALU.add)
                    dve.drain()
                    dve.tensor_tensor(rank[:, 2, :], rank[:, 0, :], rank[:, 1, :], ALU.add)
                    dve.drain()
                    dve.tensor_scalar(rank[:, 2, :], rank[:, 2, :], float(CHOSEN), None, ALU.is_lt)
                    dve.drain()
                    dve.tensor_tensor(G[:, :], G[:, :], rank[:, 2, :], ALU.mult)
        experts_stage(nc, R, "f3", 1, F3, a["L3_ffn_w1"].rearrange("(a d) f -> a d f", a=1), a["L3_ffn_b1"],
                      a["L3_ffn_w2"].rearrange("(a f) d -> a f d", a=1), a["L3_ffn_b2"].rearrange("(a d) -> a d", a=1), G,
                      R.X[:, :], ACT.Gelu_apprx_tanh)


def program(nc, a, out):
    with ExitStack() as ctx:
        R = Resident(nc, ctx)
        with nc.cleanup_on_exit():
            setup_stage(nc, R, a["x"])
            sort_stage(nc, R, "bydst", a["dst"], a["src"], R.rec_dst, R.tile_dst, a["edge_type_8"], a["edge_weight"])
            sort_stage(nc, R, "bysrc", a["src"], a["dst"], R.rec_src, R.tile_src)
            count_stage(nc, R)
        with nc.cleanup_on_exit():
            normalize_stage(nc, R, "ln0", R.X, R.XN)
            first_graph_layer(nc, R, a)
            softmax_mixer(nc, R, "m0", a["L0_mix_W_qkv"], a["L0_mix_W_out"], a["L0_mix_b_out"])
        with nc.cleanup_on_exit():
            first_feed_forward(nc, R, a)
        with nc.cleanup_on_exit():
            normalize_stage(nc, R, "ln1", R.X, R.XN)
            relation_graph_layer(nc, R, a)
        with nc.cleanup_on_exit():
            softmax_mixer(nc, R, "m1", a["L1_mix_w_qkv"], a["L1_mix_w_out"], a["L1_mix_b_out"], a["L1_mix_g_pre"],
                          a["L1_mix_mem_kv"], a["L1_mix_g_out"])
        with nc.cleanup_on_exit():
            second_feed_forward(nc, R, a)
        with nc.cleanup_on_exit():
            normalize_stage(nc, R, "ln2", R.X, R.XN)
            isomorphism_graph_layer(nc, R, a)
            head_norm_mixer(nc, R, a)
        with nc.cleanup_on_exit():
            third_feed_forward(nc, R, a)
        with nc.cleanup_on_exit():
            normalize_stage(nc, R, "ln3", R.X, R.XN)
            attention_graph_layer(nc, R, a)
        with nc.cleanup_on_exit():
            squared_mixer(nc, R, a)
        with nc.cleanup_on_exit():
            fourth_feed_forward(nc, R, a)
            store_rows_stage(nc, "out", R.X, out)


_OUT = "out_0_dram"


def _columns(a):
    return np.ascontiguousarray(np.moveaxis(a.reshape(a.shape[:-1] + (-1, 128)), -1, -2))


def kernel(**inputs):
    import concourse.bacc as _bacc
    from concourse.bass_utils import run_bass_kernel_spmd as _run

    columns = ("L0_ffn_b1", "L1_ffn_b1", "L2_ffn_b1", "L3_ffn_b1", "L2_gnn_gamma1", "L2_gnn_beta1", "L2_gnn_gamma_h",
               "L2_gnn_beta_h", "L1_mix_g_pre")
    arrays = {}
    for name, value in inputs.items():
        value = np.asarray(value)
        if name in ("L1_mix_t", "L3_ffn_attention_mask"):
            continue
        if name in ("L2_gnn_w1", "L2_gnn_w2"):
            value = value.T
        if name == "L3_ffn_wr":
            value = _columns(value[:, 0])
        if name in columns:
            value = _columns(value.reshape(1, -1) if name == "L3_ffn_b1" else value)
        arrays[name] = np.ascontiguousarray(value)
    arrays["L2_ffn_ln"] = np.ascontiguousarray(
        np.concatenate([_columns(arrays.pop("L2_ffn_ln_g")), _columns(arrays.pop("L2_ffn_ln_b"))], axis=-1))

    nc = _bacc.Bacc("TRN2", target_bir_lowering=False, num_devices=1)
    ap = {name: nc.dram_tensor(f"in_{name}", v.shape, mybir.dt.from_np(v.dtype), kind="ExternalInput").ap()
          for name, v in arrays.items()}
    out = nc.dram_tensor(_OUT, (N, D), F32, kind="ExternalOutput").ap()
    program(nc, ap, out)
    result = _run(nc, [{f"in_{name}": v for name, v in arrays.items()}], core_ids=[0])
    return result.results[0][_OUT]
```

```python
from contextlib import ExitStack

import concourse.bass as bass
from concourse import mybir
import numpy as np

F32 = mybir.dt.float32
BF16 = mybir.dt.bfloat16
I32 = mybir.dt.int32
U32 = mybir.dt.uint32
ALU = mybir.AluOpType
ACT = mybir.ActivationFunctionType
AX = mybir.AxisListType
ds = bass.ds

N, D, E = 3125, 256, 50000
P = 125
NT = N // P
KC = D // 128
EC = E // P
GE = 512
GT = GE // 128
NG = E // GE + NT
NG += -NG % 4
REC = 8
R_IDX, R_ROW, R_LOC, R_REL, R_W, R_KEY, R_HI, R_LO = range(REC)
DIGIT = 12
NOWHERE = 999.0
H0, DH = 8, 32
LN_EPS = 1e-5
NEG = -1.0e30
MEM = 4
CHUNK = 4 * P
NCH = N // CHUNK


class Resident:

    def __init__(self, nc, ctx):
        def sb(name, shape, dt=F32):
            return ctx.enter_context(nc.sbuf_tensor(name, shape, dt))

        self.nc = nc
        self.X = sb("X", [P, NT * D])
        self.XN = sb("XN", [P, NT * D])
        self.XNT = sb("XNT", [128, KC, N])
        self.identf = sb("identf", [128, 128])
        self.iota = sb("iota", [128, 128])
        self.onesf = sb("onesf", [128, 128])
        self.before = sb("before", [128, 128])
        self.upto = sb("upto", [128, 128])
        self.tile_dst = sb("tile_dst", [128, NG], I32)
        self.tile_src = sb("tile_src", [128, NG], I32)
        self.inv_count = sb("inv_count", [P, NT * 8])
        self.rec_dst = nc.dram_tensor("rec_dst", (NG * GE, REC), I32).ap()
        self.rec_src = nc.dram_tensor("rec_src", (NG * GE, REC), I32).ap()
        self.norm_row = nc.dram_tensor("norm_row", (NT, P), F32).ap()


def node_tile(buf, t, width=D):
    return buf[:, ds(t * width, width)]


def is_first(n):
    return isinstance(n, int) and n < 2


def pairs(eng, count, body, peel=False):
    if peel:
        body(0, 0)
        body(1, 1)
    if count > (3 if peel else 1):
        with eng.Fori(int(peel), count // 2) as i:
            body(i * 2, 0)
            body(i * 2 + 1, 1)
    if count % 2:
        body(count - 1, 0)


def rounds(eng, count, depth, body):
    with eng.Fori(0, count // depth) as i:
        for k in range(depth):
            body(i * depth + k, k)
    for n in range(count - count % depth, count):
        body(n, n % depth)


DEPTH = 4
LONG = 8
LEAD = 6


def skewed(eng, count, turn):
    for n in range(-LEAD, 0):
        turn(n, n % LONG)
    full = (count - LEAD) // LONG
    with eng.Fori(0, full) as i:
        for k in range(LONG):
            turn(i * LONG + k, k)
    for n in range(full * LONG, count):
        turn(n, n % LONG)


def there(n, count=NG):
    return not isinstance(n, int) or 0 <= n < count


def landed(g, slot, transfers=1, slots=DEPTH):
    return (g - slot) * (16 * transfers // slots) + 16 * transfers


def setup_stage(nc, R, x):
    with ExitStack() as ctx:
        x_loaded = nc.alloc_semaphore("x_loaded")
        zeroed = nc.alloc_semaphore("zeroed")
        block = ctx.enter_context(nc.Block())

        @block.sync
        def _(sp):
            sp.dma_start(R.X[:, :].rearrange("p (t d) -> p t d", d=D),
                         x.rearrange("(t p) d -> p t d", p=P)).then_inc(x_loaded, 16)
            sp.wait_ge(x_loaded, 16)

        @block.gpsimd
        def _(pool):
            pool.memset(R.identf[:, :], 0.0).then_inc(zeroed, 1)
            pool.memset(R.onesf[:, :], 1.0).then_inc(zeroed, 1)
            pool.iota(R.iota[:, :], pattern=[[1, 128]], base=0, channel_multiplier=0,
                      allow_small_or_imprecise_dtypes=True)
            pool.wait_ge(zeroed, 2)
            pool.affine_select(out=R.identf[:, :], in_=R.identf[:, :], compare_op=ALU.not_equal, fill=1.0,
                               base=0, pattern=[[-1, 128]], channel_multiplier=1)
            pool.affine_select(out=R.before[:, :], in_=R.onesf[:, :], compare_op=ALU.is_gt, fill=0.0,
                               base=0, pattern=[[1, 128]], channel_multiplier=-1)
            pool.affine_select(out=R.upto[:, :], in_=R.onesf[:, :], compare_op=ALU.is_ge, fill=0.0,
                               base=0, pattern=[[1, 128]], channel_multiplier=-1)


W8 = 8


class EdgeSort:

    def __init__(self, nc, ctx, name, key, gather, rec, tile_of, relation=None, weight=None):
        def sb(n, shape, dt=F32):
            return ctx.enter_context(nc.sbuf_tensor(f"{name}_{n}", shape, dt))

        def sem(n):
            return nc.alloc_semaphore(f"{name}_{n}")

        self.key, self.gather, self.rec, self.tile_of, self.relation, self.weight = key, gather, rec, tile_of, relation, weight
        self.ki = sb("ki", [P, EC], I32)
        self.kf = sb("kf", [P, EC])
        self.rc = sb("rc", [P, EC, REC], I32)
        self.gi = sb("gi", [P, EC], I32)
        self.ri = sb("ri", [P, EC], I32)
        self.wf = sb("wf", [P, EC])
        self.slot = sb("slot", [P, EC])
        self.sloti = sb("sloti", [P, EC], I32)
        self.cnt = sb("cnt", [P, NT])
        self.stage_i = sb("stage_i", [P, 2, W8], I32)
        self.stage_r = sb("stage_r", [P, 2, W8, REC], I32)
        self.loaded, self.emptied, self.counted, self.summed, self.slotted, self.staged, self.issued = (sem(n) for n in (
            "loaded", "emptied", "counted", "summed", "slotted", "staged", "issued"))
        self.scattered = [sem("scattered0"), sem("scattered1")]

    def scatter(self, pool):
        def turn(n, k):
            if not is_first(n):
                pool.wait_ge(self.scattered[k], (n - k) * (8 * W8))
            pool.sem_inc(self.issued, 1)
            pool.tensor_copy(self.stage_i[:, k, :], self.sloti[:, ds(n * W8, W8)]).then_inc(self.staged, 1)
            pool.tensor_copy(self.stage_r[:, k, :, :], self.rc[:, ds(n * W8, W8), :]).then_inc(self.staged, 1)
            pool.wait_ge(self.staged, n * 2 + 2)
            pool.sem_inc(self.issued, 1)
            for c in range(W8):
                pool.indirect_dma_start(self.rec, bass.IndirectOffsetOnAxis(self.stage_i[:, k, c:c + 1], 0),
                                        self.stage_r[:, k, c, :], None).then_inc(self.scattered[k], 16)

        pairs(pool, EC // W8, turn, peel=True)
        for k in range(2):
            pool.wait_ge(self.scattered[k], 16 * W8 * (EC // W8 // 2))


def sort_stage(nc, R, sorts):
    with ExitStack() as ctx:
        def sb(n, shape, dt=F32):
            return ctx.enter_context(nc.sbuf_tensor(f"sort_{n}", shape, dt))

        def sem(n):
            return nc.alloc_semaphore(f"sort_{n}")

        gef = sb("gef", [P, 2, EC])
        inb = sb("inb", [P, NT, EC], BF16)
        run = sb("run", [P, 2, EC])
        tot = sb("tot", [128, NT])
        grp = sb("grp", [128, NT])
        grpi = sb("grpi", [128, NT], I32)
        endg = sb("endg", [128, NT])
        one = sb("one", [128, NT])
        first = sb("first", [P, NT])
        gid = sb("gid", [128, NG])
        tf = sb("tf", [128, NG])
        FILL = NG * GE // 128
        empty = sb("empty", [128, FILL, REC], I32)
        sums = ctx.enter_context(nc.psum_tensor("sort_sums", [128, len(sorts), 2 * NT], F32))
        made_empty, iotad = sem("made_empty"), sem("iotad")
        block = ctx.enter_context(nc.Block())

        def edges(a):
            return a.rearrange("(p c) -> p c", c=EC)

        @block.sync
        def _(sp):
            for b in sorts:
                sp.dma_start(b.ki[:, :], edges(b.key)).then_inc(b.loaded, 16)
                sp.dma_start(b.gi[:, :], edges(b.gather)).then_inc(b.loaded, 16)
                if b.relation is not None:
                    sp.dma_start(b.ri[:, :], edges(b.relation)).then_inc(b.loaded, 16)
                    sp.dma_start(b.wf[:, :], edges(b.weight)).then_inc(b.loaded, 16)
            sp.wait_ge(made_empty, 1)
            for b in sorts:
                sp.dma_start(b.rec.rearrange("(p c) r -> p (c r)", p=128),
                             empty[:, :, :].rearrange("p c r -> p (c r)")).then_inc(b.emptied, 16)
            for b in sorts:
                sp.wait_ge(b.emptied, 16)

        @block.gpsimd
        def _(pool):
            pool.iota(gid[:, :], pattern=[[1, NG]], base=0, channel_multiplier=0,
                      allow_small_or_imprecise_dtypes=True).then_inc(iotad, 1)
            for b in sorts[:-1]:
                pool.wait_ge(b.emptied, 16)
                pool.wait_ge(b.slotted, 1)
                b.scatter(pool)

        @block.tensor
        def _(pe):
            for n, b in enumerate(sorts):
                pe.wait_ge(b.counted, 1)
                pe.matmul(sums[:, n, 0:NT], R.onesf[0:P, :], b.cnt[:, :], start=True, stop=True)
                pe.matmul(sums[:, n, NT:2 * NT], R.before[0:P, :], b.cnt[:, :], start=True, stop=True).then_inc(b.summed, 1)

        @block.vector
        def _(dve):
            dve.memset(empty[:, :, :], 0)
            dve.memset(one[:, :], 1.0)
            dve.drain()
            dve.memset(empty[:, :, :].bitcast(F32)[:, :, R_LOC], NOWHERE)
            dve.memset(empty[:, :, R_KEY], N)
            dve.memset(empty[:, :, :].bitcast(F32)[:, :, R_HI], float(DIGIT - 1))
            dve.drain().then_inc(made_empty, 1)
            for n, b in enumerate(sorts):
                rcf = b.rc[:, :, :].bitcast(F32)
                dve.wait_ge(b.loaded, 64 if b.relation is not None else 32)
                dve.tensor_copy(b.kf[:, :], b.ki[:, :])
                dve.tensor_copy(b.rc[:, :, R_IDX], b.gi[:, :])
                dve.tensor_copy(b.rc[:, :, R_KEY], b.ki[:, :])
                if b.relation is not None:
                    dve.tensor_scalar(run[:, 0, :], b.ri[:, :], float(N), None, ALU.mult)
                    dve.drain()
                    dve.tensor_tensor(b.rc[:, :, R_ROW], run[:, 0, :], b.gi[:, :], ALU.add)
                    dve.tensor_copy(rcf[:, :, R_REL], b.ri[:, :])
                    dve.tensor_copy(rcf[:, :, R_W], b.wf[:, :])
                else:
                    dve.memset(b.rc[:, :, R_ROW], 0)
                    dve.memset(rcf[:, :, R_REL], 0.0)
                    dve.memset(rcf[:, :, R_W], 0.0)
                dve.drain()
                dve.tensor_copy(rcf[:, :, R_LOC], b.kf[:, :])
                dve.memset(gef[:, 0, :], 1.0)
                for tile in range(NT):
                    dve.tensor_scalar(gef[:, (tile + 1) % 2, :], b.kf[:, :], float(P * (tile + 1)), None, ALU.is_ge)
                    dve.drain()
                    dve.tensor_tensor(inb[:, tile, :], gef[:, tile % 2, :], gef[:, (tile + 1) % 2, :], ALU.subtract)
                    dve.scalar_tensor_tensor(out=rcf[:, :, R_LOC], in0=gef[:, (tile + 1) % 2, :], scalar=-float(P),
                                             in1=rcf[:, :, R_LOC], op0=ALU.mult, op1=ALU.add)
                    dve.drain()
                    dve.tensor_reduce(b.cnt[:, tile:tile + 1], inb[:, tile, :], AX.X, ALU.add)
                dve.drain().then_inc(b.counted, 1)
                dve.tensor_scalar(b.ki[:, :], rcf[:, :, R_LOC], 5462.0, None, ALU.mult)
                dve.drain()
                dve.tensor_scalar(b.ki[:, :], b.ki[:, :], 16, None, ALU.arith_shift_right)
                dve.drain()
                dve.tensor_copy(rcf[:, :, R_HI], b.ki[:, :])
                dve.drain()
                dve.scalar_tensor_tensor(out=rcf[:, :, R_LO], in0=rcf[:, :, R_HI], scalar=-float(DIGIT),
                                         in1=rcf[:, :, R_LOC], op0=ALU.mult, op1=ALU.add)
                dve.wait_ge(b.summed, 1)
                dve.tensor_copy(tot[:, :], sums[:, n, 0:NT])
                dve.drain()
                dve.tensor_scalar(grpi[:, :], tot[:, :], float(GE - 1), None, ALU.add)
                dve.drain()
                dve.tensor_scalar(grpi[:, :], grpi[:, :], 9, None, ALU.arith_shift_right)
                dve.drain()
                dve.tensor_scalar(grp[:, :], grpi[:, :], 1.0, None, ALU.max)
                dve.drain()
                dve.tensor_tensor_scan(endg[:, :], one[:, :], grp[:, :], 0.0, ALU.mult, ALU.add)
                dve.drain()
                dve.tensor_tensor(grp[:, :], endg[:, :], grp[:, :], ALU.subtract)
                dve.drain()
                dve.tensor_scalar(grp[:, :], grp[:, :], float(GE), -1.0, ALU.mult, ALU.add)
                dve.drain()
                dve.tensor_tensor(first[:, :], grp[0:P, :], sums[0:P, n, NT:2 * NT], ALU.add)
                dve.wait_ge(iotad, 1)
                dve.memset(tf[:, :], 0.0)
                for tile in range(NT - 1):
                    dve.drain()
                    dve.scalar_tensor_tensor(out=tf[:, :], in0=gid[:, :], scalar=endg[:, tile:tile + 1], in1=tf[:, :],
                                             op0=ALU.is_ge, op1=ALU.add)
                dve.drain()
                dve.tensor_copy(b.tile_of[:, :], tf[:, :])
                dve.memset(gef[:, 0, :], 1.0)
                dve.memset(b.slot[:, :], 0.0)
                dve.drain()
                for tile in range(NT):
                    k = tile % 2
                    dve.tensor_tensor_scan(run[:, k, :], gef[:, 0, :], inb[:, tile, :], first[:, tile:tile + 1], ALU.mult, ALU.add)
                    dve.drain()
                    dve.tensor_tensor(run[:, k, :], run[:, k, :], inb[:, tile, :], ALU.mult)
                    dve.drain()
                    dve.tensor_tensor(b.slot[:, :], b.slot[:, :], run[:, k, :], ALU.add)
                dve.drain()
                dve.tensor_copy(b.sloti[:, :], b.slot[:, :])
                dve.drain().then_inc(b.slotted, 1)


def chunks_of(w, width):
    return w.rearrange("(c k) n -> k c n", k=128)


def row_of(v, parts):
    return v.rearrange("(a n) -> a n", a=1).partition_broadcast(parts)


def normalize_stage(nc, R, name, src, dst):
    with ExitStack() as ctx:
        def sem(n):
            return nc.alloc_semaphore(f"{name}_{n}")

        def sb(n, shape, dt=F32):
            return ctx.enter_context(nc.sbuf_tensor(f"{name}_{n}", shape, dt))

        stats = sb("stats", [P, 2, nc.vector.BN_STATS_DIM])
        mv = sb("mv", [P, 2, nc.vector.BN_AGGR_DIM])
        mean = sb("mean", [P, NT])
        var = sb("var", [P, NT])
        std = sb("std", [P, NT])
        rstd = sb("rstd", [P, NT])
        rows = sb("rows", [P, 2, D])
        pt = [ctx.enter_context(nc.psum_tensor(f"{name}_pt{k}", [128, KC * P], F32)) for k in range(2)]
        have_var, have_std, normed, turned, evacuated = sem("have_var"), sem("have_std"), sem("normed"), sem("turned"), sem("evacuated")
        copied = sem("copied")
        block = ctx.enter_context(nc.Block())

        @block.vector
        def _(dve):
            def moments(t, k):
                dve.bn_stats(stats[:, k, :], node_tile(src, t))
                dve.drain()
                dve.bn_aggr(mv[:, k, :], stats[:, k, :])
                dve.drain()
                dve.tensor_copy(mean[:, ds(t, 1)], mv[:, k, 0:1])
                dve.tensor_scalar(var[:, ds(t, 1)], mv[:, k, 1:2], LN_EPS, None, ALU.add)

            pairs(dve, NT, moments)
            dve.drain().then_inc(have_var, 1)
            dve.wait_ge(have_std, 1)
            dve.reciprocal(rstd[:, :], std[:, :])
            dve.drain()
            dve.sem_inc(copied, 2)

            def scale(t, k):
                dve.wait_ge(copied, t + 1)
                dve.wait_ge(turned, t + 1)
                dve.tensor_scalar(rows[:, k, :], node_tile(src, t), mean[:, ds(t, 1)], rstd[:, ds(t, 1)],
                                  ALU.subtract, ALU.mult).then_inc(normed, 1)

            pairs(dve, NT, scale)

        @block.scalar
        def _(act):
            act.wait_ge(have_var, 1)
            act.activation(std[:, :], var[:, :], ACT.Sqrt).then_inc(have_std, 1)

            def evacuate(t, k):
                act.wait_ge(turned, t + 3)
                act.activation(R.XNT[:, :, ds(t * P, P)], pt[k][:, :].rearrange("k (c p) -> k c p", p=P),
                               ACT.Copy).then_inc(evacuated, 1)

            def keep(t, k):
                act.wait_ge(normed, t + 1)
                act.activation(node_tile(dst, t), rows[:, k, :], ACT.Copy).then_inc(copied, 1)
                evacuate(t, k)

            act.sem_inc(evacuated, 2)
            pairs(act, NT, keep)

        @block.tensor
        def _(pe):
            pe.sem_inc(turned, 2)

            def turn(t, k):
                pe.wait_ge(normed, t + 1)
                pe.wait_ge(evacuated, t + 1)
                for c in range(KC):
                    last = pe.transpose(pt[k][:, c * P:(c + 1) * P], rows[:, k, c * 128:(c + 1) * 128],
                                        R.identf[0:P, 0:P])
                last.then_inc(turned, 1)

            pairs(pe, NT, turn)


def rows_stage(nc, R, name, weights, width, finish, rows=None, stride=D, offset=0,
               loads=(), store=None, before=None, cols=None):
    chunks = weights.shape[1]
    with ExitStack() as ctx:
        def sem(n):
            return nc.alloc_semaphore(f"{name}_{n}")

        def sb(n, shape, dt=F32):
            return ctx.enter_context(nc.sbuf_tensor(f"{name}_{n}", shape, dt))

        xt = sb("xt", [128, 2, chunks, P])
        staged = sb("staged", [P, 2, chunks * 128]) if rows is not None else None
        out = sb("out", [P, 2, width])
        pt = [ctx.enter_context(nc.psum_tensor(f"{name}_pt{k}", [128, chunks * P], F32)) for k in range(2)]
        ps = [ctx.enter_context(nc.psum_tensor(f"{name}_ps{k}", [P, width], F32)) for k in range(2)]
        loaded, copied, turned, ready, multiplied, finished = (sem(n) for n in (
            "loaded", "copied", "turned", "ready", "multiplied", "finished"))
        stored = [sem("stored0"), sem("stored1")]
        block = ctx.enter_context(nc.Block())

        @block.sync
        def _(sp):
            for to, of in loads:
                sp.dma_start(to, of).then_inc(loaded, 16)
            sp.wait_ge(loaded, 16 * len(loads)) if loads else None
            if store is not None:
                def put(t, k):
                    sp.wait_ge(finished, t + 3)
                    sp.dma_start(store(t), out[:, k, :]).then_inc(stored[k], 16)

                pairs(sp, NT, put)
                sp.wait_ge(stored[0], 16 * (NT - NT // 2))
                sp.wait_ge(stored[1], 16 * (NT // 2))

        @block.gpsimd
        def _(pool):
            if rows is not None:
                pool.wait_ge(loaded, 16 * len(loads)) if loads else None

                def stage(t, k):
                    pool.wait_ge(turned, t + 1)
                    pool.tensor_copy(staged[:, k, :], rows[:, ds(t * stride + offset, chunks * 128)]).then_inc(copied, 1)

                pairs(pool, NT, stage)

        @block.scalar
        def _(act):
            if rows is not None:
                def evacuate(t, k):
                    act.wait_ge(turned, t + 3)
                    act.wait_ge(multiplied, t + 1)
                    act.activation(xt[:, k, :, :], pt[k][:, :].rearrange("k (c p) -> k c p", p=P),
                                   ACT.Copy).then_inc(ready, 1)

                pairs(act, NT, evacuate)
            else:
                def stage(t, k):
                    act.wait_ge(multiplied, t + 1)
                    act.activation(xt[:, k, :, :], (R.XNT if cols is None else cols)[:, :, ds(t * P, P)],
                                   ACT.Copy).then_inc(ready, 1)

                pairs(act, NT, stage)

        @block.tensor
        def _(pe):
            pe.sem_inc(turned, 2)
            pe.sem_inc(multiplied, 2)
            pe.wait_ge(loaded, 16 * len(loads)) if loads else None

            def turn(t, k):
                pe.wait_ge(copied, t + 1)
                pe.wait_ge(ready, t - 1) if not isinstance(t, int) or t >= 2 else None
                for c in range(chunks):
                    last = pe.transpose(pt[k][:, c * P:(c + 1) * P], staged[:, k, c * 128:(c + 1) * 128],
                                        R.identf[0:P, 0:P])
                last.then_inc(turned, 1)

            def multiply(t, k):
                pe.wait_ge(ready, t + 1)
                pe.wait_ge(finished, t + 1)
                for a in range(0, width, 512):
                    b = min(a + 512, width)
                    for c in range(chunks):
                        last = pe.matmul(ps[k][:, a:b], xt[:, k, c, :], weights[:, c, a:b], start=(c == 0),
                                         stop=(c == chunks - 1))
                last.then_inc(multiplied, 1)

            if rows is None:
                pairs(pe, NT, multiply)
            else:
                turn(0, 0)
                turn(1, 1)
                with pe.Fori(0, NT // 2 - 1) as i:
                    multiply(i * 2, 0)
                    turn(i * 2 + 2, 0)
                    multiply(i * 2 + 1, 1)
                    turn(i * 2 + 3, 1)
                multiply(NT - 3, 0)
                turn(NT - 1, 0)
                multiply(NT - 2, 1)
                multiply(NT - 1, 0)

        @block.vector
        def _(dve):
            dve.sem_inc(finished, 2)
            dve.wait_ge(loaded, 16 * len(loads)) if loads else None
            if before is not None:
                before(dve)
                dve.drain()

            def take(t, k):
                dve.wait_ge(multiplied, t + 3)
                if store is not None and not is_first(t):
                    dve.wait_ge(stored[k], (t - k) * 8)
                finish(dve, t, ps[k], out[:, k, :])
                dve.drain().then_inc(finished, 1)

            pairs(dve, NT, take, peel=store is not None)


def edge_stage(nc, R, name, mode, rec, tile_of, acc, width, table=None, idx=R_IDX, spread=None, scatter=None):
    sw = 8 if mode == "relation" else 1
    needs_spread = mode in ("relation", "gat")
    with ExitStack() as ctx:
        def sem(n):
            return nc.alloc_semaphore(f"{name}_{n}")

        def sb(n, shape, dt=F32):
            return ctx.enter_context(nc.sbuf_tensor(f"{name}_{n}", shape, dt))

        rc = sb("rc", [128, LONG, GT, REC], I32)
        rcf = rc[:, :, :, :].bitcast(F32)
        wide = table.shape[1] if table is not None else 8
        got = sb("got", [128, LONG, GT, wide])
        place = sb("place", [128, DEPTH, GT, P])
        placew = sb("placew", [128, DEPTH, GT, P])
        placet = sb("placet", [P, DEPTH, GT, 128])
        small = sb("small", [128, DEPTH, GT, 8])
        rel = sb("rel", [128, DEPTH, GT, 8])
        coef = sb("coef", [128, DEPTH, GT])
        coef2 = sb("coef2", [128, DEPTH, GT])
        pt = ctx.enter_context(nc.psum_tensor(f"{name}_pt", [P, 2, 512], F32))
        pq = ctx.enter_context(nc.psum_tensor(f"{name}_pq", [128, 4, 512], F32))
        pa = ctx.enter_context(nc.psum_tensor(f"{name}_pa", [P, 2, 512], F32))
        rec_in = [sem(f"rec_in{k}") for k in range(LONG)]
        got_in = [sem(f"got_in{k}") for k in range(LONG)]
        names = ("ordered", "placed", "weighed", "turned", "evacuated", "spreaded", "logit", "expd", "summed", "added")
        ordered, placed, weighed, turned, evacuated, spreaded, logit, expd, summed, added = (sem(n) for n in names)
        block = ctx.enter_context(nc.Block())

        @block.sync
        def _(sp):
            def turn(n, k):
                g, s = n + 6, (k + 6) % LONG
                if not there(g):
                    return
                sp.wait_ge(added, g + 1)
                sp.dma_start(rc[:, s, :, :].rearrange("p j r -> p (j r)"),
                             rec[ds(g * GE, GE), :].rearrange("(p j) r -> p (j r)", j=GT)).then_inc(rec_in[s], 16)

            skewed(sp, NG, turn)

        @block.gpsimd
        def _(pool):
            def turn(n, k):
                g, s = n + 5, (k + 5) % LONG
                if not there(g):
                    return
                pool.wait_ge(rec_in[s], landed(g, s, slots=LONG))
                pool.sem_inc(ordered, 1)
                for j in range(GT):
                    pool.indirect_dma_start(got[:, s, j, :], None, table,
                                            bass.IndirectOffsetOnAxis(rc[:, s, j, idx:idx + 1], 0)).then_inc(got_in[s], 16)

            if table is not None:
                skewed(pool, NG, turn)
            if scatter is not None:
                scatter(pool)

        @block.scalar
        def _(act):
            act.sem_inc(evacuated, 2)

            def turn(n, k):
                g, s = n + 3, (k + 3) % DEPTH
                if there(g):
                    act.wait_ge(turned, g + 1)
                    act.activation(placet[:, s, :, :], pt[:, s % 2, :].rearrange("p (j e) -> p j e", e=128),
                                   ACT.Copy).then_inc(evacuated, 1)
                g, s = n + 2, (k + 2) % DEPTH
                if mode == "gat" and there(g):
                    act.wait_ge(logit, g + 1)
                    act.activation(coef2[:, s, :], coef[:, s, :], ACT.Exp, scale=-1.0).then_inc(expd, 1)

            if needs_spread:
                skewed(act, NG, turn)

        @block.tensor
        def _(pe):
            tile_reg = pe.alloc_register(f"{name}_pe_tile")

            def turn(n, k):
                g, s = n + 3, (k + 3) % DEPTH
                if needs_spread and there(g):
                    pe.wait_ge(placed, g + 1)
                    pe.wait_ge(evacuated, g + 1)
                    for j in range(GT):
                        last = pe.transpose(pt[:, s % 2, j * 128:(j + 1) * 128], place[:, s, j, :], R.identf[:, :])
                    last.then_inc(turned, 1)
                    pe.reg_load(tile_reg, tile_of[0:1, ds(g, 1)])
                    b = pe.snap(tile_reg)
                    pe.wait_ge(evacuated, g + 3)
                    for j in range(GT):
                        last = pe.matmul(pq[:, s, j * 8:j * 8 + sw], placet[:, s, j, :], spread[:, ds(b * sw, sw)],
                                         start=True, stop=True)
                    last.then_inc(spreaded, 1)
                g, s, sl = n + 1, (k + 1) % DEPTH, (k + 1) % LONG
                if there(g):
                    pe.wait_ge(weighed, g + 1)
                    if table is not None:
                        pe.wait_ge(got_in[sl], landed(g, sl, GT, LONG))
                    for j in range(GT):
                        rhs = rel[:, s, j, :] if mode == "count" else got[:, sl, j, 0:width]
                        lhs = place if mode == "count" else placew
                        last = pe.matmul(pa[:, s % 2, 0:width], lhs[:, s, j, :], rhs, start=(j == 0), stop=(j == GT - 1))
                    last.then_inc(summed, 1)

            skewed(pe, NG, turn)

        @block.vector
        def _(dve):
            tile_reg = dve.alloc_register(f"{name}_dve_tile")
            dve.memset(acc, 0.0)
            dve.drain()
            dve.sem_inc(added, LONG)

            def turn(n, k):
                g, s, sl = n + 3, (k + 3) % DEPTH, (k + 3) % LONG
                if there(g):
                    dve.wait_ge(rec_in[sl], landed(g, sl, slots=LONG))
                    for j in range(GT):
                        loc, w = rcf[:, sl, j, R_LOC:R_LOC + 1], rcf[:, sl, j, R_W:R_W + 1]
                        if mode == "weight":
                            dve.tensor_scalar(placew[:, s, j, :], R.iota[:, 0:P], loc, w, ALU.is_equal, ALU.mult)
                        else:
                            dve.tensor_scalar(place[:, s, j, :], R.iota[:, 0:P], loc, None, ALU.is_equal)
                        if mode in ("count", "relation"):
                            dve.tensor_scalar(rel[:, s, j, :], R.iota[:, 0:8], rcf[:, sl, j, R_REL:R_REL + 1], None,
                                              ALU.is_equal)
                    if needs_spread:
                        dve.drain().then_inc(placed, 1)
                g, s, sl = n + 2, (k + 2) % DEPTH, (k + 2) % LONG
                if there(g) and mode == "gat":
                    dve.wait_ge(spreaded, g + 1)
                    dve.wait_ge(got_in[sl], landed(g, sl, GT, LONG))
                    dve.tensor_tensor(coef[:, s, :], pq[:, s, 0:GT * 8].rearrange("p (j r) -> p j r", r=8)[:, :, 0],
                                      got[:, sl, :, wide - 1], ALU.add)
                    dve.drain()
                    dve.scalar_tensor_tensor(out=coef[:, s, :], in0=coef[:, s, :], scalar=0.2, in1=coef[:, s, :],
                                             op0=ALU.mult, op1=ALU.max)
                    dve.drain().then_inc(logit, 1)
                g, s, sl = n + 1, (k + 1) % DEPTH, (k + 1) % LONG
                if there(g) and mode == "relation":
                    dve.wait_ge(spreaded, g + 1)
                    dve.tensor_tensor(small[:, s, :, :], pq[:, s, 0:GT * 8].rearrange("p (j r) -> p j r", r=8),
                                      rel[:, s, :, :], ALU.mult)
                    dve.drain()
                    dve.tensor_reduce(coef[:, s, :], small[:, s, :, :], AX.X, ALU.add)
                    dve.drain()
                    dve.tensor_tensor(coef2[:, s, :], coef[:, s, :], rcf[:, sl, :, R_W], ALU.mult)
                    dve.drain()
                if there(g):
                    if mode == "gat":
                        dve.wait_ge(expd, g + 1)
                    if needs_spread:
                        for j in range(GT):
                            dve.tensor_scalar(placew[:, s, j, :], place[:, s, j, :], coef2[:, s, j:j + 1], None, ALU.mult)
                if there(n):
                    dve.reg_load(tile_reg, tile_of[0:1, ds(n, 1)])
                    b = dve.snap(tile_reg)
                    dve.wait_ge(summed, n + 1)
                    into = acc[:, ds(b * width, width)]
                    dve.tensor_tensor(into, into, pa[:, k % 2, 0:width], ALU.add)
                if there(n) or there(g):
                    last = dve.drain()
                if there(g):
                    last.then_inc(weighed, 1)
                if there(n):
                    dve.sem_inc(added, 1)

            skewed(dve, NG, turn)


def attention_edge_stage(nc, R, name, table, keys, masks_in, acc):
    W = D + H0
    JH = GT * H0
    with ExitStack() as ctx:
        def sem(n):
            return nc.alloc_semaphore(f"{name}_{n}")

        def sb(n, shape, dt=F32):
            return ctx.enter_context(nc.sbuf_tensor(f"{name}_{n}", shape, dt))

        rc = sb("rc", [128, LONG, GT, REC], I32)
        rcf = rc[:, :, :, :].bitcast(F32)
        got = sb("got", [128, DEPTH, GT, 2 * D])
        place = sb("place", [128, DEPTH, GT, P])
        keyed = sb("keyed", [128, DEPTH, GT, D])
        placet = sb("placet", [P, DEPTH, GT, 128])
        prod = sb("prod", [128, GT, D])
        score = sb("score", [128, DEPTH, GT, 32])
        masks = sb("masks", [128, H0 + GT * P])
        by_tile = sb("by_tile", [128, GT, P], BF16)
        by_head = masks[:, 0:H0]
        expanded = sb("expanded", [128, 2, H0, 128], BF16)
        msg = sb("msg", [128, 2, GT, W])
        spaced = sb("spaced", [P, GT, H0, 128], BF16)
        gmax = sb("gmax", [P, H0])
        high = sb("high", [P, NT * H0])
        new = sb("new", [P, 2, H0])
        drop = sb("drop", [P, 2, H0])
        alpha = sb("alpha", [P, 2, H0])
        shifted = sb("shifted", [128, 2, GT, H0])
        spread = ctx.enter_context(nc.psum_tensor(f"{name}_spread", [P, 4, 512], F32))
        pt = ctx.enter_context(nc.psum_tensor(f"{name}_pt", [128, 512], F32))
        ps = ctx.enter_context(nc.psum_tensor(f"{name}_ps", [128, 512], F32))
        pm = pt
        pa = ctx.enter_context(nc.psum_tensor(f"{name}_pa", [P, 512], F32))
        rec_in = [sem(f"rec_in{k}") for k in range(LONG)]
        got_in = [sem(f"got_in{k}") for k in range(DEPTH)]
        names = ("ordered", "placed", "turned", "evacuated", "scored", "scores_turned",
                 "have_expanded", "spread_out", "copied", "maxed", "max_spread", "shifted", "exped", "messaged", "summed",
                 "added", "masks_in", "dropped", "falls")
        (ordered, placed, turned, evacuated, scored, scores_turned, have_expanded, spread_out,
         copied, maxed, max_spread, have_shifted, exped, messaged, summed, added, masks_loaded,
         dropped, falls) = (sem(n) for n in names)
        block = ctx.enter_context(nc.Block())

        @block.sync
        def _(sp):
            sp.dma_start(masks[:, :], masks_in).then_inc(masks_loaded, 16)

            def turn(n, k):
                g, s = n + 6, (k + 6) % LONG
                if not there(g):
                    return
                sp.wait_ge(added, g + 1)
                sp.dma_start(rc[:, s, :, :].rearrange("p j r -> p (j r)"),
                             R.rec_dst[ds(g * GE, GE), :].rearrange("(p j) r -> p (j r)", j=GT)).then_inc(rec_in[s], 16)

            skewed(sp, NG, turn)

        @block.gpsimd
        def _(pool):
            def turn(n, k):
                g, s, sl = n + 3, (k + 3) % DEPTH, (k + 3) % LONG
                if not there(g):
                    return
                pool.wait_ge(added, g + (LONG - DEPTH + 1))
                pool.wait_ge(rec_in[sl], landed(g, sl, slots=LONG))
                pool.sem_inc(ordered, 1)
                for j in range(GT):
                    pool.indirect_dma_start(got[:, s, j, :], None, table,
                                            bass.IndirectOffsetOnAxis(rc[:, sl, j, R_IDX:R_IDX + 1], 0)).then_inc(got_in[s], 16)
                    pool.indirect_dma_start(keyed[:, s, j, :], None, keys,
                                            bass.IndirectOffsetOnAxis(rc[:, sl, j, R_KEY:R_KEY + 1], 0)).then_inc(got_in[s], 16)

            skewed(pool, NG, turn)

        @block.scalar
        def _(act):
            act.sem_inc(evacuated, 1)
            act.wait_ge(masks_loaded, 16)

            def turn(n, k):
                g, s = n + 3, (k + 3) % DEPTH
                if there(g):
                    act.wait_ge(turned, g + 1)
                    act.activation(placet[:, s, :, :], pt[0:P, :].rearrange("p (j e) -> p j e", e=128), ACT.Copy)
                    act.drain().then_inc(evacuated, 1)
                g, s = n + 2, (k + 2) % DEPTH
                if there(g):
                    act.wait_ge(scores_turned, g + 1)
                    for h in range(H0):
                        act.activation(expanded[:, s % 2, h, :], ps[:, 0:128], ACT.Copy, scale=by_head[:, h:h + 1])
                    act.drain().then_inc(have_expanded, 1)
                g, s = n + 1, (k + 1) % DEPTH
                if there(g):
                    act.wait_ge(dropped, g + 1)
                    act.activation(alpha[:, s % 2, :], drop[:, s % 2, :], ACT.Exp).then_inc(falls, 1)
                    act.wait_ge(have_shifted, g + 1)
                    act.activation(msg[:, s % 2, :, D:W], shifted[:, s % 2, :, :], ACT.Exp)
                    act.drain().then_inc(exped, 1)
                g = n + 2
                if there(g):
                    for u in range(2 * GT):
                        j, h = u // 2, (u % 2) * 4
                        act.wait_ge(spread_out, g * (2 * GT) + (u + 1))
                        act.activation(spaced[:, j, h:h + 4, :], spread[:, u % 4, :].rearrange("p (h e) -> p h e", e=128),
                                       ACT.Copy).then_inc(copied, 1)

            skewed(act, NG, turn)

        @block.tensor
        def _(pe):
            def turn(n, k):
                g, s = n + 3, (k + 3) % DEPTH
                if there(g):
                    pe.wait_ge(placed, g + 1)
                    pe.wait_ge(evacuated, g + 1)
                    for j in range(GT):
                        last = pe.transpose(pt[0:P, j * 128:(j + 1) * 128], place[:, s, j, :], R.identf[:, :])
                    last.then_inc(turned, 1)
                g, s = n + 2, (k + 2) % DEPTH
                if there(g):
                    pe.wait_ge(scored, g + 1)
                    pe.transpose(ps[:, 0:128], score[:, s, :, :].rearrange("p j h -> p (j h)"), R.identf[:, :])\
                        .then_inc(scores_turned, 1)
                g, s = n + 1, (k + 1) % DEPTH
                if there(g):
                    pe.wait_ge(maxed, g + 1)
                    pe.wait_ge(evacuated, g + 4 if not isinstance(n, int) or there(n + 3) else NG + 1)
                    for j in range(GT):
                        last = pe.matmul(pm[:, j * H0:(j + 1) * H0], placet[:, s, j, :], new[:, s % 2, :], start=True, stop=True)
                    last.then_inc(max_spread, 1)
                g, s = n + 2, (k + 2) % DEPTH
                if there(g):
                    pe.wait_ge(have_expanded, g + 1)
                    for u in range(2 * GT):
                        j, h = u // 2, (u % 2) * 4
                        pe.wait_ge(copied, g * (2 * GT) + (u + 1))
                        pe.matmul(spread[:, u % 4, :], by_tile[:, j, :], expanded[:, s % 2, h:h + 4, :], start=True,
                                  stop=True).then_inc(spread_out, 1)
                g, s = n + 1, (k + 1) % DEPTH
                if there(g):
                    pe.wait_ge(messaged, g + 1)
                    for j in range(GT):
                        last = pe.matmul(pa[:, 0:W], place[:, s, j, :], msg[:, s % 2, j, :], start=(j == 0), stop=(j == GT - 1))
                    last.then_inc(summed, 1)

            skewed(pe, NG, turn)

        @block.vector
        def _(dve):
            tile_regs = [dve.alloc_register(f"{name}_dve_tile{k}") for k in range(2)]
            dve.memset(acc, 0.0)
            dve.memset(high[:, :], NEG)
            dve.wait_ge(masks_loaded, 16)
            dve.tensor_copy(by_tile[:, :, :], masks[:, H0:].rearrange("q (j p) -> q j p", p=P))
            dve.drain()
            dve.sem_inc(added, LONG)
            dve.sem_inc(copied, 4)

            def turn(n, k):
                g, s, sl = n + 3, (k + 3) % DEPTH, (k + 3) % LONG
                if there(g):
                    dve.wait_ge(rec_in[sl], landed(g, sl, slots=LONG))
                    nodes = [128, GT, P]
                    dve.tensor_tensor(place[:, s, :, :],
                                      R.iota[:, 0:P].rearrange("p (a e) -> p a e", a=1).broadcast_to(nodes),
                                      rcf[:, sl, :, R_LOC:R_LOC + 1].broadcast_to(nodes), ALU.is_equal)
                if there(n + 1):
                    dve.reg_load(tile_regs[(k + 1) % 2], R.tile_dst[0:1, ds(n + 1, 1)])
                if there(g):
                    dve.drain().then_inc(placed, 1)
                g, s, sl = n + 2, (k + 2) % DEPTH, (k + 2) % LONG
                if there(g):
                    dve.wait_ge(got_in[s], landed(g, s, 2 * GT))
                    dve.tensor_tensor(prod[:, :, :], keyed[:, s, :, :], got[:, s, :, 0:D], ALU.mult)
                    digits = [128, GT, DIGIT]
                    for a, r in ((H0, R_HI), (H0 + DIGIT, R_LO)):
                        dve.tensor_tensor(score[:, s, :, a:a + DIGIT],
                                          R.iota[:, 0:DIGIT].rearrange("p (a e) -> p a e", a=1).broadcast_to(digits),
                                          rcf[:, sl, :, r:r + 1].broadcast_to(digits), ALU.is_equal)
                    dve.drain()
                    dve.tensor_reduce(score[:, s, :, 0:H0], prod[:, :, :].rearrange("p j (h e) -> p j h e", e=DH), AX.X, ALU.add)
                    dve.drain().then_inc(scored, 1)
                g, s = n + 1, (k + 1) % DEPTH
                if there(g):
                    dve.wait_ge(copied, (g + 1) * (2 * GT) + 4)
                    for a, b in ((spaced[:, 0:2, :, :], spaced[:, 2:4, :, :]), (spaced[:, 0, :, :], spaced[:, 1, :, :]),
                                 (spaced[:, 0, :, 0:64], spaced[:, 0, :, 64:128]), (spaced[:, 0, :, 0:32], spaced[:, 0, :, 32:64])):
                        dve.tensor_tensor(a, a, b, ALU.max)
                        dve.drain()
                    dve.tensor_reduce(gmax[:, :], spaced[:, 0, :, 0:32], AX.X, ALU.max)
                    b1 = dve.snap(tile_regs[(k + 1) % 2])
                    old = high[:, ds(b1 * H0, H0)]
                    dve.drain()
                    dve.tensor_tensor(new[:, s % 2, :], old, gmax[:, :], ALU.max)
                    dve.drain()
                    dve.sem_inc(maxed, 1)
                    dve.tensor_tensor(drop[:, s % 2, :], old, new[:, s % 2, :], ALU.subtract)
                    dve.drain().then_inc(dropped, 1)
                    dve.tensor_copy(old, new[:, s % 2, :])
                if there(n):
                    b0 = dve.snap(tile_regs[k % 2])
                    dve.wait_ge(summed, n + 1)
                    into = acc[:, ds(b0 * W, W)]
                    dve.tensor_tensor(into, into, pa[:, 0:W], ALU.add)
                    dve.drain().then_inc(added, 1)
                if there(g):
                    dve.wait_ge(max_spread, g + 1)
                    dve.tensor_tensor(shifted[:, s % 2, :, :], score[:, s, :, 0:H0],
                                      pm[:, 0:JH].rearrange("p (j h) -> p j h", h=H0), ALU.subtract)
                    dve.drain().then_inc(have_shifted, 1)
                    dve.wait_ge(falls, g + 1)
                    intov = acc[:, ds(b1 * W, D)].rearrange("p (h e) -> p h e", e=DH)
                    dve.tensor_tensor(intov, intov, alpha[:, s % 2, :].rearrange("p (h a) -> p h a", a=1)
                                      .broadcast_to([P, H0, DH]), ALU.mult)
                    dve.tensor_tensor(acc[:, ds(b1 * W + D, H0)], acc[:, ds(b1 * W + D, H0)], alpha[:, s % 2, :], ALU.mult)
                    dve.wait_ge(exped, g + 1)
                    dve.tensor_tensor(msg[:, s % 2, :, 0:D].rearrange("p j (h e) -> p j h e", e=DH),
                                      got[:, s, :, D:2 * D].rearrange("p j (h e) -> p j h e", e=DH),
                                      msg[:, s % 2, :, D:W].rearrange("p j (h a) -> p j h a", a=1)
                                      .broadcast_to([128, GT, H0, DH]), ALU.mult)
                    dve.drain().then_inc(messaged, 1)

            skewed(dve, NG, turn)


def first_graph_layer(nc, R, a):
    W = D + H0
    with ExitStack() as ctx:
        def sb(n, shape, dt=F32):
            return ctx.enter_context(nc.sbuf_tensor(f"g0_{n}", shape, dt))

        acc = sb("acc", [P, NT * W])
        table = nc.dram_tensor("g0_table", (N, 2 * D), F32).ap()
        keys = nc.dram_tensor("g0_keys", (N + 1, D), F32).ap()
        zero = sb("zero", [1, D])
        zeroed, zero_stored = nc.alloc_semaphore("g0_zeroed"), nc.alloc_semaphore("g0_zero_stored")
        with nc.Block() as block:
            @block.vector
            def _(dve):
                dve.memset(zero[:, :], 0.0).then_inc(zeroed, 1)

            @block.sync
            def _(sp):
                sp.wait_ge(zeroed, 1)
                sp.dma_start(keys[N:N + 1, :], zero[:, :]).then_inc(zero_stored, 16)
                sp.wait_ge(zero_stored, 16)
        with ExitStack() as inner:
            wsb = inner.enter_context(nc.sbuf_tensor("g0_w", [128, KC, 3 * D], F32))
            bsb = inner.enter_context(nc.sbuf_tensor("g0_b", [P, 3 * D], F32))

            def finish(dve, t, ps, out):
                dve.tensor_tensor(out, ps[:, 0:2 * D], bsb[:, 0:2 * D], ALU.add)
                dve.drain()
                dve.tensor_scalar(out[:, 0:D], out[:, 0:D], float(DH) ** -0.5, None, ALU.mult)

            rows_stage(nc, R, "g0qv", wsb[:, :, 0:2 * D], 2 * D, finish,
                       loads=[(wsb[:, :, 0:D], chunks_of(a["L0_gnn_Wq"], D)), (wsb[:, :, D:2 * D], chunks_of(a["L0_gnn_Wv"], D)),
                              (bsb[:, 0:D], row_of(a["L0_gnn_bq"], P)), (bsb[:, D:2 * D], row_of(a["L0_gnn_bv"], P))],
                       store=lambda t: table[ds(t * P, P), :])

            def finish_k(dve, t, ps, out):
                dve.tensor_tensor(out, ps[:, 0:D], bsb[:, 2 * D:3 * D], ALU.add)

            rows_stage(nc, R, "g0k", wsb[:, :, 2 * D:3 * D], D, finish_k,
                       loads=[(wsb[:, :, 2 * D:3 * D], chunks_of(a["L0_gnn_Wk"], D)),
                              (bsb[:, 2 * D:3 * D], row_of(a["L0_gnn_bk"], P))],
                       store=lambda t: keys[ds(t * P, P), :])
        attention_edge_stage(nc, R, "g0e", table, keys, a["spread_masks"], acc[:, :])
        z = sb("z", [P, NT, H0])
        block = ctx.enter_context(nc.Block())

        @block.vector
        def _(dve):
            accv = acc[:, :].rearrange("p (t w) -> p t w", w=W)
            dve.tensor_scalar(z[:, :, :], accv[:, :, D:W], 1e-16, None, ALU.max)
            dve.drain()
            dve.reciprocal(z[:, :, :], z[:, :, :])
            dve.drain()

            def normalize(t, k):
                v = acc[:, ds(t * W, D)].rearrange("p (h e) -> p h e", e=DH)
                zt = z[:, ds(t, 1), :].rearrange("p a h -> p h a").broadcast_to([P, H0, DH])
                dve.tensor_tensor(v, v, zt, ALU.mult)
                dve.drain()
                dve.tensor_tensor(node_tile(R.X, t), node_tile(R.X, t), acc[:, ds(t * W, D)], ALU.add)

            pairs(dve, NT, normalize)


def softmax_mixer(nc, R, name, w_qkv, w_out, b_out, g_pre=None, mem_kv=None, g_out=None):
    HID, HEADS, HD = 128, 4, 32
    S = 3 * HID + 1
    second = g_pre is not None
    with ExitStack() as ctx:
        def sb(n, shape, dt=F32):
            return ctx.enter_context(nc.sbuf_tensor(f"{name}_{n}", shape, dt))

        def sem(n):
            return nc.alloc_semaphore(f"{name}_{n}")

        qkv = sb("qkv", [P, NT * S])
        view = qkv[:, :].rearrange("p (t s) -> p t s", s=S)
        wout = sb("wout", [128, D])
        bout = sb("bout", [P, D])
        M = sb("M", [128, 1, D])
        tmp = sb("tmp", [P, NT * D])
        rn = sb("rn", [P, NT])
        ss = sb("ss", [P, NT])
        if second:
            rms_stage(nc, f"{name}_pre", R.XN, tmp, ss, rn)
            gp = sb("gp", [128, KC])
            gout = sb("gout", [P, D])
            memk = sb("memk", [MEM, HID])
            memkt = sb("memkt", [HID, MEM])
            memv = sb("memv", [MEM, HID + 1])
            O = sb("O", [P, NT * D])
        with ExitStack() as inner:
            w = inner.enter_context(nc.sbuf_tensor(f"{name}_w", [128, KC, 3 * HID], F32))
            loads = [(w[:, :, :], chunks_of(w_qkv, 3 * HID)), (wout[:, :], w_out), (bout[:, :], row_of(b_out, P))]
            if second:
                loads += [(gp[:, :], g_pre)]
                loads += [(gout[:, :], row_of(g_out, P)),
                          (memk[:, :].rearrange("m (h d) -> m h d", d=HD), mem_kv[0].rearrange("h d m -> m h d")),
                          (memv[:, 0:HID].rearrange("m (h d) -> m h d", d=HD), mem_kv[1].rearrange("h d m -> m h d")),
                          (memkt[:, :], mem_kv[0].rearrange("h d m -> (h d) m"))]

            def before(dve):
                dve.memset(view[:, :, 3 * HID:S], 1.0)

            def finish(dve, t, ps, out):
                if second:
                    dve.tensor_scalar(qkv[:, ds(t * S, 3 * HID)], ps[:, 0:3 * HID], rn[:, ds(t, 1)], None, ALU.mult)
                else:
                    dve.tensor_copy(qkv[:, ds(t * S, 3 * HID)], ps[:, 0:3 * HID])

            if second:
                scale_weights_stage(nc, f"{name}_sw", loads, w, gp, float(D) ** 0.5)
                loads = []
            rows_stage(nc, R, f"{name}_qkv", w[:, :, :], 3 * HID, finish, loads=loads, before=before)

        cmax = sb("cmax", [P, HID])
        kmax = sb("kmax", [HID, 1])
        mmax = sb("mmax", [HID, 1])
        dmax = sb("dmax", [HID, HID])
        rowmax = sb("rowmax", [P, HID])
        ctx_sb = sb("ctx_sb", [HID, HID])
        ctx_t = sb("ctx_t", [HID, HID])
        zr = sb("zr", [HID, 1])
        heads = sb("heads", [HID, HEADS])
        qred = sb("qred", [P, NT * HEADS])
        (have_cmax, cmax_turned, have_diag, row_spread, ready, exped, summed, have_ctx, ctx_turned, have_t, have_m,
         q_ready, q_exped) = (sem(n) for n in (
             "have_cmax", "cmax_turned", "have_diag", "row_spread", "shifted", "exped", "summed", "have_ctx",
             "ctx_turned", "have_t", "have_m", "q_ready", "q_exped"))
        with nc.psum_tensor(f"{name}_p", [128, 5, 512], F32) as banks, nc.Block() as block:
            p1, p2, p3, p4, p5 = (banks[:, n, :] for n in range(5))
            keysv = view[:, :, HID:2 * HID]
            queries = view[:, :, 0:HID].rearrange("p t (h e) -> p t h e", e=HD)
            qr = qred[:, :].rearrange("p (t h a) -> p t h a", h=HEADS, a=1).broadcast_to([P, NT, HEADS, HD])

            @block.vector
            def _(dve):
                if second:
                    dve.memset(memv[:, HID:HID + 1], 1.0)
                    dve.tensor_reduce(qred[:, :], queries, AX.X, ALU.max)
                    dve.drain()
                    dve.tensor_tensor(queries, queries, qr, ALU.subtract)
                    dve.drain().then_inc(q_ready, 1)
                dve.tensor_reduce(cmax[:, :], view[:, :, HID:2 * HID].rearrange("p t c -> p c t"), AX.X, ALU.max)
                dve.drain().then_inc(have_cmax, 1)
                dve.wait_ge(cmax_turned, 1)
                dve.tensor_reduce(kmax[:, :], p1[:, 0:P], AX.X, ALU.max)
                dve.drain()
                if second:
                    dve.tensor_reduce(mmax[:, :], memkt[:, :], AX.X, ALU.max)
                    dve.drain()
                    dve.tensor_tensor(kmax[:, :], kmax[:, :], mmax[:, :], ALU.max)
                    dve.drain()
                dve.tensor_scalar(dmax[:, :], R.identf[:, :], kmax[:, :], None, ALU.mult)
                dve.drain().then_inc(have_diag, 1)
                dve.wait_ge(row_spread, 1)
                dve.tensor_copy(rowmax[:, :], p2[0:P, 0:HID])
                dve.drain()
                dve.tensor_tensor(keysv, keysv, rowmax[:, :].rearrange("p (a c) -> p a c", a=1).broadcast_to([P, NT, HID]),
                                  ALU.subtract)
                if second:
                    dve.tensor_tensor(memk[:, :], memk[:, :], rowmax[0:MEM, :], ALU.subtract)
                dve.drain().then_inc(ready, 1)
                if second:
                    dve.wait_ge(q_exped, 1)
                    dve.tensor_reduce(qred[:, :], queries, AX.X, ALU.add)
                    dve.drain()
                    dve.reciprocal(qred[:, :], qred[:, :])
                    dve.drain()
                    dve.tensor_tensor(queries, queries, qr, ALU.mult)
                dve.memset(heads[:, :], 0.0)
                dve.drain()
                for h in range(HEADS):
                    dve.memset(heads[h * HD:(h + 1) * HD, h:h + 1], float(HD) ** -0.5)
                dve.wait_ge(summed, 1)
                dve.reciprocal(zr[:, :], p3[:, HID:HID + 1])
                dve.drain()
                for h in range(HEADS):
                    dve.tensor_scalar(ctx_sb[:, h * HD:(h + 1) * HD], p3[:, h * HD:(h + 1) * HD], zr[:, :],
                                      heads[:, h:h + 1], ALU.mult, ALU.mult)
                dve.drain().then_inc(have_ctx, 1)
                dve.wait_ge(ctx_turned, 1)
                dve.tensor_copy(ctx_t[:, :], p4[:, 0:HID])
                dve.drain().then_inc(have_t, 1)
                dve.wait_ge(have_m, 1)
                dve.tensor_copy(M[:, 0, :], p5[:, 0:D])

            @block.scalar
            def _(act):
                if second:
                    act.wait_ge(q_ready, 1)
                    act.activation(queries, queries, ACT.Exp)
                    act.drain().then_inc(q_exped, 1)
                act.wait_ge(ready, 1)
                act.activation(keysv, keysv, ACT.Exp)
                if second:
                    act.activation(memk[:, :], memk[:, :], ACT.Exp)
                act.drain().then_inc(exped, 1)

            @block.tensor
            def _(pe):
                pe.wait_ge(have_cmax, 1)
                pe.transpose(p1[:, 0:P], cmax[:, :], R.identf[0:P, 0:P]).then_inc(cmax_turned, 1)
                pe.wait_ge(have_diag, 1)
                pe.matmul(p2[:, 0:HID], R.onesf[:, :], dmax[:, :], start=True, stop=True).then_inc(row_spread, 1)
                pe.wait_ge(exped, 1)
                for t in range(NT):
                    last = pe.matmul(p3[:, 0:HID + 1], view[:, t, HID:2 * HID], view[:, t, 2 * HID:S], start=(t == 0),
                                     stop=(t == NT - 1 and not second))
                if second:
                    last = pe.matmul(p3[:, 0:HID + 1], memk[:, :], memv[:, :], start=False, stop=True)
                last.then_inc(summed, 1)
                pe.wait_ge(have_ctx, 1)
                pe.transpose(p4[:, 0:HID], ctx_sb[:, :], R.identf[:, :]).then_inc(ctx_turned, 1)
                pe.wait_ge(have_t, 1)
                pe.matmul(p5[:, 0:D], ctx_t[:, :], wout[:, :], start=True, stop=True).then_inc(have_m, 1)

        if not second:
            def finish_out(dve, t, ps, out):
                x = node_tile(R.X, t)
                dve.tensor_tensor(x, x, ps[:, 0:D], ALU.add)
                dve.drain()
                dve.tensor_tensor(x, x, bout[:, :], ALU.add)

            rows_stage(nc, R, f"{name}_out", M[:, :, :], D, finish_out, rows=qkv, stride=S)
            return

        def finish_out(dve, t, ps, out):
            dve.tensor_tensor(node_tile(O, t), ps[:, 0:D], bout[:, :], ALU.add)

        rows_stage(nc, R, f"{name}_out", M[:, :, :], D, finish_out, rows=qkv, stride=S)
        rms_stage(nc, f"{name}_post", O, tmp, ss, rn)
        with nc.Block() as block:
            @block.vector
            def _(dve):
                dve.tensor_scalar(gout[:, :], gout[:, :], float(D) ** 0.5, None, ALU.mult)
                dve.drain()

                def add(t, k):
                    o, x = node_tile(O, t), node_tile(R.X, t)
                    dve.scalar_tensor_tensor(out=o, in0=o, scalar=rn[:, ds(t, 1)], in1=gout[:, :], op0=ALU.mult, op1=ALU.mult)
                    dve.tensor_tensor(x, x, node_tile(R.XN, t), ALU.add)
                    dve.drain()
                    dve.tensor_tensor(x, x, o, ALU.add)

                pairs(dve, NT, add)


def rms_stage(nc, name, src, tmp, ss, rn):
    with ExitStack() as ctx:
        squared = nc.alloc_semaphore(f"{name}_squared")
        added = nc.alloc_semaphore(f"{name}_added")
        rooted = nc.alloc_semaphore(f"{name}_rooted")
        block = ctx.enter_context(nc.Block())

        @block.scalar
        def _(act):
            act.activation(tmp[:, :], src[:, :], ACT.Square)
            act.drain().then_inc(squared, 1)
            act.wait_ge(added, 1)
            act.activation(rn[:, :], ss[:, :], ACT.Sqrt).then_inc(rooted, 1)

        @block.vector
        def _(dve):
            dve.wait_ge(squared, 1)
            dve.tensor_reduce(ss[:, :], tmp[:, :].rearrange("p (t d) -> p t d", d=D), AX.X, ALU.add)
            dve.drain().then_inc(added, 1)
            dve.wait_ge(rooted, 1)
            dve.tensor_scalar(rn[:, :], rn[:, :], 1e-12, None, ALU.max)
            dve.drain()
            dve.reciprocal(rn[:, :], rn[:, :])


def scale_weights_stage(nc, name, loads, w, g, factor):
    with ExitStack() as ctx:
        loaded = nc.alloc_semaphore(f"{name}_loaded")
        block = ctx.enter_context(nc.Block())

        @block.sync
        def _(sp):
            with nc.allow_non_contiguous_dma(reason="a few hundred words"):
                for to, of in loads:
                    sp.dma_start(to, of).then_inc(loaded, 16)
            sp.wait_ge(loaded, 16 * len(loads))

        @block.vector
        def _(dve):
            dve.wait_ge(loaded, 16 * len(loads))
            for c in range(KC):
                dve.tensor_scalar(w[:, c, :], w[:, c, :], g[:, c:c + 1], factor, ALU.mult, ALU.mult)


TS = 256


def item_tiles(experts, top):
    return (top * N + experts * (TS - 1)) // TS


class Routing:

    def __init__(self, nc, ctx, name, experts, top):
        self.experts, self.top, self.tiles = experts, top, item_tiles(experts, top)
        self.weight = ctx.enter_context(nc.sbuf_tensor(f"{name}_weight", [P, top * NT], F32))
        self.slot = ctx.enter_context(nc.sbuf_tensor(f"{name}_slot", [P, top * NT], I32))
        self.expert_of = ctx.enter_context(nc.sbuf_tensor(f"{name}_expert_of", [P, self.tiles], I32))


def router_stage(nc, R, name, gate_w, gate_b, route, capacity=None):
    experts, top = route.experts, route.top
    with ExitStack() as ctx:
        def sb(n, shape, dt=F32):
            return ctx.enter_context(nc.sbuf_tensor(f"{name}_{n}", shape, dt))

        def sem(n):
            return nc.alloc_semaphore(f"{name}_{n}")

        gw = sb("gw", [128, KC, experts])
        gb = sb("gb", [P, experts])
        lg = sb("lg", [P, NT * experts])
        lgv = lg[:, :].rearrange("p (t e) -> p t e", e=experts)
        best = sb("best", [P, NT, 8])
        besti = sb("besti", [P, NT, 8])

        def finish(dve, t, ps, out):
            dve.tensor_tensor(lg[:, ds(t * experts, experts)], ps[:, 0:experts], gb[:, :], ALU.add)

        rows_stage(nc, R, f"{name}_lg", gw[:, :, :], experts, finish,
                   loads=[(gw[:, :, :], chunks_of(gate_w, experts)), (gb[:, :], row_of(gate_b, P))])
        items = top * NT
        row = sb("row", [P, 2, experts])
        top8 = sb("top8", [P, 2, 8])
        idx8 = sb("idx8", [P, 2, 8], U32)
        diff = sb("diff", [P, NT])
        pick = sb("pick", [P, items, experts])
        count = sb("count", [P, items, experts])
        totals = sb("totals", [P, items, experts])
        ones = sb("ones", [P, items])
        ex = sb("ex", [P, NT, experts])
        number = sb("number", [P, items])
        begin = sb("begin", [P, items])
        tiles = sb("tiles", [P, experts])
        tilesi = sb("tilesi", [P, experts], I32)
        end = sb("end", [P, experts])
        start = sb("start", [P, experts])
        ended = sb("ended", [P, route.tiles, experts])
        which = sb("which", [P, route.tiles])
        ps = [ctx.enter_context(nc.psum_tensor(f"{name}_ps{k}", [P, 512], F32)) for k in range(top)]
        ps2 = [ctx.enter_context(nc.psum_tensor(f"{name}_ps2{k}", [P, 512], F32)) for k in range(top)]
        shifted, exped, picked, counted = sem("shifted"), sem("exped"), sem("picked"), sem("counted")
        block = ctx.enter_context(nc.Block())
        shape = [P, NT, experts]
        w1, w2 = route.weight[:, 0:NT], route.weight[:, (top - 1) * NT:top * NT]

        @block.scalar
        def _(act):
            act.wait_ge(shifted, 1)
            if top == 2:
                act.activation(w2, diff[:, :], ACT.Exp)
            else:
                act.activation(ex[:, :, :], ex[:, :, :], ACT.Exp)
            act.drain().then_inc(exped, 1)

        @block.tensor
        def _(pe):
            pe.wait_ge(picked, 1)
            for k in range(top):
                flat = pick[:, k * NT:(k + 1) * NT, :].rearrange("p t e -> p (t e)")
                pe.matmul(ps[k][:, 0:NT * experts], R.upto[0:P, 0:P], flat, start=True, stop=True)
                last = pe.matmul(ps2[k][:, 0:NT * experts], R.onesf[0:P, 0:P], flat, start=True, stop=True)
            last.then_inc(counted, 1)

        @block.vector
        def _(dve):
            def largest(t, k):
                dve.tensor_copy(row[:, k, :], lg[:, ds(t * experts, experts)])
                dve.drain()
                dve.max(top8[:, k, :], row[:, k, :])
                dve.drain()
                dve.max_index(idx8[:, k, :], top8[:, k, :], row[:, k, :])
                dve.drain()
                dve.tensor_copy(best[:, ds(t, 1), :], top8[:, k, :].rearrange("p (a e) -> p a e", a=1))
                dve.tensor_copy(besti[:, ds(t, 1), :], idx8[:, k, :].rearrange("p (a e) -> p a e", a=1))

            pairs(dve, NT, largest)
            dve.drain()
            iota = R.iota[0:P, 0:experts].rearrange("p (a e) -> p a e", a=1).broadcast_to(shape)
            for k in range(top):
                dve.tensor_tensor(pick[:, k * NT:(k + 1) * NT, :], iota, besti[:, :, k:k + 1].broadcast_to(shape),
                                  ALU.is_equal)
            if top == 2:
                dve.tensor_tensor(diff[:, :], best[:, :, 1], best[:, :, 0], ALU.subtract)
            else:
                dve.tensor_tensor(ex[:, :, :], lgv, best[:, :, 0:1].broadcast_to(shape), ALU.subtract)
            dve.memset(ones[:, :], 1.0)
            dve.drain().then_inc(shifted, 1)
            dve.sem_inc(picked, 1)
            dve.wait_ge(exped, 1)
            if top == 2:
                dve.tensor_scalar(w1, w2, 1.0, None, ALU.add)
            else:
                dve.tensor_reduce(w1, ex[:, :, :], AX.X, ALU.add)
            dve.drain()
            dve.reciprocal(w1, w1)
            dve.drain()
            if top == 2:
                dve.tensor_tensor(w2, w2, w1, ALU.mult)
            dve.wait_ge(counted, 1)
            for k in range(top):
                dve.tensor_copy(totals[:, k * NT:(k + 1) * NT, :],
                                ps2[k][:, 0:NT * experts].rearrange("p (t e) -> p t e", e=experts))
            dve.drain()
            for e in range(experts):
                dve.tensor_tensor_scan(count[:, :, e], ones[:, :], totals[:, :, e], 0.0, ALU.mult, ALU.add)
            dve.drain()
            dve.tensor_scalar(tilesi[:, :], count[:, items - 1, :], float(TS - 1), None, ALU.add)
            dve.tensor_tensor(totals[:, :, :], count[:, :, :], totals[:, :, :], ALU.subtract)
            dve.drain()
            dve.tensor_scalar(tilesi[:, :], tilesi[:, :], 8, None, ALU.arith_shift_right)
            for k in range(top):
                dve.tensor_tensor(count[:, k * NT:(k + 1) * NT, :], totals[:, k * NT:(k + 1) * NT, :],
                                  ps[k][:, 0:NT * experts].rearrange("p (t e) -> p t e", e=experts), ALU.add)
            dve.drain()
            dve.tensor_copy(tiles[:, :], tilesi[:, :])
            dve.tensor_tensor(count[:, :, :], count[:, :, :], pick[:, :, :], ALU.mult)
            dve.drain()
            dve.tensor_tensor_scan(end[:, :], ones[:, 0:experts], tiles[:, :], 0.0, ALU.mult, ALU.add)
            dve.tensor_reduce(number[:, :], count[:, :, :], AX.X, ALU.add)
            dve.drain()
            dve.tensor_tensor(start[:, :], end[:, :], tiles[:, :], ALU.subtract)
            over = [P, route.tiles, experts - 1]
            dve.tensor_tensor(ended[:, :, 0:experts - 1],
                              end[:, 0:experts - 1].rearrange("p (a e) -> p a e", a=1).broadcast_to(over),
                              R.iota[0:P, 0:route.tiles].rearrange("p (s a) -> p s a", a=1).broadcast_to(over), ALU.is_le)
            dve.drain()
            dve.tensor_reduce(which[:, :], ended[:, :, 0:experts - 1], AX.X, ALU.add)
            if capacity is not None:
                dve.tensor_scalar(begin[:, :], number[:, :], float(capacity), None, ALU.is_le)
                dve.drain()
                dve.tensor_tensor(w1, w1, begin[:, :], ALU.mult)
            dve.drain()
            dve.tensor_copy(route.expert_of[:, :], which[:, :])
            dve.tensor_tensor(pick[:, :, :], pick[:, :, :],
                              start[:, :].rearrange("p (a e) -> p a e", a=1).broadcast_to([P, items, experts]), ALU.mult)
            dve.drain()
            dve.tensor_reduce(begin[:, :], pick[:, :, :], AX.X, ALU.add)
            dve.drain()
            dve.tensor_scalar(begin[:, :], begin[:, :], float(TS), -1.0, ALU.mult, ALU.add)
            dve.drain()
            dve.tensor_tensor(route.slot[:, :], begin[:, :], number[:, :], ALU.add)


def dispatch_stage(nc, R, name, route, rows, of_slot):
    W = 5 * route.top
    TURNS = route.top * NT // W
    cols = route.tiles * TS // 128
    with ExitStack() as ctx:
        def sb(n, shape, dt=F32):
            return ctx.enter_context(nc.sbuf_tensor(f"{name}_{n}", shape, dt))

        def sem(n):
            return nc.alloc_semaphore(f"{name}_{n}")

        nodes = nc.dram_tensor(f"{name}_nodes", (cols * 128, 1), F32).ap()
        none = sb("none", [cols, 128])
        node = sb("node", [P, route.top, NT])
        stage_i = sb("stage_i", [P, 2, W], I32)
        stage_n = sb("stage_n", [P, 2, W])
        back = sb("back", [cols, 128])
        pt = ctx.enter_context(nc.psum_tensor(f"{name}_pt", [128, cols], F32))
        zeroed, emptied, kept, staged, issued, all_in, back_in, turned, numbered = (sem(n) for n in (
            "zeroed", "emptied", "kept", "staged", "issued", "all_in", "back_in", "turned", "numbered"))
        scattered = [sem("scattered0"), sem("scattered1")]
        block = ctx.enter_context(nc.Block())

        @block.sync
        def _(sp):
            sp.wait_ge(zeroed, 1)
            sp.dma_start(nodes.rearrange("(c p) a -> c (p a)", p=128), none[:, :]).then_inc(emptied, 16)
            sp.dma_start(rows.rearrange("(t p) d -> p t d", p=P),
                         R.XN[:, :].rearrange("p (t d) -> p t d", d=D)).then_inc(kept, 16)
            sp.wait_ge(all_in, 1)
            sp.dma_start(back[:, :], nodes.rearrange("(c p) a -> c (p a)", p=128)).then_inc(back_in, 16)
            sp.wait_ge(kept, 16)

        @block.gpsimd
        def _(pool):
            pool.iota(node[:, :, :], pattern=[[0, route.top], [P, NT]], base=0, channel_multiplier=1,
                      allow_small_or_imprecise_dtypes=True).then_inc(numbered, 1)
            pool.wait_ge(emptied, 16)

            def scatter(n, k):
                pool.wait_ge(staged, n + 1)
                pool.sem_inc(issued, 1)
                for c in range(W):
                    pool.indirect_dma_start(nodes, bass.IndirectOffsetOnAxis(stage_i[:, k, c:c + 1], 0),
                                            stage_n[:, k, c:c + 1], None).then_inc(scattered[k], 16)

            pairs(pool, TURNS, scatter)
            pool.wait_ge(scattered[0], 16 * W * (TURNS - TURNS // 2))
            pool.wait_ge(scattered[1], 16 * W * (TURNS // 2))
            pool.sem_inc(all_in, 1)

        @block.tensor
        def _(pe):
            pe.wait_ge(back_in, 16)
            pe.transpose(pt[:, :], back[:, :], R.identf[0:cols, 0:cols]).then_inc(turned, 1)

        @block.vector
        def _(dve):
            dve.memset(none[:, :], 0.0).then_inc(zeroed, 1)
            dve.wait_ge(numbered, 1)

            def stage(n, k):
                if not is_first(n):
                    dve.wait_ge(scattered[k], (n - k) * (8 * W))
                dve.tensor_copy(stage_i[:, k, :], route.slot[:, ds(n * W, W)])
                dve.tensor_copy(stage_n[:, k, :], node[:, :, :].rearrange("p k t -> p (k t)")[:, ds(n * W, W)])
                dve.drain().then_inc(staged, 1)

            pairs(dve, TURNS, stage, peel=True)
            dve.wait_ge(turned, 1)
            dve.tensor_copy(of_slot[:, :], pt[:, :])


def routed_experts_stage(nc, R, name, F, w1, b1, w2, b2, route, func, combine, ln=None):
    NF = F // 128
    NS = route.tiles
    TJ = TS // 128
    top = route.top
    rows = nc.dram_tensor(f"{name}_rows", (N, D), F32).ap()
    results = nc.dram_tensor(f"{name}_results", (NS * TS, D), F32).ap()
    with ExitStack() as ctx:
        def sb(n, shape, dt=F32):
            return ctx.enter_context(nc.sbuf_tensor(f"{name}_{n}", shape, dt))

        def sem(n):
            return nc.alloc_semaphore(f"{name}_{n}")

        of_slot = sb("of_slot", [128, NS * TJ], I32)
        dispatch_stage(nc, R, f"{name}d", route, rows, of_slot)
        w1s = sb("w1s", [128, 2, KC, F])
        w2s = sb("w2s", [128, 2, NF, D])
        b1s = sb("b1s", [128, 2, NF])
        b2s = sb("b2s", [128, 2, D])
        lns = sb("lns", [128, 2, 2 * KC])
        node = sb("node", [128, 2, TJ], I32)
        got = sb("got", [128, 2, TJ, D])
        xt = sb("xt", [128, 2, KC, TS])
        hid = sb("hid", [128, NF, TS])
        y = sb("y", [128, 2, TJ, D])
        with ExitStack() as inner:
            pt = [inner.enter_context(nc.psum_tensor(f"{name}_pt{k}", [128, KC, TS], F32)) for k in range(2)]
            p1 = [inner.enter_context(nc.psum_tensor(f"{name}_p1{k}", [128, 512], F32)) for k in range(4)]
            p2 = [inner.enter_context(nc.psum_tensor(f"{name}_p2{k}", [128, 512], F32)) for k in range(TJ)]
            w_in = [sem("w_in0"), sem("w_in1")]
            got_in = [sem("got_in0"), sem("got_in1")]
            stored = [sem("stored0"), sem("stored1")]
            turned, ready, first, acted, second, taken, tile_done, named, issued = (sem(n) for n in (
                "turned", "ready", "first", "acted", "second", "taken", "tile_done", "named",
                "issued"))
            LOADS = 5 if ln is not None else 4
            block = inner.enter_context(nc.Block())

            def weights_in(s, k):
                return (s - k) * (8 * LOADS) + 16 * LOADS

            @block.sync
            def _(sp):
                expert_reg = sp.alloc_register(f"{name}_expert")

                def load(s, k):
                    sp.wait_ge(tile_done, s + 1)
                    sp.reg_load(expert_reg, route.expert_of[0:1, ds(s, 1)])
                    one = ds(sp.snap(expert_reg), 1)
                    sp.dma_start(w1s[:, k, :, :], w1[one].rearrange("a (c k) f -> k (a c) f", k=128)).then_inc(w_in[k], 16)
                    sp.dma_start(w2s[:, k, :, :], w2[one].rearrange("a (c k) d -> k (a c) d", k=128)).then_inc(w_in[k], 16)
                    sp.dma_start(b1s[:, k, :], b1[one].rearrange("a k c -> (a k) c")).then_inc(w_in[k], 16)
                    sp.dma_start(b2s[:, k, :], b2[one].broadcast_to([128, D])).then_inc(w_in[k], 16)
                    if ln is not None:
                        sp.dma_start(lns[:, k, :], ln[one].rearrange("a k c -> (a k) c")).then_inc(w_in[k], 16)

                def put(s, k):
                    sp.wait_ge(taken, (s + 2) * TJ)
                    sp.dma_start(results[ds(s * TS, TS), :].rearrange("(j p) d -> p j d", p=128),
                                 y[:, k, :, :]).then_inc(stored[k], 16)

                def turn(s, k):
                    load(s + 1, 1 - k)
                    put(s, k)

                load(0, 0)
                pairs(sp, NS - 1, turn)
                put(NS - 1, (NS - 1) % 2)
                sp.wait_ge(stored[0], 16 * (NS - NS // 2))
                sp.wait_ge(stored[1], 16 * (NS // 2))

            @block.gpsimd
            def _(pool):
                def gather(s, k):
                    pool.wait_ge(turned, s + 1)
                    pool.tensor_copy(node[:, k, :], of_slot[:, ds(s * TJ, TJ)]).then_inc(named, 1)
                    pool.wait_ge(named, s + 1)
                    pool.sem_inc(issued, 1)
                    for j in range(TJ):
                        pool.indirect_dma_start(got[:, k, j, :], None, rows,
                                                bass.IndirectOffsetOnAxis(node[:, k, j:j + 1], 0)).then_inc(got_in[k], 16)

                pairs(pool, NS, gather)

            @block.tensor
            def _(pe):
                def turn(s, k):
                    pe.wait_ge(got_in[k], (s - k) * (8 * TJ) + 16 * TJ)
                    pe.wait_ge(ready, s + 1)
                    for c in range(KC):
                        for j in range(TJ):
                            last = pe.transpose(pt[k][:, c, j * 128:(j + 1) * 128], got[:, k, j, c * 128:(c + 1) * 128],
                                                R.identf[:, :])
                    last.then_inc(turned, 1)

                def hidden(s, k):
                    pe.wait_ge(w_in[k], weights_in(s, k))
                    pe.wait_ge(ready, s + 3)
                    for f in range(NF):
                        pe.wait_ge(acted, s * NF + (f + 1))
                        for c in range(KC):
                            last = pe.matmul(p1[f % 4][:, 0:TS], w1s[:, k, c, f * 128:(f + 1) * 128], xt[:, k, c, :],
                                             start=(c == 0), stop=(c == KC - 1))
                        last.then_inc(first, 1)

                def result(s, k):
                    pe.wait_ge(acted, s * NF + (NF + 4))
                    for j in range(TJ):
                        pe.wait_ge(taken, s * TJ + (j + 1))
                        for f in range(NF):
                            last = pe.matmul(p2[j][:, 0:D], hid[:, f, j * 128:(j + 1) * 128], w2s[:, k, f, :],
                                             start=(f == 0), stop=(f == NF - 1))
                        last.then_inc(second, 1)

                def tile(s, k):
                    hidden(s, k)
                    turn(s + 1, 1 - k)
                    result(s, k)

                pe.sem_inc(turned, 2)
                turn(0, 0)
                pairs(pe, NS - 1, tile)
                hidden(NS - 1, (NS - 1) % 2)
                result(NS - 1, (NS - 1) % 2)

            @block.scalar
            def _(act):
                act.sem_inc(acted, 4)

                def tile(s, k):
                    act.wait_ge(w_in[k], weights_in(s, k))
                    for f in range(NF):
                        act.wait_ge(first, s * NF + (f + 1))
                        act.activation(hid[:, f, :], p1[f % 4][:, 0:TS], func, bias=b1s[:, k, f:f + 1]).then_inc(acted, 1)

                pairs(act, NS, tile)

            @block.vector
            def _(dve):
                def evacuate(s, k):
                    if ln is not None:
                        dve.wait_ge(w_in[k], weights_in(s, k))
                    dve.wait_ge(turned, s + 3)
                    if ln is None:
                        dve.tensor_copy(xt[:, k, :, :], pt[k][:, :, :])
                    else:
                        for c in range(KC):
                            dve.tensor_scalar(xt[:, k, c, :], pt[k][:, c, :], lns[:, k, c:c + 1],
                                              lns[:, k, KC + c:KC + c + 1], ALU.mult, ALU.add)
                    dve.drain().then_inc(ready, 1)

                def take(s, k):
                    dve.wait_ge(w_in[k], weights_in(s, k))
                    if not is_first(s):
                        dve.wait_ge(stored[k], (s - k) * 8)
                    for j in range(TJ):
                        dve.wait_ge(second, s * TJ + (j + 1))
                        dve.tensor_tensor(y[:, k, j, :], p2[j][:, 0:D], b2s[:, k, :], ALU.add).then_inc(taken, 1)
                    dve.drain().then_inc(tile_done, 1)

                def tile(s, k):
                    evacuate(s + 1, 1 - k)
                    take(s, k)

                dve.sem_inc(ready, 2)
                dve.sem_inc(taken, TJ)
                dve.sem_inc(tile_done, 2)
                evacuate(0, 0)
                pairs(dve, NS - 1, tile, peel=True)
                take(NS - 1, (NS - 1) % 2)

        from_slot = sb("from_slot", [P, DEPTH, top], I32)
        back = sb("back", [P, DEPTH, top, D])
        back_in = [sem(f"back_in{k}") for k in range(DEPTH)]
        combined, slot_named, fetched = sem("combined"), sem("slot_named"), sem("fetched")
        columns = route.slot[:, :].rearrange("p (k t) -> p t k", k=top)
        with nc.Block() as block:
            @block.gpsimd
            def _(pool):
                def fetch(t, k):
                    pool.wait_ge(combined, t + 1)
                    pool.tensor_copy(from_slot[:, k, :], columns[:, ds(t, 1), :].rearrange("p a k -> p (a k)"))\
                        .then_inc(slot_named, 1)
                    pool.wait_ge(slot_named, t + 1)
                    pool.sem_inc(fetched, 1)
                    for j in range(top):
                        pool.indirect_dma_start(back[:, k, j, :], None, results,
                                                bass.IndirectOffsetOnAxis(from_slot[:, k, j:j + 1], 0)).then_inc(back_in[k], 16)

                rounds(pool, NT, DEPTH, fetch)

            @block.vector
            def _(dve):
                dve.sem_inc(combined, DEPTH)

                def add(t, k):
                    dve.wait_ge(back_in[k], landed(t, k, top))
                    combine(dve, t, back[:, k, :, :])
                    dve.drain().then_inc(combined, 1)

                rounds(dve, NT, DEPTH, add)


def weighted_sum(dve, route, to, t, back):
    for j in range(route.top):
        dve.scalar_tensor_tensor(out=to, in0=back[:, j, :], scalar=route.weight[:, ds(t + j * NT, 1)], in1=to,
                                 op0=ALU.mult, op1=ALU.add)
        dve.drain()


def experts_stage(nc, R, name, experts, F, w1, b1, w2, b2, G, acc, func, ln=None):
    NF = F // 128
    NQ = NCH + 1
    with ExitStack() as ctx:
        def sb(n, shape, dt=F32):
            return ctx.enter_context(nc.sbuf_tensor(f"{name}_{n}", shape, dt))

        def sem(n):
            return nc.alloc_semaphore(f"{name}_{n}")

        w1s = sb("w1s", [128, 2, KC, F])
        w2s = sb("w2s", [128, 2, NF, D])
        b1s = sb("b1s", [128, 2, NF])
        b2s = sb("b2s", [P, 2, D])
        fold = ln is not None
        if fold:
            lgs = sb("lgs", [128, 2, 2 * KC])
            w1g = sb("w1g", [128, KC, F])
            b1g = sb("b1g", [128, 2, NF])
        hid = sb("hid", [128, NF, CHUNK])
        y = sb("y", [P, 2, D])
        p1 = [ctx.enter_context(nc.psum_tensor(f"{name}_p1{k}", [128, 512], F32)) for k in range(4)]
        p2 = [ctx.enter_context(nc.psum_tensor(f"{name}_p2{k}", [P, 512], F32)) for k in range(4)]
        w_in = [sem("w_in0"), sem("w_in1")]
        first, acted, second, taken, expert_done, folded, bias_ready, begun = (sem(n) for n in (
            "first", "acted", "second", "taken", "expert_done", "folded", "bias_ready", "begun"))
        LOADS = 5 if fold else 4
        block = ctx.enter_context(nc.Block())

        @block.sync
        def _(sp):
            def load(e, k):
                sp.wait_ge(expert_done, e + 1)
                one = ds(e, 1)
                sp.dma_start(w1s[:, k, :, :], w1[one].rearrange("a (c k) f -> k (a c) f", k=128)).then_inc(w_in[k], 16)
                sp.dma_start(w2s[:, k, :, :], w2[one].rearrange("a (c k) d -> k (a c) d", k=128)).then_inc(w_in[k], 16)
                sp.dma_start(b1s[:, k, :], b1[one].rearrange("a k c -> (a k) c")).then_inc(w_in[k], 16)
                sp.dma_start(b2s[:, k, :], b2[one].broadcast_to([P, D])).then_inc(w_in[k], 16)
                if fold:
                    sp.dma_start(lgs[:, k, :], ln[one].rearrange("a k c -> (a k) c")).then_inc(w_in[k], 16)

            pairs(sp, experts, load)

        def chunk_loop(eng, e, k, body):
            eng.sem_inc(begun, 1)
            with eng.Fori(0, NCH) as c:
                body(e * NQ + c, c * CHUNK, 4, c * 4)
            body(e * NQ + NCH, NCH * CHUNK, NT - 4 * NCH, 4 * NCH)

        @block.tensor
        def _(pe):
            def expert(e, k):
                pe.wait_ge(w_in[k], (e - k) * (8 * LOADS) + 16 * LOADS)
                wk = w1g if fold else w1s[:, k, :, :]
                if fold:
                    pe.wait_ge(taken, e * NT + 4)
                    for f in range(NF):
                        for c in range(KC):
                            last = pe.matmul(p1[0][:, f:f + 1],
                                             w1s[:, k, c, f * 128:(f + 1) * 128], lgs[:, k, KC + c:KC + c + 1],
                                             start=(c == 0), stop=(c == KC - 1))
                    last.then_inc(bias_ready, 1)
                    pe.wait_ge(folded, e + 1)

                def chunk(q, at, tiles, tile):
                    n = tiles * P
                    for f in range(NF):
                        pe.wait_ge(acted, q * NF + (f + 1))
                        for c in range(KC):
                            last = pe.matmul(p1[f % 4][:, 0:n], wk[:, c, f * 128:(f + 1) * 128], R.XNT[:, c, ds(at, n)],
                                             start=(c == 0), stop=(c == KC - 1))
                        last.then_inc(first, 1)
                    pe.wait_ge(acted, q * NF + (NF + 4))
                    for j in range(tiles):
                        pe.wait_ge(taken, e * NT + tile + (j + 1 if j > 0 else 4))
                        for f in range(NF):
                            last = pe.matmul(p2[j][:, 0:D], hid[:, f, j * P:(j + 1) * P], w2s[:, k, f, :], start=(f == 0),
                                             stop=(f == NF - 1))
                        last.then_inc(second, 1)

                chunk_loop(pe, e, k, chunk)

            pairs(pe, experts, expert)

        @block.scalar
        def _(act):
            act.sem_inc(acted, 4)

            def expert(e, k):
                act.wait_ge(w_in[k], (e - k) * (8 * LOADS) + 16 * LOADS)
                bias = b1s
                if fold:
                    act.wait_ge(folded, e + 1)
                    bias = b1g

                def chunk(q, at, tiles, tile):
                    n = tiles * P
                    for f in range(NF):
                        act.wait_ge(first, q * NF + (f + 1))
                        act.activation(hid[:, f, 0:n], p1[f % 4][:, 0:n], func, bias=bias[:, k, f:f + 1]).then_inc(acted, 1)

                chunk_loop(act, e, k, chunk)

            pairs(act, experts, expert)

        @block.vector
        def _(dve):
            dve.sem_inc(taken, 4)
            dve.sem_inc(expert_done, 2)

            def expert(e, k):
                dve.wait_ge(w_in[k], (e - k) * (8 * LOADS) + 16 * LOADS)
                if fold:
                    dve.wait_ge(bias_ready, e + 1)
                    dve.tensor_tensor(b1g[:, k, :], p1[0][:, 0:NF], b1s[:, k, :], ALU.add)
                    for c in range(KC):
                        dve.tensor_scalar(w1g[:, c, :], w1s[:, k, c, :], lgs[:, k, c:c + 1], None, ALU.mult)
                    dve.drain().then_inc(folded, 1)

                def chunk(q, at, tiles, tile):
                    for j in range(tiles):
                        dve.wait_ge(second, e * NT + tile + (j + 1))
                        dve.tensor_tensor(y[:, j % 2, :], p2[j][:, 0:D], b2s[:, k, :], ALU.add)
                        dve.drain().then_inc(taken, 1)
                        to = acc[:, ds((tile + j) * D, D)]
                        dve.scalar_tensor_tensor(out=to, in0=y[:, j % 2, :], scalar=G[:, ds((tile + j) * experts + e, 1)],
                                                 in1=to, op0=ALU.mult, op1=ALU.add)
                        dve.drain()

                chunk_loop(dve, e, k, chunk)
                dve.sem_inc(expert_done, 1)

            pairs(dve, experts, expert)


def add_stage(nc, pieces):
    with nc.Block() as block:
        @block.vector
        def _(dve):
            for to, of in pieces:
                def add(t, k):
                    dve.tensor_tensor(node_tile(to, t), node_tile(to, t), node_tile(of, t), ALU.add)

                pairs(dve, NT, add)
                dve.drain()


def first_feed_forward(nc, R, a):
    E0, F0 = a["L0_ffn_w1"].shape[0], a["L0_ffn_w1"].shape[2]
    with ExitStack() as ctx:
        route = Routing(nc, ctx, "f0", E0, 2)
        gamma = ctx.enter_context(nc.sbuf_tensor("f0_gamma", [P, D], F32))
        beta = ctx.enter_context(nc.sbuf_tensor("f0_beta", [P, D], F32))
        loaded = nc.alloc_semaphore("f0_loaded")
        normalize_stage(nc, R, "f0ln", R.X, R.XN)
        router_stage(nc, R, "f0r", a["L0_ffn_gate_w"], a["L0_ffn_gate_b"], route)
        routed_experts_stage(nc, R, "f0", F0, a["L0_ffn_w1"], a["L0_ffn_b1"], a["L0_ffn_w2"], a["L0_ffn_b2"], route,
                             ACT.Relu, lambda dve, t, back: weighted_sum(dve, route, node_tile(R.XN, t), t, back))
        normalize_stage(nc, R, "f0ln2", R.XN, R.XN)
        with nc.Block() as block:
            @block.sync
            def _(sp):
                sp.dma_start(gamma[:, :], row_of(a["L0_ffn_gamma"], P)).then_inc(loaded, 16)
                sp.dma_start(beta[:, :], row_of(a["L0_ffn_beta"], P)).then_inc(loaded, 16)

            @block.vector
            def _(dve):
                dve.wait_ge(loaded, 32)

                def add(t, k):
                    n, x = node_tile(R.XN, t), node_tile(R.X, t)
                    dve.tensor_tensor(n, n, gamma[:, :], ALU.mult)
                    dve.tensor_tensor(x, x, beta[:, :], ALU.add)
                    dve.drain()
                    dve.tensor_tensor(x, x, n, ALU.add)

                pairs(dve, NT, add)


def count_stage(nc, R, scatter=None):
    edge_stage(nc, R, "cnt", "count", R.rec_dst, R.tile_dst, R.inv_count[:, :], 8, scatter=scatter)
    with ExitStack() as ctx:
        deg = ctx.enter_context(nc.sbuf_tensor("deg", [P, NT], F32))
        turned = ctx.enter_context(nc.sbuf_tensor("deg_turned", [NT, P], F32))
        pt = ctx.enter_context(nc.psum_tensor("deg_pt", [NT, P], F32))
        have_deg, rooted, inverted, have_t, copied, stored = (nc.alloc_semaphore(f"deg_{n}") for n in (
            "have", "rooted", "inverted", "have_t", "copied", "stored"))
        block = ctx.enter_context(nc.Block())

        @block.vector
        def _(dve):
            counts = R.inv_count[:, :].rearrange("p (t r) -> p t r", r=8)
            dve.tensor_reduce(deg[:, :], counts, AX.X, ALU.add)
            dve.drain()
            dve.tensor_scalar(deg[:, :], deg[:, :], 1.0, None, ALU.max)
            dve.tensor_scalar(R.inv_count[:, :], R.inv_count[:, :], 1.0, None, ALU.max)
            dve.drain().then_inc(have_deg, 1)
            dve.reciprocal(R.inv_count[:, :], R.inv_count[:, :])
            dve.wait_ge(rooted, 1)
            dve.reciprocal(deg[:, :], deg[:, :])
            dve.drain().then_inc(inverted, 1)
            dve.wait_ge(have_t, 1)
            dve.tensor_copy(turned[:, :], pt[:, :]).then_inc(copied, 1)

        @block.scalar
        def _(act):
            act.wait_ge(have_deg, 1)
            act.activation(deg[:, :], deg[:, :], ACT.Sqrt).then_inc(rooted, 1)

        @block.tensor
        def _(pe):
            pe.wait_ge(inverted, 1)
            pe.transpose(pt[:, :], deg[:, :], R.identf[0:P, 0:P]).then_inc(have_t, 1)

        @block.sync
        def _(sp):
            sp.wait_ge(copied, 1)
            sp.dma_start(R.norm_row, turned[:, :]).then_inc(stored, 16)
            sp.wait_ge(stored, 16)


def relation_graph_layer(nc, R, a):
    W = a["L1_gnn_weight"]
    RN = W.shape[0]
    table = nc.dram_tensor("g1_table", (RN * N, D), F32).ap()
    to = table.rearrange("(r n) d -> n r d", r=RN)
    with ExitStack() as ctx:
        w = ctx.enter_context(nc.sbuf_tensor("g1_w", [128, KC, 2 * D], F32))
        for r in range(0, RN, 2):
            def finish(dve, t, ps, out):
                dve.tensor_copy(out, ps[:, 0:2 * D])

            rows_stage(nc, R, f"g1t{r}", w[:, :, :], 2 * D, finish,
                       loads=[(w[:, :, 0:D], chunks_of(W[r], D)), (w[:, :, D:2 * D], chunks_of(W[r + 1], D))],
                       store=lambda t, r=r: to[ds(t * P, P), r:r + 2, :])
    with ExitStack() as ctx:
        w = ctx.enter_context(nc.sbuf_tensor("g1_root", [128, KC, D], F32))
        b = ctx.enter_context(nc.sbuf_tensor("g1_bias", [P, D], F32))

        def finish_root(dve, t, ps, out):
            x = node_tile(R.X, t)
            dve.tensor_tensor(x, x, ps[:, 0:D], ALU.add)
            dve.drain()
            dve.tensor_tensor(x, x, b[:, :], ALU.add)

        rows_stage(nc, R, "g1root", w[:, :, :], D, finish_root,
                   loads=[(w[:, :, :], chunks_of(a["L1_gnn_root"], D)), (b[:, :], row_of(a["L1_gnn_bias"], P))])
    with ExitStack() as ctx:
        acc = ctx.enter_context(nc.sbuf_tensor("g1_acc", [P, NT * D], F32))
        edge_stage(nc, R, "g1e", "relation", R.rec_dst, R.tile_dst, acc[:, :], D, table=table, idx=R_ROW,
                   spread=R.inv_count[:, :])
        add_stage(nc, [(R.X, acc)])


def second_feed_forward(nc, R, a):
    E1, F1 = a["L1_ffn_w1"].shape[0], a["L1_ffn_w1"].shape[2]
    capacity = -(-5 * N // (4 * E1))
    with ExitStack() as ctx:
        route = Routing(nc, ctx, "f1", E1, 1)
        normalize_stage(nc, R, "f1ln", R.X, R.XN)
        router_stage(nc, R, "f1r", a["L1_ffn_gate_w"], a["L1_ffn_gate_b"], route, capacity)
        with ExitStack() as inner:
            def weigh(dve, t, back):
                dve.tensor_scalar(node_tile(R.XN, t), back[:, 0, :], route.weight[:, ds(t, 1)], None, ALU.mult)

            routed_experts_stage(nc, R, "f1", F1, a["L1_ffn_w1"], a["L1_ffn_b1"], a["L1_ffn_w2"], a["L1_ffn_b2"], route,
                                 ACT.Relu, weigh)
            mask = inner.enter_context(nc.sbuf_tensor("f1_mask", [P, NT * D], U32))
            clean = inner.enter_context(nc.sbuf_tensor("f1_clean", [P, NT * D], F32))
            fill = inner.enter_context(nc.sbuf_tensor("f1_fill", [P, 1], F32))
            with nc.Block() as block:
                @block.vector
                def _(dve):
                    dve.tensor_tensor(mask[:, :], R.XN[:, :], R.XN[:, :], ALU.is_equal)
                    dve.memset(clean[:, :], 0.0)
                    dve.memset(fill[:, :], 1e4)
                    dve.drain()
                    dve.copy_predicated(clean[:, :], mask[:, :], R.XN[:, :])
                    dve.drain()
                    dve.tensor_scalar(mask[:, :], clean[:, :], 3.4028235e38, None, ALU.is_gt)
                    dve.drain()
                    dve.copy_predicated(clean[:, :], mask[:, :], fill[:, 0:1].broadcast_to([P, NT * D]))
                    dve.drain()
                    dve.tensor_scalar(mask[:, :], clean[:, :], -3.4028235e38, None, ALU.is_lt)
                    dve.memset(fill[:, :], -1e4)
                    dve.drain()
                    dve.copy_predicated(clean[:, :], mask[:, :], fill[:, 0:1].broadcast_to([P, NT * D]))
            add_stage(nc, [(R.X, clean)])


def turn_stage(nc, R, name, src, dst):
    with ExitStack() as ctx:
        staged = ctx.enter_context(nc.sbuf_tensor(f"{name}_staged", [P, 2, D], F32))
        pt = [ctx.enter_context(nc.psum_tensor(f"{name}_pt{k}", [128, KC * P], F32)) for k in range(2)]
        copied, turned, evacuated = (nc.alloc_semaphore(f"{name}_{n}") for n in ("copied", "turned", "evacuated"))
        block = ctx.enter_context(nc.Block())

        @block.gpsimd
        def _(pool):
            def stage(t, k):
                pool.wait_ge(turned, t + 1)
                pool.tensor_copy(staged[:, k, :], node_tile(src, t)).then_inc(copied, 1)

            pairs(pool, NT, stage)

        @block.tensor
        def _(pe):
            pe.sem_inc(turned, 2)

            def turn(t, k):
                pe.wait_ge(copied, t + 1)
                pe.wait_ge(evacuated, t + 1)
                for c in range(KC):
                    last = pe.transpose(pt[k][:, c * P:(c + 1) * P], staged[:, k, c * 128:(c + 1) * 128],
                                        R.identf[0:P, 0:P])
                last.then_inc(turned, 1)

            pairs(pe, NT, turn)

        @block.scalar
        def _(act):
            act.sem_inc(evacuated, 2)

            def evacuate(t, k):
                act.wait_ge(turned, t + 3)
                act.activation(dst[:, :, ds(t * P, P)], pt[k][:, :].rearrange("k (c p) -> k c p", p=P),
                               ACT.Copy).then_inc(evacuated, 1)

            pairs(act, NT, evacuate)


def batchnorm_product_stage(nc, R, name, w, src, dst, cols, scale_row=None):
    NQ = NCH + 1
    with ExitStack() as ctx:
        def sb(n, shape, dt=F32):
            return ctx.enter_context(nc.sbuf_tensor(f"{name}_{n}", shape, dt))

        def sem(n):
            return nc.alloc_semaphore(f"{name}_{n}")

        ws = sb("ws", [128, KC, D])
        gb = sb("gb", [128, 2, KC])
        stats = sb("stats", [128, NT * nc.vector.BN_STATS_DIM])
        mv = sb("mv", [128, KC, nc.vector.BN_AGGR_DIM])
        std = sb("std", [128, KC])
        scale = sb("scale", [128, KC])
        shift = sb("shift", [128, KC])
        row = sb("row", [128, N]) if scale_row is not None else None
        ps = [ctx.enter_context(nc.psum_tensor(f"{name}_ps{k}", [128, KC, 512], F32)) for k in range(2)]
        loaded, multiplied, taken, have_var, rooted, scaled = (sem(n) for n in (
            "loaded", "multiplied", "taken", "have_var", "rooted", "scaled"))
        LOADS = 3 + (scale_row is not None)
        block = ctx.enter_context(nc.Block())

        def chunk_pairs(eng, body):
            with eng.Fori(0, NCH // 2) as i:
                for k in range(2):
                    body(i * 2 + k, k, i * (2 * CHUNK) + k * CHUNK, CHUNK)
            body(NCH, 0, NCH * CHUNK, N - NCH * CHUNK)

        @block.sync
        def _(sp):
            sp.dma_start(ws[:, :, :], chunks_of(w, D)).then_inc(loaded, 16)
            sp.dma_start(gb[:, 0, :], cols[0]).then_inc(loaded, 16)
            sp.dma_start(gb[:, 1, :], cols[1]).then_inc(loaded, 16)
            if row is not None:
                sp.dma_start(row[:, :], scale_row.rearrange("t p -> (t p)").rearrange("(a n) -> a n", a=1)
                             .partition_broadcast(128)).then_inc(loaded, 16)

        @block.tensor
        def _(pe):
            pe.wait_ge(loaded, 16 * LOADS)

            def chunk(q, k, at, n):
                pe.wait_ge(taken, q + 1)
                for m in range(KC):
                    for c in range(KC):
                        last = pe.matmul(ps[k][:, m, 0:n], ws[:, c, m * 128:(m + 1) * 128], src[:, c, ds(at, n)],
                                         start=(c == 0), stop=(c == KC - 1))
                last.then_inc(multiplied, 1)

            chunk_pairs(pe, chunk)

        @block.vector
        def _(dve):
            dve.wait_ge(loaded, 16 * LOADS)
            dve.sem_inc(taken, 2)

            def chunk(q, k, at, n):
                dve.wait_ge(multiplied, q + 1)
                for m in range(KC):
                    if row is not None:
                        dve.tensor_tensor(dst[:, m, ds(at, n)], ps[k][:, m, 0:n], row[:, ds(at, n)], ALU.mult)
                    else:
                        dve.tensor_copy(dst[:, m, ds(at, n)], ps[k][:, m, 0:n])
                dve.drain().then_inc(taken, 1)

            chunk_pairs(dve, chunk)
            for m in range(KC):
                def moments(t, k):
                    dve.bn_stats(stats[:, ds(t * nc.vector.BN_STATS_DIM, nc.vector.BN_STATS_DIM)], dst[:, m, ds(t * P, P)])

                dve.drain()
                pairs(dve, NT, moments)
                dve.drain()
                dve.bn_aggr(mv[:, m, :], stats[:, :])
            dve.drain()
            dve.tensor_scalar(std[:, :], mv[:, :, 1], LN_EPS, None, ALU.add)
            dve.drain().then_inc(have_var, 1)
            dve.wait_ge(rooted, 1)
            dve.reciprocal(std[:, :], std[:, :])
            dve.drain()
            dve.tensor_tensor(scale[:, :], gb[:, 0, :], std[:, :], ALU.mult)
            dve.drain()
            dve.tensor_tensor(shift[:, :], mv[:, :, 0], scale[:, :], ALU.mult)
            dve.drain()
            dve.tensor_tensor(shift[:, :], gb[:, 1, :], shift[:, :], ALU.subtract)
            dve.drain().then_inc(scaled, 1)

        @block.scalar
        def _(act):
            act.wait_ge(have_var, 1)
            act.activation(std[:, :], std[:, :], ACT.Sqrt).then_inc(rooted, 1)
            act.wait_ge(scaled, 1)
            for m in range(KC):
                act.activation(dst[:, m, :], dst[:, m, :], ACT.Relu, bias=shift[:, m:m + 1], scale=scale[:, m:m + 1])


def store_rows_stage(nc, name, src, table):
    stored = nc.alloc_semaphore(f"{name}_stored")
    with nc.Block() as block:
        @block.sync
        def _(sp):
            sp.dma_start(table.rearrange("(t p) d -> p t d", p=P),
                         src[:, :].rearrange("p (t d) -> p t d", d=D)).then_inc(stored, 16)
            sp.wait_ge(stored, 16)


def isomorphism_graph_layer(nc, R, a):
    table = nc.dram_tensor("g2_table", (N, D), F32).ap()
    store_rows_stage(nc, "g2t", R.XN, table)
    with ExitStack() as ctx:
        acc = ctx.enter_context(nc.sbuf_tensor("g2_acc", [P, NT * D], F32))
        eps = ctx.enter_context(nc.sbuf_tensor("g2_eps", [P, 1], F32))
        loaded = nc.alloc_semaphore("g2_loaded")
        edge_stage(nc, R, "g2e", "weight", R.rec_dst, R.tile_dst, acc[:, :], D, table=table)
        with nc.Block() as block:
            @block.sync
            def _(sp):
                sp.dma_start(eps[:, :], row_of(a["L2_gnn_eps_weight"], P)).then_inc(loaded, 16)

            @block.vector
            def _(dve):
                dve.wait_ge(loaded, 16)

                def add(t, k):
                    dve.scalar_tensor_tensor(out=node_tile(acc, t), in0=node_tile(R.XN, t), scalar=eps[:, 0:1],
                                             in1=node_tile(acc, t), op0=ALU.mult, op1=ALU.add)

                pairs(dve, NT, add)
        yt = ctx.enter_context(nc.sbuf_tensor("g2_yt", [128, KC, N], F32))
        zt = ctx.enter_context(nc.sbuf_tensor("g2_zt", [128, KC, N], F32))
        turn_stage(nc, R, "g2turn", acc, yt)
        batchnorm_product_stage(nc, R, "g2a", a["L2_gnn_w1"], yt, zt,
                                (a["L2_gnn_gamma1"], a["L2_gnn_beta1"]))
        batchnorm_product_stage(nc, R, "g2b", a["L2_gnn_w2"], zt, yt,
                                (a["L2_gnn_gamma_h"], a["L2_gnn_beta_h"]), scale_row=R.norm_row)
        eye = ctx.enter_context(nc.sbuf_tensor("g2_eye", [128, KC, D], F32))

        def before(dve):
            dve.memset(eye[:, :, :], 0.0)
            dve.drain()
            for c in range(KC):
                dve.tensor_copy(eye[:, c, c * 128:(c + 1) * 128], R.identf[:, :])
            dve.drain()

        with nc.Block() as block:
            @block.vector
            def _(dve):
                before(dve)

        def finish(dve, t, ps, out):
            x = node_tile(R.X, t)
            dve.tensor_tensor(x, x, ps[:, 0:D], ALU.add)
            dve.drain()
            dve.tensor_tensor(x, x, node_tile(R.XN, t), ALU.add)

        rows_stage(nc, R, "g2back", eye[:, :, :], D, finish, cols=yt)


def head_norm_mixer(nc, R, a):
    HEADS = D // DH
    with ExitStack() as ctx:
        def sb(n, shape, dt=F32):
            return ctx.enter_context(nc.sbuf_tensor(f"m2_{n}", shape, dt))

        def sem(n):
            return nc.alloc_semaphore(f"m2_{n}")

        K = sb("K", [P, NT * D])
        V = sb("V", [P, NT * D])
        dev = sb("dev", [P, NT * D])
        red = sb("red", [P, NT * HEADS])
        par = sb("par", [P, 4, D])
        M = sb("M", [128, KC, D])
        loaded, deviated, squared, summed, rooted, ready, multiplied = (sem(n) for n in (
            "loaded", "deviated", "squared", "summed", "rooted", "ready", "multiplied"))

        def by_head(b):
            return b[:, :].rearrange("p (t e) -> p t e", e=DH)

        redw = red[:, :].rearrange("p (t a) -> p t a", a=1).broadcast_to([P, NT * HEADS, DH])
        with nc.psum_tensor("m2_ps", [128, KC, 512], F32) as ps, nc.Block() as block:
            @block.sync
            def _(sp):
                for n, v in enumerate(("kln_weight", "kln_bias", "vln_weight", "vln_bias")):
                    sp.dma_start(par[:, n, :], row_of(a[f"L2_mix_{v}"].rearrange("h a e -> (h a e)"), P)).then_inc(loaded, 16)

            @block.vector
            def _(dve):
                dve.tensor_reduce(red[:, :], by_head(R.XN), AX.X, ALU.add)
                dve.drain()
                dve.tensor_scalar(red[:, :], red[:, :], 1.0 / DH, None, ALU.mult)
                dve.drain()
                dve.tensor_tensor(by_head(dev), by_head(R.XN), redw, ALU.subtract)
                dve.drain().then_inc(deviated, 1)
                dve.wait_ge(squared, 1)
                dve.tensor_reduce(red[:, :], by_head(K), AX.X, ALU.add)
                dve.drain().then_inc(summed, 1)
                dve.wait_ge(rooted, 1)
                dve.tensor_scalar(red[:, :], red[:, :], LN_EPS, None, ALU.add)
                dve.drain()
                dve.reciprocal(red[:, :], red[:, :])
                dve.drain()
                dve.tensor_tensor(by_head(dev), by_head(dev), redw, ALU.mult)
                dve.drain()
                dve.wait_ge(loaded, 64)
                for n, to in ((0, K), (2, V)):
                    def affine(t, k):
                        dve.tensor_tensor(node_tile(to, t), node_tile(dev, t), par[:, n, :], ALU.mult)
                        dve.drain()
                        dve.tensor_tensor(node_tile(to, t), node_tile(to, t), par[:, n + 1, :], ALU.add)

                    pairs(dve, NT, affine)
                dve.drain().then_inc(ready, 1)
                dve.memset(M[:, :, :], 0.0)
                dve.wait_ge(multiplied, 1)
                dve.drain()
                for c in range(KC):
                    for h in range(128 // DH):
                        b, at = slice(h * DH, (h + 1) * DH), c * 128 + h * DH
                        dve.tensor_scalar(M[b, c, at:at + DH], ps[b, c, h * DH:(h + 1) * DH], 1.0 / N, None, ALU.mult)

            @block.scalar
            def _(act):
                act.wait_ge(deviated, 1)
                act.activation(K[:, :], dev[:, :], ACT.Square)
                act.drain().then_inc(squared, 1)
                act.wait_ge(summed, 1)
                act.activation(red[:, :], red[:, :], ACT.Sqrt, scale=1.0 / (DH - 1))
                act.drain().then_inc(rooted, 1)

            @block.tensor
            def _(pe):
                pe.wait_ge(ready, 1)
                for c in range(KC):
                    for t in range(NT):
                        b = slice(t * D + c * 128, t * D + (c + 1) * 128)
                        last = pe.matmul(ps[:, c, 0:128], K[:, b], V[:, b], start=(t == 0), stop=(t == NT - 1))
                last.then_inc(multiplied, 1)

        def finish(dve, t, ps, out):
            x = node_tile(R.X, t)
            dve.tensor_tensor(x, x, ps[:, 0:D], ALU.add)
            dve.drain()
            dve.tensor_tensor(x, x, node_tile(R.XN, t), ALU.add)

        rows_stage(nc, R, "m2out", M[:, :, :], D, finish)


def third_feed_forward(nc, R, a):
    E2, F2 = a["L2_ffn_W1"].shape[0], a["L2_ffn_W1"].shape[2]
    with ExitStack() as ctx:
        route = Routing(nc, ctx, "f2", E2, 2)
        normalize_stage(nc, R, "f2ln", R.X, R.XN)
        router_stage(nc, R, "f2r", a["L2_ffn_Wr"], a["L2_ffn_br"], route)
        normalize_stage(nc, R, "f2ln2", R.XN, R.XN)
        routed_experts_stage(nc, R, "f2", F2, a["L2_ffn_W1"], a["L2_ffn_b1"], a["L2_ffn_W2"], a["L2_ffn_b2"], route,
                             ACT.Gelu, lambda dve, t, back: weighted_sum(dve, route, node_tile(R.X, t), t, back),
                             ln=a["L2_ffn_ln"])


def attention_graph_layer(nc, R, a):
    W = D + 1
    table = nc.dram_tensor("g3_table", (N, D + 2), F32).ap()
    with ExitStack() as ctx:
        def sb(n, shape, dt=F32):
            return ctx.enter_context(nc.sbuf_tensor(f"g3_{n}", shape, dt))

        S = sb("S", [P, NT])
        acc = sb("acc", [P, NT * W])
        with ExitStack() as inner:
            w = inner.enter_context(nc.sbuf_tensor("g3_w", [128, KC, D + 2], F32))
            av = inner.enter_context(nc.sbuf_tensor("g3_a", [P, 2, D], F32))
            tmp = inner.enter_context(nc.sbuf_tensor("g3_tmp", [P, 2, D], F32))

            def finish(dve, t, ps, out):
                dve.tensor_copy(out[:, 0:D], ps[:, 0:D])
                dve.memset(out[:, D:D + 1], 1.0)
                dve.tensor_tensor(tmp[:, 0, :], ps[:, 0:D], av[:, 0, :], ALU.mult)
                dve.tensor_tensor(tmp[:, 1, :], ps[:, 0:D], av[:, 1, :], ALU.mult)
                dve.drain()
                dve.tensor_reduce(S[:, ds(t, 1)], tmp[:, 0, :], AX.X, ALU.add)
                dve.tensor_reduce(out[:, D + 1:D + 2], tmp[:, 1, :], AX.X, ALU.add)

            def before(dve):
                dve.memset(w[:, :, D:D + 2], 0.0)

            with nc.Block() as block:
                @block.vector
                def _(dve):
                    before(dve)

            rows_stage(nc, R, "g3h", w[:, :, :], D + 2, finish,
                       loads=[(w[:, :, 0:D], chunks_of(a["L3_gnn_W"], D)),
                              (av[:, 0, :], row_of(a["L3_gnn_a"][0:D], P)), (av[:, 1, :], row_of(a["L3_gnn_a"][D:2 * D], P))],
                       store=lambda t: table[ds(t * P, P), :])
        edge_stage(nc, R, "g3e", "gat", R.rec_src, R.tile_src, acc[:, :], W, table=table, spread=S[:, :])
        accv = acc[:, :].rearrange("p (t w) -> p t w", w=W)
        with nc.Block() as block:
            @block.vector
            def _(dve):
                dve.reciprocal(S[:, :], accv[:, :, D])
                dve.drain()

                def add(t, k):
                    h = acc[:, ds(t * W, D)]
                    dve.tensor_scalar(h, h, 0.0, None, ALU.max)
                    dve.drain()
                    dve.scalar_tensor_tensor(out=node_tile(R.X, t), in0=h, scalar=S[:, ds(t, 1)], in1=node_tile(R.X, t),
                                             op0=ALU.mult, op1=ALU.add)

                pairs(dve, NT, add)


def squared_mixer(nc, R, a):
    S = 3 * D
    with ExitStack() as ctx:
        def sb(n, shape, dt=F32):
            return ctx.enter_context(nc.sbuf_tensor(f"m3_{n}", shape, dt))

        def sem(n):
            return nc.alloc_semaphore(f"m3_{n}")

        q, kk, v = sb("q", [P, NT * D]), sb("k", [P, NT * D]), sb("v", [P, NT * D])
        wout = sb("wout", [128, KC, D])
        bout = sb("bout", [P, D])
        M = sb("M", [128, KC, D])
        with ExitStack() as inner:
            w = inner.enter_context(nc.sbuf_tensor("m3_w", [128, KC, D], F32))
            b = inner.enter_context(nc.sbuf_tensor("m3_b", [P, D], F32))
            for n, to in enumerate((q, kk, v)):
                part = slice(n * D, (n + 1) * D)

                def finish(dve, t, ps, out):
                    dve.tensor_tensor(node_tile(to, t), ps[:, 0:D], b[:, :], ALU.add)

                rows_stage(nc, R, f"m3p{n}", w[:, :, :], D, finish,
                           loads=[(w[:, :, :], chunks_of(a["L3_mix_W_qkv"][:, part], D)),
                                  (b[:, :], row_of(a["L3_mix_b_qkv"][part], P))])
        tmp = sb("tmp", [P, NT * D])
        red = sb("red", [P, 2, NT])
        ss = sb("ss", [P, 2, NT])
        ksum = sb("ksum", [128, KC])
        (centered, squared, normed, squared2, summed, rooted, have_norm, norm_rooted, have_kv, loaded) = (sem(n) for n in (
            "centered", "squared", "normed", "squared2", "summed", "rooted", "have_norm", "norm_rooted", "have_kv", "loaded"))
        with nc.psum_tensor("m3_ps", [128, KC, 512], F32) as ps, nc.psum_tensor("m3_pn", [128, KC, 512], F32) as pn, \
                nc.Block() as block:
            def tiles(x):
                return x[:, :].rearrange("p (t d) -> p t d", d=D)

            def wide(r):
                return r.rearrange("p (t a) -> p t a", a=1).broadcast_to([P, NT, D])

            @block.sync
            def _(sp):
                sp.dma_start(wout[:, :, :], chunks_of(a["L3_mix_W_out"], D)).then_inc(loaded, 16)
                sp.dma_start(bout[:, :], row_of(a["L3_mix_b_out"], P)).then_inc(loaded, 16)
                sp.wait_ge(loaded, 32)

            @block.vector
            def _(dve):
                both = ((0, q), (1, kk))
                for n, x in both:
                    dve.tensor_reduce(red[:, n, :], tiles(x), AX.X, ALU.add)
                dve.drain()
                dve.tensor_scalar(red[:, :, :], red[:, :, :], 1.0 / D, None, ALU.mult)
                dve.drain()
                for n, x in both:
                    dve.tensor_tensor(tiles(x), tiles(x), wide(red[:, n, :]), ALU.subtract)
                dve.drain().then_inc(centered, 1)
                dve.wait_ge(squared, 1)
                for n, x in both:
                    dve.tensor_reduce(red[:, n, :], tiles(x), AX.X, ALU.add)
                dve.drain()
                dve.tensor_scalar(red[:, :, :], red[:, :, :], 1e-7, None, ALU.add)
                dve.drain()
                dve.reciprocal(red[:, :, :], red[:, :, :])
                dve.drain()
                for n, x in both:
                    dve.tensor_tensor(tiles(x), tiles(x), wide(red[:, n, :]), ALU.mult)
                dve.drain().then_inc(normed, 1)
                dve.wait_ge(squared2, 1)
                dve.tensor_reduce(ss[:, 0, :], tiles(tmp), AX.X, ALU.add)
                dve.drain().then_inc(summed, 1)
                dve.wait_ge(rooted, 1)
                dve.tensor_scalar(ss[:, 0, :], ss[:, 0, :], 1e-12, None, ALU.max)
                dve.drain()
                dve.reciprocal(ss[:, 0, :], ss[:, 0, :])
                dve.drain()
                dve.tensor_tensor(tiles(q), tiles(q), wide(ss[:, 0, :]), ALU.mult)
                dve.wait_ge(have_kv, 1)
                dve.tensor_copy(ksum[:, :], pn[:, :, 0])
                dve.drain().then_inc(have_norm, 1)
                dve.wait_ge(norm_rooted, 1)
                dve.tensor_scalar(ksum[:, :], ksum[:, :], 1e-12, None, ALU.max)
                dve.drain()
                dve.reciprocal(ksum[:, :], ksum[:, :])
                dve.drain()
                for c in range(KC):
                    dve.tensor_scalar(M[:, c, :], ps[:, c, 0:D], ksum[:, c:c + 1], float(N) ** -0.5, ALU.mult, ALU.mult)

            @block.scalar
            def _(act):
                act.wait_ge(centered, 1)
                act.activation(q[:, :], q[:, :], ACT.Square)
                act.activation(kk[:, :], kk[:, :], ACT.Square)
                act.drain().then_inc(squared, 1)
                act.wait_ge(normed, 1)
                act.activation(tmp[:, :], q[:, :], ACT.Square)
                act.drain().then_inc(squared2, 1)
                act.wait_ge(summed, 1)
                act.activation(ss[:, 0, :], ss[:, 0, :], ACT.Sqrt)
                act.activation(tmp[:, :], kk[:, :], ACT.Square)
                act.drain().then_inc(rooted, 1)
                act.wait_ge(have_norm, 1)
                act.activation(ksum[:, :], ksum[:, :], ACT.Sqrt)
                act.drain().then_inc(norm_rooted, 1)

            @block.tensor
            def _(pe):
                pe.wait_ge(rooted, 1)
                for c in range(KC):
                    for t in range(NT):
                        at = t * D + c * 128
                        pe.matmul(ps[:, c, 0:D], kk[:, at:at + 128], v[:, t * D:(t + 1) * D], start=(t == 0), stop=(t == NT - 1))
                        last = pe.matmul(pn[:, c, 0:1], tmp[:, at:at + 128], R.onesf[0:P, 0:1], start=(t == 0), stop=(t == NT - 1))
                last.then_inc(have_kv, 1)

        def add_v(dve, t, ps, out):
            dve.tensor_tensor(node_tile(v, t), node_tile(v, t), ps[:, 0:D], ALU.add)

        rows_stage(nc, R, "m3a", M[:, :, :], D, add_v, rows=q)

        def finish_out(dve, t, ps, out):
            x = node_tile(R.X, t)
            dve.tensor_tensor(x, x, ps[:, 0:D], ALU.add)
            dve.drain()
            dve.tensor_tensor(x, x, bout[:, :], ALU.add)

        rows_stage(nc, R, "m3b", wout[:, :, :], D, finish_out, rows=v)


def fourth_feed_forward(nc, R, a):
    CAP = max(1, int(0.5 * N))
    CHOSEN = CAP - 1 if CAP > 1 else 1
    F3 = a["L3_ffn_w1"].shape[1]
    with ExitStack() as ctx:
        def sb(n, shape, dt=F32):
            return ctx.enter_context(nc.sbuf_tensor(f"f3_{n}", shape, dt))

        normalize_stage(nc, R, "f3ln", R.X, R.XN)
        add_stage(nc, [(R.X, R.XN)])
        G = sb("G", [P, NT])
        with ExitStack() as inner:
            def sbi(n, shape, dt=F32):
                return inner.enter_context(nc.sbuf_tensor(f"f3_{n}", shape, dt))

            wr = sbi("wr", [128, KC, 1])
            br = sbi("br", [P, 1])

            def finish(dve, t, ps, out):
                dve.tensor_tensor(G[:, ds(t, 1)], ps[:, 0:1], br[:, :], ALU.add)

            rows_stage(nc, R, "f3r", wr[:, :, :], 1, finish,
                       loads=[(wr[:, :, :].rearrange("k c a -> k (c a)"), a["L3_ffn_wr"]), (br[:, :], row_of(a["L3_ffn_br"], P))])
            row_dram = nc.dram_tensor("f3_row_dram", (NT, P), F32).ap()
            turned = sbi("turned", [NT, P])
            row = sbi("row", [P, N])
            ge = sbi("ge", [P, 2, N])
            own = sbi("own", [P, 2, P])
            rank = sbi("rank", [P, 3, NT])
            pt = inner.enter_context(nc.psum_tensor("f3_pt", [NT, P], F32))
            have_t, copied, stored, spread = (nc.alloc_semaphore(f"f3_{n}") for n in (
                "have_t", "copied", "stored", "spread"))
            with nc.Block() as block:
                @block.tensor
                def _(pe):
                    pe.transpose(pt[:, :], G[:, :], R.identf[0:P, 0:P]).then_inc(have_t, 1)

                @block.sync
                def _(sp):
                    sp.wait_ge(copied, 1)
                    sp.dma_start(row_dram, turned[:, :]).then_inc(stored, 16)
                    sp.wait_ge(stored, 16)
                    sp.dma_start(row[:, :], row_dram.rearrange("t p -> (t p)").rearrange("(a n) -> a n", a=1)
                                 .partition_broadcast(P)).then_inc(spread, 16)

                @block.vector
                def _(dve):
                    dve.wait_ge(have_t, 1)
                    dve.tensor_copy(turned[:, :], pt[:, :]).then_inc(copied, 1)
                    dve.wait_ge(spread, 16)

                    dve.memset(rank[:, 1, 0:1], 0.0)
                    for t in range(NT):
                        k = t % 2
                        mine = G[:, t:t + 1]
                        at = t * P
                        if t > 0:
                            dve.tensor_scalar(ge[:, k, 0:at], row[:, 0:at], mine, 0.0, ALU.is_ge, ALU.add,
                                              accum_out=rank[:, 1, t:t + 1])
                        dve.tensor_scalar(ge[:, k, at:N], row[:, at:N], mine, 0.0, ALU.is_gt, ALU.add,
                                          accum_out=rank[:, 0, t:t + 1])
                        dve.tensor_scalar(own[:, k, :], row[:, at:at + P], mine, None, ALU.is_equal)
                        dve.drain()
                        dve.scalar_tensor_tensor(out=own[:, k, :], in0=R.upto[0:P, 0:P], scalar=0.0, in1=own[:, k, :],
                                                 op0=ALU.is_equal, op1=ALU.mult)
                        dve.drain()
                        dve.tensor_reduce(rank[:, 2, t:t + 1], own[:, k, :], AX.X, ALU.add)
                    dve.drain()
                    for part in range(2):
                        dve.tensor_tensor(rank[:, 2, :], rank[:, 2, :], rank[:, part, :], ALU.add)
                        dve.drain()
                    dve.tensor_scalar(rank[:, 2, :], rank[:, 2, :], float(CHOSEN), None, ALU.is_lt)
                    dve.drain()
                    dve.tensor_tensor(G[:, :], G[:, :], rank[:, 2, :], ALU.mult)
        experts_stage(nc, R, "f3", 1, F3, a["L3_ffn_w1"].rearrange("(a d) f -> a d f", a=1), a["L3_ffn_b1"],
                      a["L3_ffn_w2"].rearrange("(a f) d -> a f d", a=1), a["L3_ffn_b2"].rearrange("(a d) -> a d", a=1), G,
                      R.X[:, :], ACT.Gelu_apprx_tanh)


def prepare_edges(nc, R, a):
    with ExitStack() as ctx:
        by_dst = EdgeSort(nc, ctx, "bydst", a["dst"], a["src"], R.rec_dst, R.tile_dst, a["edge_type_8"], a["edge_weight"])
        by_src = EdgeSort(nc, ctx, "bysrc", a["src"], a["dst"], R.rec_src, R.tile_src)
        sort_stage(nc, R, [by_dst, by_src])
        count_stage(nc, R, scatter=by_src.scatter)


def program(nc, a, out):
    with ExitStack() as ctx:
        R = Resident(nc, ctx)
        with nc.cleanup_on_exit():
            setup_stage(nc, R, a["x"])
            prepare_edges(nc, R, a)
        with nc.cleanup_on_exit():
            normalize_stage(nc, R, "ln0", R.X, R.XN)
            first_graph_layer(nc, R, a)
            softmax_mixer(nc, R, "m0", a["L0_mix_W_qkv"], a["L0_mix_W_out"], a["L0_mix_b_out"])
        with nc.cleanup_on_exit():
            first_feed_forward(nc, R, a)
        with nc.cleanup_on_exit():
            normalize_stage(nc, R, "ln1", R.X, R.XN)
            relation_graph_layer(nc, R, a)
        with nc.cleanup_on_exit():
            softmax_mixer(nc, R, "m1", a["L1_mix_w_qkv"], a["L1_mix_w_out"], a["L1_mix_b_out"], a["L1_mix_g_pre"],
                          a["L1_mix_mem_kv"], a["L1_mix_g_out"])
        with nc.cleanup_on_exit():
            second_feed_forward(nc, R, a)
        with nc.cleanup_on_exit():
            normalize_stage(nc, R, "ln2", R.X, R.XN)
            isomorphism_graph_layer(nc, R, a)
            head_norm_mixer(nc, R, a)
        with nc.cleanup_on_exit():
            third_feed_forward(nc, R, a)
        with nc.cleanup_on_exit():
            normalize_stage(nc, R, "ln3", R.X, R.XN)
            attention_graph_layer(nc, R, a)
        with nc.cleanup_on_exit():
            squared_mixer(nc, R, a)
        with nc.cleanup_on_exit():
            fourth_feed_forward(nc, R, a)
            store_rows_stage(nc, "out", R.X, out)


_OUT = "out_0_dram"


def _columns(a):
    return np.ascontiguousarray(np.moveaxis(a.reshape(a.shape[:-1] + (-1, 128)), -1, -2))


def _spread_masks():
    head = np.ones((GT, 32, H0), np.float32)
    head[:, :H0] = np.eye(H0)
    node = np.arange(P)
    tile = np.ones((32, P), np.float32)
    tile[H0:H0 + DIGIT] = NEG * (node // DIGIT != np.arange(DIGIT)[:, None])
    tile[H0 + DIGIT:] = NEG * (node % DIGIT != np.arange(DIGIT)[:, None])
    tiles = np.einsum("jk,rp->jrkp", np.eye(GT), tile).astype(np.float32)
    return np.concatenate([head.reshape(128, H0), tiles.reshape(128, GT * P)], axis=1)


def kernel(**inputs):
    import concourse.bacc as _bacc
    from concourse.bass_utils import run_bass_kernel_spmd as _run

    columns = ("L0_ffn_b1", "L1_ffn_b1", "L2_ffn_b1", "L3_ffn_b1", "L2_gnn_gamma1", "L2_gnn_beta1", "L2_gnn_gamma_h",
               "L2_gnn_beta_h", "L1_mix_g_pre")
    arrays = {}
    for name, value in inputs.items():
        value = np.asarray(value)
        if name in ("L1_mix_t", "L3_ffn_attention_mask"):
            continue
        if name in ("L2_gnn_w1", "L2_gnn_w2"):
            value = value.T
        if name == "L3_ffn_wr":
            value = _columns(value[:, 0])
        if name in columns:
            value = _columns(value.reshape(1, -1) if name == "L3_ffn_b1" else value)
        arrays[name] = np.ascontiguousarray(value)
    arrays["L2_ffn_ln"] = np.ascontiguousarray(
        np.concatenate([_columns(arrays.pop("L2_ffn_ln_g")), _columns(arrays.pop("L2_ffn_ln_b"))], axis=-1))

    arrays["spread_masks"] = _spread_masks()

    nc = _bacc.Bacc("TRN2", target_bir_lowering=False, num_devices=1)
    ap = {name: nc.dram_tensor(f"in_{name}", v.shape, mybir.dt.from_np(v.dtype), kind="ExternalInput").ap()
          for name, v in arrays.items()}
    out = nc.dram_tensor(_OUT, (N, D), F32, kind="ExternalOutput").ap()
    program(nc, ap, out)
    result = _run(nc, [{f"in_{name}": v for name, v in arrays.items()}], core_ids=[0])
    return result.results[0][_OUT]
```
